# Optimizing a Trainium2 kernel written in Bass

```python
import numpy as np
import jax
import jax.numpy as jnp

def _softmax(x, axis=-1):
    return jax.nn.softmax(x, axis=axis)

def _gelu(x):
    return jax.nn.gelu(x, approximate=True)

def _silu(x):
    return jax.nn.silu(x)

def _sigmoid(x):
    return jax.nn.sigmoid(x)

def _layernorm(x, axis=-1, eps=1e-05):
    m = jnp.mean(x, axis=axis, keepdims=True)
    v = jnp.var(x, axis=axis, keepdims=True)
    return (x - m) / jnp.sqrt(v + eps)

def _scatter_add(tgt, idx, src, axis=0):
    return tgt.at[idx].add(src)

def _segment_sum(src, seg, n):
    return jax.ops.segment_sum(src, seg, n)
kernel_name = 'mk_decoder_preln_d4_seqx_r8_3357f6'

def setup_inputs(seed: int=0):
    np.random.seed(seed)
    _w = jnp.asarray

    def _rec_inputs():
        import jax
        import jax.numpy as jnp
        _rk = jax.random.key(seed)
        x = -0.0002928 + 1 * jax.random.normal(jax.random.fold_in(_rk, 1), (8, 128, 128), jnp.float32)
        _lenS = 128 - jax.random.randint(jax.random.fold_in(_rk, 7), (8,), 0, max(1, 128 // 4) + 1, jnp.int32)
        _lenS2 = 128 - jax.random.randint(jax.random.fold_in(_rk, 8), (8,), 0, max(1, 128 // 4) + 1, jnp.int32)
        _ctx_1024P = jax.random.normal(jax.random.fold_in(_rk, 11), (8, 16, 128), jnp.float32)
        _ctx_1024c = jax.random.dirichlet(jax.random.fold_in(_rk, 511), 0.3 * jnp.ones((16,), jnp.float32), (8, 128))
        _ctx_1024t = jnp.einsum('bsk,bkd->bsd', _ctx_1024c, _ctx_1024P)
        _ctx_1024t = _ctx_1024t * jax.lax.rsqrt(jnp.mean(jnp.square(_ctx_1024t)) + 1e-12) * 0.953939
        ctx_1024 = -1.39393e-06 + 0.999914 * (_ctx_1024t + 0.3 * jax.random.normal(jax.random.fold_in(_rk, 611), (8, 128, 128), jnp.float32))
        _validS = jnp.arange(128)[None, :] < _lenS[:, None]
        _validS2 = jnp.arange(128)[None, :] < _lenS2[:, None]
        _causal = jnp.tril(jnp.ones((128, 128), dtype=bool))
        mask_BxSxS2_bf0 = jnp.logical_not(jnp.ones((8, 128, 128), dtype=bool))
        return (x, ctx_1024, mask_BxSxS2_bf0)
    x, ctx_1024, mask_BxSxS2_bf0 = _rec_inputs()

    def _L0_attn_setup():
        import jax, jax.numpy as jnp
        import numpy as np
        HEADS = 16
        DIM_HEAD = 64
        key = jax.random.key(seed)
        ks = jax.random.split(key, 5)
        b, n, dim = (4, 256, 128)
        return {'x': jax.random.normal(ks[0], (b, n, dim), dtype=jnp.float32), 'Wq': jax.random.normal(ks[1], (dim, HEADS * DIM_HEAD), dtype=jnp.float32) * dim ** (-0.5), 'Wkv': jax.random.normal(ks[2], (dim, DIM_HEAD), dtype=jnp.float32) * dim ** (-0.5), 'null_kv': jax.random.normal(ks[3], (DIM_HEAD,), dtype=jnp.float32), 'Wout': jax.random.normal(ks[4], (HEADS * DIM_HEAD, dim), dtype=jnp.float32) * (HEADS * DIM_HEAD) ** (-0.5)}
    _L0_attn_all = _L0_attn_setup()
    _L0_attn_in = {k: v for k, v in _L0_attn_all.items() if k in ('Wq', 'Wkv', 'null_kv', 'Wout')}
    del _L0_attn_all

    def _L0_xattn_setup():
        import jax, jax.numpy as jnp
        import numpy as np
        N, T, D_KQ, E_KQ, D_V, E_V, H = (2, 256, 128, 128, 128, 128, 16)

        def _shifted_causal_mask(T):
            row = jnp.arange(T)[:, None]
            col = jnp.arange(T)[None, :]
            mask = jnp.where(col < row, 0.0, -jnp.inf).astype(jnp.float32)
            return mask.at[0, 0].set(0.0)
        key = jax.random.key(seed)
        ks = jax.random.split(key, 12)

        def lin(k, fan_in, fan_out):
            return jax.random.normal(k, (fan_in, fan_out), jnp.float32) * (1.0 / np.sqrt(fan_in))
        return {'kq': jax.random.normal(ks[0], (N, T, D_KQ), jnp.float32), 'v': jax.random.normal(ks[1], (N, T, D_V), jnp.float32), 'Wk': lin(ks[2], D_KQ, E_KQ), 'bk': jnp.zeros((E_KQ,), jnp.float32), 'Wq': lin(ks[3], D_KQ, E_KQ), 'bq': jnp.zeros((E_KQ,), jnp.float32), 'Wv': lin(ks[4], D_V, E_V), 'bv': jnp.zeros((E_V,), jnp.float32), 'W1': lin(ks[5], E_V, 4 * E_V), 'b1': jnp.zeros((4 * E_V,), jnp.float32), 'W2': lin(ks[6], 4 * E_V, E_V), 'b2': jnp.zeros((E_V,), jnp.float32)}
    _L0_xattn_all = _L0_xattn_setup()
    _L0_xattn_in = {k: v for k, v in _L0_xattn_all.items() if k in ('Wk', 'bk', 'Wq', 'bq', 'Wv', 'bv', 'W1', 'b1', 'W2', 'b2')}
    del _L0_xattn_all

    def _L0_ffn_setup():
        import jax, jax.numpy as jnp
        import numpy as np
        HIDDEN = 128
        INNER = 512

        def _weight_quant(w):
            scale = 1.0 / jnp.clip(jnp.mean(jnp.abs(w)), 1e-05)
            wq = jnp.clip(jnp.round(w * scale), -1.0, 1.0) / scale
            return w + jax.lax.stop_gradient(wq - w)

        def _act_quant(x):
            scale = 127.0 / jnp.clip(jnp.max(jnp.abs(x), axis=-1, keepdims=True), 1e-05)
            xq = jnp.clip(jnp.round(x * scale), -128.0, 127.0) / scale
            return x + jax.lax.stop_gradient(xq - x)

        def _bitlinear(x, w):
            return jnp.einsum('bsi,oi->bso', _act_quant(x), _weight_quant(w))
        key = jax.random.key(seed)
        k0, k1, k2, k3 = jax.random.split(key, 4)
        x = jax.random.normal(k0, (4, 256, HIDDEN), dtype=jnp.float32)
        w_gate = jax.random.normal(k1, (INNER, HIDDEN), dtype=jnp.float32) / np.sqrt(HIDDEN)
        w_up = jax.random.normal(k2, (INNER, HIDDEN), dtype=jnp.float32) / np.sqrt(HIDDEN)
        w_down = jax.random.normal(k3, (HIDDEN, INNER), dtype=jnp.float32) / np.sqrt(INNER)
        return {'x': x, 'w_gate': w_gate, 'w_up': w_up, 'w_down': w_down}
    _L0_ffn_all = _L0_ffn_setup()
    _L0_ffn_in = {k: v for k, v in _L0_ffn_all.items() if k in ('w_gate', 'w_up', 'w_down')}
    del _L0_ffn_all

    def _L1_attn_setup():
        import jax, jax.numpy as jnp
        import numpy as np
        D_MODEL, D_STATE, D_CONV, EXPAND, HEADDIM, NGROUPS, CHUNK = (128, 64, 4, 2, 64, 1, 64)
        D_INNER = EXPAND * D_MODEL
        NHEADS = D_INNER // HEADDIM
        CONV_DIM = D_INNER + 2 * NGROUPS * D_STATE
        D_IN_PROJ = 2 * D_INNER + 2 * NGROUPS * D_STATE + NHEADS
        EPS = 1e-05

        def segsum(x):
            T = x.shape[-1]
            i = jnp.arange(T)[:, None]
            j = jnp.arange(T)[None, :]
            xr = jnp.where(i > j, x[..., :, None], 0.0)
            s = jnp.cumsum(xr, axis=-2)
            return jnp.where(i >= j, s, -jnp.inf)

        def _forward(u, in_proj_w, conv_w, conv_b, init_states, dt_bias, A_log, D, norm_w, out_proj_w):
            b, L, _ = u.shape
            zxbcdt = jnp.einsum('bld,ed->ble', u, in_proj_w)
            z = zxbcdt[..., :D_INNER]
            xBC = zxbcdt[..., D_INNER:D_INNER + CONV_DIM]
            dt = jax.nn.softplus(zxbcdt[..., D_INNER + CONV_DIM:] + dt_bias)
            xp = jnp.pad(xBC, ((0, 0), (D_CONV - 1, 0), (0, 0)))
            xBC = sum((xp[:, k:k + L, :] * conv_w[:, k] for k in range(D_CONV))) + conv_b
            xBC = jax.nn.silu(xBC)
            x = xBC[..., :D_INNER].reshape(b, L, NHEADS, HEADDIM)
            Bm = xBC[..., D_INNER:D_INNER + NGROUPS * D_STATE].reshape(b, L, NGROUPS, D_STATE)
            Cm = xBC[..., D_INNER + NGROUPS * D_STATE:].reshape(b, L, NGROUPS, D_STATE)
            A = -jnp.exp(A_log)
            Bm = jnp.repeat(Bm, NHEADS // NGROUPS, axis=2)
            Cm = jnp.repeat(Cm, NHEADS // NGROUPS, axis=2)
            X = x * dt[..., None]
            Adt = A * dt
            c = L // CHUNK
            Xc = X.reshape(b, c, CHUNK, NHEADS, HEADDIM)
            Bc = Bm.reshape(b, c, CHUNK, NHEADS, D_STATE)
            Cc = Cm.reshape(b, c, CHUNK, NHEADS, D_STATE)
            Ac = Adt.reshape(b, c, CHUNK, NHEADS).transpose(0, 3, 1, 2)
            A_cumsum = jnp.cumsum(Ac, axis=-1)
            Lmat = jnp.exp(segsum(Ac))
            Y_diag = jnp.einsum('bclhn,bcshn,bhcls,bcshp->bclhp', Cc, Bc, Lmat, Xc)
            decay_states = jnp.exp(A_cumsum[..., -1:] - A_cumsum)
            states = jnp.einsum('bclhn,bhcl,bclhp->bchpn', Bc, decay_states, Xc)
            init = jnp.broadcast_to(init_states, (b,) + init_states.shape)[:, None]
            states = jnp.concatenate([init, states], axis=1)
            decay_chunk = jnp.exp(segsum(jnp.pad(A_cumsum[..., -1], ((0, 0), (0, 0), (1, 0)))))
            new_states = jnp.einsum('bhzc,bchpn->bzhpn', decay_chunk, states)
            states = new_states[:, :-1]
            state_decay_out = jnp.exp(A_cumsum)
            Y_off = jnp.einsum('bclhn,bchpn,bhcl->bclhp', Cc, states, state_decay_out)
            Y = (Y_diag + Y_off).reshape(b, L, NHEADS, HEADDIM) + x * D[:, None]
            y = Y.reshape(b, L, D_INNER)
            y = y * jax.nn.silu(z)
            y = y * jax.lax.rsqrt(jnp.mean(y * y, axis=-1, keepdims=True) + EPS) * norm_w
            return jnp.einsum('bld,ed->ble', y, out_proj_w)
        key = jax.random.key(seed)
        ks = jax.random.split(key, 10)
        B, L = (4, 512)
        u = jax.random.normal(ks[0], (B, L, D_MODEL), dtype=jnp.float32)
        in_proj_w = jax.random.normal(ks[1], (D_IN_PROJ, D_MODEL), dtype=jnp.float32) * D_MODEL ** (-0.5)
        conv_w = jax.random.normal(ks[2], (CONV_DIM, D_CONV), dtype=jnp.float32) * D_CONV ** (-0.5)
        conv_b = jax.random.normal(ks[3], (CONV_DIM,), dtype=jnp.float32) * 0.02
        init_states = jax.random.normal(ks[4], (NHEADS, HEADDIM, D_STATE), dtype=jnp.float32) * 0.02
        dt = jnp.exp(jax.random.uniform(ks[5], (NHEADS,)) * (np.log(0.1) - np.log(0.001)) + np.log(0.001))
        dt = jnp.clip(dt, 0.0001, None)
        dt_bias = dt + jnp.log(-jnp.expm1(-dt))
        A_log = jnp.log(jax.random.uniform(ks[6], (NHEADS,), minval=1.0, maxval=16.0))
        D = jnp.ones((NHEADS,), dtype=jnp.float32)
        norm_w = jnp.ones((D_INNER,), dtype=jnp.float32)
        out_proj_w = jax.random.normal(ks[7], (D_MODEL, D_INNER), dtype=jnp.float32) * D_INNER ** (-0.5)
        return {'u': u, 'in_proj_w': in_proj_w, 'conv_w': conv_w, 'conv_b': conv_b, 'init_states': init_states, 'dt_bias': dt_bias, 'A_log': A_log, 'D': D, 'norm_w': norm_w, 'out_proj_w': out_proj_w}
    _L1_attn_all = _L1_attn_setup()
    _L1_attn_in = {k: v for k, v in _L1_attn_all.items() if k in ('in_proj_w', 'conv_w', 'conv_b', 'init_states', 'dt_bias', 'A_log', 'D', 'norm_w', 'out_proj_w')}
    del _L1_attn_all

    def _L1_xattn_setup():
        import jax, jax.numpy as jnp
        import numpy as np
        B, T, D, H = (2, 256, 128, 16)
        DH = D // H
        key = jax.random.key(seed)
        ks = jax.random.split(key, 11)
        s = 1.0 / np.sqrt(D)
        return {'q': jax.random.normal(ks[0], (B, T, D), jnp.float32), 'k': jax.random.normal(ks[1], (B, T, D), jnp.float32), 'v': jax.random.normal(ks[2], (B, T, D), jnp.float32), 'wq_w': jax.random.normal(ks[3], (D, D), jnp.float32) * s, 'wq_b': jnp.zeros((D,), jnp.float32), 'wk_w': jax.random.normal(ks[4], (D, D), jnp.float32) * s, 'wk_b': jnp.zeros((D,), jnp.float32), 'wv_w': jax.random.normal(ks[5], (D, D), jnp.float32) * s, 'wv_b': jnp.zeros((D,), jnp.float32), 'wo_w': jax.random.normal(ks[6], (D, D), jnp.float32) * s, 'wo_b': jnp.zeros((D,), jnp.float32)}
    _L1_xattn_all = _L1_xattn_setup()
    _L1_xattn_in = {k: v for k, v in _L1_xattn_all.items() if k in ('wq_w', 'wq_b', 'wk_w', 'wk_b', 'wv_w', 'wv_b', 'wo_w', 'wo_b')}
    del _L1_xattn_all

    def _L1_ffn_setup():
        import jax, jax.numpy as jnp
        import numpy as np
        B, L, D = (2, 128, 128)
        HID, E, K = (256, 8, 2)
        key = jax.random.key(seed)
        ks = jax.random.split(key, 4)
        std = 0.02
        return {'x': jax.random.normal(ks[0], (B, L, D), dtype=jnp.float32), 'router_scale': jnp.ones((D,), dtype=jnp.float32), 'router_w': jax.random.normal(ks[1], (D, E), dtype=jnp.float32) * std, 'gating_w': jax.random.normal(ks[2], (E, 2, HID, D), dtype=jnp.float32) * std, 'linear_w': jax.random.normal(ks[3], (E, HID, D), dtype=jnp.float32) * std, 'per_expert_scale': jnp.ones((E,), dtype=jnp.float32)}
    _L1_ffn_all = _L1_ffn_setup()
    _L1_ffn_in = {k: v for k, v in _L1_ffn_all.items() if k in ('router_scale', 'router_w', 'gating_w', 'linear_w', 'per_expert_scale')}
    del _L1_ffn_all

    def _L2_attn_setup():
        import jax, jax.numpy as jnp
        import numpy as np
        import math
        B, L, HID = (2, 512, 128)
        NH, DK, DV = (12, 64, 128)
        KD, VD, CS = (NH * DK, NH * DV, 4)
        SCALE = DK ** (-0.5)

        def _causal_depthwise_conv(x, w):
            c, k = w.shape
            xt = jnp.transpose(x, (0, 2, 1))
            out = jax.lax.conv_general_dilated(xt, w[:, None, :], window_strides=(1,), padding=[(k - 1, 0)], feature_group_count=c, dimension_numbers=('NCH', 'OIH', 'NCH'))
            return jnp.transpose(out, (0, 2, 1))

        def _l2norm(x, eps=1e-06):
            return x * jax.lax.rsqrt(jnp.sum(x * x, axis=-1, keepdims=True) + eps)

        def _gated_delta_net(hidden_states, Wq, Wk, Wv, Wg, Wo, conv_q, conv_k, conv_v, Wgk, Wb, b_b, A_log, dt_bias, g_norm_weight):
            b, l, _ = hidden_states.shape
            q = jax.nn.silu(_causal_depthwise_conv(hidden_states @ Wq, conv_q))
            k = jax.nn.silu(_causal_depthwise_conv(hidden_states @ Wk, conv_k))
            v = jax.nn.silu(_causal_depthwise_conv(hidden_states @ Wv, conv_v))
            gk = -jnp.exp(A_log) * jax.nn.softplus(hidden_states @ Wgk + dt_bias)
            beta = jax.nn.sigmoid(hidden_states @ Wb + b_b)
            q = jnp.transpose(q.reshape(b, l, NH, DK), (0, 2, 1, 3))
            k = jnp.transpose(k.reshape(b, l, NH, DK), (0, 2, 1, 3))
            v = jnp.transpose(v.reshape(b, l, NH, DV), (0, 2, 1, 3))
            q = _l2norm(q) * SCALE
            k = _l2norm(k)
            qs = jnp.moveaxis(q, 2, 0)
            ks_ = jnp.moveaxis(k, 2, 0)
            vs = jnp.moveaxis(v, 2, 0)
            bs = jnp.moveaxis(beta, 1, 0)
            gs = jnp.moveaxis(gk, 1, 0)

            def step(S, inp):
                qt, kt, vt, bt, gt = inp
                S = S * jnp.exp(gt)[..., None, None]
                kv = jnp.einsum('bhk,bhkv->bhv', kt, S)
                delta = (vt - kv) * bt[..., None]
                S = S + jnp.einsum('bhk,bhv->bhkv', kt, delta)
                ot = jnp.einsum('bhk,bhkv->bhv', qt, S)
                return (S, ot)
            S0 = jnp.zeros((b, NH, DK, DV), hidden_states.dtype)
            _, os_ = jax.lax.scan(step, S0, (qs, ks_, vs, bs, gs))
            o = jnp.moveaxis(os_, 0, 1)
            g = (hidden_states @ Wg).reshape(b, l, NH, DV)
            var = jnp.mean(o * o, axis=-1, keepdims=True)
            o = o * jax.lax.rsqrt(var + 1e-05) * g_norm_weight
            o = o * g * jax.nn.sigmoid(g)
            return o.reshape(b, l, VD) @ Wo
        key = jax.random.key(seed)
        ks = jax.random.split(key, 16)
        rn = lambda i, shape, s: jax.random.normal(ks[i], shape, jnp.float32) * s
        hidden_states = rn(0, (B, L, HID), 1.0)
        Wq = rn(1, (HID, KD), HID ** (-0.5))
        Wk = rn(2, (HID, KD), HID ** (-0.5))
        Wv = rn(3, (HID, VD), HID ** (-0.5))
        Wg = rn(4, (HID, VD), HID ** (-0.5))
        Wo = rn(5, (VD, HID), VD ** (-0.5))
        conv_q = rn(6, (KD, CS), 0.5)
        conv_k = rn(7, (KD, CS), 0.5)
        conv_v = rn(8, (VD, CS), 0.5)
        Wgk = rn(9, (HID, NH), HID ** (-0.5))
        Wb = rn(10, (HID, NH), HID ** (-0.5))
        b_b = rn(11, (NH,), 0.1)
        A = jax.random.uniform(ks[12], (NH,), jnp.float32, 0.5, 16.0)
        A_log = jnp.log(A)
        dt = jnp.exp(jax.random.uniform(ks[13], (NH,), jnp.float32) * (math.log(0.1) - math.log(0.001)) + math.log(0.001))
        dt = jnp.clip(dt, 0.0001, None)
        dt_bias = dt + jnp.log(-jnp.expm1(-dt))
        g_norm_weight = jnp.ones((DV,), jnp.float32)
        return dict(hidden_states=hidden_states, Wq=Wq, Wk=Wk, Wv=Wv, Wg=Wg, Wo=Wo, conv_q=conv_q, conv_k=conv_k, conv_v=conv_v, Wgk=Wgk, Wb=Wb, b_b=b_b, A_log=A_log, dt_bias=dt_bias, g_norm_weight=g_norm_weight)
    _L2_attn_all = _L2_attn_setup()
    _L2_attn_in = {k: v for k, v in _L2_attn_all.items() if k in ('Wq', 'Wk', 'Wv', 'Wg', 'Wo', 'conv_q', 'conv_k', 'conv_v', 'Wgk', 'Wb', 'b_b', 'A_log', 'dt_bias', 'g_norm_weight')}
    del _L2_attn_all

    def _L2_xattn_setup():
        import jax, jax.numpy as jnp
        import numpy as np
        D_MODEL = 128
        N_HEAD = 16

        def _split_heads(x):
            B, S, D = x.shape
            return x.reshape(B, S, N_HEAD, D // N_HEAD).transpose(0, 2, 1, 3)
        key = jax.random.key(seed)
        ks = jax.random.split(key, 11)
        B, S, D = (2, 256, D_MODEL)
        s = 1.0 / np.sqrt(D)
        inp = {'q': jax.random.normal(ks[0], (B, S, D), jnp.float32), 'k': jax.random.normal(ks[1], (B, S, D), jnp.float32), 'v': jax.random.normal(ks[2], (B, S, D), jnp.float32), 'w_q': jax.random.normal(ks[3], (D, D), jnp.float32) * s, 'b_q': jnp.zeros((D,), jnp.float32), 'w_k': jax.random.normal(ks[4], (D, D), jnp.float32) * s, 'b_k': jnp.zeros((D,), jnp.float32), 'w_v': jax.random.normal(ks[5], (D, D), jnp.float32) * s, 'b_v': jnp.zeros((D,), jnp.float32), 'w_o': jax.random.normal(ks[6], (D, D), jnp.float32) * s, 'b_o': jnp.zeros((D,), jnp.float32)}
        return inp
    _L2_xattn_all = _L2_xattn_setup()
    _L2_xattn_in = {k: v for k, v in _L2_xattn_all.items() if k in ('w_q', 'b_q', 'w_k', 'b_k', 'w_v', 'b_v', 'w_o', 'b_o')}
    del _L2_xattn_all

    def _L2_ffn_setup():
        import jax, jax.numpy as jnp
        import numpy as np
        H = 128
        E = 64
        K = 8
        G = 8
        TOPK_GROUP = 4
        I_MOE = 64
        I_SHARED = 256
        SCALE = 2.5

        def relu2(x):
            return jnp.square(jax.nn.relu(x))

        def _route(xf, router_w, correction_bias):
            T = xf.shape[0]
            logits = xf @ router_w.T
            scores = jax.nn.sigmoid(logits)
            sfc = scores + correction_bias[None, :]
            grp = sfc.reshape(T, G, E // G)
            top2, _ = jax.lax.top_k(grp, 2)
            group_scores = top2.sum(-1)
            _, gidx = jax.lax.top_k(group_scores, TOPK_GROUP)
            gmask = jnp.zeros((T, G), sfc.dtype).at[jnp.arange(T)[:, None], gidx].set(1.0)
            emask = jnp.repeat(gmask, E // G, axis=1)
            masked = jnp.where(emask > 0, sfc, 0.0)
            _, tidx = jax.lax.top_k(masked, K)
            tw = jnp.take_along_axis(scores, tidx, axis=1)
            tw = tw / (tw.sum(-1, keepdims=True) + 1e-20)
            return (tidx, tw * SCALE)
        key = jax.random.key(seed)
        ks = jax.random.split(key, 7)
        x = jax.random.normal(ks[0], (2, 128, H), dtype=jnp.float32)
        router_w = jax.random.normal(ks[1], (E, H), dtype=jnp.float32) * 0.02
        correction_bias = jax.random.normal(ks[2], (E,), dtype=jnp.float32) * 0.01
        up_w = jax.random.normal(ks[3], (E, H, I_MOE), dtype=jnp.float32) * 0.02
        down_w = jax.random.normal(ks[4], (E, I_MOE, H), dtype=jnp.float32) * 0.02
        shared_up_w = jax.random.normal(ks[5], (H, I_SHARED), dtype=jnp.float32) * 0.02
        shared_down_w = jax.random.normal(ks[6], (I_SHARED, H), dtype=jnp.float32) * 0.02
        return {'x': x, 'router_w': router_w, 'correction_bias': correction_bias, 'up_w': up_w, 'down_w': down_w, 'shared_up_w': shared_up_w, 'shared_down_w': shared_down_w}
    _L2_ffn_all = _L2_ffn_setup()
    _L2_ffn_in = {k: v for k, v in _L2_ffn_all.items() if k in ('router_w', 'correction_bias', 'up_w', 'down_w', 'shared_up_w', 'shared_down_w')}
    del _L2_ffn_all

    def _L3_attn_setup():
        import jax, jax.numpy as jnp
        import numpy as np
        D = 128
        H = 16
        N = D // H
        B = 4
        T = 256
        NLAYERS = 12
        LAYER_ID = 6
        EPS = 1e-05 * 64

        def _forward(x, w_r, w_k, w_v, w_g, w_o, time_maa_k, time_maa_v, time_maa_r, time_maa_g, time_decay, time_faaaa, ln_g, ln_b):
            Bs, Ts, C = x.shape
            if Ts % 32 == 0:
                Q = 32
            elif Ts % 128 == 0:
                Q = 128
            else:
                Q = Ts
            nC = Ts // Q
            xs = jnp.pad(x, ((0, 0), (1, 0), (0, 0)))[:, :-1]
            xx = xs - x
            xk = x + xx * time_maa_k
            xv = x + xx * time_maa_v
            xr = x + xx * time_maa_r
            xg = x + xx * time_maa_g
            r = (xr @ w_r.T).reshape(Bs, Ts, H, N).transpose(0, 2, 1, 3)
            k = (xk @ w_k.T).reshape(Bs, Ts, H, N).transpose(0, 2, 3, 1)
            v = (xv @ w_v.T).reshape(Bs, Ts, H, N).transpose(0, 2, 1, 3)
            g = jax.nn.silu(xg @ w_g.T)
            w = jnp.exp(-jnp.exp(time_decay))
            u = time_faaaa
            ws = (w ** Q)[None, :, None, None]
            q = jnp.arange(Q)
            wk = (w[:, None] ** (Q - 1 - q)[None, :])[None, :, None, :]
            wb = (w[:, None] ** q[None, :])[None, :, :, None]
            ii = q[:, None]
            jj = q[None, :]
            e = jnp.maximum(ii - jj - 1, 0)
            Wmat = jnp.where((jj < ii)[None], w[:, None, None] ** e[None], 0.0)
            Wmat = Wmat + jnp.eye(Q, dtype=x.dtype)[None] * u[:, None, None]
            Wmat = Wmat[None]
            rC = r.reshape(Bs, H, nC, Q, N).transpose(2, 0, 1, 3, 4)
            kC = k.reshape(Bs, H, N, nC, Q).transpose(3, 0, 1, 2, 4)
            vC = v.reshape(Bs, H, nC, Q, N).transpose(2, 0, 1, 3, 4)

            def step(state, inp):
                rr, kk, vv = inp
                y = rr @ kk * Wmat @ vv + rr @ state * wb
                state = ws * state + kk * wk @ vv
                return (state, y)
            state0 = jnp.zeros((Bs, H, N, N), x.dtype)
            _, yC = jax.lax.scan(step, state0, (rC, kC, vC))
            y = yC.transpose(1, 2, 0, 3, 4).reshape(Bs, H, Ts, N)
            y = y.transpose(0, 2, 1, 3).reshape(Bs * Ts, H, N)
            mu = y.mean(-1, keepdims=True)
            var = y.var(-1, keepdims=True)
            y = (y - mu) / jnp.sqrt(var + EPS)
            y = y.reshape(Bs, Ts, C) * ln_g + ln_b
            y = y * g
            return y @ w_o.T
        key = jax.random.key(seed)
        ks = jax.random.split(key, 6)
        r01 = LAYER_ID / (NLAYERS - 1)
        r10 = 1.0 - LAYER_ID / NLAYERS
        ddd = np.arange(D, dtype=np.float64) / D
        maa_k = (1.0 - ddd ** r10).astype(np.float32)
        maa_v = (1.0 - (ddd ** r10 + 0.3 * r01)).astype(np.float32)
        maa_r = (1.0 - ddd ** (0.5 * r10)).astype(np.float32)
        maa_g = maa_r.copy()
        hh = np.arange(H, dtype=np.float64)
        decay = (-6.0 + 5.0 * (hh / (H - 1)) ** (0.7 + 1.3 * r01)).astype(np.float32)
        faaaa = (r01 * (1.0 - hh / (H - 1))).astype(np.float32)
        s = 0.02
        return {'x': jax.random.normal(ks[0], (B, T, D), jnp.float32), 'w_r': jax.random.normal(ks[1], (D, D), jnp.float32) * s, 'w_k': jax.random.normal(ks[2], (D, D), jnp.float32) * s, 'w_v': jax.random.normal(ks[3], (D, D), jnp.float32) * s, 'w_g': jax.random.normal(ks[4], (D, D), jnp.float32) * s, 'w_o': jax.random.normal(ks[5], (D, D), jnp.float32) * s, 'time_maa_k': jnp.asarray(maa_k), 'time_maa_v': jnp.asarray(maa_v), 'time_maa_r': jnp.asarray(maa_r), 'time_maa_g': jnp.asarray(maa_g), 'time_decay': jnp.asarray(decay), 'time_faaaa': jnpp if False else jnp.asarray(faaaa), 'ln_g': jnp.ones((D,), jnp.float32), 'ln_b': jnp.zeros((D,), jnp.float32)}
    _L3_attn_all = _L3_attn_setup()
    _L3_attn_in = {k: v for k, v in _L3_attn_all.items() if k in ('w_r', 'w_k', 'w_v', 'w_g', 'w_o', 'time_maa_k', 'time_maa_v', 'time_maa_r', 'time_maa_g', 'time_decay', 'time_faaaa', 'ln_g', 'ln_b')}
    del _L3_attn_all

    def _L3_xattn_setup():
        import jax, jax.numpy as jnp
        import numpy as np
        EMBED_DIM = 128
        N_HEADS = 16
        HEAD_DIM = EMBED_DIM // N_HEADS
        key = jax.random.key(seed)
        ks = jax.random.split(key, 7)
        B, T, D = (2, 256, EMBED_DIM)
        query = jax.random.normal(ks[0], (B, T, D), dtype=jnp.float32)
        k_in = jax.random.normal(ks[1], (B, T, D), dtype=jnp.float32)
        v_in = jax.random.normal(ks[2], (B, T, D), dtype=jnp.float32)
        mask = jnp.zeros((B, T, T), dtype=jnp.bool_)
        s = 1.0 / np.sqrt(D)
        Wq = jax.random.normal(ks[3], (D, D), dtype=jnp.float32) * s
        Wk = jax.random.normal(ks[4], (D, D), dtype=jnp.float32) * s
        Wv = jax.random.normal(ks[5], (D, D), dtype=jnp.float32) * s
        Wo = jax.random.normal(ks[6], (D, D), dtype=jnp.float32) * s
        return {'query': query, 'key': k_in, 'value': v_in, 'mask': mask, 'Wq': Wq, 'Wk': Wk, 'Wv': Wv, 'Wo': Wo}
    _L3_xattn_all = _L3_xattn_setup()
    _L3_xattn_in = {k: v for k, v in _L3_xattn_all.items() if k in ('Wq', 'Wk', 'Wv', 'Wo')}
    del _L3_xattn_all

    def _L3_ffn_setup():
        import jax, jax.numpy as jnp
        import numpy as np
        from jax import lax
        D = 128
        H = 512
        E = 8
        TOPK = 2
        key = jax.random.key(seed)
        ks = jax.random.split(key, 7)
        s = 0.02
        return {'x': jax.random.normal(ks[0], (2, 256, D), dtype=jnp.float32), 'W1': jax.random.normal(ks[1], (E, D, H), dtype=jnp.float32) * s, 'b1': jnp.zeros((E, H), dtype=jnp.float32), 'W2': jax.random.normal(ks[2], (E, H, D), dtype=jnp.float32) * s, 'b2': jnp.zeros((E, D), dtype=jnp.float32), 'Wr': jax.random.normal(ks[3], (D, E), dtype=jnp.float32) * s, 'br': jnp.zeros((E,), dtype=jnp.float32)}
    _L3_ffn_all = _L3_ffn_setup()
    _L3_ffn_in = {k: v for k, v in _L3_ffn_all.items() if k in ('W1', 'b1', 'W2', 'b2', 'Wr', 'br')}
    del _L3_ffn_all
    return {'x': x, 'ctx_1024': ctx_1024, 'mask_BxSxS2_bf0': mask_BxSxS2_bf0, 'L0_attn_Wq': _L0_attn_in['Wq'], 'L0_attn_Wkv': _L0_attn_in['Wkv'], 'L0_attn_null_kv': _L0_attn_in['null_kv'], 'L0_attn_Wout': _L0_attn_in['Wout'], 'L0_xattn_Wk': _L0_xattn_in['Wk'], 'L0_xattn_bk': _L0_xattn_in['bk'], 'L0_xattn_Wq': _L0_xattn_in['Wq'], 'L0_xattn_bq': _L0_xattn_in['bq'], 'L0_xattn_Wv': _L0_xattn_in['Wv'], 'L0_xattn_bv': _L0_xattn_in['bv'], 'L0_xattn_W1': _L0_xattn_in['W1'], 'L0_xattn_b1': _L0_xattn_in['b1'], 'L0_xattn_W2': _L0_xattn_in['W2'], 'L0_xattn_b2': _L0_xattn_in['b2'], 'L0_ffn_w_gate': _L0_ffn_in['w_gate'], 'L0_ffn_w_up': _L0_ffn_in['w_up'], 'L0_ffn_w_down': _L0_ffn_in['w_down'], 'L1_attn_in_proj_w': _L1_attn_in['in_proj_w'], 'L1_attn_conv_w': _L1_attn_in['conv_w'], 'L1_attn_conv_b': _L1_attn_in['conv_b'], 'L1_attn_init_states': _L1_attn_in['init_states'], 'L1_attn_dt_bias': _L1_attn_in['dt_bias'], 'L1_attn_A_log': _L1_attn_in['A_log'], 'L1_attn_D': _L1_attn_in['D'], 'L1_attn_norm_w': _L1_attn_in['norm_w'], 'L1_attn_out_proj_w': _L1_attn_in['out_proj_w'], 'L1_xattn_wq_w': _L1_xattn_in['wq_w'], 'L1_xattn_wq_b': _L1_xattn_in['wq_b'], 'L1_xattn_wk_w': _L1_xattn_in['wk_w'], 'L1_xattn_wk_b': _L1_xattn_in['wk_b'], 'L1_xattn_wv_w': _L1_xattn_in['wv_w'], 'L1_xattn_wv_b': _L1_xattn_in['wv_b'], 'L1_xattn_wo_w': _L1_xattn_in['wo_w'], 'L1_xattn_wo_b': _L1_xattn_in['wo_b'], 'L1_ffn_router_scale': _L1_ffn_in['router_scale'], 'L1_ffn_router_w': _L1_ffn_in['router_w'], 'L1_ffn_gating_w': _L1_ffn_in['gating_w'], 'L1_ffn_linear_w': _L1_ffn_in['linear_w'], 'L1_ffn_per_expert_scale': _L1_ffn_in['per_expert_scale'], 'L2_attn_Wq': _L2_attn_in['Wq'], 'L2_attn_Wk': _L2_attn_in['Wk'], 'L2_attn_Wv': _L2_attn_in['Wv'], 'L2_attn_Wg': _L2_attn_in['Wg'], 'L2_attn_Wo': _L2_attn_in['Wo'], 'L2_attn_conv_q': _L2_attn_in['conv_q'], 'L2_attn_conv_k': _L2_attn_in['conv_k'], 'L2_attn_conv_v': _L2_attn_in['conv_v'], 'L2_attn_Wgk': _L2_attn_in['Wgk'], 'L2_attn_Wb': _L2_attn_in['Wb'], 'L2_attn_b_b': _L2_attn_in['b_b'], 'L2_attn_A_log': _L2_attn_in['A_log'], 'L2_attn_dt_bias': _L2_attn_in['dt_bias'], 'L2_attn_g_norm_weight': _L2_attn_in['g_norm_weight'], 'L2_xattn_w_q': _L2_xattn_in['w_q'], 'L2_xattn_b_q': _L2_xattn_in['b_q'], 'L2_xattn_w_k': _L2_xattn_in['w_k'], 'L2_xattn_b_k': _L2_xattn_in['b_k'], 'L2_xattn_w_v': _L2_xattn_in['w_v'], 'L2_xattn_b_v': _L2_xattn_in['b_v'], 'L2_xattn_w_o': _L2_xattn_in['w_o'], 'L2_xattn_b_o': _L2_xattn_in['b_o'], 'L2_ffn_router_w': _L2_ffn_in['router_w'], 'L2_ffn_correction_bias': _L2_ffn_in['correction_bias'], 'L2_ffn_up_w': _L2_ffn_in['up_w'], 'L2_ffn_down_w': _L2_ffn_in['down_w'], 'L2_ffn_shared_up_w': _L2_ffn_in['shared_up_w'], 'L2_ffn_shared_down_w': _L2_ffn_in['shared_down_w'], 'L3_attn_w_r': _L3_attn_in['w_r'], 'L3_attn_w_k': _L3_attn_in['w_k'], 'L3_attn_w_v': _L3_attn_in['w_v'], 'L3_attn_w_g': _L3_attn_in['w_g'], 'L3_attn_w_o': _L3_attn_in['w_o'], 'L3_attn_time_maa_k': _L3_attn_in['time_maa_k'], 'L3_attn_time_maa_v': _L3_attn_in['time_maa_v'], 'L3_attn_time_maa_r': _L3_attn_in['time_maa_r'], 'L3_attn_time_maa_g': _L3_attn_in['time_maa_g'], 'L3_attn_time_decay': _L3_attn_in['time_decay'], 'L3_attn_time_faaaa': _L3_attn_in['time_faaaa'], 'L3_attn_ln_g': _L3_attn_in['ln_g'], 'L3_attn_ln_b': _L3_attn_in['ln_b'], 'L3_xattn_Wq': _L3_xattn_in['Wq'], 'L3_xattn_Wk': _L3_xattn_in['Wk'], 'L3_xattn_Wv': _L3_xattn_in['Wv'], 'L3_xattn_Wo': _L3_xattn_in['Wo'], 'L3_ffn_W1': _L3_ffn_in['W1'], 'L3_ffn_b1': _L3_ffn_in['b1'], 'L3_ffn_W2': _L3_ffn_in['W2'], 'L3_ffn_b2': _L3_ffn_in['b2'], 'L3_ffn_Wr': _L3_ffn_in['Wr'], 'L3_ffn_br': _L3_ffn_in['br']}

def reference(x, ctx_1024, mask_BxSxS2_bf0, L0_attn_Wq, L0_attn_Wkv, L0_attn_null_kv, L0_attn_Wout, L0_xattn_Wk, L0_xattn_bk, L0_xattn_Wq, L0_xattn_bq, L0_xattn_Wv, L0_xattn_bv, L0_xattn_W1, L0_xattn_b1, L0_xattn_W2, L0_xattn_b2, L0_ffn_w_gate, L0_ffn_w_up, L0_ffn_w_down, L1_attn_in_proj_w, L1_attn_conv_w, L1_attn_conv_b, L1_attn_init_states, L1_attn_dt_bias, L1_attn_A_log, L1_attn_D, L1_attn_norm_w, L1_attn_out_proj_w, L1_xattn_wq_w, L1_xattn_wq_b, L1_xattn_wk_w, L1_xattn_wk_b, L1_xattn_wv_w, L1_xattn_wv_b, L1_xattn_wo_w, L1_xattn_wo_b, L1_ffn_router_scale, L1_ffn_router_w, L1_ffn_gating_w, L1_ffn_linear_w, L1_ffn_per_expert_scale, L2_attn_Wq, L2_attn_Wk, L2_attn_Wv, L2_attn_Wg, L2_attn_Wo, L2_attn_conv_q, L2_attn_conv_k, L2_attn_conv_v, L2_attn_Wgk, L2_attn_Wb, L2_attn_b_b, L2_attn_A_log, L2_attn_dt_bias, L2_attn_g_norm_weight, L2_xattn_w_q, L2_xattn_b_q, L2_xattn_w_k, L2_xattn_b_k, L2_xattn_w_v, L2_xattn_b_v, L2_xattn_w_o, L2_xattn_b_o, L2_ffn_router_w, L2_ffn_correction_bias, L2_ffn_up_w, L2_ffn_down_w, L2_ffn_shared_up_w, L2_ffn_shared_down_w, L3_attn_w_r, L3_attn_w_k, L3_attn_w_v, L3_attn_w_g, L3_attn_w_o, L3_attn_time_maa_k, L3_attn_time_maa_v, L3_attn_time_maa_r, L3_attn_time_maa_g, L3_attn_time_decay, L3_attn_time_faaaa, L3_attn_ln_g, L3_attn_ln_b, L3_xattn_Wq, L3_xattn_Wk, L3_xattn_Wv, L3_xattn_Wo, L3_ffn_W1, L3_ffn_b1, L3_ffn_W2, L3_ffn_b2, L3_ffn_Wr, L3_ffn_br):
    import jax
    import jax.numpy as jnp

    def _L0_attn_ref(x, Wq, Wkv, null_kv, Wout):
        import jax, jax.numpy as jnp
        import numpy as np
        HEADS = 16
        DIM_HEAD = 64
        b, n, dim = x.shape
        scale = DIM_HEAD ** (-0.5)
        q = (x @ Wq).reshape(b, n, HEADS, DIM_HEAD).transpose(0, 2, 1, 3) * scale
        kv = x @ Wkv
        kv = jnp.concatenate([jnp.broadcast_to(null_kv, (b, 1, DIM_HEAD)), kv], axis=1)
        sim = jnp.einsum('bhid,bjd->bhij', q, kv)
        mask_value = -jnp.finfo(sim.dtype).max
        i, j = (sim.shape[-2], sim.shape[-1])
        causal_mask = jnp.triu(jnp.ones((i, j), dtype=bool), k=j - i + 1)
        sim = jnp.where(causal_mask, mask_value, sim)
        attn = jax.nn.softmax(sim.astype(jnp.float32), axis=-1)
        out = jnp.einsum('bhij,bjd->bhid', attn, kv.astype(jnp.float32))
        out = out.transpose(0, 2, 1, 3).reshape(b, n, HEADS * DIM_HEAD)
        return out @ Wout

    def _L0_xattn_ref(kq, v, Wk, bk, Wq, bq, Wv, bv, W1, b1, W2, b2):
        import jax, jax.numpy as jnp
        import numpy as np
        N, T, D_KQ, E_KQ, D_V, E_V, H = (2, 256, 128, 128, 128, 128, 16)

        def _shifted_causal_mask(T):
            row = jnp.arange(T)[:, None]
            col = jnp.arange(T)[None, :]
            mask = jnp.where(col < row, 0.0, -jnp.inf).astype(jnp.float32)
            return mask.at[0, 0].set(0.0)
        n, T, _ = kq.shape
        hd_kq = E_KQ // H
        hd_v = E_V // H
        k = (kq @ Wk + bk).reshape(n, T, H, hd_kq).transpose(0, 2, 1, 3)
        q = (kq @ Wq + bq).reshape(n, T, H, hd_kq).transpose(0, 2, 1, 3)
        vv = (v @ Wv + bv).reshape(n, T, H, hd_v).transpose(0, 2, 1, 3)
        scores = jnp.einsum('bhqd,bhkd->bhqk', q, k) + _shifted_causal_mask(T)
        attn = jax.nn.softmax(scores, axis=-1)
        out = jnp.einsum('bhqk,bhkd->bhqd', attn, vv)
        out = out.transpose(0, 2, 1, 3).reshape(n, T, E_V)
        h = jax.nn.gelu(out @ W1 + b1, approximate=False)
        return h @ W2 + b2

    def _L0_ffn_ref(x, w_gate, w_up, w_down):
        import jax, jax.numpy as jnp
        import numpy as np
        HIDDEN = 128
        INNER = 512

        def _weight_quant(w):
            scale = 1.0 / jnp.clip(jnp.mean(jnp.abs(w)), 1e-05)
            wq = jnp.clip(jnp.round(w * scale), -1.0, 1.0) / scale
            return w + jax.lax.stop_gradient(wq - w)

        def _act_quant(x):
            scale = 127.0 / jnp.clip(jnp.max(jnp.abs(x), axis=-1, keepdims=True), 1e-05)
            xq = jnp.clip(jnp.round(x * scale), -128.0, 127.0) / scale
            return x + jax.lax.stop_gradient(xq - x)

        def _bitlinear(x, w):
            return jnp.einsum('bsi,oi->bso', _act_quant(x), _weight_quant(w))
        gate = jax.nn.silu(_bitlinear(x, w_gate))
        up = _bitlinear(x, w_up)
        return _bitlinear(gate * up, w_down)

    def _L1_attn_ref(u, in_proj_w, conv_w, conv_b, init_states, dt_bias, A_log, D, norm_w, out_proj_w):
        import jax, jax.numpy as jnp
        import numpy as np
        D_MODEL, D_STATE, D_CONV, EXPAND, HEADDIM, NGROUPS, CHUNK = (128, 64, 4, 2, 64, 1, 64)
        D_INNER = EXPAND * D_MODEL
        NHEADS = D_INNER // HEADDIM
        CONV_DIM = D_INNER + 2 * NGROUPS * D_STATE
        D_IN_PROJ = 2 * D_INNER + 2 * NGROUPS * D_STATE + NHEADS
        EPS = 1e-05

        def segsum(x):
            T = x.shape[-1]
            i = jnp.arange(T)[:, None]
            j = jnp.arange(T)[None, :]
            xr = jnp.where(i > j, x[..., :, None], 0.0)
            s = jnp.cumsum(xr, axis=-2)
            return jnp.where(i >= j, s, -jnp.inf)

        def _forward(u, in_proj_w, conv_w, conv_b, init_states, dt_bias, A_log, D, norm_w, out_proj_w):
            b, L, _ = u.shape
            zxbcdt = jnp.einsum('bld,ed->ble', u, in_proj_w)
            z = zxbcdt[..., :D_INNER]
            xBC = zxbcdt[..., D_INNER:D_INNER + CONV_DIM]
            dt = jax.nn.softplus(zxbcdt[..., D_INNER + CONV_DIM:] + dt_bias)
            xp = jnp.pad(xBC, ((0, 0), (D_CONV - 1, 0), (0, 0)))
            xBC = sum((xp[:, k:k + L, :] * conv_w[:, k] for k in range(D_CONV))) + conv_b
            xBC = jax.nn.silu(xBC)
            x = xBC[..., :D_INNER].reshape(b, L, NHEADS, HEADDIM)
            Bm = xBC[..., D_INNER:D_INNER + NGROUPS * D_STATE].reshape(b, L, NGROUPS, D_STATE)
            Cm = xBC[..., D_INNER + NGROUPS * D_STATE:].reshape(b, L, NGROUPS, D_STATE)
            A = -jnp.exp(A_log)
            Bm = jnp.repeat(Bm, NHEADS // NGROUPS, axis=2)
            Cm = jnp.repeat(Cm, NHEADS // NGROUPS, axis=2)
            X = x * dt[..., None]
            Adt = A * dt
            c = L // CHUNK
            Xc = X.reshape(b, c, CHUNK, NHEADS, HEADDIM)
            Bc = Bm.reshape(b, c, CHUNK, NHEADS, D_STATE)
            Cc = Cm.reshape(b, c, CHUNK, NHEADS, D_STATE)
            Ac = Adt.reshape(b, c, CHUNK, NHEADS).transpose(0, 3, 1, 2)
            A_cumsum = jnp.cumsum(Ac, axis=-1)
            Lmat = jnp.exp(segsum(Ac))
            Y_diag = jnp.einsum('bclhn,bcshn,bhcls,bcshp->bclhp', Cc, Bc, Lmat, Xc)
            decay_states = jnp.exp(A_cumsum[..., -1:] - A_cumsum)
            states = jnp.einsum('bclhn,bhcl,bclhp->bchpn', Bc, decay_states, Xc)
            init = jnp.broadcast_to(init_states, (b,) + init_states.shape)[:, None]
            states = jnp.concatenate([init, states], axis=1)
            decay_chunk = jnp.exp(segsum(jnp.pad(A_cumsum[..., -1], ((0, 0), (0, 0), (1, 0)))))
            new_states = jnp.einsum('bhzc,bchpn->bzhpn', decay_chunk, states)
            states = new_states[:, :-1]
            state_decay_out = jnp.exp(A_cumsum)
            Y_off = jnp.einsum('bclhn,bchpn,bhcl->bclhp', Cc, states, state_decay_out)
            Y = (Y_diag + Y_off).reshape(b, L, NHEADS, HEADDIM) + x * D[:, None]
            y = Y.reshape(b, L, D_INNER)
            y = y * jax.nn.silu(z)
            y = y * jax.lax.rsqrt(jnp.mean(y * y, axis=-1, keepdims=True) + EPS) * norm_w
            return jnp.einsum('bld,ed->ble', y, out_proj_w)
        return _forward(u, in_proj_w, conv_w, conv_b, init_states, dt_bias, A_log, D, norm_w, out_proj_w)

    def _L1_xattn_ref(q, k, v, wq_w, wq_b, wk_w, wk_b, wv_w, wv_b, wo_w, wo_b):
        import jax, jax.numpy as jnp
        import numpy as np
        B, T, D, H = (2, 256, 128, 16)
        DH = D // H
        b, t, d = q.shape
        wq = (q @ wq_w.T + wq_b).reshape(b, t, H, DH)
        wk = (k @ wk_w.T + wk_b).reshape(b, t, H, DH)
        wv = (v @ wv_w.T + wv_b).reshape(b, t, H, DH)
        scores = jnp.einsum('bthd,bshd->bhts', wq, wk) / jnp.sqrt(jnp.float32(DH))
        probs = jax.nn.softmax(scores, axis=-1)
        attn = jnp.einsum('bhts,bshd->bthd', probs, wv)
        attn = attn.reshape(b, t, d)
        return attn @ wo_w.T + wo_b

    def _L1_ffn_ref(x, router_scale, router_w, gating_w, linear_w, per_expert_scale):
        import jax, jax.numpy as jnp
        import numpy as np
        B, L, D = (2, 128, 128)
        HID, E, K = (256, 8, 2)
        d = x.shape[-1]
        var = jnp.mean(jnp.square(x), axis=-1, keepdims=True)
        r_in = x * jax.lax.rsqrt(var + 1e-06)
        r_in = r_in * jax.lax.rsqrt(jnp.array(d, dtype=r_in.dtype)) * router_scale
        logits = jnp.dot(r_in, router_w).astype(jnp.float32)
        probs = jax.nn.softmax(logits, axis=-1)
        _, top_k_idx = jax.lax.top_k(logits, K)
        indicator = jax.nn.one_hot(top_k_idx, probs.shape[-1], dtype=probs.dtype)
        gate_weights = indicator.sum(axis=-2) * probs
        renorm = jnp.sum(gate_weights, axis=-1, keepdims=True)
        renorm = jnp.where(renorm > 0.0, renorm, 1.0)
        weights = probs / renorm
        top_k_w = jnp.take_along_axis(weights, top_k_idx, axis=-1)
        combine = jnp.einsum('blke,blk->ble', indicator, top_k_w)
        combine = combine * per_expert_scale
        gate0 = jnp.einsum('bld,ehd->bleh', x, gating_w[:, 0])
        gate1 = jnp.einsum('bld,ehd->bleh', x, gating_w[:, 1])
        act = jax.nn.gelu(gate0) * gate1
        out = jnp.einsum('bleh,ehd,ble->bld', act, linear_w, combine)
        return out.astype(x.dtype)

    def _L2_attn_ref(hidden_states, Wq, Wk, Wv, Wg, Wo, conv_q, conv_k, conv_v, Wgk, Wb, b_b, A_log, dt_bias, g_norm_weight):
        import jax, jax.numpy as jnp
        import numpy as np
        import math
        B, L, HID = (2, 512, 128)
        NH, DK, DV = (12, 64, 128)
        KD, VD, CS = (NH * DK, NH * DV, 4)
        SCALE = DK ** (-0.5)

        def _causal_depthwise_conv(x, w):
            c, k = w.shape
            xt = jnp.transpose(x, (0, 2, 1))
            out = jax.lax.conv_general_dilated(xt, w[:, None, :], window_strides=(1,), padding=[(k - 1, 0)], feature_group_count=c, dimension_numbers=('NCH', 'OIH', 'NCH'))
            return jnp.transpose(out, (0, 2, 1))

        def _l2norm(x, eps=1e-06):
            return x * jax.lax.rsqrt(jnp.sum(x * x, axis=-1, keepdims=True) + eps)

        def _gated_delta_net(hidden_states, Wq, Wk, Wv, Wg, Wo, conv_q, conv_k, conv_v, Wgk, Wb, b_b, A_log, dt_bias, g_norm_weight):
            b, l, _ = hidden_states.shape
            q = jax.nn.silu(_causal_depthwise_conv(hidden_states @ Wq, conv_q))
            k = jax.nn.silu(_causal_depthwise_conv(hidden_states @ Wk, conv_k))
            v = jax.nn.silu(_causal_depthwise_conv(hidden_states @ Wv, conv_v))
            gk = -jnp.exp(A_log) * jax.nn.softplus(hidden_states @ Wgk + dt_bias)
            beta = jax.nn.sigmoid(hidden_states @ Wb + b_b)
            q = jnp.transpose(q.reshape(b, l, NH, DK), (0, 2, 1, 3))
            k = jnp.transpose(k.reshape(b, l, NH, DK), (0, 2, 1, 3))
            v = jnp.transpose(v.reshape(b, l, NH, DV), (0, 2, 1, 3))
            q = _l2norm(q) * SCALE
            k = _l2norm(k)
            qs = jnp.moveaxis(q, 2, 0)
            ks_ = jnp.moveaxis(k, 2, 0)
            vs = jnp.moveaxis(v, 2, 0)
            bs = jnp.moveaxis(beta, 1, 0)
            gs = jnp.moveaxis(gk, 1, 0)

            def step(S, inp):
                qt, kt, vt, bt, gt = inp
                S = S * jnp.exp(gt)[..., None, None]
                kv = jnp.einsum('bhk,bhkv->bhv', kt, S)
                delta = (vt - kv) * bt[..., None]
                S = S + jnp.einsum('bhk,bhv->bhkv', kt, delta)
                ot = jnp.einsum('bhk,bhkv->bhv', qt, S)
                return (S, ot)
            S0 = jnp.zeros((b, NH, DK, DV), hidden_states.dtype)
            _, os_ = jax.lax.scan(step, S0, (qs, ks_, vs, bs, gs))
            o = jnp.moveaxis(os_, 0, 1)
            g = (hidden_states @ Wg).reshape(b, l, NH, DV)
            var = jnp.mean(o * o, axis=-1, keepdims=True)
            o = o * jax.lax.rsqrt(var + 1e-05) * g_norm_weight
            o = o * g * jax.nn.sigmoid(g)
            return o.reshape(b, l, VD) @ Wo
        return _gated_delta_net(hidden_states, Wq, Wk, Wv, Wg, Wo, conv_q, conv_k, conv_v, Wgk, Wb, b_b, A_log, dt_bias, g_norm_weight)

    def _L2_xattn_ref(q, k, v, w_q, b_q, w_k, b_k, w_v, b_v, w_o, b_o):
        import jax, jax.numpy as jnp
        import numpy as np
        D_MODEL = 128
        N_HEAD = 16

        def _split_heads(x):
            B, S, D = x.shape
            return x.reshape(B, S, N_HEAD, D // N_HEAD).transpose(0, 2, 1, 3)
        qh = _split_heads(q @ w_q.T + b_q)
        kh = _split_heads(k @ w_k.T + b_k)
        vh = _split_heads(v @ w_v.T + b_v)
        d_k = qh.shape[-1]
        scores = jnp.einsum('bhqd,bhkd->bhqk', qh, kh) / jnp.sqrt(jnp.float32(d_k))
        attn = jax.nn.softmax(scores, axis=-1)
        out = jnp.einsum('bhqk,bhkd->bhqd', attn, vh)
        B, H, S, d = out.shape
        out = out.transpose(0, 2, 1, 3).reshape(B, S, H * d)
        return out @ w_o.T + b_o

    def _L2_ffn_ref(x, router_w, correction_bias, up_w, down_w, shared_up_w, shared_down_w):
        import jax, jax.numpy as jnp
        import numpy as np
        H = 128
        E = 64
        K = 8
        G = 8
        TOPK_GROUP = 4
        I_MOE = 64
        I_SHARED = 256
        SCALE = 2.5

        def relu2(x):
            return jnp.square(jax.nn.relu(x))

        def _route(xf, router_w, correction_bias):
            T = xf.shape[0]
            logits = xf @ router_w.T
            scores = jax.nn.sigmoid(logits)
            sfc = scores + correction_bias[None, :]
            grp = sfc.reshape(T, G, E // G)
            top2, _ = jax.lax.top_k(grp, 2)
            group_scores = top2.sum(-1)
            _, gidx = jax.lax.top_k(group_scores, TOPK_GROUP)
            gmask = jnp.zeros((T, G), sfc.dtype).at[jnp.arange(T)[:, None], gidx].set(1.0)
            emask = jnp.repeat(gmask, E // G, axis=1)
            masked = jnp.where(emask > 0, sfc, 0.0)
            _, tidx = jax.lax.top_k(masked, K)
            tw = jnp.take_along_axis(scores, tidx, axis=1)
            tw = tw / (tw.sum(-1, keepdims=True) + 1e-20)
            return (tidx, tw * SCALE)
        B, S, Hd = x.shape
        xf = x.reshape(-1, Hd)
        T = xf.shape[0]
        tidx, tw = _route(xf.astype(jnp.float32), router_w, correction_bias)
        combine = jnp.zeros((T, E), xf.dtype).at[jnp.arange(T)[:, None], tidx].add(tw.astype(xf.dtype))

        def body(acc, ew):
            wu, wd, c = ew
            return (acc + c[:, None] * (relu2(xf @ wu) @ wd), None)
        routed, _ = jax.lax.scan(body, jnp.zeros_like(xf), (up_w, down_w, combine.T))
        shared = relu2(xf @ shared_up_w) @ shared_down_w
        return (routed + shared).reshape(B, S, Hd)

    def _L3_attn_ref(x, w_r, w_k, w_v, w_g, w_o, time_maa_k, time_maa_v, time_maa_r, time_maa_g, time_decay, time_faaaa, ln_g, ln_b):
        import jax, jax.numpy as jnp
        import numpy as np
        D = 128
        H = 16
        N = D // H
        B = 4
        T = 256
        NLAYERS = 12
        LAYER_ID = 6
        EPS = 1e-05 * 64

        def _forward(x, w_r, w_k, w_v, w_g, w_o, time_maa_k, time_maa_v, time_maa_r, time_maa_g, time_decay, time_faaaa, ln_g, ln_b):
            Bs, Ts, C = x.shape
            if Ts % 32 == 0:
                Q = 32
            elif Ts % 128 == 0:
                Q = 128
            else:
                Q = Ts
            nC = Ts // Q
            xs = jnp.pad(x, ((0, 0), (1, 0), (0, 0)))[:, :-1]
            xx = xs - x
            xk = x + xx * time_maa_k
            xv = x + xx * time_maa_v
            xr = x + xx * time_maa_r
            xg = x + xx * time_maa_g
            r = (xr @ w_r.T).reshape(Bs, Ts, H, N).transpose(0, 2, 1, 3)
            k = (xk @ w_k.T).reshape(Bs, Ts, H, N).transpose(0, 2, 3, 1)
            v = (xv @ w_v.T).reshape(Bs, Ts, H, N).transpose(0, 2, 1, 3)
            g = jax.nn.silu(xg @ w_g.T)
            w = jnp.exp(-jnp.exp(time_decay))
            u = time_faaaa
            ws = (w ** Q)[None, :, None, None]
            q = jnp.arange(Q)
            wk = (w[:, None] ** (Q - 1 - q)[None, :])[None, :, None, :]
            wb = (w[:, None] ** q[None, :])[None, :, :, None]
            ii = q[:, None]
            jj = q[None, :]
            e = jnp.maximum(ii - jj - 1, 0)
            Wmat = jnp.where((jj < ii)[None], w[:, None, None] ** e[None], 0.0)
            Wmat = Wmat + jnp.eye(Q, dtype=x.dtype)[None] * u[:, None, None]
            Wmat = Wmat[None]
            rC = r.reshape(Bs, H, nC, Q, N).transpose(2, 0, 1, 3, 4)
            kC = k.reshape(Bs, H, N, nC, Q).transpose(3, 0, 1, 2, 4)
            vC = v.reshape(Bs, H, nC, Q, N).transpose(2, 0, 1, 3, 4)

            def step(state, inp):
                rr, kk, vv = inp
                y = rr @ kk * Wmat @ vv + rr @ state * wb
                state = ws * state + kk * wk @ vv
                return (state, y)
            state0 = jnp.zeros((Bs, H, N, N), x.dtype)
            _, yC = jax.lax.scan(step, state0, (rC, kC, vC))
            y = yC.transpose(1, 2, 0, 3, 4).reshape(Bs, H, Ts, N)
            y = y.transpose(0, 2, 1, 3).reshape(Bs * Ts, H, N)
            mu = y.mean(-1, keepdims=True)
            var = y.var(-1, keepdims=True)
            y = (y - mu) / jnp.sqrt(var + EPS)
            y = y.reshape(Bs, Ts, C) * ln_g + ln_b
            y = y * g
            return y @ w_o.T
        return _forward(x, w_r, w_k, w_v, w_g, w_o, time_maa_k, time_maa_v, time_maa_r, time_maa_g, time_decay, time_faaaa, ln_g, ln_b)

    def _L3_xattn_ref(query, key, value, mask, Wq, Wk, Wv, Wo):
        import jax, jax.numpy as jnp
        import numpy as np
        EMBED_DIM = 128
        N_HEADS = 16
        HEAD_DIM = EMBED_DIM // N_HEADS
        B, Tq, D = query.shape
        Tk = key.shape[1]
        H, Dh = (N_HEADS, HEAD_DIM)
        Q = (query @ Wq.T).reshape(B, Tq, H, Dh).transpose(0, 2, 1, 3)
        K = (key @ Wk.T).reshape(B, Tk, H, Dh).transpose(0, 2, 1, 3)
        V = (value @ Wv.T).reshape(B, Tk, H, Dh).transpose(0, 2, 1, 3)
        scale = jnp.sqrt(jnp.asarray(Dh, dtype=Q.dtype))
        scores = jnp.einsum('bhqd,bhkd->bhqk', Q, K) / scale
        scores = jnp.where(mask[:, None, :, :], -jnp.inf, scores)
        attn = jax.nn.softmax(scores, axis=-1)
        out = jnp.einsum('bhqk,bhkd->bhqd', attn, V)
        out = out.transpose(0, 2, 1, 3).reshape(B, Tq, D)
        return out @ Wo.T

    def _L3_ffn_ref(x, W1, b1, W2, b2, Wr, br):
        import jax, jax.numpy as jnp
        import numpy as np
        from jax import lax
        D = 128
        H = 512
        E = 8
        TOPK = 2
        B, S, _ = x.shape
        xf = x.reshape(-1, D)
        logits = xf @ Wr + br
        topv, _ = lax.top_k(logits, TOPK)
        thresh = topv[:, TOPK - 1:TOPK]
        masked = jnp.where(logits >= thresh, logits, -jnp.inf)
        weights = jax.nn.softmax(masked, axis=-1)
        h = jax.nn.gelu(jnp.einsum('td,edh->eth', xf, W1) + b1[:, None, :], approximate=False)
        expert_out = jnp.einsum('eth,ehd->etd', h, W2) + b2[:, None, :]
        out = jnp.einsum('etd,te->td', expert_out, weights)
        return out.reshape(B, S, D)
    x = x + _L0_attn_ref(_layernorm(x, axis=-1), L0_attn_Wq, L0_attn_Wkv, L0_attn_null_kv, L0_attn_Wout)
    x = x + _L0_xattn_ref(_layernorm(x, axis=-1), ctx_1024, L0_xattn_Wk, L0_xattn_bk, L0_xattn_Wq, L0_xattn_bq, L0_xattn_Wv, L0_xattn_bv, L0_xattn_W1, L0_xattn_b1, L0_xattn_W2, L0_xattn_b2)
    x = x + _L0_ffn_ref(_layernorm(x, axis=-1), L0_ffn_w_gate, L0_ffn_w_up, L0_ffn_w_down)
    x = x + _L1_attn_ref(_layernorm(x, axis=-1), L1_attn_in_proj_w, L1_attn_conv_w, L1_attn_conv_b, L1_attn_init_states, L1_attn_dt_bias, L1_attn_A_log, L1_attn_D, L1_attn_norm_w, L1_attn_out_proj_w)
    x = x + _L1_xattn_ref(_layernorm(x, axis=-1), ctx_1024, ctx_1024, L1_xattn_wq_w, L1_xattn_wq_b, L1_xattn_wk_w, L1_xattn_wk_b, L1_xattn_wv_w, L1_xattn_wv_b, L1_xattn_wo_w, L1_xattn_wo_b)
    x = x + _L1_ffn_ref(_layernorm(x, axis=-1), L1_ffn_router_scale, L1_ffn_router_w, L1_ffn_gating_w, L1_ffn_linear_w, L1_ffn_per_expert_scale)
    x = x + _L2_attn_ref(_layernorm(x, axis=-1), L2_attn_Wq, L2_attn_Wk, L2_attn_Wv, L2_attn_Wg, L2_attn_Wo, L2_attn_conv_q, L2_attn_conv_k, L2_attn_conv_v, L2_attn_Wgk, L2_attn_Wb, L2_attn_b_b, L2_attn_A_log, L2_attn_dt_bias, L2_attn_g_norm_weight)
    x = x + _L2_xattn_ref(_layernorm(x, axis=-1), ctx_1024, ctx_1024, L2_xattn_w_q, L2_xattn_b_q, L2_xattn_w_k, L2_xattn_b_k, L2_xattn_w_v, L2_xattn_b_v, L2_xattn_w_o, L2_xattn_b_o)
    x = x + _L2_ffn_ref(_layernorm(x, axis=-1), L2_ffn_router_w, L2_ffn_correction_bias, L2_ffn_up_w, L2_ffn_down_w, L2_ffn_shared_up_w, L2_ffn_shared_down_w)
    x = x + _L3_attn_ref(_layernorm(x, axis=-1), L3_attn_w_r, L3_attn_w_k, L3_attn_w_v, L3_attn_w_g, L3_attn_w_o, L3_attn_time_maa_k, L3_attn_time_maa_v, L3_attn_time_maa_r, L3_attn_time_maa_g, L3_attn_time_decay, L3_attn_time_faaaa, L3_attn_ln_g, L3_attn_ln_b)
    x = x + _L3_xattn_ref(_layernorm(x, axis=-1), ctx_1024, ctx_1024, mask_BxSxS2_bf0, L3_xattn_Wq, L3_xattn_Wk, L3_xattn_Wv, L3_xattn_Wo)
    x = x + _L3_ffn_ref(_layernorm(x, axis=-1), L3_ffn_W1, L3_ffn_b1, L3_ffn_W2, L3_ffn_b2, L3_ffn_Wr, L3_ffn_br)
    return x

_drawn_inputs = setup_inputs


def setup_inputs(seed=0):
    import zlib

    import numpy as np

    out = dict(_drawn_inputs(seed))
    spreads = {'L0_xattn_bk': (0.0, 2.0),
     'L0_xattn_bq': (0.0, 0.1),
     'L0_xattn_bv': (0.0, 0.1),
     'L0_xattn_b1': (0.0, 0.1),
     'L0_xattn_b2': (0.0, 0.1),
     'L1_attn_D': (1.0, 0.2),
     'L1_attn_norm_w': (1.0, 0.2),
     'L1_xattn_wq_b': (0.0, 0.49),
     'L1_xattn_wk_b': (0.0, 2.0),
     'L1_xattn_wv_b': (0.0, 0.1),
     'L1_xattn_wo_b': (0.0, 0.1),
     'L1_ffn_router_scale': (1.0, 0.6),
     'L1_ffn_per_expert_scale': (1.0, 0.6),
     'L2_attn_g_norm_weight': (1.0, 0.2),
     'L2_xattn_b_q': (0.0, 0.8),
     'L2_xattn_b_k': (0.0, 2.0),
     'L2_xattn_b_v': (0.0, 0.1),
     'L2_xattn_b_o': (0.0, 0.1),
     'L3_attn_ln_g': (1.0, 0.6),
     'L3_attn_ln_b': (0.0, 0.8),
     'L3_ffn_b1': (0.0, 0.8),
     'L3_ffn_b2': (0.0, 0.8),
     'L3_ffn_br': (0.0, 0.362)}
    factors = {'L1_attn_conv_b': 4.347,
     'L1_attn_init_states': 4.831,
     'L1_ffn_router_w': 8.0,
     'L1_ffn_gating_w': 8.0,
     'L1_ffn_linear_w': 8.0,
     'L2_attn_b_b': 8.0,
     'L2_ffn_router_w': 8.0,
     'L2_ffn_correction_bias': 8.0,
     'L2_ffn_up_w': 8.0,
     'L2_ffn_down_w': 8.0,
     'L2_ffn_shared_up_w': 6.709,
     'L2_ffn_shared_down_w': 6.216,
     'L3_attn_w_r': 5.455,
     'L3_attn_w_k': 5.399,
     'L3_attn_w_v': 5.423,
     'L3_attn_w_g': 5.394,
     'L3_attn_w_o': 5.394,
     'L3_attn_time_maa_k': 8.0,
     'L3_attn_time_maa_v': 8.0,
     'L3_attn_time_maa_r': 8.0,
     'L3_attn_time_maa_g': 8.0,
     'L3_attn_time_decay': 64.0,
     'L3_attn_time_faaaa': 8.0,
     'L3_ffn_W1': 3.463,
     'L3_ffn_W2': 3.151}
    for name, (base, spread) in spreads.items():
        noise = np.random.default_rng([zlib.crc32(name.encode()), seed]).standard_normal(out[name].shape)
        drawn = base * np.exp(spread * noise) if base else spread * noise
        out[name] = jnp.asarray(drawn.astype(out[name].dtype))
    for name, factor in factors.items():
        out[name] = (out[name] * factor).astype(out[name].dtype)
    return out
```

```python
import numpy as np

import concourse.bass as bass
from concourse import mybir

F32 = mybir.dt.float32
BF16 = mybir.dt.bfloat16
U8 = mybir.dt.uint8
ALU = mybir.AluOpType
ACT = mybir.ActivationFunctionType
X = mybir.AxisListType.X

B, T, D = 8, 128, 128
H, HD = 16, 8
TOK = B * T
HALF = 512
NEG = -1.0e30
ROUND = 1.5 * 2.0 ** 23
CREDIT = 24


def done(m):
    return m + 1 + CREDIT


def credit(engine, *sems):
    for s in sems:
        engine.sem_inc(s, CREDIT)


class Stage:

    def __init__(self, nc, name):
        self.nc, self.name = nc, name
        self.scope = nc.cleanup_on_exit()

    def __enter__(self):
        self.scope.__enter__()
        return self

    def __exit__(self, *exc):
        self.scope.__exit__(*exc)
        self.nc.all_engine_barrier()

    def sb(self, name, shape, dtype=F32):
        return self.nc.alloc_sbuf_tensor(f"{self.name}_{name}", shape, dtype)

    def sem(self, name):
        return self.nc.alloc_semaphore(f"{self.name}_{name}")


class Pack:

    def __init__(self, tile, places, loaded):
        self.tile, self.places, self.loaded = tile, places, loaded

    def __getitem__(self, name):
        at, rows, cols = self.places[name]
        return self.tile[0:rows, at:at + cols]


class Net:
    pass


def bc(ap, axis, n):
    a = ap.unsqueeze(axis)
    shape = list(a.shape)
    shape[axis] = n
    return a.to_broadcast(shape)


def rows_of(ap, n):
    return ap.rearrange("p (a b) -> p a b", a=n)


def layer_norm(nc, g, name, loads, eps=1e-5):
    with Stage(nc, name) as st:
        total, mean = st.sb("total", [T, B]), st.sb("mean", [T, B])
        sq, sumsq = st.sb("sq", [T, B, D]), st.sb("sumsq", [T, B])
        var, rstd, power = st.sb("var", [T, B]), st.sb("rstd", [T, B]), st.sb("power", [T, B])
        var_ready, rstd_ready, h_ready, turned, power_set = (
            st.sem(s) for s in ("var_ready", "rstd_ready", "h_ready", "turned", "power_set"))
        x, h, hT = g.x, g.h, g.hT

        with nc.Block() as block:
            @block.sync
            def _(sp):
                for pack, source in loads:
                    sp.dma_start(pack.tile, source).then_inc(pack.loaded, 16)

            @block.vector
            def _(dve):
                nc.vector.tensor_reduce(total[:], x[:], X, ALU.add)
                dve.drain()
                nc.vector.tensor_scalar(mean[:], total[:], 1.0 / D, None, ALU.mult)
                dve.drain()
                nc.vector.tensor_tensor(h[:], x[:], bc(mean[:], 2, D), ALU.subtract)
                dve.drain()
                nc.vector.tensor_tensor(sq[:], h[:], h[:], ALU.mult)
                dve.drain()
                nc.vector.tensor_reduce(sumsq[:], sq[:], X, ALU.add)
                dve.drain()
                nc.vector.tensor_scalar(var[:], sumsq[:], 1.0 / D, eps, ALU.mult, ALU.add).then_inc(var_ready, 1)
                dve.wait_ge(rstd_ready, 1)
                for half in range(2):
                    b = slice(4 * half, 4 * half + 4)
                    nc.vector.tensor_tensor(h[:, b, :], h[:, b, :], bc(rstd[:, b], 2, D),
                                            ALU.mult).then_inc(h_ready, 1)

            @block.gpsimd
            def _(pool):
                nc.gpsimd.memset(power[:], -0.5).then_inc(power_set, 1)
                pool.wait_ge(power_set, 1)
                pool.wait_ge(var_ready, 1)
                nc.gpsimd.tensor_tensor(rstd[:], var[:], power[:], ALU.pow).then_inc(rstd_ready, 1)

            @block.tensor
            def _(pe):
                for half in range(2):
                    pe.wait_ge(h_ready, half + 1)
                    for j in range(4):
                        last = nc.tensor.transpose(g.bank[half][:, j * T:(j + 1) * T], h[:, 4 * half + j, :], g.ident)
                    last.then_inc(turned, 1)

            @block.scalar
            def _(act):
                for half in range(2):
                    act.wait_ge(turned, half + 1)
                    nc.scalar.activation(hT[:, half * HALF:(half + 1) * HALF], g.bank[half][:], ACT.Copy)


def turn_context(nc, g):
    with Stage(nc, "context") as st:
        ctx = st.sb("ctx", [T, B, D])
        loaded, turned = st.sem("loaded"), st.sem("turned")
        with nc.Block() as block:
            @block.sync
            def _(sp):
                sp.dma_start(ctx[:], g.dram["ctx_1024"].rearrange("b t d -> t b d")).then_inc(loaded, 16)

            @block.tensor
            def _(pe):
                pe.wait_ge(g.const.loaded, 16)
                pe.wait_ge(loaded, 16)
                for half in range(2):
                    for j in range(4):
                        last = nc.tensor.transpose(g.bank[half][:, j * T:(j + 1) * T], ctx[:, 4 * half + j, :], g.ident)
                    last.then_inc(turned, 1)

            @block.scalar
            def _(act):
                for half in range(2):
                    act.wait_ge(turned, half + 1)
                    nc.scalar.activation(g.ctxT[:, half * HALF:(half + 1) * HALF], g.bank[half][:], ACT.Copy)

            @block.vector
            def _(dve):
                dve.wait_ge(g.const.loaded, 16)
                dve.wait_ge(g.x_loaded, 16)
                nc.vector.tensor_copy(g.ident_bf[:], g.ident)
                nc.vector.tensor_copy(g.causal_bf[:, 0, :], g.const["neg_causal"])
                nc.vector.tensor_copy(g.shifted_bf[:, 0, :], g.const["neg_shifted"])



def multi_query_attention(nc, g, w, name):
    NH, DH, Q = 16, 64, 4
    UN = NH // Q
    SCALE = DH ** -0.5
    with Stage(nc, name) as st:
        qT = st.sb("qT", [128, NH // 2, TOK])
        kvT = st.sb("kvT", [128, TOK])
        kv = st.sb("kv", [T, B, DH + 1])
        qs, kvs = st.sb("qs", [128, 2, NH // 2, T]), st.sb("kvs", [128, 2, 2, T])
        top, top0 = st.sb("top", [T, 2, Q]), st.sb("top0", [T, 2, Q])
        p = st.sb("p", [T, 2, Q * T + Q])
        pT = st.sb("pT", [T, 2, Q * T])
        null_q, null_score = st.sb("null_q", [D, NH]), st.sb("null_score", [T, B, NH])
        null_part = st.sb("null_part", [T, 2, Q, DH + 1])
        inv, o = st.sb("inv", [T, 2, Q]), st.sb("o", [T, 2, Q * DH])
        oT = st.sb("oT", [128, 2, 2, T])
        proj, proj_kept, kv_made, null_made, null_kept = (
            st.sem(s) for s in ("proj", "proj_kept", "kv_made", "null_made", "null_kept"))
        names = ("staged", "scored", "centered", "exped", "turned", "pT_kept", "mixed", "normed", "o_turned",
                 "oT_kept", "projected", "added", "null_weighed")
        staged, scored, centered, exped, turned, pT_kept, mixed, normed, o_turned, oT_kept, projected, added, null_weighed = (
            st.sem(s) for s in names)
        bank = g.bank

        with nc.Block() as block:
            @block.gpsimd
            def _(pool):
                nc.gpsimd.memset(kv[:, :, DH:DH + 1], 1.0)

            @block.tensor
            def _(pe):
                pe.wait_ge(w.loaded, 16)
                for m in range(2 * (NH // 2 + 1)):
                    j, half = m // 2, m % 2
                    if m >= 6:
                        pe.wait_ge(proj_kept, m - 5)
                    lhsT = w["wq"][:, j * 128:(j + 1) * 128] if j < NH // 2 else w["wkv2"]
                    nc.tensor.matmul(bank[m % 6][:], lhsT, g.hT[:, half * HALF:(half + 1) * HALF],
                                     start=True, stop=True).then_inc(proj, 1)
                for b in range(B):
                    last = nc.tensor.matmul(bank[6][:, b * DH:(b + 1) * DH], g.hT[:, b * T:(b + 1) * T],
                                            w["wkv2"][:, 0:DH], start=True, stop=True)
                last.then_inc(kv_made, 1)
                for j in range(NH // 2):
                    last = nc.tensor.matmul(bank[7][:, 2 * j:2 * j + 2], w["wqT"][:, j * D:(j + 1) * D], w["null2"],
                                            start=True, stop=True)
                last.then_inc(null_made, 1)
                pe.wait_ge(null_kept, 1)
                for b in range(B):
                    last = nc.tensor.matmul(bank[7][:, b * NH:(b + 1) * NH], g.hT[:, b * T:(b + 1) * T], null_q[:],
                                            start=True, stop=True)
                last.then_inc(null_made, 1)

            @block.scalar
            def _(act):
                for m in range(2 * (NH // 2 + 1)):
                    j, half = m // 2, m % 2
                    act.wait_ge(proj, m + 1)
                    dst = qT[:, j, :] if j < NH // 2 else kvT[:]
                    nc.scalar.activation(dst[:, half * HALF:(half + 1) * HALF], bank[m % 6][:],
                                         ACT.Copy).then_inc(proj_kept, 1)

            @block.vector
            def _(dve):
                dve.wait_ge(kv_made, 1)
                nc.vector.tensor_copy(kv[:, :, 0:DH], rows_of(bank[6][:], B))
                dve.wait_ge(null_made, 1)
                nc.vector.tensor_copy(null_q[:], bank[7][:, 0:NH]).then_inc(null_kept, 1)
                dve.wait_ge(null_made, 2)
                nc.vector.tensor_copy(null_score[:], rows_of(bank[7][:, 0:B * NH], B))

        score, tps, mix, o_tps, outp = bank[0:2], bank[2:4], bank[4:6], bank[6][:, 0:2 * T], bank[7]
        with nc.Block() as block:
            @block.gpsimd
            def _(pool):
                credit(pool, staged, null_weighed)
                with pool.Fori(0, B // 2) as i:
                    for u in range(2):
                        n = 2 * i + u
                        pool.wait_ge(scored, done(UN * (n - 2) + UN - 1))
                        nc.gpsimd.tensor_tensor(kvs[:, u, :, :], bc(kvT[:, bass.ds(n * T, T)], 1, 2),
                                                bc(g.const["half"], 2, T), ALU.mult)
                        nc.gpsimd.tensor_copy(qs[:, u, :, :], qT[:, :, bass.ds(n * T, T)]).then_inc(staged, 1)
                        for k in range(UN * u, UN * u + UN):
                            m, e = 2 * UN * i + k, k % 2
                            pool.wait_ge(exped, done(m))
                            pool.wait_ge(mixed, done(m - 2))
                            nc.gpsimd.tensor_tensor(null_part[:, e, :, :], bc(p[:, e, Q * T:], 2, DH + 1),
                                                    bc(w["null_row"], 1, Q), ALU.mult).then_inc(null_weighed, 1)

            @block.tensor
            def _(pe):
                credit(pe, scored, turned, mixed, o_turned, projected)
                with pe.Fori(0, B // 2) as i:
                    def scores(k):
                        m, u, q, e = 2 * UN * i + k, k // UN, k % UN, k % 2
                        if q == 0:
                            pe.wait_ge(staged, done(2 * i + u))
                        pe.wait_ge(centered, done(m - 2))
                        for j in range(Q // 2):
                            cols = score[e][:, 2 * j * T:2 * (j + 1) * T]
                            nc.tensor.matmul(cols, g.ident_bf[:], bc(g.causal_bf[:, 0, :], 1, 2),
                                             start=True, stop=False)
                            last = nc.tensor.matmul(cols, qs[:, u, q * 2 + j, :], kvs[:, u, :, :],
                                                    start=False, stop=True)
                        last.then_inc(scored, 1)

                    def turns(k):
                        m, e = 2 * UN * i + k, k % 2
                        pe.wait_ge(exped, done(m))
                        pe.wait_ge(pT_kept, done(m - 2))
                        for j in range(Q):
                            last = nc.tensor.transpose(tps[e][:, j * T:(j + 1) * T], p[:, e, j * T:(j + 1) * T], g.ident)
                        last.then_inc(turned, 1)

                    def mix_values(k):
                        m, u, e = 2 * UN * i + k, k // UN, k % 2
                        pe.wait_ge(pT_kept, done(m))
                        pe.wait_ge(null_weighed, done(m))
                        pe.wait_ge(normed, done(m - 2))
                        for j in range(Q):
                            cols = slice(j * (DH + 1), (j + 1) * (DH + 1))
                            nc.tensor.matmul(mix[e][:, cols], g.ident, null_part[:, e, j, :],
                                             start=True, stop=False)
                            last = nc.tensor.matmul(mix[e][:, cols], pT[:, e, j * T:(j + 1) * T],
                                                    kv[:, 2 * i + u, :], start=False, stop=True)
                        last.then_inc(mixed, 1)

                    def project(k):
                        m, q, e = 2 * UN * i + k, k % UN, k % 2
                        pe.wait_ge(normed, done(m))
                        pe.wait_ge(oT_kept, done(m - 1))
                        for j in range(2):
                            last = nc.tensor.transpose(o_tps[:, j * T:(j + 1) * T], o[:, e, j * T:(j + 1) * T], g.ident)
                        last.then_inc(o_turned, 1)
                        if q == 0:
                            pe.wait_ge(added, done(2 * i + k // UN - 1))
                        pe.wait_ge(oT_kept, done(m))
                        for j in range(2):
                            last = nc.tensor.matmul(outp[:, 0:D], oT[:, e, j, :], w["wout"][:, (2 * q + j) * D:(2 * q + j + 1) * D],
                                                    start=(q == 0 and j == 0), stop=(q == UN - 1 and j == 1))
                        if q == UN - 1:
                            last.then_inc(projected, 1)

                    for k in range(2 * UN + 3):
                        if k < 2 * UN:
                            scores(k)
                        if 0 <= k - 1 < 2 * UN:
                            turns(k - 1)
                        if 0 <= k - 2 < 2 * UN:
                            mix_values(k - 2)
                        if 0 <= k - 3 < 2 * UN:
                            project(k - 3)

            @block.scalar
            def _(act):
                credit(act, exped, pT_kept, oT_kept)
                with act.Fori(0, B // 2) as i:
                    for k in range(2 * UN + 3):
                        if k < 2 * UN:
                            m, e = 2 * UN * i + k, k % 2
                            act.wait_ge(centered, done(m))
                            nc.scalar.activation(p[:, e, :], p[:, e, :], ACT.Exp, scale=SCALE).then_inc(exped, 1)
                        if 0 <= k - 1 < 2 * UN:
                            m, e = 2 * UN * i + k - 1, (k - 1) % 2
                            act.wait_ge(turned, done(m))
                            act.wait_ge(mixed, done(m - 2))
                            nc.scalar.activation(pT[:, e, :], tps[e][:], ACT.Copy).then_inc(pT_kept, 1)
                        if 0 <= k - 3 < 2 * UN:
                            m, e = 2 * UN * i + k - 3, (k - 3) % 2
                            act.wait_ge(o_turned, done(m))
                            nc.scalar.activation(oT[:, e, :, :], rows_of(o_tps, 2), ACT.Copy).then_inc(oT_kept, 1)

            @block.vector
            def _(dve):
                credit(dve, centered, normed, added)
                with dve.Fori(0, B // 2) as i:
                    for k in range(2 * UN + 3):
                        if k < 2 * UN:
                            m, e = 2 * UN * i + k, k % 2
                            dve.wait_ge(scored, done(m))
                            nc.vector.tensor_reduce(top[:, e, :], rows_of(score[e][:], Q), X, ALU.max)
                            dve.drain()
                            null = null_score[:, 2 * i + k // UN, (k % UN) * Q:(k % UN + 1) * Q]
                            nc.vector.tensor_tensor(top0[:, e, :], top[:, e, :], null, ALU.max)
                            dve.drain()
                            dve.wait_ge(turned, done(m - 2))
                            dve.wait_ge(null_weighed, done(m - 2))
                            nc.vector.tensor_tensor(p[:, e, Q * T:], null, top0[:, e, :], ALU.subtract)
                            nc.vector.tensor_tensor(rows_of(p[:, e, 0:Q * T], Q), rows_of(score[e][:], Q),
                                                    bc(top0[:, e, :], 2, T), ALU.subtract).then_inc(centered, 1)
                        if 0 <= k - 2 < 2 * UN:
                            m, e = 2 * UN * i + k - 2, (k - 2) % 2
                            out = mix[e][:, 0:Q * (DH + 1)].rearrange("p (a b) -> p a b", a=Q)
                            dve.wait_ge(mixed, done(m))
                            nc.vector.reciprocal(inv[:, e, :], out[:, :, DH])
                            dve.drain()
                            dve.wait_ge(o_turned, done(m - 2))
                            nc.vector.tensor_tensor(rows_of(o[:, e, :], Q), out[:, :, 0:DH],
                                                    bc(inv[:, e, :], 2, DH), ALU.mult).then_inc(normed, 1)
                        if k in (UN + 2, 2 * UN + 2):
                            n = 2 * i + (k - 3) // UN
                            dve.wait_ge(projected, done(n))
                            nc.vector.tensor_tensor(g.x[:, n, :], g.x[:, n, :], outp[:, 0:D], ALU.add).then_inc(added, 1)



def small_head_attention(nc, g, w, st, q_source, k_source, scale, mask=None):
    Q, UN = 4, H // 4
    qT, kT = st.sb("qT", [128, TOK]), st.sb("kT", [128, TOK])
    v = st.sb("v", [T, B, H, HD + 1])
    qs, ks = st.sb("qs", [128, 2, T]), st.sb("ks", [128, 2, H, T])
    top, inv = st.sb("top", [T, 2, Q]), st.sb("inv", [T, 2, Q])
    p, pT = st.sb("p", [T, 2, Q * T]), st.sb("pT", [T, 2, Q * T])
    o, oT = st.sb("o", [T, 2, H * HD]), st.sb("oT", [128, TOK])
    proj, v_made, ones_set = (st.sem(s) for s in ("proj", "v_made", "ones_set"))
    staged, scored, centered, exped, turned, pT_kept, mixed, normed, o_turned, oT_kept = (
        st.sem(s) for s in ("staged", "scored", "centered", "exped", "turned", "pT_kept", "mixed", "normed",
                            "o_turned", "oT_kept"))
    bank = g.bank

    with nc.Block() as block:
        @block.gpsimd
        def _(pool):
            nc.gpsimd.memset(v[:, :, :, HD:HD + 1], 1.0)

        @block.tensor
        def _(pe):
            pe.wait_ge(w.loaded, 16)
            for j, (weight, source) in enumerate((("wq", q_source), ("wk", k_source))):
                for half in range(2):
                    nc.tensor.matmul(bank[2 * j + half][:], w[weight], source[:, half * HALF:(half + 1) * HALF],
                                     start=True, stop=True).then_inc(proj, 1)
            for half in range(2):
                for j in range(4):
                    b = 4 * half + j
                    last = nc.tensor.matmul(bank[4 + half][:, j * D:(j + 1) * D], g.ctxT[:, b * T:(b + 1) * T],
                                            w["wv"], start=True, stop=True)
                last.then_inc(v_made, 1)

        @block.scalar
        def _(act):
            for m in range(4):
                act.wait_ge(proj, m + 1)
                dst, bias = ((qT, "bq"), (kT, "bk"))[m // 2]
                nc.scalar.activation(dst[:, (m % 2) * HALF:(m % 2 + 1) * HALF], bank[m][:], ACT.Identity, bias=w[bias])

        @block.vector
        def _(dve):
            for half in range(2):
                dve.wait_ge(v_made, half + 1)
                for j in range(4):
                    nc.vector.tensor_tensor(v[:, 4 * half + j, :, 0:HD], rows_of(bank[4 + half][:, j * D:(j + 1) * D], H),
                                            rows_of(w["bv"], H), ALU.add)

    score, tps, mix, o_tps = bank[0:2], bank[2:4], bank[4:6], bank[6][:, 0:T]
    with nc.Block() as block:
        @block.gpsimd
        def _(pool):
            credit(pool, staged)
            with pool.Fori(0, B // 2) as i:
                for u in range(2):
                    n = 2 * i + u
                    pool.wait_ge(scored, done(UN * (n - 2) + UN - 1))
                    nc.gpsimd.tensor_copy(qs[:, u, :], qT[:, bass.ds(n * T, T)])
                    nc.gpsimd.tensor_tensor(ks[:, u, :, :], bc(kT[:, bass.ds(n * T, T)], 1, H),
                                            bc(g.const["head"], 2, T), ALU.mult).then_inc(staged, 1)

        @block.tensor
        def _(pe):
            credit(pe, scored, turned, mixed, o_turned)
            with pe.Fori(0, B // 2) as i:
                def scores(k):
                    m, u, q, e = 2 * UN * i + k, k // UN, k % UN, k % 2
                    if q == 0:
                        pe.wait_ge(staged, done(2 * i + u))
                    pe.wait_ge(centered, done(m - 2))
                    if mask is not None:
                        nc.tensor.matmul(score[e][:], g.ident_bf[:], bc(mask(2 * i + u), 1, Q),
                                         start=True, stop=False)
                    nc.tensor.matmul(score[e][:], qs[:, u, :], ks[:, u, Q * q:Q * (q + 1), :],
                                     start=mask is None, stop=True).then_inc(scored, 1)

                def turns(k):
                    m, e = 2 * UN * i + k, k % 2
                    pe.wait_ge(exped, done(m))
                    pe.wait_ge(pT_kept, done(m - 2))
                    for j in range(Q):
                        last = nc.tensor.transpose(tps[e][:, j * T:(j + 1) * T], p[:, e, j * T:(j + 1) * T], g.ident)
                    last.then_inc(turned, 1)

                def mix_values(k):
                    m, u, q, e = 2 * UN * i + k, k // UN, k % UN, k % 2
                    pe.wait_ge(pT_kept, done(m))
                    pe.wait_ge(normed, done(m - 2))
                    for j in range(Q):
                        last = nc.tensor.matmul(mix[e][:, j * (HD + 1):(j + 1) * (HD + 1)], pT[:, e, j * T:(j + 1) * T],
                                                v[:, 2 * i + u, Q * q + j, :], start=True, stop=True)
                    last.then_inc(mixed, 1)

                for k in range(2 * UN + 3):
                    if k < 2 * UN:
                        scores(k)
                    if 0 <= k - 1 < 2 * UN:
                        turns(k - 1)
                    if 0 <= k - 2 < 2 * UN:
                        mix_values(k - 2)
                    if k in (UN + 2, 2 * UN + 2):
                        n = 2 * i + (k - 3) // UN
                        pe.wait_ge(normed, done(UN * n + UN - 1))
                        pe.wait_ge(oT_kept, done(n - 1))
                        nc.tensor.transpose(o_tps, o[:, (k - 3) // UN, :], g.ident).then_inc(o_turned, 1)

        @block.scalar
        def _(act):
            credit(act, exped, pT_kept, oT_kept)
            with act.Fori(0, B // 2) as i:
                for k in range(2 * UN + 3):
                    if k < 2 * UN:
                        m, e = 2 * UN * i + k, k % 2
                        act.wait_ge(centered, done(m))
                        nc.scalar.activation(p[:, e, :], p[:, e, :], ACT.Exp, scale=scale).then_inc(exped, 1)
                    if 0 <= k - 1 < 2 * UN:
                        m, e = 2 * UN * i + k - 1, (k - 1) % 2
                        act.wait_ge(turned, done(m))
                        act.wait_ge(mixed, done(m - 2))
                        nc.scalar.activation(pT[:, e, :], tps[e][:], ACT.Copy).then_inc(pT_kept, 1)
                    if k in (UN + 2, 2 * UN + 2):
                        n = 2 * i + (k - 3) // UN
                        act.wait_ge(o_turned, done(n))
                        nc.scalar.activation(oT[:, bass.ds(n * T, T)], o_tps, ACT.Copy).then_inc(oT_kept, 1)

        @block.vector
        def _(dve):
            credit(dve, centered, normed)
            with dve.Fori(0, B // 2) as i:
                for k in range(2 * UN + 2):
                    if k < 2 * UN:
                        m, e = 2 * UN * i + k, k % 2
                        dve.wait_ge(scored, done(m))
                        nc.vector.tensor_reduce(top[:, e, :], rows_of(score[e][:], Q), X, ALU.max)
                        dve.drain()
                        dve.wait_ge(turned, done(m - 2))
                        nc.vector.tensor_tensor(rows_of(p[:, e, :], Q), rows_of(score[e][:], Q),
                                                bc(top[:, e, :], 2, T), ALU.subtract).then_inc(centered, 1)
                    if 0 <= k - 2 < 2 * UN:
                        m, e, u, q = 2 * UN * i + k - 2, (k - 2) % 2, (k - 2) // UN, (k - 2) % UN
                        out = mix[e][:, 0:Q * (HD + 1)].rearrange("p (a b) -> p a b", a=Q)
                        dve.wait_ge(mixed, done(m))
                        nc.vector.reciprocal(inv[:, e, :], out[:, :, HD])
                        dve.drain()
                        if q == 0:
                            dve.wait_ge(o_turned, done(2 * i + u - 2))
                        nc.vector.tensor_tensor(rows_of(o[:, u, Q * HD * q:Q * HD * (q + 1)], Q), out[:, :, 0:HD],
                                                bc(inv[:, e, :], 2, HD), ALU.mult).then_inc(normed, 1)
    return oT


def add_projection(nc, g, w, st, oT):
    bank = g.bank
    biased, projected = st.sem("biased"), st.sem("projected")
    with nc.Block() as block:
        @block.tensor
        def _(pe):
            for half in range(2):
                for j in range(4):
                    b = 4 * half + j
                    last = nc.tensor.matmul(bank[half][:, j * D:(j + 1) * D], oT[:, b * T:(b + 1) * T], w["wo"],
                                            start=True, stop=True)
                last.then_inc(projected, 1)

        @block.vector
        def _(dve):
            if "bo" in w.places:
                nc.vector.tensor_tensor(g.x[:], g.x[:], bc(w["bo"], 1, B), ALU.add)
                dve.drain()
            for half in range(2):
                b = slice(4 * half, 4 * half + 4)
                dve.wait_ge(projected, half + 1)
                nc.vector.tensor_tensor(g.x[:, b, :], g.x[:, b, :], rows_of(bank[half][:], 4), ALU.add)


def cross_attention(nc, g, w, name):
    with Stage(nc, name) as st:
        oT = small_head_attention(nc, g, w, st, g.hT, g.ctxT, HD ** -0.5)
        add_projection(nc, g, w, st, oT)


def masked_cross_attention(nc, g, w, name):
    with Stage(nc, name) as st:
        mask8, mask = st.sb("mask8", [T, B, T], U8), st.sb("mask", [T, B, T], BF16)
        mask_loaded = st.sem("mask_loaded")
        with nc.Block() as block:
            @block.sync
            def _(sp):
                sp.dma_start(mask8[:], g.dram["mask"].rearrange("b q k -> q b k")).then_inc(mask_loaded, 16)

            @block.vector
            def _(dve):
                dve.wait_ge(mask_loaded, 16)
                nc.vector.tensor_scalar(mask[:], mask8[:], NEG, None, ALU.mult)
        oT = small_head_attention(nc, g, w, st, g.hT, g.ctxT, HD ** -0.5, lambda n: mask[:, n, :])
        add_projection(nc, g, w, st, oT)


def attention_with_mlp(nc, g, w, name):
    NJ = 4
    bank = g.bank
    with Stage(nc, name) as st:
        oT = small_head_attention(nc, g, w, st, g.hT, g.hT, 1.0, lambda n: g.shifted_bf[:, 0, :])
        hid = st.sb("hid", [128, NJ, TOK])
        up, kept, down = st.sem("up"), st.sem("kept"), st.sem("down")
        with nc.Block() as block:
            @block.tensor
            def _(pe):
                for m in range(2 * NJ):
                    j, half = m % NJ, m // NJ
                    if m >= 6:
                        pe.wait_ge(kept, m - 5)
                    nc.tensor.matmul(bank[m % 6][:], w["w1"][:, j * 128:(j + 1) * 128],
                                     oT[:, half * HALF:(half + 1) * HALF], start=True, stop=True).then_inc(up, 1)
                for b in range(B):
                    if b % 4 == 0:
                        pe.wait_ge(kept, NJ * (b // 4 + 1))
                    for j in range(NJ):
                        last = nc.tensor.matmul(bank[6 + b // 4][:, (b % 4) * D:(b % 4 + 1) * D],
                                                hid[:, j, b * T:(b + 1) * T], w["w2"][:, j * D:(j + 1) * D],
                                                start=(j == 0), stop=(j == NJ - 1))
                    if b % 4 == 3:
                        last.then_inc(down, 1)

            @block.scalar
            def _(act):
                for m in range(2 * NJ):
                    j, half = m % NJ, m // NJ
                    act.wait_ge(up, m + 1)
                    nc.scalar.activation(hid[:, j, half * HALF:(half + 1) * HALF], bank[m % 6][:], ACT.Gelu,
                                         bias=w["b1"][:, j:j + 1]).then_inc(kept, 1)

            @block.vector
            def _(dve):
                nc.vector.tensor_tensor(g.x[:], g.x[:], bc(w["b2"], 1, B), ALU.add)
                dve.drain()
                for half in range(2):
                    b = slice(4 * half, 4 * half + 4)
                    dve.wait_ge(down, half + 1)
                    nc.vector.tensor_tensor(g.x[:, b, :], g.x[:, b, :], rows_of(bank[6 + half][:], 4), ALU.add)



def route_top2_softmax(nc, g, w, st, combine):
    E = 8
    bank = g.bank
    logit, best, keep = st.sb("logit", [T, B, E]), st.sb("best", [T, B, 8]), st.sb("keep", [T, B, E])
    total, combT = st.sb("total", [T, B]), st.sb("combT", [E, TOK])
    made, centered, exped, routed, combine_turned, combT_kept, biases = (
        st.sem(s) for s in ("made", "centered", "exped", "routed", "combine_turned", "combT_kept", "biases"))
    with nc.Block() as block:
        @block.tensor
        def _(pe):
            pe.wait_ge(w.loaded, 16)
            for b in range(B):
                last = nc.tensor.matmul(bank[0][:, b * E:(b + 1) * E], g.hT[:, b * T:(b + 1) * T], w["router"],
                                        start=True, stop=True)
            last.then_inc(made, 1)
            pe.wait_ge(routed, 1)
            for b in range(B):
                last = nc.tensor.transpose(bank[1 + b // 4][0:E, (b % 4) * T:(b % 4 + 1) * T], combine[:, b, :], g.ident)
            last.then_inc(combine_turned, 1)
            pe.wait_ge(combT_kept, 1)
            for b in range(B):
                last = nc.tensor.matmul(bank[3 + b // 4][:, (b % 4) * D:(b % 4 + 1) * D], combT[:, b * T:(b + 1) * T],
                                        w["b2"], start=True, stop=True)
            last.then_inc(biases, 1)

        @block.scalar
        def _(act):
            act.wait_ge(centered, 1)
            nc.scalar.activation(logit[:], logit[:], ACT.Exp).then_inc(exped, 1)
            act.wait_ge(combine_turned, 1)
            for half in range(2):
                last = nc.scalar.activation(combT[:, half * HALF:(half + 1) * HALF], bank[1 + half][0:E, :], ACT.Copy)
            last.then_inc(combT_kept, 1)

        @block.vector
        def _(dve):
            dve.wait_ge(made, 1)
            nc.vector.tensor_tensor(logit[:], rows_of(bank[0][:, 0:B * E], B), bc(w["br"], 1, B), ALU.add)
            dve.drain()
            for b in range(B):
                nc.vector.max(best[:, b, :], logit[:, b, :])
            dve.drain()
            nc.vector.tensor_tensor(keep[:], logit[:], best[:, :, 1:2].to_broadcast([T, B, E]), ALU.is_ge)
            dve.drain()
            nc.vector.tensor_tensor(logit[:], logit[:], best[:, :, 0:1].to_broadcast([T, B, E]),
                                    ALU.subtract).then_inc(centered, 1)
            dve.wait_ge(exped, 1)
            nc.vector.tensor_tensor(keep[:], keep[:], logit[:], ALU.mult)
            dve.drain()
            nc.vector.tensor_reduce(total[:], keep[:], X, ALU.add)
            dve.drain()
            nc.vector.reciprocal(total[:], total[:])
            dve.drain()
            nc.vector.tensor_tensor(combine[:], keep[:], bc(total[:], 2, E), ALU.mult).then_inc(routed, 1)
            dve.wait_ge(biases, 1)
            for half in range(2):
                b = slice(4 * half, 4 * half + 4)
                nc.vector.tensor_tensor(g.x[:, b, :], g.x[:, b, :], rows_of(bank[3 + half][:], 4), ALU.add)


def route_top2_renormed(nc, g, w, st, combine):
    E = 8
    bank = g.bank
    sq, meansq, rms = st.sb("sq", [T, B, D]), st.sb("meansq", [T, B]), st.sb("rms", [T, B])
    power, router = st.sb("power", [T, B]), st.sb("router", [D, E])
    logit, best, keep = st.sb("logit", [T, B, E]), st.sb("best", [T, B, 8]), st.sb("keep", [T, B, E])
    total, fix = st.sb("total", [T, B]), st.sb("fix", [T, B])
    power_set, squared, rms_ready, router_ready, made, centered, exped = (
        st.sem(s) for s in ("power_set", "squared", "rms_ready", "router_ready", "made", "centered", "exped"))
    with nc.Block() as block:
        @block.gpsimd
        def _(pool):
            nc.gpsimd.memset(power[:], -0.5).then_inc(power_set, 1)
            pool.wait_ge(power_set, 1)
            pool.wait_ge(squared, 1)
            nc.gpsimd.tensor_tensor(rms[:], meansq[:], power[:], ALU.pow).then_inc(rms_ready, 1)

        @block.tensor
        def _(pe):
            pe.wait_ge(router_ready, 1)
            for b in range(B):
                last = nc.tensor.matmul(bank[0][:, b * E:(b + 1) * E], g.hT[:, b * T:(b + 1) * T], router[:],
                                        start=True, stop=True)
            last.then_inc(made, 1)

        @block.scalar
        def _(act):
            act.wait_ge(centered, 1)
            nc.scalar.activation(logit[:], logit[:], ACT.Exp).then_inc(exped, 1)

        @block.vector
        def _(dve):
            dve.wait_ge(w.loaded, 16)
            nc.vector.tensor_scalar(router[:], w["router"], w["router_scale"], float(D) ** -0.5,
                                    ALU.mult, ALU.mult).then_inc(router_ready, 1)
            nc.vector.tensor_tensor(sq[:], g.h[:], g.h[:], ALU.mult)
            dve.drain()
            nc.vector.tensor_reduce(meansq[:], sq[:], X, ALU.add)
            dve.drain()
            nc.vector.tensor_scalar(meansq[:], meansq[:], 1.0 / D, 1e-6, ALU.mult, ALU.add).then_inc(squared, 1)
            dve.wait_ge(rms_ready, 1)
            dve.wait_ge(made, 1)
            nc.vector.tensor_tensor(logit[:], rows_of(bank[0][:, 0:B * E], B), bc(rms[:], 2, E), ALU.mult)
            dve.drain()
            for b in range(B):
                nc.vector.max(best[:, b, :], logit[:, b, :])
            dve.drain()
            nc.vector.tensor_tensor(keep[:], logit[:], best[:, :, 1:2].to_broadcast([T, B, E]), ALU.is_ge)
            dve.drain()
            nc.vector.tensor_tensor(logit[:], logit[:], best[:, :, 0:1].to_broadcast([T, B, E]),
                                    ALU.subtract).then_inc(centered, 1)
            dve.wait_ge(exped, 1)
            nc.vector.tensor_tensor(keep[:], keep[:], logit[:], ALU.mult)
            dve.drain()
            nc.vector.tensor_reduce(total[:], keep[:], X, ALU.add)
            dve.drain()
            nc.vector.tensor_scalar(fix[:], total[:], 0.0, None, ALU.is_le)
            dve.drain()
            nc.vector.tensor_tensor(total[:], total[:], fix[:], ALU.add)
            dve.drain()
            nc.vector.reciprocal(total[:], total[:])
            dve.drain()
            nc.vector.tensor_tensor(keep[:], keep[:], bc(total[:], 2, E), ALU.mult)
            dve.drain()
            nc.vector.tensor_tensor(combine[:], keep[:], bc(w["expert_scale"], 1, B), ALU.mult)


def route_grouped_top8(nc, g, w, st, combine):
    E, G = 64, 8
    bank = g.bank
    score, biased, chosen = st.sb("score", [T, B, E]), st.sb("biased", [T, B, E]), st.sb("chosen", [T, B, E])
    rest = st.sb("rest", [T, B, E])
    top1, top2, count = st.sb("top1", [T, B * G]), st.sb("top2", [T, B * G]), st.sb("count", [T, B * G])
    gsum, gbest, gkeep = st.sb("gsum", [T, B, G]), st.sb("gbest", [T, B, 8]), st.sb("gkeep", [T, B * G])
    best, total = st.sb("best", [T, B, 8]), st.sb("total", [T, B])
    made, sigmoid_ready = st.sem("made"), st.sem("sigmoid_ready")
    groups = lambda t: t[:].rearrange("p b (g e) -> p (b g) e", e=G)
    with nc.Block() as block:
        @block.tensor
        def _(pe):
            pe.wait_ge(w.loaded, 16)
            for b in range(B):
                last = nc.tensor.matmul(bank[0][:, b * E:(b + 1) * E], g.hT[:, b * T:(b + 1) * T], w["router"],
                                        start=True, stop=True)
            last.then_inc(made, 1)

        @block.scalar
        def _(act):
            act.wait_ge(made, 1)
            nc.scalar.activation(score[:], rows_of(bank[0][:], B), ACT.Sigmoid).then_inc(sigmoid_ready, 1)

        @block.vector
        def _(dve):
            dve.wait_ge(sigmoid_ready, 1)
            nc.vector.tensor_tensor(biased[:], score[:], bc(w["correction"], 1, B), ALU.add)
            dve.drain()
            nc.vector.tensor_reduce(top1[:], groups(biased), X, ALU.max)
            dve.drain()
            nc.vector.tensor_tensor(groups(chosen), groups(biased), bc(top1[:], 2, G), ALU.is_ge)
            dve.drain()
            nc.vector.tensor_reduce(count[:], groups(chosen), X, ALU.add)
            nc.vector.scalar_tensor_tensor(groups(rest), groups(chosen), NEG, groups(biased), ALU.mult, ALU.add)
            dve.drain()
            nc.vector.tensor_reduce(top2[:], groups(rest), X, ALU.max)
            nc.vector.tensor_scalar(count[:], count[:], 1.5, NEG, ALU.is_lt, ALU.mult)
            dve.drain()
            nc.vector.tensor_tensor(count[:], count[:], top1[:], ALU.add)
            dve.drain()
            nc.vector.tensor_tensor(top2[:], top2[:], count[:], ALU.max)
            dve.drain()
            nc.vector.tensor_tensor(gsum[:].rearrange("p b g -> p (b g)"), top1[:], top2[:], ALU.add)
            dve.drain()
            for b in range(B):
                nc.vector.max(gbest[:, b, :], gsum[:, b, :])
            dve.drain()
            nc.vector.tensor_tensor(rows_of(gkeep[:], B), gsum[:], gbest[:, :, 3:4].to_broadcast([T, B, G]), ALU.is_ge)
            dve.drain()
            nc.vector.tensor_tensor(groups(biased), groups(biased), bc(gkeep[:], 2, G), ALU.mult)
            dve.drain()
            for b in range(B):
                nc.vector.max(best[:, b, :], biased[:, b, :])
            dve.drain()
            for b in range(B):
                nc.vector.match_replace(rest[:, b, :], best[:, b, :], biased[:, b, :], NEG)
            dve.drain()
            nc.vector.tensor_scalar(chosen[:], rest[:], NEG, None, ALU.is_equal)
            dve.drain()
            nc.vector.tensor_tensor(chosen[:], chosen[:], score[:], ALU.mult)
            dve.drain()
            nc.vector.tensor_reduce(total[:], chosen[:], X, ALU.add)
            dve.drain()
            nc.vector.tensor_scalar(total[:], total[:], 1e-20, None, ALU.add)
            dve.drain()
            nc.vector.reciprocal(total[:], total[:])
            dve.drain()
            nc.vector.tensor_scalar(total[:], total[:], 2.5, None, ALU.mult)
            dve.drain()
            nc.vector.tensor_tensor(combine[:, :, 0:E], chosen[:], bc(total[:], 2, E), ALU.mult)


GATED, SQUARED, BIASED = range(3)


def experts(nc, g, w, st, combine, kind, widths):
    UN = len(widths)
    bank = g.bank
    hs = st.sb("hs", [D, 2, T])
    a, aT = st.sb("a", [T, 2, HALF]), st.sb("aT", [128, 2, 4, T])
    r = st.sb("r", [T, 2, HALF])
    staged, hidden, part, weighed, scaled, turned, aT_kept, summed, added = (
        st.sem(s) for s in ("staged", "hidden", "part", "weighed", "scaled", "turned", "aT_kept", "summed", "added"))
    up, tps, acc = bank[0:2], bank[2:4], bank[4:6]
    tile_at = [sum(widths[:q]) // 128 for q in range(UN)]
    up_width = [2 * x if kind == GATED else x for x in widths]
    up_at = [sum(up_width[:q]) for q in range(UN)]
    EXPERTS = 8

    with nc.Block() as block:
        @block.gpsimd
        def _(pool):
            credit(pool, staged)
            if kind == SQUARED:
                credit(pool, weighed)
            with pool.Fori(0, B // 2) as i:
                for u in range(2):
                    n = 2 * i + u
                    pool.wait_ge(hidden, done(UN * (n - 2) + UN - 1))
                    nc.gpsimd.tensor_copy(hs[:, u, :], g.hT[:, bass.ds(n * T, T)]).then_inc(staged, 1)
                    if kind == SQUARED:
                        for q in range(UN):
                            k = UN * u + q
                            m, e, wide = 2 * UN * i + k, k % 2, widths[q]
                            pool.wait_ge(part, done(m))
                            ex = wide // (HALF // EXPERTS)
                            rows = r[:, e, 0:wide].rearrange("p (a b) -> p a b", a=ex)
                            nc.gpsimd.tensor_tensor(rows, rows, bc(combine[:, n, EXPERTS * q:EXPERTS * q + ex], 2,
                                                                   HALF // EXPERTS), ALU.mult).then_inc(weighed, 1)

        @block.tensor
        def _(pe):
            credit(pe, hidden, turned, summed)
            with pe.Fori(0, B // 2) as i:
                def hidden_layer(k):
                    m, u, q, e = 2 * UN * i + k, k // UN, k % UN, k % 2
                    if q == 0:
                        pe.wait_ge(staged, done(2 * i + u))
                    pe.wait_ge(scaled, done(m - 2))
                    nc.tensor.matmul(up[e][:, 0:up_width[q]], hs[:, u, :], w["up"][:, up_at[q]:up_at[q] + up_width[q]],
                                     start=True, stop=True).then_inc(hidden, 1)

                def turns(k):
                    m, q, e = 2 * UN * i + k, k % UN, k % 2
                    pe.wait_ge(scaled, done(m))
                    pe.wait_ge(aT_kept, done(m - 2))
                    for j in range(widths[q] // 128):
                        last = nc.tensor.transpose(tps[e][:, j * T:(j + 1) * T], a[:, e, j * 128:(j + 1) * 128], g.ident)
                    last.then_inc(turned, 1)

                def sums(k):
                    m, u, q, e = 2 * UN * i + k, k // UN, k % UN, k % 2
                    pe.wait_ge(aT_kept, done(m))
                    if q == 0:
                        pe.wait_ge(added, done(2 * i + u - 2))
                    tiles = widths[q] // 128
                    for j in range(tiles):
                        at = (tile_at[q] + j) * D
                        last = nc.tensor.matmul(acc[u][:, 0:D], aT[:, e, j, :], w["down"][:, at:at + D],
                                                start=(q == 0 and j == 0), stop=(q == UN - 1 and j == tiles - 1))
                    last.then_inc(summed, 1)

                for k in range(2 * UN + 2):
                    if k < 2 * UN:
                        hidden_layer(k)
                    if 0 <= k - 2 < 2 * UN:
                        sums(k - 2)
                    if 0 <= k - 1 < 2 * UN:
                        turns(k - 1)

        @block.scalar
        def _(act):
            credit(act, part, aT_kept)
            with act.Fori(0, B // 2) as i:
                for k in range(2 * UN + 1):
                    if k < 2 * UN:
                        m, q, e = 2 * UN * i + k, k % UN, k % 2
                        wide = widths[q]
                        if kind == GATED:
                            act.wait_ge(hidden, done(m))
                            act.wait_ge(scaled, done(m - 2))
                            nc.scalar.activation(r[:, e, 0:wide], up[e][:, 0:wide], ACT.Gelu_apprx_tanh).then_inc(part, 1)
                        elif kind == SQUARED:
                            act.wait_ge(hidden, done(m))
                            act.wait_ge(scaled, done(m - 2))
                            nc.scalar.activation(r[:, e, 0:wide], up[e][:, 0:wide], ACT.Relu).then_inc(part, 1)
                        else:
                            act.wait_ge(weighed, done(m))
                            act.wait_ge(scaled, done(m - 2))
                            nc.scalar.activation(r[:, e, 0:wide], a[:, e, 0:wide], ACT.Gelu).then_inc(part, 1)
                    if 0 <= k - 1 < 2 * UN:
                        m, q, e = 2 * UN * i + k - 1, (k - 1) % UN, (k - 1) % 2
                        act.wait_ge(turned, done(m))
                        act.wait_ge(summed, done(m - 2))
                        tiles = widths[q] // 128
                        nc.scalar.activation(aT[:, e, 0:tiles, :], rows_of(tps[e][:, 0:widths[q]], tiles),
                                             ACT.Copy).then_inc(aT_kept, 1)

        @block.vector
        def _(dve):
            credit(dve, scaled, added)
            if kind == BIASED:
                credit(dve, weighed)
            with dve.Fori(0, B // 2) as i:
                def bias(k):
                    m, q, e = 2 * UN * i + k, k % UN, k % 2
                    dve.wait_ge(hidden, done(m))
                    dve.wait_ge(turned, done(m - 2))
                    nc.vector.tensor_tensor(a[:, e, :], up[e][:], w["b1"][:, q * HALF:(q + 1) * HALF],
                                            ALU.add).then_inc(weighed, 1)

                def scale(k):
                    m, u, q, e, wide = 2 * UN * i + k, k // UN, k % UN, k % 2, widths[k % UN]
                    dve.wait_ge(part, done(m))
                    dve.wait_ge(turned, done(m - 2))
                    if kind == GATED:
                        nc.vector.scalar_tensor_tensor(a[:, e, 0:wide], up[e][:, wide:2 * wide],
                                                       combine[:, 2 * i + u, q:q + 1], r[:, e, 0:wide],
                                                       ALU.mult, ALU.mult).then_inc(scaled, 1)
                    elif kind == SQUARED:
                        dve.wait_ge(weighed, done(m))
                        nc.vector.scalar_tensor_tensor(a[:, e, 0:wide], up[e][:, 0:wide], 0.0, r[:, e, 0:wide],
                                                       ALU.max, ALU.mult).then_inc(scaled, 1)
                    else:
                        nc.vector.tensor_scalar(a[:, e, :], r[:, e, :], combine[:, 2 * i + u, q:q + 1], None,
                                                ALU.mult).then_inc(scaled, 1)

                for k in range(2 * UN + 3):
                    if kind == BIASED:
                        if k < 2 * UN:
                            bias(k)
                        if 0 <= k - 1 < 2 * UN:
                            scale(k - 1)
                    elif k < 2 * UN:
                        scale(k)
                    if k in (UN + 2, 2 * UN + 2):
                        n, u = 2 * i + (k - 3) // UN, (k - 3) // UN
                        dve.wait_ge(summed, done(UN * n + UN - 1))
                        nc.vector.tensor_tensor(g.x[:, n, :], g.x[:, n, :], acc[u][:, 0:D], ALU.add).then_inc(added, 1)


def gated_experts(nc, g, w, name):
    with Stage(nc, name) as st:
        combine = st.sb("combine", [T, B, 8])
        route_top2_renormed(nc, g, w, st, combine)
        experts(nc, g, w, st, combine, GATED, [256] * 8)


def many_experts(nc, g, w, name):
    with Stage(nc, name) as st:
        combine = st.sb("combine", [T, B, 68])
        with nc.Block() as block:
            @block.gpsimd
            def _(pool):
                nc.gpsimd.memset(combine[:, :, 64:68], 1.0)
        route_grouped_top8(nc, g, w, st, combine)
        experts(nc, g, w, st, combine, SQUARED, [HALF] * 8 + [256])


def wide_experts(nc, g, w, name):
    with Stage(nc, name) as st:
        combine = st.sb("combine", [T, B, 8])
        route_top2_softmax(nc, g, w, st, combine)
        experts(nc, g, w, st, combine, BIASED, [HALF] * 8)



def ternary_ffn(nc, g, w, name):
    INNER = 512
    bank = g.bank
    with Stage(nc, name) as st:
        mats = ("gate", "up", "down")
        rowsum = st.sb("rowsum", [128, 3])
        unit, unit_inv = st.sb("unit", [128, 3]), st.sb("unit_inv", [128, 3])
        wf, wq = st.sb("wf", [128, INNER]), st.sb("wq", [128, 3, INNER], BF16)
        peak, inv = st.sb("peak", [T, B]), st.sb("inv", [T, B])
        gate_scale, up_scale = st.sb("gate_scale", [T, B]), st.sb("up_scale", [T, B])
        hf, hq, hqT = st.sb("hf", [T, B, D]), st.sb("hq", [T, B, D], BF16), st.sb("hqT", [D, TOK], BF16)
        summed, means, quantised, turned, hqT_kept = (
            st.sem(s) for s in ("summed", "means", "quantised", "turned", "hqT_kept"))
        with nc.Block() as block:
            @block.tensor
            def _(pe):
                pe.wait_ge(summed, 1)
                nc.tensor.matmul(bank[2][:, 0:3], g.const["ones"], rowsum[:], start=True, stop=True).then_inc(means, 1)
                for half in range(2):
                    pe.wait_ge(quantised, 1)
                    for j in range(4):
                        last = nc.tensor.transpose(g.bank_bf[half][:, j * T:(j + 1) * T], hq[:, 4 * half + j, :],
                                                   g.ident_bf[:])
                    last.then_inc(turned, 1)

            @block.scalar
            def _(act):
                for half in range(2):
                    act.wait_ge(turned, half + 1)
                    nc.scalar.activation(hqT[:, half * HALF:(half + 1) * HALF], g.bank_bf[half][:, 0:HALF], ACT.Copy)

            @block.vector
            def _(dve):
                dve.wait_ge(w.loaded, 16)
                for j, name in enumerate(mats):
                    nc.vector.tensor_reduce(rowsum[:, j:j + 1], w[name], X, ALU.add, apply_absolute_value=True)
                dve.drain()
                nc.vector.tensor_scalar(rowsum[:], rowsum[:], 1.0 / (INNER * D), None, ALU.mult).then_inc(summed, 1)
                nc.vector.tensor_reduce(peak[:], g.h[:], X, ALU.max, apply_absolute_value=True)
                dve.drain()
                nc.vector.tensor_scalar(peak[:], peak[:], 1e-5, 1.0 / 127.0, ALU.max, ALU.mult)
                dve.drain()
                nc.vector.reciprocal(inv[:], peak[:])
                dve.drain()
                nc.vector.tensor_tensor(hf[:], g.h[:], bc(inv[:], 2, D), ALU.mult)
                dve.drain()
                nc.vector.tensor_scalar(hf[:], hf[:], ROUND, ROUND, ALU.add, ALU.subtract)
                dve.drain()
                nc.vector.tensor_scalar(hq[:], hf[:], 127.0, -128.0, ALU.min, ALU.max).then_inc(quantised, 1)
                dve.wait_ge(means, 1)
                nc.vector.tensor_scalar(unit[:], bank[2][:, 0:3], 1e-5, None, ALU.max)
                dve.drain()
                nc.vector.reciprocal(unit_inv[:], unit[:])
                dve.drain()
                for j, name in enumerate(mats):
                    nc.vector.tensor_scalar(wf[:], w[name], unit_inv[:, j:j + 1], None, ALU.mult)
                    dve.drain()
                    nc.vector.tensor_scalar(wf[:], wf[:], ROUND, ROUND, ALU.add, ALU.subtract)
                    dve.drain()
                    nc.vector.tensor_scalar(wq[:, j, :], wf[:], 1.0, -1.0, ALU.min, ALU.max)
                    dve.drain()
                nc.vector.tensor_scalar(gate_scale[:], peak[:], unit[:, 0:1], None, ALU.mult)
                nc.vector.tensor_scalar(up_scale[:], peak[:], unit[:, 1:2], None, ALU.mult)

        gated, prod = st.sb("gated", [T, 2, INNER]), st.sb("prod", [T, 2, INNER])
        prodf, prodq = st.sb("prodf", [T, 2, INNER]), st.sb("prodq", [T, 2, INNER], BF16)
        peak2, inv2, out_scale = st.sb("peak2", [T, 2]), st.sb("inv2", [T, 2]), st.sb("out_scale", [T, 2])
        prodT = st.sb("prodT", [128, 2, 4, T], BF16)
        hidden, silu_ready, rounded, prod_turned, prodT_kept, made, added = (
            st.sem(s) for s in ("hidden", "silu_ready", "rounded", "prod_turned", "prodT_kept", "made", "added"))
        gate, up, tps, out = bank[0:2], bank[2:4], g.bank_bf[4:6], bank[6:8]
        with nc.Block() as block:
            @block.tensor
            def _(pe):
                credit(pe, hidden, prod_turned, made)
                with pe.Fori(0, B // 2) as i:
                    for u in range(2):
                        n = 2 * i + u
                        pe.wait_ge(rounded, done(n - 2))
                        for at, j in ((gate[u], 0), (up[u], 1)):
                            last = nc.tensor.matmul(at[:], hqT[:, bass.ds(n * T, T)], wq[:, j, :], start=True, stop=True)
                        last.then_inc(hidden, 1)
                    for u in range(2):
                        n = 2 * i + u
                        pe.wait_ge(rounded, done(n))
                        pe.wait_ge(prodT_kept, done(n - 2))
                        for j in range(4):
                            last = nc.tensor.transpose(tps[u][:, j * T:(j + 1) * T], prodq[:, u, j * 128:(j + 1) * 128],
                                                       g.ident_bf[:])
                        last.then_inc(prod_turned, 1)
                        pe.wait_ge(prodT_kept, done(n))
                        pe.wait_ge(added, done(n - 2))
                        for j in range(4):
                            last = nc.tensor.matmul(out[u][:, 0:D], prodT[:, u, j, :], wq[:, 2, j * D:(j + 1) * D],
                                                    start=(j == 0), stop=(j == 3))
                        last.then_inc(made, 1)

            @block.scalar
            def _(act):
                credit(act, silu_ready, prodT_kept)
                with act.Fori(0, B // 2) as i:
                    for u in range(2):
                        n = 2 * i + u
                        act.wait_ge(hidden, done(n))
                        act.wait_ge(rounded, done(n - 2))
                        nc.scalar.activation(gated[:, u, :], gate[u][:], ACT.Silu,
                                             scale=gate_scale[:, bass.ds(n, 1)]).then_inc(silu_ready, 1)
                    for u in range(2):
                        n = 2 * i + u
                        act.wait_ge(prod_turned, done(n))
                        act.wait_ge(made, done(n - 2))
                        nc.scalar.activation(prodT[:, u, :, :], rows_of(tps[u][:, 0:HALF], 4),
                                             ACT.Copy).then_inc(prodT_kept, 1)

            @block.vector
            def _(dve):
                credit(dve, rounded, added)
                with dve.Fori(0, B // 2) as i:
                    for u in range(2):
                        n = 2 * i + u
                        dve.wait_ge(silu_ready, done(n))
                        nc.vector.scalar_tensor_tensor(prod[:, u, :], up[u][:], up_scale[:, bass.ds(n, 1)], gated[:, u, :],
                                                       ALU.mult, ALU.mult)
                        dve.drain()
                        nc.vector.tensor_reduce(peak2[:, u:u + 1], prod[:, u, :], X, ALU.max, apply_absolute_value=True)
                        dve.drain()
                        nc.vector.tensor_scalar(peak2[:, u:u + 1], peak2[:, u:u + 1], 1e-5, 1.0 / 127.0, ALU.max, ALU.mult)
                        dve.drain()
                        nc.vector.reciprocal(inv2[:, u:u + 1], peak2[:, u:u + 1])
                        nc.vector.tensor_scalar(out_scale[:, u:u + 1], peak2[:, u:u + 1], unit[:, 2:3], None, ALU.mult)
                        dve.drain()
                        nc.vector.tensor_scalar(prodf[:, u, :], prod[:, u, :], inv2[:, u:u + 1], ROUND, ALU.mult, ALU.add)
                        dve.drain()
                        dve.wait_ge(prod_turned, done(n - 2))
                        nc.vector.tensor_scalar(prodq[:, u, :], prodf[:, u, :], ROUND, None,
                                                ALU.subtract).then_inc(rounded, 1)
                    for u in range(2):
                        n = 2 * i + u
                        dve.wait_ge(made, done(n))
                        nc.vector.scalar_tensor_tensor(g.x[:, n, :], out[u][:, 0:D], out_scale[:, u:u + 1], g.x[:, n, :],
                                                       ALU.mult, ALU.add).then_inc(added, 1)



def time_mix(nc, g, w, name):
    bank = g.bank
    Q, UN = 4, H // 4
    with Stage(nc, name) as st:
        xx = st.sb("xx", [D, B, T])
        mixed = {c: st.sb("x" + c, [D, TOK]) for c in "rkvg"}
        rT, kT = st.sb("rT", [D, TOK]), st.sb("kT", [D, TOK])
        v, gate = st.sb("v", [T, B, D]), st.sb("gate", [T, B, D])
        rate, weight = st.sb("rate", [T, H]), st.sb("weight", [T, H, T])
        bonus = st.sb("bonus", [T, H, T])
        exped, projT, proj, blended, rates, powers, powers_ready = (
            st.sem(s) for s in ("exped", "projT", "proj", "blended", "rates", "powers", "powers_ready"))
        hT3 = rows_of(g.hT[:], B)
        with nc.Block() as block:
            @block.vector
            def _(dve):
                dve.wait_ge(w.loaded, 16)
                nc.vector.tensor_tensor(xx[:, :, 1:T], hT3[:, :, 0:T - 1], hT3[:, :, 1:T], ALU.subtract)
                nc.vector.tensor_scalar(xx[:, :, 0:1], hT3[:, :, 0:1], -1.0, None, ALU.mult)
                dve.drain()
                for c in "rkvg":
                    nc.vector.scalar_tensor_tensor(mixed[c][:], xx[:].rearrange("p b t -> p (b t)"), w["maa_" + c], g.hT[:],
                                                   ALU.mult, ALU.add).then_inc(blended, 1)
                dve.wait_ge(rates, 1)
                nc.vector.tensor_tensor(weight[:], bc(g.const["steps"], 1, H), bc(rate[:], 2, T), ALU.mult).then_inc(powers, 1)
                nc.vector.tensor_tensor(bonus[:], bc(g.ident, 1, H), bc(w["bonus"], 2, T), ALU.mult)
                dve.wait_ge(powers_ready, 1)
                nc.vector.tensor_tensor(weight[:], weight[:], bc(g.const["lt"], 1, H), ALU.mult)
                dve.drain()
                nc.vector.tensor_tensor(weight[:], weight[:], bonus[:], ALU.add)
                for half in range(2):
                    dve.wait_ge(proj, half + 1)
                    nc.vector.tensor_copy(v[:, 4 * half:4 * half + 4, :], rows_of(bank[4 + half][:], 4))

            @block.tensor
            def _(pe):
                for j, c in enumerate("rk"):
                    pe.wait_ge(blended, j + 1)
                    for half in range(2):
                        nc.tensor.matmul(bank[2 * j + half][:], w["w_" + c], mixed[c][:, half * HALF:(half + 1) * HALF],
                                         start=True, stop=True).then_inc(projT, 1)
                for j, c in enumerate("vg"):
                    pe.wait_ge(blended, j + 3)
                    for half in range(2):
                        for q in range(4):
                            b = 4 * half + q
                            last = nc.tensor.matmul(bank[4 + 2 * j + half][:, q * D:(q + 1) * D],
                                                    mixed[c][:, b * T:(b + 1) * T], w["w_" + c], start=True, stop=True)
                        last.then_inc(proj, 1)

            @block.scalar
            def _(act):
                act.wait_ge(w.loaded, 16)
                nc.scalar.activation(rate[:], w["decay"], ACT.Exp).then_inc(rates, 1)
                act.wait_ge(powers, 1)
                nc.scalar.activation(weight[:], weight[:], ACT.Exp, scale=-1.0).then_inc(powers_ready, 1)
                for m in range(4):
                    act.wait_ge(projT, m + 1)
                    nc.scalar.activation((rT, kT)[m // 2][:, (m % 2) * HALF:(m % 2 + 1) * HALF], bank[m][:], ACT.Copy)
                for half in range(2):
                    act.wait_ge(proj, 3 + half)
                    nc.scalar.activation(gate[:, 4 * half:4 * half + 4, :], rows_of(bank[6 + half][:], 4), ACT.Silu)

        ks, rs = st.sb("ks", [128, 2, T]), st.sb("rs", [128, 2, H, T])
        s, y = st.sb("s", [T, 2, Q, T]), st.sb("y", [T, 2, D])
        mean, var, rstd = st.sb("mean", [T, 2, H]), st.sb("var", [T, 2, H]), st.sb("rstd", [T, 2, H])
        sq, power = st.sb("sq", [T, 2, D]), st.sb("power", [T, H])
        yT = st.sb("yT", [D, 2, T])
        staged, scored, decayed, summed, var_ready, rstd_ready, y_ready, y_turned, yT_kept, made, added = (
            st.sem(x) for x in ("staged", "scored", "decayed", "summed", "var_ready", "rstd_ready", "y_ready", "y_turned",
                                "yT_kept", "made", "added"))
        score, ysum, yps, out = bank[0:4], bank[4:6], bank[6], bank[7]
        with nc.Block() as block:
            @block.gpsimd
            def _(pool):
                nc.gpsimd.memset(power[:], -0.5)
                credit(pool, staged, rstd_ready)
                with pool.Fori(0, B // 2) as i:
                    for u in range(2):
                        n = 2 * i + u
                        pool.wait_ge(scored, done(UN * (n - 2) + UN - 1))
                        nc.gpsimd.tensor_copy(ks[:, u, :], kT[:, bass.ds(n * T, T)])
                        nc.gpsimd.tensor_tensor(rs[:, u, :, :], bc(rT[:, bass.ds(n * T, T)], 1, H),
                                                bc(g.const["head"], 2, T), ALU.mult).then_inc(staged, 1)
                    for u in range(2):
                        n = 2 * i + u
                        pool.wait_ge(var_ready, done(n))
                        nc.gpsimd.tensor_tensor(rstd[:, u, :], var[:, u, :], power[:], ALU.pow).then_inc(rstd_ready, 1)

            @block.tensor
            def _(pe):
                credit(pe, scored, summed, y_turned, made)
                with pe.Fori(0, B // 2) as i:
                    def scores(k):
                        m, u, q = 2 * UN * i + k, k // UN, k % UN
                        if q == 0:
                            pe.wait_ge(staged, done(2 * i + u))
                        pe.wait_ge(decayed, done(m - 4))
                        nc.tensor.matmul(score[k % 4][:], ks[:, u, :], rs[:, u, Q * q:Q * (q + 1), :],
                                         start=True, stop=True).then_inc(scored, 1)

                    def sums(k):
                        m, u, q, e = 2 * UN * i + k, k // UN, k % UN, k % 2
                        pe.wait_ge(decayed, done(m))
                        if q == 0:
                            pe.wait_ge(y_ready, done(2 * i + u - 2))
                        for j in range(Q):
                            at = (Q * q + j) * HD
                            last = nc.tensor.matmul(ysum[u][:, at:at + HD], s[:, e, j, :], v[:, 2 * i + u, at:at + HD],
                                                    start=True, stop=True)
                        last.then_inc(summed, 1)

                    def project(u):
                        n = 2 * i + u
                        pe.wait_ge(y_ready, done(n))
                        pe.wait_ge(yT_kept, done(n - 1))
                        nc.tensor.transpose(yps[:, 0:T], y[:, u, :], g.ident).then_inc(y_turned, 1)
                        pe.wait_ge(yT_kept, done(n))
                        pe.wait_ge(added, done(n - 1))
                        nc.tensor.matmul(out[:, 0:D], yT[:, u, :], w["w_o"], start=True, stop=True).then_inc(made, 1)

                    for k in range(2 * UN + 1):
                        if k < 2 * UN:
                            scores(k)
                        if k >= 1:
                            sums(k - 1)
                    for u in range(2):
                        project(u)

            @block.scalar
            def _(act):
                credit(act, yT_kept)
                with act.Fori(0, B // 2) as i:
                    for u in range(2):
                        n = 2 * i + u
                        act.wait_ge(y_turned, done(n))
                        act.wait_ge(made, done(n - 2))
                        nc.scalar.activation(yT[:, u, :], yps[:, 0:T], ACT.Copy).then_inc(yT_kept, 1)

            @block.vector
            def _(dve):
                credit(dve, decayed, var_ready, y_ready, added)
                with dve.Fori(0, B // 2) as i:
                    for k in range(2 * UN):
                        m, u, q, e = 2 * UN * i + k, k // UN, k % UN, k % 2
                        dve.wait_ge(scored, done(m))
                        dve.wait_ge(summed, done(m - 2))
                        nc.vector.tensor_tensor(s[:, e, :, :], rows_of(score[k % 4][:], Q), weight[:, Q * q:Q * (q + 1), :],
                                                ALU.mult).then_inc(decayed, 1)
                    for u in range(2):
                        n = 2 * i + u
                        heads = lambda t: t[:, u, :].rearrange("p (h d) -> p h d", h=H)
                        dve.wait_ge(summed, done(UN * n + UN - 1))
                        nc.vector.tensor_reduce(mean[:, u, :], rows_of(ysum[u][:, 0:D], H), X, ALU.add)
                        dve.drain()
                        nc.vector.tensor_scalar(mean[:, u, :], mean[:, u, :], 1.0 / HD, None, ALU.mult)
                        dve.drain()
                        dve.wait_ge(y_turned, done(n - 2))
                        nc.vector.tensor_tensor(heads(y), rows_of(ysum[u][:, 0:D], H), bc(mean[:, u, :], 2, HD), ALU.subtract)
                        dve.drain()
                        nc.vector.tensor_tensor(sq[:, u, :], y[:, u, :], y[:, u, :], ALU.mult)
                        dve.drain()
                        nc.vector.tensor_reduce(var[:, u, :], heads(sq), X, ALU.add)
                        dve.drain()
                        nc.vector.tensor_scalar(var[:, u, :], var[:, u, :], 1.0 / HD, 64e-5, ALU.mult,
                                                ALU.add).then_inc(var_ready, 1)
                        dve.wait_ge(rstd_ready, done(n))
                        nc.vector.tensor_tensor(heads(y), heads(y), bc(rstd[:, u, :], 2, HD), ALU.mult)
                        dve.drain()
                        nc.vector.tensor_tensor(y[:, u, :], y[:, u, :], w["ln_g"], ALU.mult)
                        dve.drain()
                        nc.vector.tensor_tensor(y[:, u, :], y[:, u, :], w["ln_b"], ALU.add)
                        dve.drain()
                        nc.vector.tensor_tensor(y[:, u, :], y[:, u, :], gate[:, n, :], ALU.mult).then_inc(y_ready, 1)
                    for u in range(2):
                        n = 2 * i + u
                        dve.wait_ge(made, done(n))
                        nc.vector.tensor_tensor(g.x[:, n, :], g.x[:, n, :], out[:, 0:D], ALU.add).then_inc(added, 1)


def softplus_tail(nc, dve, e, u, log_u, fix):
    nc.vector.tensor_scalar(u, u, -1.0, None, ALU.add)
    dve.drain()
    nc.vector.tensor_scalar(fix, u, 0.0, None, ALU.is_equal)
    dve.drain()
    nc.vector.tensor_tensor(u, u, fix, ALU.add)
    nc.vector.tensor_tensor(log_u, log_u, fix, ALU.add)
    dve.drain()
    nc.vector.reciprocal(u, u)
    nc.vector.tensor_tensor(e, e, log_u, ALU.mult)
    dve.drain()
    nc.vector.tensor_tensor(e, e, u, ALU.mult)



def state_space(nc, g, w, name):
    NH, DH, DS, TAPS = 4, 64, 64, 4
    DI = NH * DH
    bank = g.bank
    with Stage(nc, name) as st:
        raw = st.sb("raw", [128, 4, B, T + TAPS - 1])
        c = st.sb("c", [128, 4, B, T])
        z = st.sb("z", [T, B, DI])
        dt, e, u1, log_u, fix = (st.sb(x, [T, B, NH]) for x in ("dt", "e", "u1", "log_u", "fix"))
        a, rate = st.sb("a", [T, B, NH]), st.sb("rate", [T, NH])
        rows = (128, 128, DS, DS)
        proj, raw_kept, convolved, z_made, z_kept, dt_made, pads_set, abs_ready, e_ready, u_ready, log_ready, rate_ready = (
            st.sem(x) for x in ("proj", "raw_kept", "convolved", "z_made", "z_kept", "dt_made", "pads_set", "abs_ready",
                                "e_ready", "u_ready", "log_ready", "rate_ready"))
        with nc.Block() as block:
            @block.gpsimd
            def _(pool):
                nc.gpsimd.memset(raw[:, :, :, 0:TAPS - 1], 0.0).then_inc(pads_set, 1)

            @block.tensor
            def _(pe):
                pe.wait_ge(w.loaded, 16)
                for b in range(B):
                    last = nc.tensor.matmul(bank[7][:, b * NH:(b + 1) * NH], g.hT[:, b * T:(b + 1) * T], w["w_dt"],
                                            start=True, stop=True)
                last.then_inc(dt_made, 1)
                at = 0
                for m in range(8):
                    j, half = m // 2, m % 2
                    if m >= 6:
                        pe.wait_ge(raw_kept, m - 5)
                    nc.tensor.matmul(bank[m % 6][0:rows[j], :], w["w_conv"][:, at:at + rows[j]],
                                     g.hT[:, half * HALF:(half + 1) * HALF], start=True, stop=True).then_inc(proj, 1)
                    at += rows[j] if half else 0
                pe.wait_ge(raw_kept, 8)
                for m in range(4):
                    for q in range(2):
                        b = 2 * m + q
                        last = nc.tensor.matmul(bank[m][:, q * DI:(q + 1) * DI], g.hT[:, b * T:(b + 1) * T], w["w_z"],
                                                start=True, stop=True)
                    last.then_inc(z_made, 1)

            @block.scalar
            def _(act):
                act.wait_ge(w.loaded, 16)
                nc.scalar.activation(rate[:], w["a_log"], ACT.Exp).then_inc(rate_ready, 1)
                act.wait_ge(abs_ready, 1)
                nc.scalar.activation(e[:], e[:], ACT.Exp, scale=-1.0).then_inc(e_ready, 1)
                act.wait_ge(u_ready, 1)
                nc.scalar.activation(log_u[:], u1[:], ACT.Ln).then_inc(log_ready, 1)
                act.wait_ge(pads_set, 1)
                for m in range(8):
                    j, half = m // 2, m % 2
                    act.wait_ge(proj, m + 1)
                    nc.scalar.activation(raw[0:rows[j], j, 4 * half:4 * half + 4, TAPS - 1:],
                                         rows_of(bank[m % 6][0:rows[j], :], 4), ACT.Copy).then_inc(raw_kept, 1)
                for m in range(4):
                    act.wait_ge(z_made, m + 1)
                    nc.scalar.activation(z[:, 2 * m:2 * m + 2, :], rows_of(bank[m][:], 2), ACT.Silu)
                for j in range(4):
                    act.wait_ge(convolved, j + 1)
                    tile = c[0:rows[j], j, :, :]
                    nc.scalar.activation(tile, tile, ACT.Silu, bias=w["conv_b"][0:rows[j], j:j + 1])

            @block.vector
            def _(dve):
                dve.wait_ge(w.loaded, 16)
                dve.wait_ge(dt_made, 1)
                nc.vector.tensor_tensor(dt[:], rows_of(bank[7][:, 0:B * NH], B), bc(w["dt_bias"], 1, B), ALU.add)
                dve.drain()
                nc.vector.scalar_tensor_tensor(e[:], dt[:], -1.0, dt[:], ALU.mult, ALU.max).then_inc(abs_ready, 1)
                dve.drain()
                nc.vector.tensor_scalar(dt[:], dt[:], 0.0, None, ALU.max)
                dve.wait_ge(e_ready, 1)
                nc.vector.tensor_scalar(u1[:], e[:], 1.0, None, ALU.add).then_inc(u_ready, 1)
                dve.wait_ge(log_ready, 1)
                softplus_tail(nc, dve, e[:], u1[:], log_u[:], fix[:])
                dve.drain()
                nc.vector.tensor_tensor(dt[:], dt[:], e[:], ALU.add)
                dve.drain()
                dve.wait_ge(rate_ready, 1)
                nc.vector.scalar_tensor_tensor(a[:], dt[:], -1.0, bc(rate[:], 1, B), ALU.mult, ALU.mult)
                for j in range(4):
                    dve.wait_ge(raw_kept, 2 * j + 2)
                    out = c[0:rows[j], j, :, :]
                    for k in range(TAPS):
                        src = raw[0:rows[j], j, :, k:k + T]
                        tap = w["conv_w"][0:rows[j], j * TAPS + k:j * TAPS + k + 1]
                        if k == 0:
                            last = nc.vector.tensor_scalar(out, src, tap, None, ALU.mult)
                        else:
                            last = nc.vector.scalar_tensor_tensor(out, src, tap, out, ALU.mult, ALU.add)
                        if k < TAPS - 1:
                            dve.drain()
                    last.then_inc(convolved, 1)

        xs, bcs = st.sb("xs", [128, 2, 2, T]), st.sb("bcs", [DS, 2, 2, T])
        later = st.sb("later", [T, 2, NH, T])
        decay, decay0 = st.sb("decay", [T, 2, NH, T]), st.sb("decay0", [T, 2, NH])
        cb = st.sb("cb", [T, 2, T])
        xt, xdt, base, y = (st.sb(x, [T, 2, DI]) for x in ("xt", "xdt", "base", "y"))
        sq, meansq, rstd, power = st.sb("sq", [T, DI]), st.sb("meansq", [T, 2]), st.sb("rstd", [T, 2]), st.sb("power", [T, 1])
        yT = st.sb("yT", [128, 2, 2, T])
        staged, prods, decay_ready, pairs, summed, y_made, rms_ready, y_ready, y_turned, yT_kept, made, added = (
            st.sem(x) for x in ("staged", "prods", "decay_ready", "pairs", "summed", "y_made", "rms_ready", "y_ready",
                                "y_turned", "yT_kept", "made", "added"))
        heads = lambda t: t.rearrange("p (h d) -> p h d", h=NH)
        mixed, seg = bank[0:2], bank[2:4]
        xps, ysum, yps, out = bank[4], bank[5], bank[6], bank[7]
        with nc.Block() as block:
            @block.gpsimd
            def _(pool):
                nc.gpsimd.memset(power[:], -0.5)
                credit(pool, staged, rms_ready)
                with pool.Fori(0, B // 2) as i:
                    for u in range(2):
                        n = 2 * i + u
                        pool.wait_ge(prods, done(n - 2))
                        nc.gpsimd.tensor_copy(xs[:, u, :, :], c[:, 0:2, n, :])
                        nc.gpsimd.tensor_copy(bcs[:, u, :, :], c[0:DS, 2:4, n, :])
                        nc.gpsimd.tensor_tensor(later[:, u, :, :], bc(g.const["gt"], 1, NH), bc(a[:, n, :], 2, T),
                                                ALU.mult).then_inc(staged, 1)
                    for u in range(2):
                        n = 2 * i + u
                        pool.wait_ge(y_made, done(n))
                        nc.gpsimd.tensor_tensor(rstd[:, u:u + 1], meansq[:, u:u + 1], power[:], ALU.pow).then_inc(rms_ready, 1)

            @block.tensor
            def _(pe):
                credit(pe, prods, summed, y_turned, made)
                with pe.Fori(0, B // 2) as i:
                    for u in range(2):
                        n = 2 * i + u
                        pe.wait_ge(staged, done(n))
                        pe.wait_ge(pairs, done(n - 1))
                        nc.tensor.matmul(mixed[u][:, 0:T], bcs[:, u, 0, :], bcs[:, u, 1, :], start=True, stop=True)
                        nc.tensor.matmul(mixed[u][:, T:T + DI], bcs[:, u, 1, :], w["init"], start=True, stop=True)
                        nc.tensor.matmul(mixed[u][:, T + DI:T + DI + NH], g.const["le"], a[:, n, :], start=True, stop=True)
                        for h in range(NH):
                            nc.tensor.matmul(seg[u][:, h * T:(h + 1) * T], later[:, u, h, :], g.const["le"],
                                             start=True, stop=True)
                        for j in range(2):
                            last = nc.tensor.transpose(xps[:, j * 128:(j + 1) * 128], xs[:, u, j, :], g.ident)
                        last.then_inc(prods, 1)
                    for u in range(2):
                        n = 2 * i + u
                        pe.wait_ge(pairs, done(n))
                        pe.wait_ge(y_made, done(n - 1))
                        for h in range(NH):
                            last = nc.tensor.matmul(ysum[:, h * DH:(h + 1) * DH], decay[:, u, h, :],
                                                    xdt[:, u, h * DH:(h + 1) * DH], start=True, stop=True)
                        last.then_inc(summed, 1)
                    for u in range(2):
                        n = 2 * i + u
                        pe.wait_ge(y_ready, done(n))
                        pe.wait_ge(yT_kept, done(n - 1))
                        for j in range(2):
                            last = nc.tensor.transpose(yps[:, j * T:(j + 1) * T], y[:, u, j * 128:(j + 1) * 128], g.ident)
                        last.then_inc(y_turned, 1)
                        pe.wait_ge(yT_kept, done(n))
                        pe.wait_ge(added, done(n - 1))
                        for j in range(2):
                            last = nc.tensor.matmul(out[:, 0:D], yT[:, u, j, :], w["w_out"][:, j * D:(j + 1) * D],
                                                    start=(j == 0), stop=(j == 1))
                        last.then_inc(made, 1)

            @block.scalar
            def _(act):
                credit(act, decay_ready, yT_kept)
                with act.Fori(0, B // 2) as i:
                    for u in range(2):
                        n = 2 * i + u
                        act.wait_ge(prods, done(n))
                        act.wait_ge(summed, done(n - 2))
                        nc.scalar.activation(decay[:, u, :, :], rows_of(seg[u][:], NH), ACT.Exp)
                        nc.scalar.activation(decay0[:, u, :], mixed[u][:, T + DI:T + DI + NH], ACT.Exp).then_inc(decay_ready, 1)
                    for u in range(2):
                        n = 2 * i + u
                        act.wait_ge(y_turned, done(n))
                        nc.scalar.activation(yT[:, u, :, :], rows_of(yps[:, 0:DI], 2), ACT.Copy).then_inc(yT_kept, 1)

            @block.vector
            def _(dve):
                credit(dve, pairs, y_made, y_ready, added)
                with dve.Fori(0, B // 2) as i:
                    for u in range(2):
                        n = 2 * i + u
                        dve.wait_ge(decay_ready, done(n))
                        nc.vector.tensor_copy(xt[:, u, :], xps[:, 0:DI])
                        nc.vector.tensor_tensor(cb[:, u, :], mixed[u][:, 0:T], g.const["le"], ALU.mult)
                        nc.vector.tensor_tensor(heads(base[:, u, :]), heads(mixed[u][:, T:T + DI]), bc(decay0[:, u, :], 2, DH),
                                                ALU.mult)
                        dve.drain()
                        nc.vector.tensor_tensor(heads(xdt[:, u, :]), heads(xt[:, u, :]), bc(dt[:, n, :], 2, DH), ALU.mult)
                        nc.vector.tensor_tensor(heads(xt[:, u, :]), heads(xt[:, u, :]), bc(w["skip"], 2, DH), ALU.mult)
                        nc.vector.tensor_tensor(decay[:, u, :, :], decay[:, u, :, :], bc(cb[:, u, :], 1, NH),
                                                ALU.mult).then_inc(pairs, 1)
                        dve.drain()
                        nc.vector.tensor_tensor(base[:, u, :], base[:, u, :], xt[:, u, :], ALU.add)
                    for u in range(2):
                        n = 2 * i + u
                        dve.wait_ge(summed, done(n))
                        nc.vector.tensor_tensor(base[:, u, :], base[:, u, :], ysum[:, 0:DI], ALU.add)
                        dve.drain()
                        dve.wait_ge(y_turned, done(n - 2))
                        nc.vector.tensor_tensor(y[:, u, :], base[:, u, :], z[:, n, :], ALU.mult)
                        dve.drain()
                        nc.vector.tensor_tensor(sq[:], y[:, u, :], y[:, u, :], ALU.mult)
                        dve.drain()
                        nc.vector.tensor_reduce(meansq[:, u:u + 1], sq[:], X, ALU.add)
                        dve.drain()
                        nc.vector.tensor_scalar(meansq[:, u:u + 1], meansq[:, u:u + 1], 1.0 / DI, 1e-5, ALU.mult,
                                                ALU.add).then_inc(y_made, 1)
                    for u in range(2):
                        n = 2 * i + u
                        dve.wait_ge(rms_ready, done(n))
                        nc.vector.scalar_tensor_tensor(y[:, u, :], y[:, u, :], rstd[:, u:u + 1], w["norm_w"],
                                                       ALU.mult, ALU.mult).then_inc(y_ready, 1)
                    for u in range(2):
                        n = 2 * i + u
                        dve.wait_ge(made, done(n))
                        nc.vector.tensor_tensor(g.x[:, n, :], g.x[:, n, :], out[:, 0:D], ALU.add).then_inc(added, 1)



def delta_gates(nc, g, w, st, rate_of, beta):
    NH = 12
    bank = g.bank
    e, u1, log_u, fix = (st.sb(x, [T, B, NH]) for x in ("e", "u1", "log_u", "fix"))
    a_rate = st.sb("a_rate", [T, NH])
    made, beta_in, beta_kept, abs_ready, e_ready, u_ready, log_ready = (
        st.sem(x) for x in ("made", "beta_in", "beta_kept", "abs_ready", "e_ready", "u_ready", "log_ready"))
    with nc.Block() as block:
        @block.tensor
        def _(pe):
            pe.wait_ge(w.loaded, 16)
            for j, name in enumerate(("w_rate", "w_beta")):
                for b in range(B):
                    last = nc.tensor.matmul(bank[j][:, b * NH:(b + 1) * NH], g.hT[:, b * T:(b + 1) * T], w[name],
                                            start=True, stop=True)
                last.then_inc(made, 1)

        @block.scalar
        def _(act):
            act.wait_ge(w.loaded, 16)
            nc.scalar.activation(a_rate[:], w["a_log"], ACT.Exp)
            act.wait_ge(abs_ready, 1)
            nc.scalar.activation(e[:], e[:], ACT.Exp, scale=-1.0).then_inc(e_ready, 1)
            act.wait_ge(u_ready, 1)
            nc.scalar.activation(log_u[:], u1[:], ACT.Ln).then_inc(log_ready, 1)
            act.wait_ge(beta_in, 1)
            nc.scalar.activation(beta[:], beta[:], ACT.Sigmoid).then_inc(beta_kept, 1)

        @block.vector
        def _(dve):
            dve.wait_ge(made, 1)
            dt = rate_of
            nc.vector.tensor_tensor(dt[:], rows_of(bank[0][:, 0:B * NH], B), bc(w["dt_bias"], 1, B), ALU.add)
            dve.wait_ge(made, 2)
            nc.vector.tensor_tensor(beta[:], rows_of(bank[1][:, 0:B * NH], B), bc(w["b_b"], 1, B), ALU.add).then_inc(beta_in, 1)
            dve.drain()
            nc.vector.scalar_tensor_tensor(e[:], dt[:], -1.0, dt[:], ALU.mult, ALU.max).then_inc(abs_ready, 1)
            dve.drain()
            nc.vector.tensor_scalar(dt[:], dt[:], 0.0, None, ALU.max)
            dve.wait_ge(e_ready, 1)
            nc.vector.tensor_scalar(u1[:], e[:], 1.0, None, ALU.add).then_inc(u_ready, 1)
            dve.wait_ge(log_ready, 1)
            softplus_tail(nc, dve, e[:], u1[:], log_u[:], fix[:])
            dve.drain()
            nc.vector.tensor_tensor(dt[:], dt[:], e[:], ALU.add)
            dve.drain()
            nc.vector.scalar_tensor_tensor(dt[:], dt[:], -1.0, bc(a_rate[:], 1, B), ALU.mult, ALU.mult)


def delta_rule(nc, g, w, name):
    NH, DK, DV, TAPS, G = 12, 64, 128, 4, 4
    LEVELS = 6
    QK = 4
    bank = g.bank
    with Stage(nc, name) as st:
        rate, beta = st.sb("rate", [T, B, NH]), st.sb("beta", [T, B, NH])
        delta_gates(nc, g, w, st, rate, beta)

        c = g.region_a[:, 0:8 * TOK].rearrange("p (m b t) -> p m b t", m=8, b=B)
        raw = st.sb("raw", [128, 2, B, T + TAPS - 1])
        spare = g.region_b[:, w.tile.shape[1]:]
        gate = spare[:, 0:B * G * DV].rearrange("p (b d) -> p b d", b=B)
        sq = spare[:, B * G * DV:B * G * DV + TOK]
        norms, power = st.sb("norms", [T, B, 2 * G]), st.sb("power", [T, B, 2 * G])
        coef, vscale, oscale, oscale2 = (st.sb(x, [T, B, G]) for x in ("coef", "vscale", "oscale", "oscale2"))
        qks, kb, vs = st.sb("qks", [128, 2, QK, T]), st.sb("kb", [128, 2, G, T]), st.sb("vs", [DV, 2, G, T])
        later, mcoef = st.sb("later", [T, 2, G, T]), st.sb("mcoef", [T, 2, G, T])
        dec, A, P = st.sb("dec", [T, 2, G, T]), st.sb("A", [T, 2, G, T]), st.sb("P", [T, 2, G, T])
        W, V, join = st.sb("W", [T, 2, G, T]), st.sb("V", [T, 2, G, T]), st.sb("join", [T, 2, G, T])
        R, PT = st.sb("R", [T, 2, G, DV]), st.sb("PT", [T, 2, G, T])
        delta, o, osq, y, yT = P, dec, A, W, join
        ssum, rstd = st.sb("ssum", [T, 2, G]), st.sb("rstd", [T, 2, G])

        for hg in range(NH // G):
            names = ("pads_set", "proj", "raw_kept", "convolved", "silu_ready", "squared", "norms_made", "norms_in",
                     "norms_ready", "gate_made", "gate_kept")
            (pads_set, proj, raw_kept, convolved, silu_ready, squared, norms_made, norms_in, norms_ready, gate_made,
             gate_kept) = (st.sem(f"{x}{hg}") for x in names)
            heads_of = slice(hg * G, hg * G + G)

            def weights_of(m):
                name, j = ("q", 2 * hg + m) if m < 2 else ("k", 2 * hg + m - 2) if m < 4 else ("v", G * hg + m - 4)
                return w["w" + name][:, j * 128:(j + 1) * 128], w["conv_" + name][:, j * TAPS:(j + 1) * TAPS]

            with nc.Block() as block:
                @block.gpsimd
                def _(pool):
                    nc.gpsimd.memset(raw[:, :, :, 0:TAPS - 1], 0.0).then_inc(pads_set, 1)
                    nc.gpsimd.memset(power[:], -0.5).then_inc(pads_set, 1)
                    pool.wait_ge(pads_set, 2)
                    pool.wait_ge(norms_in, 1)
                    nc.gpsimd.tensor_tensor(norms[:], norms[:], power[:], ALU.pow).then_inc(norms_ready, 1)

                @block.tensor
                def _(pe):
                    for m in range(8 + 1):
                        if m < 8:
                            if m >= 3:
                                pe.wait_ge(raw_kept, m - 2)
                            for half in range(2):
                                last = nc.tensor.matmul(bank[2 * (m % 3) + half][:], weights_of(m)[0],
                                                        g.hT[:, half * HALF:(half + 1) * HALF], start=True, stop=True)
                            last.then_inc(proj, 1)
                        if 1 <= m <= QK:
                            pe.wait_ge(squared, m)
                            for b in range(B):
                                at = b * 2 * G + 2 * (m - 1)
                                last = nc.tensor.matmul(bank[6][:, at:at + 2], sq[:, b * T:(b + 1) * T], g.const["half"],
                                                        start=True, stop=True)
                            last.then_inc(norms_made, 1)
                    for b in range(B):
                        j = b % 2
                        if b < 2:
                            pe.wait_ge(raw_kept, 8)
                        else:
                            pe.wait_ge(gate_kept, b - 1)
                        nc.tensor.matmul(bank[j][:], g.hT[:, b * T:(b + 1) * T], w["wg"][:, hg * HALF:(hg + 1) * HALF],
                                         start=True, stop=True).then_inc(gate_made, 1)

                @block.scalar
                def _(act):
                    for m in range(8 + 1):
                        if m < 8:
                            if m == 0:
                                act.wait_ge(pads_set, 1)
                            if m >= 2:
                                act.wait_ge(convolved, m - 1)
                            act.wait_ge(proj, m + 1)
                            for half in range(2):
                                last = nc.scalar.activation(raw[:, m % 2, 4 * half:4 * half + 4, TAPS - 1:],
                                                            rows_of(bank[2 * (m % 3) + half][:], 4), ACT.Copy)
                            last.then_inc(raw_kept, 1)
                        if m >= 1:
                            act.wait_ge(convolved, m)
                            tile = c[:, m - 1, :, :]
                            nc.scalar.activation(tile, tile, ACT.Silu).then_inc(silu_ready, 1)
                            if m <= QK:
                                act.wait_ge(silu_ready, m)
                                if m >= 2:
                                    act.wait_ge(norms_made, m - 1)
                                nc.scalar.activation(sq, tile.rearrange("p b t -> p (b t)"),
                                                     ACT.Square).then_inc(squared, 1)
                    for b in range(B):
                        act.wait_ge(gate_made, b + 1)
                        nc.scalar.activation(gate[:, b, :], bank[b % 2][:], ACT.Silu).then_inc(gate_kept, 1)

                @block.vector
                def _(dve):
                    for m in range(8):
                        dve.wait_ge(raw_kept, m + 1)
                        taps = weights_of(m)[1]
                        for k in range(TAPS):
                            src = raw[:, m % 2, :, k:k + T]
                            if k == 0:
                                last = nc.vector.tensor_scalar(c[:, m, :, :], src, taps[:, 0:1], None, ALU.mult)
                            else:
                                last = nc.vector.scalar_tensor_tensor(c[:, m, :, :], src, taps[:, k:k + 1], c[:, m, :, :],
                                                                      ALU.mult, ALU.add)
                            if k < TAPS - 1:
                                dve.drain()
                        last.then_inc(convolved, 1)
                        if m == QK + 1:
                            dve.wait_ge(norms_made, QK)
                            nc.vector.tensor_scalar(norms[:], rows_of(bank[6][:, 0:B * 2 * G], B), 1e-6, None,
                                                    ALU.add).then_inc(norms_in, 1)
                    dve.wait_ge(norms_ready, 1)
                    rq, rk, bt = norms[:, :, 0:G], norms[:, :, G:2 * G], beta[:, :, heads_of]
                    nc.vector.tensor_tensor(vscale[:], rk, bt, ALU.mult)
                    nc.vector.tensor_scalar(oscale[:], rq, DK ** -0.5, None, ALU.mult)
                    dve.drain()
                    nc.vector.scalar_tensor_tensor(coef[:], vscale[:], -1.0, rk, ALU.mult, ALU.mult)
                    nc.vector.scalar_tensor_tensor(oscale2[:], oscale[:], 1.0 / DV, oscale[:], ALU.mult, ALU.mult)
                    for b in range(B):
                        dve.wait_ge(gate_kept, b + 1)
                        nc.vector.tensor_tensor(rows_of(gate[:, b, :], G), rows_of(gate[:, b, :], G), bc(w["o_norm"], 1, G),
                                                ALU.mult)

            names = ("staged", "prods", "dec_ready", "a_ready", "p_made", "p_ready", "a_turned", "p_turned", "w_ready",
                     "v_ready", "pT_kept", "joined", "join_kept", "grown", "grown_kept", "delta_made", "delta_kept",
                     "o_made", "o_kept", "var_ready", "rstd_ready", "y_ready", "y_turned", "yT_kept", "out_made", "added")
            (staged, prods, dec_ready, a_ready, p_made, p_ready, a_turned, p_turned, w_ready, v_ready, pT_kept, joined,
             join_kept, grown, grown_kept, delta_made, delta_kept, o_made, o_kept, var_ready, rstd_ready, y_ready,
             y_turned, yT_kept, out_made, added) = (st.sem(f"{x}{hg}") for x in names)

            def level(i, u, l):
                return done(2 * LEVELS * i + 2 * l + u)

            def four(t, u):
                return t[:, u, :, :]

            def flat(bk):
                return rows_of(bk[:], G)

            kk, qk, seg, vps = (lambda u, j=j: bank[4 * u + j] for j in range(4))
            with nc.Block() as block:
                @block.gpsimd
                def _(pool):
                    credit(pool, staged, w_ready, p_ready, rstd_ready)
                    with pool.Fori(0, B // 2) as i:
                        for u in range(2):
                            n = 2 * i + u
                            pool.wait_ge(prods, done(n - 2))
                            pool.wait_ge(a_ready, done(n - 2))
                            nc.gpsimd.tensor_copy(four(qks, u), c[:, 0:QK, n, :])
                            nc.gpsimd.tensor_copy(four(vs, u), c[:, QK:8, n, :])
                            for j in range(2):
                                nc.gpsimd.tensor_tensor(kb[:, u, 2 * j:2 * j + 2, :], bc(c[:, 2 + j, n, :], 1, 2),
                                                        bc(g.const["half"], 2, T), ALU.mult)
                            nc.gpsimd.tensor_tensor(four(later, u), bc(g.const["gt"], 1, G), bc(rate[:, n, heads_of], 2, T),
                                                    ALU.mult)
                            nc.gpsimd.tensor_tensor(four(mcoef, u), bc(g.const["gt"], 1, G), bc(coef[:, n, :], 2, T),
                                                    ALU.mult).then_inc(staged, 1)
                        for u in range(2):
                            n = 2 * i + u
                            pool.wait_ge(a_ready, done(n))
                            nc.gpsimd.tensor_tensor(four(W, u), four(A, u), bc(g.const["low0"], 1, G), ALU.mult).then_inc(w_ready, 1)
                            pool.wait_ge(p_made, done(n))
                            nc.gpsimd.tensor_tensor(four(P, u), four(P, u), bc(g.const["ge"], 1, G), ALU.mult).then_inc(p_ready, 1)
                        for u in range(2):
                            n = 2 * i + u
                            pool.wait_ge(var_ready, done(n))
                            nc.gpsimd.tensor_tensor(rstd[:, u, :], ssum[:, u, :], power[:, 0, 0:G], ALU.pow).then_inc(rstd_ready, 1)

                @block.tensor
                def _(pe):
                    credit(pe, prods, a_turned, p_turned, joined, grown, delta_made, o_made, y_turned, out_made)
                    with pe.Fori(0, B // 2) as i:
                        for u in range(2):
                            n = 2 * i + u
                            pe.wait_ge(staged, done(n))
                            pe.wait_ge(added, done(n - 2))
                            for j in range(2):
                                cols = slice(2 * j * T, 2 * (j + 1) * T)
                                keys = kb[:, u, 2 * j:2 * j + 2, :]
                                nc.tensor.matmul(kk(u)[:, cols], qks[:, u, 2 + j, :], keys, start=True, stop=True)
                                nc.tensor.matmul(qk(u)[:, cols], qks[:, u, j, :], keys, start=True, stop=True)
                            nc.tensor.matmul(seg(u)[:], g.const["le"], four(later, u), start=True, stop=True)
                            for h in range(G):
                                last = nc.tensor.transpose(vps(u)[:, h * DV:(h + 1) * DV], vs[:, u, h, :], g.ident)
                            last.then_inc(prods, 1)
                        for u in range(2):
                            n = 2 * i + u
                            pe.wait_ge(a_ready, done(n))
                            for h in range(G):
                                last = nc.tensor.transpose(kk(u)[:, h * T:(h + 1) * T], A[:, u, h, :], g.ident)
                            last.then_inc(a_turned, 1)
                            pe.wait_ge(p_ready, done(n))
                            for h in range(G):
                                last = nc.tensor.transpose(qk(u)[:, h * T:(h + 1) * T], P[:, u, h, :], g.ident)
                            last.then_inc(p_turned, 1)
                        for l in range(LEVELS):
                            for u in range(2):
                                n = 2 * i + u
                                if l == 0:
                                    pe.wait_ge(v_ready, done(n))
                                else:
                                    pe.wait_ge(grown_kept, level(i, u, l - 1))
                                for h in range(G):
                                    last = nc.tensor.matmul(seg(u)[:, h * T:(h + 1) * T], A[:, u, h, :], V[:, u, h, :],
                                                            start=True, stop=True)
                                last.then_inc(joined, 1)
                            for u in range(2):
                                n = 2 * i + u
                                pe.wait_ge(join_kept, level(i, u, l))
                                for h in range(G):
                                    last = nc.tensor.matmul(vps(u)[:, h * T:(h + 1) * T], W[:, u, h, :], join[:, u, h, :],
                                                            start=True, stop=True)
                                if l < LEVELS - 1:
                                    for h in range(G):
                                        last = nc.tensor.matmul(kk(u)[:, h * T:(h + 1) * T], join[:, u, h, :], W[:, u, h, :],
                                                                start=True, stop=True)
                                last.then_inc(grown, 1)
                        for u in range(2):
                            n = 2 * i + u
                            pe.wait_ge(grown_kept, level(i, u, LEVELS - 1))
                            pe.wait_ge(pT_kept, done(n))
                            for h in range(G):
                                last = nc.tensor.matmul(qk(u)[:, h * DV:(h + 1) * DV], V[:, u, h, :], R[:, u, h, :],
                                                        start=True, stop=True)
                            last.then_inc(delta_made, 1)
                        for u in range(2):
                            n = 2 * i + u
                            pe.wait_ge(delta_kept, done(n))
                            for h in range(G):
                                last = nc.tensor.matmul(seg(u)[:, h * DV:(h + 1) * DV], PT[:, u, h, :], delta[:, u, h, :],
                                                        start=True, stop=True)
                            last.then_inc(o_made, 1)
                        for u in range(2):
                            n = 2 * i + u
                            pe.wait_ge(y_ready, done(n))
                            for h in range(G):
                                last = nc.tensor.transpose(vps(u)[:, h * T:(h + 1) * T], y[:, u, h, :], g.ident)
                            last.then_inc(y_turned, 1)
                        for u in range(2):
                            n = 2 * i + u
                            pe.wait_ge(yT_kept, done(n))
                            for h in range(G):
                                at = (hg * G + h) * D
                                last = nc.tensor.matmul(kk(u)[:, 0:D], yT[:, u, h, :], w["wo"][:, at:at + D],
                                                        start=(h == 0), stop=(h == G - 1))
                            last.then_inc(out_made, 1)

                @block.scalar
                def _(act):
                    credit(act, dec_ready, pT_kept, delta_kept, o_kept, yT_kept)
                    with act.Fori(0, B // 2) as i:
                        for u in range(2):
                            act.wait_ge(prods, done(2 * i + u))
                            nc.scalar.activation(four(dec, u), flat(seg(u)), ACT.Exp).then_inc(dec_ready, 1)
                        for ready, dst, src, kept in ((p_turned, PT, qk, pT_kept), (delta_made, delta, qk, delta_kept),
                                                      (o_made, o, seg, o_kept), (y_turned, yT, vps, yT_kept)):
                            for u in range(2):
                                act.wait_ge(ready, done(2 * i + u))
                                nc.scalar.activation(four(dst, u), flat(src(u)), ACT.Copy).then_inc(kept, 1)

                @block.vector
                def _(dve):
                    credit(dve, a_ready, p_made, v_ready, join_kept, grown_kept, var_ready, y_ready, added)
                    with dve.Fori(0, B // 2) as i:
                        for u in range(2):
                            n = 2 * i + u
                            dve.wait_ge(dec_ready, done(n))
                            nc.vector.tensor_tensor(four(A, u), flat(kk(u)), four(dec, u), ALU.mult)
                            nc.vector.tensor_tensor(four(P, u), flat(qk(u)), four(dec, u), ALU.mult).then_inc(p_made, 1)
                            nc.vector.tensor_tensor(four(R, u), flat(vps(u)), bc(vscale[:, n, :], 2, DV), ALU.mult)
                            dve.drain()
                            nc.vector.tensor_tensor(four(A, u), four(A, u), four(mcoef, u), ALU.mult).then_inc(a_ready, 1)
                        for u in range(2):
                            n = 2 * i + u
                            dve.wait_ge(a_turned, done(n))
                            nc.vector.tensor_tensor(four(V, u), flat(kk(u)), bc(g.const["join0"], 1, G), ALU.mult)
                            dve.drain()
                            nc.vector.tensor_tensor(four(V, u), four(V, u), bc(g.ident, 1, G), ALU.add)
                            dve.wait_ge(w_ready, done(n))
                            nc.vector.tensor_tensor(four(W, u), four(W, u), bc(g.ident, 1, G), ALU.add).then_inc(v_ready, 1)
                        for l in range(LEVELS):
                            for u in range(2):
                                n = 2 * i + u
                                dve.wait_ge(joined, level(i, u, l))
                                nc.vector.tensor_tensor(four(join, u), flat(seg(u)), bc(g.const[f"join{l + 1}"], 1, G),
                                                        ALU.mult).then_inc(join_kept, 1)
                            for u in range(2):
                                n = 2 * i + u
                                dve.wait_ge(grown, level(i, u, l))
                                if l < LEVELS - 1:
                                    nc.vector.tensor_tensor(four(W, u), four(W, u), flat(kk(u)), ALU.add)
                                nc.vector.tensor_tensor(four(V, u), four(V, u), flat(vps(u)), ALU.add).then_inc(grown_kept, 1)
                        for u in range(2):
                            n = 2 * i + u
                            dve.wait_ge(o_kept, done(n))
                            nc.vector.tensor_tensor(four(osq, u), four(o, u), four(o, u), ALU.mult)
                            dve.drain()
                            nc.vector.tensor_reduce(ssum[:, u, :], four(osq, u), X, ALU.add)
                            dve.drain()
                            nc.vector.tensor_tensor(ssum[:, u, :], ssum[:, u, :], oscale2[:, n, :], ALU.mult)
                            dve.drain()
                            nc.vector.tensor_scalar(ssum[:, u, :], ssum[:, u, :], 1e-5, None, ALU.add).then_inc(var_ready, 1)
                        for u in range(2):
                            n = 2 * i + u
                            dve.wait_ge(rstd_ready, done(n))
                            nc.vector.tensor_tensor(rstd[:, u, :], rstd[:, u, :], oscale[:, n, :], ALU.mult)
                            nc.vector.tensor_tensor(four(y, u), four(o, u), rows_of(gate[:, n, :], G), ALU.mult)
                            dve.drain()
                            nc.vector.tensor_tensor(four(y, u), four(y, u), bc(rstd[:, u, :], 2, DV), ALU.mult).then_inc(y_ready, 1)
                        for u in range(2):
                            n = 2 * i + u
                            dve.wait_ge(out_made, done(n))
                            nc.vector.tensor_tensor(g.x[:, n, :], g.x[:, n, :], kk(u)[:, 0:D], ALU.add).then_inc(added, 1)


STAGES = [
    ("L0_attn", multi_query_attention), ("L0_xattn", attention_with_mlp), ("L0_ffn", ternary_ffn),
    ("L1_attn", state_space), ("L1_xattn", cross_attention), ("L1_ffn", gated_experts),
    ("L2_attn", delta_rule), ("L2_xattn", cross_attention), ("L2_ffn", many_experts),
    ("L3_attn", time_mix), ("L3_xattn", masked_cross_attention), ("L3_ffn", wide_experts),
]



def build(nc, dram, out, layouts, first=0, last=12):
    g = Net()
    g.dram = dram
    g.bank = [nc.alloc_psum_tensor(f"bank{n}", [128, HALF], F32) for n in range(8)]
    g.bank_bf = [t[:].bitcast(BF16) for t in g.bank]
    sb = nc.alloc_sbuf_tensor
    g.x, g.h = sb("x", [T, B, D], F32), sb("h", [T, B, D], F32)
    g.hT, g.ctxT = sb("hT", [D, TOK], F32), sb("ctxT", [D, TOK], F32)
    g.ident_bf = sb("ident_bf", [T, T], BF16)
    g.causal_bf, g.shifted_bf = sb("causal_bf", [T, 1, T], BF16), sb("shifted_bf", [T, 1, T], BF16)
    x_loaded, stored = nc.alloc_semaphore("x_loaded"), nc.alloc_semaphore("stored")
    g.x_loaded = x_loaded

    g.region_a = sb("region_a", [128, max(layouts[n][1] for n in ("L1_ffn", "L2_ffn"))], F32)
    first_b = ("L0_attn", "L0_xattn", "L0_ffn")
    g.region_b = sb("region_b", [128, max(sum(layouts[n][1] for n in first_b), layouts["L2_attn"][1],
                                          layouts["L3_ffn"][1])], F32)

    def place(name):
        places, cols = layouts[name]
        if name in ("L1_ffn", "L2_ffn"):
            tile = g.region_a[:, 0:cols]
        elif name in ("L2_attn", "L3_ffn"):
            tile = g.region_b[:, 0:cols]
        elif name in first_b:
            at = sum(layouts[n][1] for n in first_b[:first_b.index(name)])
            tile = g.region_b[:, at:at + cols]
        else:
            tile = sb(f"w_{name}", [128, cols], F32)[:]
        return Pack(tile, places, nc.alloc_semaphore(f"{name}_loaded"))

    g.const = place("const")
    run = STAGES[first:last]
    packs = {name: place(name) for name, _ in run}
    late = {"L1_attn": ["L2_attn"], "L2_xattn": ["L2_ffn", "L3_ffn"]}
    late = {at: [n for n in names if n in packs] if at in packs else [] for at, names in late.items()}
    g.ident = g.const["ident"]
    with nc.Block() as block:
        @block.sync
        def _(sp):
            sp.dma_start(g.const.tile, dram["const"]).then_inc(g.const.loaded, 16)
            sp.dma_start(g.x[:], dram["x"].rearrange("b t d -> t b d")).then_inc(x_loaded, 16)
            for name, _ in run:
                if not any(name in names for names in late.values()):
                    sp.dma_start(packs[name].tile, dram[name]).then_inc(packs[name].loaded, 16)
    turn_context(nc, g)
    for name, stage in run:
        layer_norm(nc, g, name + "_norm", [(packs[n], dram[n]) for n in late.get(name, [])])
        stage(nc, g, packs[name], name)
    with nc.Block() as block:
        @block.sync
        def _(sp):
            sp.dma_start(out.rearrange("b t d -> t b d"), g.x[:]).then_inc(stored, 16)
            sp.wait_ge(stored, 16)



def constants():
    r, c = np.arange(128)[:, None], np.arange(128)[None, :]
    f = np.float32
    return [
        ("ident", np.eye(128, dtype=f)),
        ("head", (r // HD == np.arange(H)[None, :]).astype(f)),
        ("half", (r // 64 == np.arange(2)[None, :]).astype(f)),
        ("neg_causal", np.where(c <= r, 0.0, NEG).astype(f)),
        ("neg_shifted", np.where((c < r) | ((c == 0) & (r == 0)), 0.0, NEG).astype(f)),
        ("le", (r <= c).astype(f)),
        ("gt", (r > c).astype(f)),
        ("lt", (r < c).astype(f)),
        ("ge", (r >= c).astype(f)),
        *[(f"join{l}", (r >> l + 1 == c >> l + 1).astype(f) * (r >> l < c >> l)) for l in range(7)],
        ("low0", ((r >> 1 == c >> 1) & (r > c)).astype(f)),
        ("steps", np.maximum(c - r - 1, 0).astype(f)),
        ("ones", np.ones((128, 128), f)),
    ]


def packed(pieces):
    places, at = {}, 0
    for name, a in pieces:
        places[name] = (at, a.shape[0], a.shape[1])
        at += a.shape[1]
    whole = np.zeros((128, at), np.float32)
    for name, a in pieces:
        whole[:a.shape[0], places[name][0]:places[name][0] + a.shape[1]] = a
    return whole, (places, at)


def every_row(v, rows=128):
    return np.repeat(np.asarray(v).reshape(1, -1), rows, 0)


def side_by_side(a):
    return np.ascontiguousarray(np.asarray(a).transpose(1, 0, 2)).reshape(a.shape[1], -1)


def column_tiles(a, p=128):
    a = np.asarray(a)
    return side_by_side(a.reshape(-1, p, a.shape[1]))


def column(v):
    return np.asarray(v).reshape(-1, 1)


def attention_pieces(weights, biases=None):
    pieces = [(n, np.ascontiguousarray(a.T)) for n, a in zip(("wq", "wk", "wv", "wo"), weights)]
    if biases is None:
        zeros = np.zeros(D, np.float32)
        return pieces + [("bq", column(zeros)), ("bk", column(zeros)), ("bv", every_row(zeros))]
    bq, bk, bv, bo = biases
    return pieces + [("bq", column(bq)), ("bk", column(bk)), ("bv", every_row(bv)), ("bo", every_row(bo))]


def state_space_pieces(i):
    w_in, conv_w, conv_b = i["L1_attn_in_proj_w"], i["L1_attn_conv_w"], i["L1_attn_conv_b"]
    parts = ((0, 128), (128, 256), (256, 320), (320, 384))
    taps, shift = np.zeros((128, 4, 4), np.float32), np.zeros((128, 4), np.float32)
    for j, (lo, hi) in enumerate(parts):
        taps[:hi - lo, j] = conv_w[lo:hi]
        shift[:hi - lo, j] = conv_b[lo:hi]
    return [("w_z", w_in[0:256].T), ("w_conv", w_in[256:640].T), ("w_dt", w_in[640:644].T),
            ("conv_w", taps.reshape(128, 16)), ("conv_b", shift),
            ("init", i["L1_attn_init_states"].transpose(2, 0, 1).reshape(64, 256)),
            ("dt_bias", every_row(i["L1_attn_dt_bias"])), ("a_log", every_row(i["L1_attn_A_log"])),
            ("skip", every_row(i["L1_attn_D"])), ("norm_w", every_row(i["L1_attn_norm_w"])),
            ("w_out", column_tiles(i["L1_attn_out_proj_w"].T))]


def pieces_of(i):
    null = i["L0_attn_null_kv"]
    null2 = np.zeros((128, 2), np.float32)
    null2[:64, 0] = null
    null2[64:, 1] = null
    return {
        "const": constants(),
        "L0_attn": [("wq", i["L0_attn_Wq"]), ("wkv2", np.concatenate([i["L0_attn_Wkv"]] * 2, 1)),
                    ("wout", column_tiles(i["L0_attn_Wout"])), ("null2", null2),
                    ("wqT", column_tiles(i["L0_attn_Wq"].T)), ("null_row", every_row(np.append(null, np.float32(1))))],
        "L0_xattn": [("wq", i["L0_xattn_Wq"]), ("wk", i["L0_xattn_Wk"]), ("wv", i["L0_xattn_Wv"]),
                     ("bq", column(i["L0_xattn_bq"])), ("bk", column(i["L0_xattn_bk"])),
                     ("bv", every_row(i["L0_xattn_bv"])), ("w1", i["L0_xattn_W1"]),
                     ("b1", i["L0_xattn_b1"].reshape(4, 128).T), ("w2", column_tiles(i["L0_xattn_W2"])),
                     ("b2", every_row(i["L0_xattn_b2"]))],
        "L1_attn": state_space_pieces(i),
        "L2_attn": [("w" + c.lower(), i["L2_attn_W" + c]) for c in "qkvg"]
                   + [("conv_" + c, column_tiles(i["L2_attn_conv_" + c])) for c in "qkv"]
                   + [("wo", column_tiles(i["L2_attn_Wo"])), ("w_rate", i["L2_attn_Wgk"]), ("w_beta", i["L2_attn_Wb"]),
                      ("b_b", every_row(i["L2_attn_b_b"])), ("a_log", every_row(i["L2_attn_A_log"])),
                      ("dt_bias", every_row(i["L2_attn_dt_bias"])), ("o_norm", every_row(i["L2_attn_g_norm_weight"]))],
        "L0_ffn": [("gate", i["L0_ffn_w_gate"].T), ("up", i["L0_ffn_w_up"].T),
                   ("down", column_tiles(i["L0_ffn_w_down"].T))],
        "L3_attn": [("w_" + c, i[f"L3_attn_w_{c}"].T) for c in "rkvgo"]
                   + [("maa_" + c, column(i[f"L3_attn_time_maa_{c}"])) for c in "rkvg"]
                   + [("decay", every_row(i["L3_attn_time_decay"])), ("bonus", every_row(i["L3_attn_time_faaaa"])),
                      ("ln_g", every_row(i["L3_attn_ln_g"])), ("ln_b", every_row(i["L3_attn_ln_b"]))],
        "L1_ffn": [("router", i["L1_ffn_router_w"]), ("router_scale", column(i["L1_ffn_router_scale"])),
                   ("expert_scale", every_row(i["L1_ffn_per_expert_scale"])),
                   ("up", i["L1_ffn_gating_w"].transpose(3, 0, 1, 2).reshape(D, -1)),
                   ("down", column_tiles(i["L1_ffn_linear_w"].reshape(-1, D)))],
        "L2_ffn": [("router", i["L2_ffn_router_w"].T), ("correction", every_row(i["L2_ffn_correction_bias"])),
                   ("up", np.concatenate([side_by_side(i["L2_ffn_up_w"]), i["L2_ffn_shared_up_w"]], 1)),
                   ("down", np.concatenate([column_tiles(i["L2_ffn_down_w"].reshape(-1, D)),
                                            column_tiles(i["L2_ffn_shared_down_w"])], 1))],
        "L3_ffn": [("router", i["L3_ffn_Wr"]), ("br", every_row(i["L3_ffn_br"])), ("b2", i["L3_ffn_b2"]),
                   ("up", side_by_side(i["L3_ffn_W1"])), ("b1", every_row(i["L3_ffn_b1"])),
                   ("down", column_tiles(i["L3_ffn_W2"].reshape(-1, D)))],
        "L1_xattn": attention_pieces([i[f"L1_xattn_w{c}_w"] for c in "qkvo"], [i[f"L1_xattn_w{c}_b"] for c in "qkvo"]),
        "L2_xattn": attention_pieces([i[f"L2_xattn_w_{c}"] for c in "qkvo"], [i[f"L2_xattn_b_{c}"] for c in "qkvo"]),
        "L3_xattn": attention_pieces([i[f"L3_xattn_W{c}"] for c in "qkvo"]),
    }


def laid_out(inputs):
    inputs = {k: np.asarray(v) for k, v in inputs.items()}
    arrays, layouts = {}, {}
    for name, pieces in pieces_of(inputs).items():
        arrays[name], layouts[name] = packed(pieces)
    arrays["x"] = np.ascontiguousarray(inputs["x"])
    arrays["ctx_1024"] = np.ascontiguousarray(inputs["ctx_1024"])
    arrays["mask"] = np.ascontiguousarray(inputs["mask_BxSxS2_bf0"])
    return arrays, layouts


def program(nc, arrays, layouts, first=0, last=12):
    dram = {k: nc.dram_tensor(f"in_{k}", a.shape, mybir.dt.from_np(a.dtype), kind="ExternalInput").ap()
            for k, a in arrays.items()}
    out = nc.dram_tensor("out", (B, T, D), F32, kind="ExternalOutput").ap()
    build(nc, dram, out, layouts, first, last)


def kernel(**inputs):
    import concourse.bacc as bacc
    from concourse.bass_utils import run_bass_kernel_spmd

    nc = bacc.Bacc("TRN2", target_bir_lowering=False, num_devices=1)
    arrays, layouts = laid_out(inputs)
    program(nc, arrays, layouts)
    r = run_bass_kernel_spmd(nc, [{f"in_{k}": a for k, a in arrays.items()}], core_ids=[0])
    return r.results[0]["out"]
```

```python
import numpy as np

import concourse.bass as bass
from concourse import mybir

F32 = mybir.dt.float32
BF16 = mybir.dt.bfloat16
U8 = mybir.dt.uint8
ALU = mybir.AluOpType
ACT = mybir.ActivationFunctionType
X = mybir.AxisListType.X

B, T, D = 8, 128, 128
H, HD = 16, 8
TOK = B * T
HALF = 512
NEG = -1.0e30
ROUND = 1.5 * 2.0 ** 23
CREDIT = 24


def done(m):
    return m + 1 + CREDIT


def credit(engine, *sems):
    for s in sems:
        engine.sem_inc(s, CREDIT)


def pipeline(engine, step, per, lag, units=None):
    units = B // 2 * per if units is None else units
    rounds = (units - lag) // per
    for r in range(lag):
        step(0, r)
    with engine.Fori(0, rounds) as i:
        for r in range(lag, lag + per):
            step(i, r)
    for r in range(lag, lag + units - per * rounds):
        step(rounds, r)


def has_unit(i, r, back, per, units=None):
    units = B // 2 * per if units is None else units
    return not isinstance(i, int) or 0 <= per * i + r - back < units


class Stage:

    def __init__(self, nc, name):
        self.nc, self.name = nc, name
        self.scope = nc.cleanup_on_exit()

    def __enter__(self):
        self.scope.__enter__()
        return self

    def __exit__(self, *exc):
        self.scope.__exit__(*exc)
        self.nc.all_engine_barrier()

    def sb(self, name, shape, dtype=F32):
        return self.nc.alloc_sbuf_tensor(f"{self.name}_{name}", shape, dtype)

    def sem(self, name):
        return self.nc.alloc_semaphore(f"{self.name}_{name}")


class Pack:

    def __init__(self, tile, places, loaded):
        self.tile, self.places, self.loaded = tile, places, loaded

    def __getitem__(self, name):
        at, rows, cols = self.places[name]
        return self.tile[0:rows, at:at + cols]


class Net:
    pass


def bc(ap, axis, n):
    a = ap.unsqueeze(axis)
    shape = list(a.shape)
    shape[axis] = n
    return a.to_broadcast(shape)


def rows_of(ap, n):
    return ap.rearrange("p (a b) -> p a b", a=n)


def layer_norm(nc, g, name, loads, eps=1e-5):
    with Stage(nc, name) as st:
        total, mean = st.sb("total", [T, B]), st.sb("mean", [T, B])
        sq, sumsq = st.sb("sq", [T, B, D]), st.sb("sumsq", [T, B])
        var, rstd, power = st.sb("var", [T, B]), st.sb("rstd", [T, B]), st.sb("power", [T, B])
        var_ready, rstd_ready, h_ready, turned, power_set = (
            st.sem(s) for s in ("var_ready", "rstd_ready", "h_ready", "turned", "power_set"))
        x, h, hT = g.x, g.h, g.hT

        with nc.Block() as block:
            @block.sync
            def _(sp):
                for pack, source in loads:
                    sp.dma_start(pack.tile, source).then_inc(pack.loaded, 16)

            @block.vector
            def _(dve):
                nc.vector.tensor_reduce(total[:], x[:], X, ALU.add)
                dve.drain()
                nc.vector.tensor_scalar(mean[:], total[:], 1.0 / D, None, ALU.mult)
                dve.drain()
                nc.vector.tensor_tensor(h[:], x[:], bc(mean[:], 2, D), ALU.subtract)
                dve.drain()
                nc.vector.tensor_tensor(sq[:], h[:], h[:], ALU.mult)
                dve.drain()
                nc.vector.tensor_reduce(sumsq[:], sq[:], X, ALU.add)
                dve.drain()
                nc.vector.tensor_scalar(var[:], sumsq[:], 1.0 / D, eps, ALU.mult, ALU.add).then_inc(var_ready, 1)
                dve.wait_ge(rstd_ready, 1)
                for half in range(2):
                    b = slice(4 * half, 4 * half + 4)
                    nc.vector.tensor_tensor(h[:, b, :], h[:, b, :], bc(rstd[:, b], 2, D),
                                            ALU.mult).then_inc(h_ready, 1)

            @block.gpsimd
            def _(pool):
                nc.gpsimd.memset(power[:], -0.5).then_inc(power_set, 1)
                pool.wait_ge(power_set, 1)
                pool.wait_ge(var_ready, 1)
                nc.gpsimd.tensor_tensor(rstd[:], var[:], power[:], ALU.pow).then_inc(rstd_ready, 1)

            @block.tensor
            def _(pe):
                for half in range(2):
                    pe.wait_ge(h_ready, half + 1)
                    for j in range(4):
                        last = nc.tensor.transpose(g.bank[half][:, j * T:(j + 1) * T], h[:, 4 * half + j, :], g.ident)
                    last.then_inc(turned, 1)

            @block.scalar
            def _(act):
                for half in range(2):
                    act.wait_ge(turned, half + 1)
                    nc.scalar.activation(hT[:, half * HALF:(half + 1) * HALF], g.bank[half][:], ACT.Copy)


def turn_context(nc, g):
    with Stage(nc, "context") as st:
        ctx = st.sb("ctx", [T, B, D])
        loaded, turned = st.sem("loaded"), st.sem("turned")
        with nc.Block() as block:
            @block.sync
            def _(sp):
                sp.dma_start(ctx[:], g.dram["ctx_1024"].rearrange("b t d -> t b d")).then_inc(loaded, 16)

            @block.tensor
            def _(pe):
                pe.wait_ge(g.const.loaded, 16)
                pe.wait_ge(loaded, 16)
                for half in range(2):
                    for j in range(4):
                        last = nc.tensor.transpose(g.bank[half][:, j * T:(j + 1) * T], ctx[:, 4 * half + j, :], g.ident)
                    last.then_inc(turned, 1)

            @block.scalar
            def _(act):
                for half in range(2):
                    act.wait_ge(turned, half + 1)
                    nc.scalar.activation(g.ctxT[:, half * HALF:(half + 1) * HALF], g.bank[half][:], ACT.Copy)

            @block.vector
            def _(dve):
                dve.wait_ge(g.const.loaded, 16)
                dve.wait_ge(g.x_loaded, 16)
                nc.vector.tensor_copy(g.ident_bf[:], g.ident)
                nc.vector.tensor_copy(g.causal_bf[:, 0, :], g.const["neg_causal"])
                nc.vector.tensor_copy(g.shifted_bf[:, 0, :], g.const["neg_shifted"])



def multi_query_attention(nc, g, w, name):
    NH, DH, Q = 16, 64, 4
    UN = NH // Q
    SCALE = DH ** -0.5
    with Stage(nc, name) as st:
        qT = st.sb("qT", [128, NH // 2, TOK])
        kvT = st.sb("kvT", [128, TOK])
        kv = st.sb("kv", [T, B, DH + 1])
        qs, kvs = st.sb("qs", [128, 2, NH // 2, T]), st.sb("kvs", [128, 2, 2, T])
        top, top0 = st.sb("top", [T, 2, Q]), st.sb("top0", [T, 2, Q])
        p = st.sb("p", [T, 2, Q * T + Q])
        pT = st.sb("pT", [T, 2, Q * T])
        null_q, null_score = st.sb("null_q", [D, NH]), st.sb("null_score", [T, B, NH])
        null_part = st.sb("null_part", [T, 2, Q, DH + 1])
        inv, o = st.sb("inv", [T, 2, Q]), st.sb("o", [T, 2, Q * DH])
        oT = st.sb("oT", [128, 2, 2, T])
        proj, proj_kept, kv_made, null_made, null_kept = (
            st.sem(s) for s in ("proj", "proj_kept", "kv_made", "null_made", "null_kept"))
        names = ("staged", "scored", "centered", "exped", "turned", "pT_kept", "mixed", "normed", "o_turned",
                 "oT_kept", "projected", "added", "null_weighed")
        staged, scored, centered, exped, turned, pT_kept, mixed, normed, o_turned, oT_kept, projected, added, null_weighed = (
            st.sem(s) for s in names)
        bank = g.bank

        with nc.Block() as block:
            @block.gpsimd
            def _(pool):
                nc.gpsimd.memset(kv[:, :, DH:DH + 1], 1.0)

            @block.tensor
            def _(pe):
                pe.wait_ge(w.loaded, 16)
                for m in range(2 * (NH // 2 + 1)):
                    j, half = m // 2, m % 2
                    if m >= 6:
                        pe.wait_ge(proj_kept, m - 5)
                    lhsT = w["wq"][:, j * 128:(j + 1) * 128] if j < NH // 2 else w["wkv2"]
                    nc.tensor.matmul(bank[m % 6][:], lhsT, g.hT[:, half * HALF:(half + 1) * HALF],
                                     start=True, stop=True).then_inc(proj, 1)
                for b in range(B):
                    last = nc.tensor.matmul(bank[6][:, b * DH:(b + 1) * DH], g.hT[:, b * T:(b + 1) * T],
                                            w["wkv2"][:, 0:DH], start=True, stop=True)
                last.then_inc(kv_made, 1)
                for j in range(NH // 2):
                    last = nc.tensor.matmul(bank[7][:, 2 * j:2 * j + 2], w["wqT"][:, j * D:(j + 1) * D], w["null2"],
                                            start=True, stop=True)
                last.then_inc(null_made, 1)
                pe.wait_ge(null_kept, 1)
                for b in range(B):
                    last = nc.tensor.matmul(bank[7][:, b * NH:(b + 1) * NH], g.hT[:, b * T:(b + 1) * T], null_q[:],
                                            start=True, stop=True)
                last.then_inc(null_made, 1)

            @block.scalar
            def _(act):
                for m in range(2 * (NH // 2 + 1)):
                    j, half = m // 2, m % 2
                    act.wait_ge(proj, m + 1)
                    dst = qT[:, j, :] if j < NH // 2 else kvT[:]
                    nc.scalar.activation(dst[:, half * HALF:(half + 1) * HALF], bank[m % 6][:],
                                         ACT.Copy).then_inc(proj_kept, 1)

            @block.vector
            def _(dve):
                dve.wait_ge(kv_made, 1)
                nc.vector.tensor_copy(kv[:, :, 0:DH], rows_of(bank[6][:], B))
                dve.wait_ge(null_made, 1)
                nc.vector.tensor_copy(null_q[:], bank[7][:, 0:NH]).then_inc(null_kept, 1)
                dve.wait_ge(null_made, 2)
                nc.vector.tensor_copy(null_score[:], rows_of(bank[7][:, 0:B * NH], B))

        score, tps, mix, o_tps, outp = bank[0:2], bank[2:4], bank[4:6], bank[6][:, 0:2 * T], bank[7]
        PER, LAG = 2 * UN, 6

        def unit_of(i, k):
            return PER * i + k, 2 * i + k // UN, k // UN % 2, k % UN, k % 2

        with nc.Block() as block:
            @block.gpsimd
            def _(pool):
                def step(i, r):
                    if has_unit(i, r, 0, PER) and r % UN == 0:
                        m, n, u, q, e = unit_of(i, r)
                        pool.wait_ge(scored, done(UN * (n - 2) + UN - 1))
                        nc.gpsimd.tensor_tensor(kvs[:, u, :, :], bc(kvT[:, bass.ds(n * T, T)], 1, 2),
                                                bc(g.const["half"], 2, T), ALU.mult)
                        nc.gpsimd.tensor_copy(qs[:, u, :, :], qT[:, :, bass.ds(n * T, T)]).then_inc(staged, 1)
                    if has_unit(i, r, 2, PER):
                        m, n, u, q, e = unit_of(i, r - 2)
                        pool.wait_ge(exped, done(m))
                        pool.wait_ge(mixed, done(m - 2))
                        nc.gpsimd.tensor_tensor(null_part[:, e, :, :], bc(p[:, e, Q * T:], 2, DH + 1),
                                                bc(w["null_row"], 1, Q), ALU.mult).then_inc(null_weighed, 1)

                credit(pool, staged, null_weighed)
                pipeline(pool, step, PER, LAG)

            @block.tensor
            def _(pe):
                def step(i, r):
                    if has_unit(i, r, 0, PER):
                        m, n, u, q, e = unit_of(i, r)
                        if q == 0:
                            pe.wait_ge(staged, done(n))
                        pe.wait_ge(centered, done(m - 2))
                        for j in range(Q // 2):
                            cols = score[e][:, 2 * j * T:2 * (j + 1) * T]
                            nc.tensor.matmul(cols, g.ident_bf[:], bc(g.causal_bf[:, 0, :], 1, 2),
                                             start=True, stop=False)
                            last = nc.tensor.matmul(cols, qs[:, u, q * 2 + j, :], kvs[:, u, :, :],
                                                    start=False, stop=True)
                        last.then_inc(scored, 1)
                    if has_unit(i, r, 2, PER):
                        m, n, u, q, e = unit_of(i, r - 2)
                        pe.wait_ge(exped, done(m))
                        pe.wait_ge(pT_kept, done(m - 2))
                        for j in range(Q):
                            last = nc.tensor.transpose(tps[e][:, j * T:(j + 1) * T], p[:, e, j * T:(j + 1) * T], g.ident)
                        last.then_inc(turned, 1)
                    if has_unit(i, r, 3, PER):
                        m, n, u, q, e = unit_of(i, r - 3)
                        pe.wait_ge(pT_kept, done(m))
                        pe.wait_ge(null_weighed, done(m))
                        pe.wait_ge(normed, done(m - 2))
                        for j in range(Q):
                            cols = slice(j * (DH + 1), (j + 1) * (DH + 1))
                            nc.tensor.matmul(mix[e][:, cols], g.ident, null_part[:, e, j, :],
                                             start=True, stop=False)
                            last = nc.tensor.matmul(mix[e][:, cols], pT[:, e, j * T:(j + 1) * T],
                                                    kv[:, n, :], start=False, stop=True)
                        last.then_inc(mixed, 1)
                    if has_unit(i, r, 5, PER):
                        m, n, u, q, e = unit_of(i, r - 5)
                        if q == 0:
                            pe.wait_ge(added, done(n - 1))
                        pe.wait_ge(oT_kept, done(m))
                        for j in range(2):
                            last = nc.tensor.matmul(outp[:, 0:D], oT[:, e, j, :],
                                                    w["wout"][:, (2 * q + j) * D:(2 * q + j + 1) * D],
                                                    start=(q == 0 and j == 0), stop=(q == UN - 1 and j == 1))
                        last.then_inc(projected, 1)
                    if has_unit(i, r, 4, PER):
                        m, n, u, q, e = unit_of(i, r - 4)
                        pe.wait_ge(normed, done(m))
                        pe.wait_ge(oT_kept, done(m - 1))
                        for j in range(2):
                            last = nc.tensor.transpose(o_tps[:, j * T:(j + 1) * T], o[:, e, j * T:(j + 1) * T], g.ident)
                        last.then_inc(o_turned, 1)

                credit(pe, scored, turned, mixed, o_turned, projected)
                pipeline(pe, step, PER, LAG)

            @block.scalar
            def _(act):
                def step(i, r):
                    if has_unit(i, r, 2, PER):
                        m, n, u, q, e = unit_of(i, r - 2)
                        act.wait_ge(turned, done(m))
                        act.wait_ge(mixed, done(m - 2))
                        nc.scalar.activation(pT[:, e, :], tps[e][:], ACT.Copy).then_inc(pT_kept, 1)
                    if has_unit(i, r, 0, PER):
                        m, n, u, q, e = unit_of(i, r)
                        act.wait_ge(centered, done(m))
                        nc.scalar.activation(p[:, e, :], p[:, e, :], ACT.Exp, scale=SCALE).then_inc(exped, 1)
                    if has_unit(i, r, 4, PER):
                        m, n, u, q, e = unit_of(i, r - 4)
                        act.wait_ge(o_turned, done(m))
                        act.wait_ge(projected, done(m - 2))
                        nc.scalar.activation(oT[:, e, :, :], rows_of(o_tps, 2), ACT.Copy).then_inc(oT_kept, 1)

                credit(act, exped, pT_kept, oT_kept)
                pipeline(act, step, PER, LAG)

            @block.vector
            def _(dve):
                def step(i, r):
                    if has_unit(i, r, 0, PER):
                        m, n, u, q, e = unit_of(i, r)
                        dve.wait_ge(scored, done(m))
                        nc.vector.tensor_reduce(top[:, e, :], rows_of(score[e][:], Q), X, ALU.max)
                        dve.drain()
                        null = null_score[:, n, q * Q:(q + 1) * Q]
                        nc.vector.tensor_tensor(top0[:, e, :], top[:, e, :], null, ALU.max)
                        dve.drain()
                        dve.wait_ge(turned, done(m - 2))
                        dve.wait_ge(null_weighed, done(m - 2))
                        nc.vector.tensor_tensor(p[:, e, Q * T:], null, top0[:, e, :], ALU.subtract)
                        nc.vector.tensor_tensor(rows_of(p[:, e, 0:Q * T], Q), rows_of(score[e][:], Q),
                                                bc(top0[:, e, :], 2, T), ALU.subtract).then_inc(centered, 1)
                    if has_unit(i, r, 3, PER):
                        m, n, u, q, e = unit_of(i, r - 3)
                        out = mix[e][:, 0:Q * (DH + 1)].rearrange("p (a b) -> p a b", a=Q)
                        dve.wait_ge(mixed, done(m))
                        nc.vector.reciprocal(inv[:, e, :], out[:, :, DH])
                        dve.drain()
                        dve.wait_ge(o_turned, done(m - 2))
                        nc.vector.tensor_tensor(rows_of(o[:, e, :], Q), out[:, :, 0:DH],
                                                bc(inv[:, e, :], 2, DH), ALU.mult).then_inc(normed, 1)
                    if has_unit(i, r, LAG, PER) and (r - LAG) % UN == UN - 1:
                        m, n, u, q, e = unit_of(i, r - LAG)
                        dve.wait_ge(projected, done(m))
                        nc.vector.tensor_tensor(g.x[:, n, :], g.x[:, n, :], outp[:, 0:D], ALU.add).then_inc(added, 1)

                credit(dve, centered, normed, added)
                pipeline(dve, step, PER, LAG)



def small_head_attention(nc, g, w, st, q_source, k_source, scale, mask=None):
    Q, UN = 4, H // 4
    qT, kT = st.sb("qT", [128, TOK]), st.sb("kT", [128, TOK])
    v = st.sb("v", [T, B, H, HD + 1])
    qs, ks = st.sb("qs", [128, 2, T]), st.sb("ks", [128, 2, H, T])
    top, inv = st.sb("top", [T, 2, Q]), st.sb("inv", [T, 2, Q])
    p, pT = st.sb("p", [T, 2, Q * T]), st.sb("pT", [T, 2, Q * T])
    o, oT = st.sb("o", [T, 2, H * HD]), st.sb("oT", [128, TOK])
    proj, v_made, ones_set = (st.sem(s) for s in ("proj", "v_made", "ones_set"))
    staged, scored, centered, exped, turned, pT_kept, mixed, normed, o_turned, oT_kept = (
        st.sem(s) for s in ("staged", "scored", "centered", "exped", "turned", "pT_kept", "mixed", "normed",
                            "o_turned", "oT_kept"))
    bank = g.bank

    with nc.Block() as block:
        @block.gpsimd
        def _(pool):
            nc.gpsimd.memset(v[:, :, :, HD:HD + 1], 1.0)

        @block.tensor
        def _(pe):
            pe.wait_ge(w.loaded, 16)
            for j, (weight, source) in enumerate((("wq", q_source), ("wk", k_source))):
                for half in range(2):
                    nc.tensor.matmul(bank[2 * j + half][:], w[weight], source[:, half * HALF:(half + 1) * HALF],
                                     start=True, stop=True).then_inc(proj, 1)
            for half in range(2):
                for j in range(4):
                    b = 4 * half + j
                    last = nc.tensor.matmul(bank[4 + half][:, j * D:(j + 1) * D], g.ctxT[:, b * T:(b + 1) * T],
                                            w["wv"], start=True, stop=True)
                last.then_inc(v_made, 1)

        @block.scalar
        def _(act):
            for m in range(4):
                act.wait_ge(proj, m + 1)
                dst, bias = ((qT, "bq"), (kT, "bk"))[m // 2]
                nc.scalar.activation(dst[:, (m % 2) * HALF:(m % 2 + 1) * HALF], bank[m][:], ACT.Identity, bias=w[bias])

        @block.vector
        def _(dve):
            for half in range(2):
                dve.wait_ge(v_made, half + 1)
                for j in range(4):
                    nc.vector.tensor_tensor(v[:, 4 * half + j, :, 0:HD], rows_of(bank[4 + half][:, j * D:(j + 1) * D], H),
                                            rows_of(w["bv"], H), ALU.add)

    PER, LAG = 2 * UN, 4

    def unit_of(i, k):
        return PER * i + k, k // UN % 2, k % UN, k % 2

    score, tps, mix, o_tps = bank[0:2], bank[2:4], bank[4:6], bank[6][:, 0:T]
    with nc.Block() as block:
        @block.gpsimd
        def _(pool):
            credit(pool, staged)
            with pool.Fori(0, B // 2) as i:
                for u in range(2):
                    n = 2 * i + u
                    pool.wait_ge(scored, done(UN * (n - 2) + UN - 1))
                    nc.gpsimd.tensor_copy(qs[:, u, :], qT[:, bass.ds(n * T, T)])
                    nc.gpsimd.tensor_tensor(ks[:, u, :, :], bc(kT[:, bass.ds(n * T, T)], 1, H),
                                            bc(g.const["head"], 2, T), ALU.mult).then_inc(staged, 1)

        @block.tensor
        def _(pe):
            def step(i, r):
                if has_unit(i, r, 0, PER):
                    m, u, q, e = unit_of(i, r)
                    if q == 0:
                        pe.wait_ge(staged, done(2 * i + r // UN))
                    pe.wait_ge(centered, done(m - 2))
                    if mask is not None:
                        nc.tensor.matmul(score[e][:], g.ident_bf[:], bc(mask(2 * i + r // UN), 1, Q),
                                         start=True, stop=False)
                    nc.tensor.matmul(score[e][:], qs[:, u, :], ks[:, u, Q * q:Q * (q + 1), :],
                                     start=mask is None, stop=True).then_inc(scored, 1)
                if has_unit(i, r, 2, PER):
                    m, u, q, e = unit_of(i, r - 2)
                    pe.wait_ge(exped, done(m))
                    pe.wait_ge(pT_kept, done(m - 2))
                    for j in range(Q):
                        last = nc.tensor.transpose(tps[e][:, j * T:(j + 1) * T], p[:, e, j * T:(j + 1) * T], g.ident)
                    last.then_inc(turned, 1)
                if has_unit(i, r, 3, PER):
                    m, u, q, e = unit_of(i, r - 3)
                    pe.wait_ge(pT_kept, done(m))
                    pe.wait_ge(normed, done(m - 2))
                    for j in range(Q):
                        last = nc.tensor.matmul(mix[e][:, j * (HD + 1):(j + 1) * (HD + 1)], pT[:, e, j * T:(j + 1) * T],
                                                v[:, 2 * i + (r - 3) // UN, Q * q + j, :], start=True, stop=True)
                    last.then_inc(mixed, 1)
                if has_unit(i, r, LAG, PER) and (r - LAG) % UN == UN - 1:
                    m, u, q, e = unit_of(i, r - LAG)
                    n = 2 * i + (r - LAG) // UN
                    pe.wait_ge(normed, done(m))
                    pe.wait_ge(oT_kept, done(n - 1))
                    nc.tensor.transpose(o_tps, o[:, u, :], g.ident).then_inc(o_turned, 1)

            credit(pe, scored, turned, mixed, o_turned)
            pipeline(pe, step, PER, LAG)

        @block.scalar
        def _(act):
            def step(i, r):
                if has_unit(i, r, 2, PER):
                    m, u, q, e = unit_of(i, r - 2)
                    act.wait_ge(turned, done(m))
                    act.wait_ge(mixed, done(m - 2))
                    nc.scalar.activation(pT[:, e, :], tps[e][:], ACT.Copy).then_inc(pT_kept, 1)
                if has_unit(i, r, LAG, PER) and (r - LAG) % UN == UN - 1:
                    n = 2 * i + (r - LAG) // UN
                    act.wait_ge(o_turned, done(n))
                    nc.scalar.activation(oT[:, bass.ds(n * T, T)], o_tps, ACT.Copy).then_inc(oT_kept, 1)
                if has_unit(i, r, 0, PER):
                    m, u, q, e = unit_of(i, r)
                    act.wait_ge(centered, done(m))
                    nc.scalar.activation(p[:, e, :], p[:, e, :], ACT.Exp, scale=scale).then_inc(exped, 1)

            credit(act, exped, pT_kept, oT_kept)
            pipeline(act, step, PER, LAG)

        @block.vector
        def _(dve):
            def step(i, r):
                if has_unit(i, r, 0, PER):
                    m, u, q, e = unit_of(i, r)
                    dve.wait_ge(scored, done(m))
                    nc.vector.tensor_reduce(top[:, e, :], rows_of(score[e][:], Q), X, ALU.max)
                    dve.drain()
                    dve.wait_ge(turned, done(m - 2))
                    nc.vector.tensor_tensor(rows_of(p[:, e, :], Q), rows_of(score[e][:], Q),
                                            bc(top[:, e, :], 2, T), ALU.subtract).then_inc(centered, 1)
                if has_unit(i, r, 3, PER):
                    m, u, q, e = unit_of(i, r - 3)
                    out = mix[e][:, 0:Q * (HD + 1)].rearrange("p (a b) -> p a b", a=Q)
                    dve.wait_ge(mixed, done(m))
                    nc.vector.reciprocal(inv[:, e, :], out[:, :, HD])
                    dve.drain()
                    if q == 0:
                        dve.wait_ge(o_turned, done(2 * i + (r - 3) // UN - 2))
                    nc.vector.tensor_tensor(rows_of(o[:, u, Q * HD * q:Q * HD * (q + 1)], Q), out[:, :, 0:HD],
                                            bc(inv[:, e, :], 2, HD), ALU.mult).then_inc(normed, 1)

            credit(dve, centered, normed)
            pipeline(dve, step, PER, LAG)
    return oT


def add_projection(nc, g, w, st, oT):
    bank = g.bank
    biased, projected = st.sem("biased"), st.sem("projected")
    with nc.Block() as block:
        @block.tensor
        def _(pe):
            for half in range(2):
                for j in range(4):
                    b = 4 * half + j
                    last = nc.tensor.matmul(bank[half][:, j * D:(j + 1) * D], oT[:, b * T:(b + 1) * T], w["wo"],
                                            start=True, stop=True)
                last.then_inc(projected, 1)

        @block.vector
        def _(dve):
            if "bo" in w.places:
                nc.vector.tensor_tensor(g.x[:], g.x[:], bc(w["bo"], 1, B), ALU.add)
                dve.drain()
            for half in range(2):
                b = slice(4 * half, 4 * half + 4)
                dve.wait_ge(projected, half + 1)
                nc.vector.tensor_tensor(g.x[:, b, :], g.x[:, b, :], rows_of(bank[half][:], 4), ALU.add)


def cross_attention(nc, g, w, name):
    with Stage(nc, name) as st:
        oT = small_head_attention(nc, g, w, st, g.hT, g.ctxT, HD ** -0.5)
        add_projection(nc, g, w, st, oT)


def masked_cross_attention(nc, g, w, name):
    with Stage(nc, name) as st:
        mask8, mask = st.sb("mask8", [T, B, T], U8), st.sb("mask", [T, B, T], BF16)
        mask_loaded = st.sem("mask_loaded")
        with nc.Block() as block:
            @block.sync
            def _(sp):
                sp.dma_start(mask8[:], g.dram["mask"].rearrange("b q k -> q b k")).then_inc(mask_loaded, 16)

            @block.vector
            def _(dve):
                dve.wait_ge(mask_loaded, 16)
                nc.vector.tensor_scalar(mask[:], mask8[:], NEG, None, ALU.mult)
        oT = small_head_attention(nc, g, w, st, g.hT, g.ctxT, HD ** -0.5, lambda n: mask[:, n, :])
        add_projection(nc, g, w, st, oT)


def attention_with_mlp(nc, g, w, name):
    NJ = 4
    bank = g.bank
    with Stage(nc, name) as st:
        oT = small_head_attention(nc, g, w, st, g.hT, g.hT, 1.0, lambda n: g.shifted_bf[:, 0, :])
        hid = st.sb("hid", [128, NJ, TOK])
        up, kept, down = st.sem("up"), st.sem("kept"), st.sem("down")
        with nc.Block() as block:
            @block.tensor
            def _(pe):
                for m in range(2 * NJ):
                    j, half = m % NJ, m // NJ
                    if m >= 6:
                        pe.wait_ge(kept, m - 5)
                    nc.tensor.matmul(bank[m % 6][:], w["w1"][:, j * 128:(j + 1) * 128],
                                     oT[:, half * HALF:(half + 1) * HALF], start=True, stop=True).then_inc(up, 1)
                for b in range(B):
                    if b % 4 == 0:
                        pe.wait_ge(kept, NJ * (b // 4 + 1))
                    for j in range(NJ):
                        last = nc.tensor.matmul(bank[6 + b // 4][:, (b % 4) * D:(b % 4 + 1) * D],
                                                hid[:, j, b * T:(b + 1) * T], w["w2"][:, j * D:(j + 1) * D],
                                                start=(j == 0), stop=(j == NJ - 1))
                    if b % 4 == 3:
                        last.then_inc(down, 1)

            @block.scalar
            def _(act):
                for m in range(2 * NJ):
                    j, half = m % NJ, m // NJ
                    act.wait_ge(up, m + 1)
                    nc.scalar.activation(hid[:, j, half * HALF:(half + 1) * HALF], bank[m % 6][:], ACT.Gelu,
                                         bias=w["b1"][:, j:j + 1]).then_inc(kept, 1)

            @block.vector
            def _(dve):
                nc.vector.tensor_tensor(g.x[:], g.x[:], bc(w["b2"], 1, B), ALU.add)
                dve.drain()
                for half in range(2):
                    b = slice(4 * half, 4 * half + 4)
                    dve.wait_ge(down, half + 1)
                    nc.vector.tensor_tensor(g.x[:, b, :], g.x[:, b, :], rows_of(bank[6 + half][:], 4), ALU.add)



def route_top2_softmax(nc, g, w, st, combine):
    E = 8
    bank = g.bank
    logit, best, keep = st.sb("logit", [T, B, E]), st.sb("best", [T, B, 8]), st.sb("keep", [T, B, E])
    total, combT = st.sb("total", [T, B]), st.sb("combT", [E, TOK])
    made, centered, exped, routed, combine_turned, combT_kept, biases = (
        st.sem(s) for s in ("made", "centered", "exped", "routed", "combine_turned", "combT_kept", "biases"))
    with nc.Block() as block:
        @block.tensor
        def _(pe):
            pe.wait_ge(w.loaded, 16)
            for b in range(B):
                last = nc.tensor.matmul(bank[0][:, b * E:(b + 1) * E], g.hT[:, b * T:(b + 1) * T], w["router"],
                                        start=True, stop=True)
            last.then_inc(made, 1)
            pe.wait_ge(routed, 1)
            for b in range(B):
                last = nc.tensor.transpose(bank[1 + b // 4][0:E, (b % 4) * T:(b % 4 + 1) * T], combine[:, b, :], g.ident)
            last.then_inc(combine_turned, 1)
            pe.wait_ge(combT_kept, 1)
            for b in range(B):
                last = nc.tensor.matmul(bank[3 + b // 4][:, (b % 4) * D:(b % 4 + 1) * D], combT[:, b * T:(b + 1) * T],
                                        w["b2"], start=True, stop=True)
            last.then_inc(biases, 1)

        @block.scalar
        def _(act):
            act.wait_ge(centered, 1)
            nc.scalar.activation(logit[:], logit[:], ACT.Exp).then_inc(exped, 1)
            act.wait_ge(combine_turned, 1)
            for half in range(2):
                last = nc.scalar.activation(combT[:, half * HALF:(half + 1) * HALF], bank[1 + half][0:E, :], ACT.Copy)
            last.then_inc(combT_kept, 1)

        @block.vector
        def _(dve):
            dve.wait_ge(made, 1)
            nc.vector.tensor_tensor(logit[:], rows_of(bank[0][:, 0:B * E], B), bc(w["br"], 1, B), ALU.add)
            dve.drain()
            for b in range(B):
                nc.vector.max(best[:, b, :], logit[:, b, :])
            dve.drain()
            nc.vector.tensor_tensor(keep[:], logit[:], best[:, :, 1:2].to_broadcast([T, B, E]), ALU.is_ge)
            dve.drain()
            nc.vector.tensor_tensor(logit[:], logit[:], best[:, :, 0:1].to_broadcast([T, B, E]),
                                    ALU.subtract).then_inc(centered, 1)
            dve.wait_ge(exped, 1)
            nc.vector.tensor_tensor(keep[:], keep[:], logit[:], ALU.mult)
            dve.drain()
            nc.vector.tensor_reduce(total[:], keep[:], X, ALU.add)
            dve.drain()
            nc.vector.reciprocal(total[:], total[:])
            dve.drain()
            nc.vector.tensor_tensor(combine[:], keep[:], bc(total[:], 2, E), ALU.mult).then_inc(routed, 1)
            dve.wait_ge(biases, 1)
            for half in range(2):
                b = slice(4 * half, 4 * half + 4)
                nc.vector.tensor_tensor(g.x[:, b, :], g.x[:, b, :], rows_of(bank[3 + half][:], 4), ALU.add)


def route_top2_renormed(nc, g, w, st, combine):
    E = 8
    bank = g.bank
    sq, meansq, rms = st.sb("sq", [T, B, D]), st.sb("meansq", [T, B]), st.sb("rms", [T, B])
    power, router = st.sb("power", [T, B]), st.sb("router", [D, E])
    logit, best, keep = st.sb("logit", [T, B, E]), st.sb("best", [T, B, 8]), st.sb("keep", [T, B, E])
    total, fix = st.sb("total", [T, B]), st.sb("fix", [T, B])
    power_set, squared, rms_ready, router_ready, made, centered, exped = (
        st.sem(s) for s in ("power_set", "squared", "rms_ready", "router_ready", "made", "centered", "exped"))
    with nc.Block() as block:
        @block.gpsimd
        def _(pool):
            nc.gpsimd.memset(power[:], -0.5).then_inc(power_set, 1)
            pool.wait_ge(power_set, 1)
            pool.wait_ge(squared, 1)
            nc.gpsimd.tensor_tensor(rms[:], meansq[:], power[:], ALU.pow).then_inc(rms_ready, 1)

        @block.tensor
        def _(pe):
            pe.wait_ge(router_ready, 1)
            for b in range(B):
                last = nc.tensor.matmul(bank[0][:, b * E:(b + 1) * E], g.hT[:, b * T:(b + 1) * T], router[:],
                                        start=True, stop=True)
            last.then_inc(made, 1)

        @block.scalar
        def _(act):
            act.wait_ge(centered, 1)
            nc.scalar.activation(logit[:], logit[:], ACT.Exp).then_inc(exped, 1)

        @block.vector
        def _(dve):
            dve.wait_ge(w.loaded, 16)
            nc.vector.tensor_scalar(router[:], w["router"], w["router_scale"], float(D) ** -0.5,
                                    ALU.mult, ALU.mult).then_inc(router_ready, 1)
            nc.vector.tensor_tensor(sq[:], g.h[:], g.h[:], ALU.mult)
            dve.drain()
            nc.vector.tensor_reduce(meansq[:], sq[:], X, ALU.add)
            dve.drain()
            nc.vector.tensor_scalar(meansq[:], meansq[:], 1.0 / D, 1e-6, ALU.mult, ALU.add).then_inc(squared, 1)
            dve.wait_ge(rms_ready, 1)
            dve.wait_ge(made, 1)
            nc.vector.tensor_tensor(logit[:], rows_of(bank[0][:, 0:B * E], B), bc(rms[:], 2, E), ALU.mult)
            dve.drain()
            for b in range(B):
                nc.vector.max(best[:, b, :], logit[:, b, :])
            dve.drain()
            nc.vector.tensor_tensor(keep[:], logit[:], best[:, :, 1:2].to_broadcast([T, B, E]), ALU.is_ge)
            dve.drain()
            nc.vector.tensor_tensor(logit[:], logit[:], best[:, :, 0:1].to_broadcast([T, B, E]),
                                    ALU.subtract).then_inc(centered, 1)
            dve.wait_ge(exped, 1)
            nc.vector.tensor_tensor(keep[:], keep[:], logit[:], ALU.mult)
            dve.drain()
            nc.vector.tensor_reduce(total[:], keep[:], X, ALU.add)
            dve.drain()
            nc.vector.tensor_scalar(fix[:], total[:], 0.0, None, ALU.is_le)
            dve.drain()
            nc.vector.tensor_tensor(total[:], total[:], fix[:], ALU.add)
            dve.drain()
            nc.vector.reciprocal(total[:], total[:])
            dve.drain()
            nc.vector.tensor_tensor(keep[:], keep[:], bc(total[:], 2, E), ALU.mult)
            dve.drain()
            nc.vector.tensor_tensor(combine[:], keep[:], bc(w["expert_scale"], 1, B), ALU.mult)


def route_grouped_top8(nc, g, w, st, combine):
    E, G = 64, 8
    bank = g.bank
    score, biased, chosen = st.sb("score", [T, B, E]), st.sb("biased", [T, B, E]), st.sb("chosen", [T, B, E])
    rest = st.sb("rest", [T, B, E])
    top1, top2, count = st.sb("top1", [T, B * G]), st.sb("top2", [T, B * G]), st.sb("count", [T, B * G])
    gsum, gbest, gkeep = st.sb("gsum", [T, B, G]), st.sb("gbest", [T, B, 8]), st.sb("gkeep", [T, B * G])
    best, total = st.sb("best", [T, B, 8]), st.sb("total", [T, B])
    made, sigmoid_ready = st.sem("made"), st.sem("sigmoid_ready")
    groups = lambda t: t[:].rearrange("p b (g e) -> p (b g) e", e=G)
    with nc.Block() as block:
        @block.tensor
        def _(pe):
            pe.wait_ge(w.loaded, 16)
            for b in range(B):
                last = nc.tensor.matmul(bank[0][:, b * E:(b + 1) * E], g.hT[:, b * T:(b + 1) * T], w["router"],
                                        start=True, stop=True)
            last.then_inc(made, 1)

        @block.scalar
        def _(act):
            act.wait_ge(made, 1)
            nc.scalar.activation(score[:], rows_of(bank[0][:], B), ACT.Sigmoid).then_inc(sigmoid_ready, 1)

        @block.vector
        def _(dve):
            dve.wait_ge(sigmoid_ready, 1)
            nc.vector.tensor_tensor(biased[:], score[:], bc(w["correction"], 1, B), ALU.add)
            dve.drain()
            nc.vector.tensor_reduce(top1[:], groups(biased), X, ALU.max)
            dve.drain()
            nc.vector.tensor_tensor(groups(chosen), groups(biased), bc(top1[:], 2, G), ALU.is_ge)
            dve.drain()
            nc.vector.tensor_reduce(count[:], groups(chosen), X, ALU.add)
            nc.vector.scalar_tensor_tensor(groups(rest), groups(chosen), NEG, groups(biased), ALU.mult, ALU.add)
            dve.drain()
            nc.vector.tensor_reduce(top2[:], groups(rest), X, ALU.max)
            nc.vector.tensor_scalar(count[:], count[:], 1.5, NEG, ALU.is_lt, ALU.mult)
            dve.drain()
            nc.vector.tensor_tensor(count[:], count[:], top1[:], ALU.add)
            dve.drain()
            nc.vector.tensor_tensor(top2[:], top2[:], count[:], ALU.max)
            dve.drain()
            nc.vector.tensor_tensor(gsum[:].rearrange("p b g -> p (b g)"), top1[:], top2[:], ALU.add)
            dve.drain()
            for b in range(B):
                nc.vector.max(gbest[:, b, :], gsum[:, b, :])
            dve.drain()
            nc.vector.tensor_tensor(rows_of(gkeep[:], B), gsum[:], gbest[:, :, 3:4].to_broadcast([T, B, G]), ALU.is_ge)
            dve.drain()
            nc.vector.tensor_tensor(groups(biased), groups(biased), bc(gkeep[:], 2, G), ALU.mult)
            dve.drain()
            for b in range(B):
                nc.vector.max(best[:, b, :], biased[:, b, :])
            dve.drain()
            for b in range(B):
                nc.vector.match_replace(rest[:, b, :], best[:, b, :], biased[:, b, :], NEG)
            dve.drain()
            nc.vector.tensor_scalar(chosen[:], rest[:], NEG, None, ALU.is_equal)
            dve.drain()
            nc.vector.tensor_tensor(chosen[:], chosen[:], score[:], ALU.mult)
            dve.drain()
            nc.vector.tensor_reduce(total[:], chosen[:], X, ALU.add)
            dve.drain()
            nc.vector.tensor_scalar(total[:], total[:], 1e-20, None, ALU.add)
            dve.drain()
            nc.vector.reciprocal(total[:], total[:])
            dve.drain()
            nc.vector.tensor_scalar(total[:], total[:], 2.5, None, ALU.mult)
            dve.drain()
            nc.vector.tensor_tensor(combine[:, :, 0:E], chosen[:], bc(total[:], 2, E), ALU.mult)


GATED, SQUARED, BIASED = range(3)


def experts(nc, g, w, st, combine, kind, widths):
    UN = len(widths)
    bank = g.bank
    hs = st.sb("hs", [D, 2, T])
    a, aT = st.sb("a", [T, 2, HALF]), st.sb("aT", [128, 2, 4, T])
    act_out = st.sb("act_out", [T, 2, HALF])
    staged, hidden, part, weighed, scaled, turned, aT_kept, summed, added = (
        st.sem(s) for s in ("staged", "hidden", "part", "weighed", "scaled", "turned", "aT_kept", "summed", "added"))
    up, tps, acc = bank[0:2], bank[2:4], bank[4:6]
    tile_at = [sum(widths[:q]) // 128 for q in range(UN)]
    up_width = [2 * x if kind == GATED else x for x in widths]
    up_at = [sum(up_width[:q]) for q in range(UN)]
    EXPERTS = 8

    PER, LAG = 2 * UN, 4

    def unit_of(i, k):
        return PER * i + k, 2 * i + k // UN, k // UN % 2, k % UN, k % 2

    with nc.Block() as block:
        @block.gpsimd
        def _(pool):
            def step(i, r):
                if has_unit(i, r, 0, PER) and r % UN == 0:
                    m, n, u, q, e = unit_of(i, r)
                    pool.wait_ge(hidden, done(UN * (n - 2) + UN - 1))
                    nc.gpsimd.tensor_copy(hs[:, u, :], g.hT[:, bass.ds(n * T, T)]).then_inc(staged, 1)
                if kind == SQUARED and has_unit(i, r, 2, PER):
                    m, n, u, q, e = unit_of(i, r - 2)
                    wide = widths[q]
                    pool.wait_ge(part, done(m))
                    ex = wide // (HALF // EXPERTS)
                    rows = act_out[:, e, 0:wide].rearrange("p (a b) -> p a b", a=ex)
                    nc.gpsimd.tensor_tensor(rows, rows, bc(combine[:, n, EXPERTS * q:EXPERTS * q + ex], 2,
                                                           HALF // EXPERTS), ALU.mult).then_inc(weighed, 1)

            credit(pool, staged)
            if kind == SQUARED:
                credit(pool, weighed)
            pipeline(pool, step, PER, LAG)

        @block.tensor
        def _(pe):
            def step(i, r):
                if has_unit(i, r, 0, PER):
                    m, n, u, q, e = unit_of(i, r)
                    if q == 0:
                        pe.wait_ge(staged, done(n))
                    pe.wait_ge(weighed if kind == BIASED else scaled, done(m - 2))
                    nc.tensor.matmul(up[e][:, 0:up_width[q]], hs[:, u, :], w["up"][:, up_at[q]:up_at[q] + up_width[q]],
                                     start=True, stop=True).then_inc(hidden, 1)
                if has_unit(i, r, 2, PER):
                    m, n, u, q, e = unit_of(i, r - 2)
                    pe.wait_ge(scaled, done(m))
                    pe.wait_ge(aT_kept, done(m - 2))
                    for j in range(widths[q] // 128):
                        last = nc.tensor.transpose(tps[e][:, j * T:(j + 1) * T], a[:, e, j * 128:(j + 1) * 128], g.ident)
                    last.then_inc(turned, 1)
                if has_unit(i, r, 3, PER):
                    m, n, u, q, e = unit_of(i, r - 3)
                    pe.wait_ge(aT_kept, done(m))
                    if q == 0:
                        pe.wait_ge(added, done(n - 2))
                    tiles = widths[q] // 128
                    for j in range(tiles):
                        at = (tile_at[q] + j) * D
                        last = nc.tensor.matmul(acc[u][:, 0:D], aT[:, e, j, :], w["down"][:, at:at + D],
                                                start=(q == 0 and j == 0), stop=(q == UN - 1 and j == tiles - 1))
                    last.then_inc(summed, 1)

            credit(pe, hidden, turned, summed)
            pipeline(pe, step, PER, LAG)

        @block.scalar
        def _(act):
            def activate(i, r):
                if has_unit(i, r, 0, PER):
                    m, n, u, q, e = unit_of(i, r)
                    wide = widths[q]
                    if kind == BIASED:
                        act.wait_ge(weighed, done(m))
                        nc.scalar.activation(act_out[:, e, :], act_out[:, e, :], ACT.Gelu).then_inc(part, 1)
                    else:
                        act.wait_ge(scaled, done(m - 2))
                        act.wait_ge(hidden, done(m))
                        nc.scalar.activation(act_out[:, e, 0:wide], up[e][:, 0:wide],
                                             ACT.Gelu_apprx_tanh if kind == GATED else ACT.Relu).then_inc(part, 1)

            def step(i, r):
                if kind != BIASED:
                    activate(i, r)
                if has_unit(i, r, 2, PER):
                    m, n, u, q, e = unit_of(i, r - 2)
                    act.wait_ge(turned, done(m))
                    act.wait_ge(summed, done(m - 2))
                    tiles = widths[q] // 128
                    nc.scalar.activation(aT[:, e, 0:tiles, :], rows_of(tps[e][:, 0:widths[q]], tiles),
                                         ACT.Copy).then_inc(aT_kept, 1)
                if kind == BIASED:
                    activate(i, r)

            credit(act, part, aT_kept)
            pipeline(act, step, PER, LAG)

        @block.vector
        def _(dve):
            def step(i, r):
                if kind == BIASED and has_unit(i, r, 0, PER):
                    m, n, u, q, e = unit_of(i, r)
                    dve.wait_ge(hidden, done(m))
                    dve.wait_ge(scaled, done(m - 2))
                    nc.vector.tensor_tensor(act_out[:, e, :], up[e][:], w["b1"][:, q * HALF:(q + 1) * HALF],
                                            ALU.add).then_inc(weighed, 1)
                back = 1 if kind != GATED else 0
                if has_unit(i, r, back, PER):
                    m, n, u, q, e = unit_of(i, r - back)
                    wide = widths[q]
                    dve.wait_ge(part, done(m))
                    dve.wait_ge(turned, done(m - 2))
                    if kind == GATED:
                        nc.vector.scalar_tensor_tensor(a[:, e, 0:wide], up[e][:, wide:2 * wide],
                                                       combine[:, n, q:q + 1], act_out[:, e, 0:wide],
                                                       ALU.mult, ALU.mult).then_inc(scaled, 1)
                    elif kind == SQUARED:
                        dve.wait_ge(weighed, done(m))
                        nc.vector.scalar_tensor_tensor(a[:, e, 0:wide], up[e][:, 0:wide], 0.0, act_out[:, e, 0:wide],
                                                       ALU.max, ALU.mult).then_inc(scaled, 1)
                    else:
                        nc.vector.tensor_scalar(a[:, e, :], act_out[:, e, :], combine[:, n, q:q + 1], None,
                                                ALU.mult).then_inc(scaled, 1)
                if has_unit(i, r, LAG, PER) and (r - LAG) % UN == UN - 1:
                    m, n, u, q, e = unit_of(i, r - LAG)
                    dve.wait_ge(summed, done(m))
                    nc.vector.tensor_tensor(g.x[:, n, :], g.x[:, n, :], acc[u][:, 0:D], ALU.add).then_inc(added, 1)

            credit(dve, scaled, added)
            if kind == BIASED:
                credit(dve, weighed)
            pipeline(dve, step, PER, LAG)


def gated_experts(nc, g, w, name):
    with Stage(nc, name) as st:
        combine = st.sb("combine", [T, B, 8])
        route_top2_renormed(nc, g, w, st, combine)
        experts(nc, g, w, st, combine, GATED, [256] * 8)


def many_experts(nc, g, w, name):
    with Stage(nc, name) as st:
        combine = st.sb("combine", [T, B, 68])
        with nc.Block() as block:
            @block.gpsimd
            def _(pool):
                nc.gpsimd.memset(combine[:, :, 64:68], 1.0)
        route_grouped_top8(nc, g, w, st, combine)
        experts(nc, g, w, st, combine, SQUARED, [HALF] * 8 + [256])


def wide_experts(nc, g, w, name):
    with Stage(nc, name) as st:
        combine = st.sb("combine", [T, B, 8])
        route_top2_softmax(nc, g, w, st, combine)
        experts(nc, g, w, st, combine, BIASED, [HALF] * 8)



def ternary_ffn(nc, g, w, name):
    INNER = 512
    bank = g.bank
    with Stage(nc, name) as st:
        mats = ("gate", "up", "down")
        rowsum = st.sb("rowsum", [128, 3])
        unit, unit_inv = st.sb("unit", [128, 3]), st.sb("unit_inv", [128, 3])
        wf, wq = st.sb("wf", [128, INNER]), st.sb("wq", [128, 3, INNER], BF16)
        peak, inv = st.sb("peak", [T, B]), st.sb("inv", [T, B])
        gate_scale, up_scale = st.sb("gate_scale", [T, B]), st.sb("up_scale", [T, B])
        hf, hq, hqT = st.sb("hf", [T, B, D]), st.sb("hq", [T, B, D], BF16), st.sb("hqT", [D, TOK], BF16)
        summed, means, quantised, turned, hqT_kept = (
            st.sem(s) for s in ("summed", "means", "quantised", "turned", "hqT_kept"))
        with nc.Block() as block:
            @block.tensor
            def _(pe):
                pe.wait_ge(summed, 1)
                nc.tensor.matmul(bank[2][:, 0:3], g.const["ones"], rowsum[:], start=True, stop=True).then_inc(means, 1)
                for half in range(2):
                    pe.wait_ge(quantised, 1)
                    for j in range(4):
                        last = nc.tensor.transpose(g.bank_bf[half][:, j * T:(j + 1) * T], hq[:, 4 * half + j, :],
                                                   g.ident_bf[:])
                    last.then_inc(turned, 1)

            @block.scalar
            def _(act):
                for half in range(2):
                    act.wait_ge(turned, half + 1)
                    nc.scalar.activation(hqT[:, half * HALF:(half + 1) * HALF], g.bank_bf[half][:, 0:HALF], ACT.Copy)

            @block.vector
            def _(dve):
                dve.wait_ge(w.loaded, 16)
                for j, name in enumerate(mats):
                    nc.vector.tensor_reduce(rowsum[:, j:j + 1], w[name], X, ALU.add, apply_absolute_value=True)
                dve.drain()
                nc.vector.tensor_scalar(rowsum[:], rowsum[:], 1.0 / (INNER * D), None, ALU.mult).then_inc(summed, 1)
                nc.vector.tensor_reduce(peak[:], g.h[:], X, ALU.max, apply_absolute_value=True)
                dve.drain()
                nc.vector.tensor_scalar(peak[:], peak[:], 1e-5, 1.0 / 127.0, ALU.max, ALU.mult)
                dve.drain()
                nc.vector.reciprocal(inv[:], peak[:])
                dve.drain()
                nc.vector.tensor_tensor(hf[:], g.h[:], bc(inv[:], 2, D), ALU.mult)
                dve.drain()
                nc.vector.tensor_scalar(hf[:], hf[:], ROUND, ROUND, ALU.add, ALU.subtract)
                dve.drain()
                nc.vector.tensor_scalar(hq[:], hf[:], 127.0, -128.0, ALU.min, ALU.max).then_inc(quantised, 1)
                dve.wait_ge(means, 1)
                nc.vector.tensor_scalar(unit[:], bank[2][:, 0:3], 1e-5, None, ALU.max)
                dve.drain()
                nc.vector.reciprocal(unit_inv[:], unit[:])
                dve.drain()
                for j, name in enumerate(mats):
                    nc.vector.tensor_scalar(wf[:], w[name], unit_inv[:, j:j + 1], None, ALU.mult)
                    dve.drain()
                    nc.vector.tensor_scalar(wf[:], wf[:], ROUND, ROUND, ALU.add, ALU.subtract)
                    dve.drain()
                    nc.vector.tensor_scalar(wq[:, j, :], wf[:], 1.0, -1.0, ALU.min, ALU.max)
                    dve.drain()
                nc.vector.tensor_scalar(gate_scale[:], peak[:], unit[:, 0:1], None, ALU.mult)
                nc.vector.tensor_scalar(up_scale[:], peak[:], unit[:, 1:2], None, ALU.mult)

        gated, prod = st.sb("gated", [T, 2, INNER]), st.sb("prod", [T, 2, INNER])
        prodf, prodq = st.sb("prodf", [T, 2, INNER]), st.sb("prodq", [T, 2, INNER], BF16)
        peak2, inv2, out_scale = st.sb("peak2", [T, 2]), st.sb("inv2", [T, 2]), st.sb("out_scale", [T, 2])
        prodT = st.sb("prodT", [128, 2, 4, T], BF16)
        hidden, silu_ready, rounded, prod_turned, prodT_kept, made, added = (
            st.sem(s) for s in ("hidden", "silu_ready", "rounded", "prod_turned", "prodT_kept", "made", "added"))
        gate, up, tps, out = bank[0:2], bank[2:4], g.bank_bf[4:6], bank[6:8]
        with nc.Block() as block:
            @block.tensor
            def _(pe):
                credit(pe, hidden, prod_turned, made)
                with pe.Fori(0, B // 2) as i:
                    for u in range(2):
                        n = 2 * i + u
                        pe.wait_ge(rounded, done(n - 2))
                        for at, j in ((gate[u], 0), (up[u], 1)):
                            last = nc.tensor.matmul(at[:], hqT[:, bass.ds(n * T, T)], wq[:, j, :], start=True, stop=True)
                        last.then_inc(hidden, 1)
                    for u in range(2):
                        n = 2 * i + u
                        pe.wait_ge(rounded, done(n))
                        pe.wait_ge(prodT_kept, done(n - 2))
                        for j in range(4):
                            last = nc.tensor.transpose(tps[u][:, j * T:(j + 1) * T], prodq[:, u, j * 128:(j + 1) * 128],
                                                       g.ident_bf[:])
                        last.then_inc(prod_turned, 1)
                        pe.wait_ge(prodT_kept, done(n))
                        pe.wait_ge(added, done(n - 2))
                        for j in range(4):
                            last = nc.tensor.matmul(out[u][:, 0:D], prodT[:, u, j, :], wq[:, 2, j * D:(j + 1) * D],
                                                    start=(j == 0), stop=(j == 3))
                        last.then_inc(made, 1)

            @block.scalar
            def _(act):
                credit(act, silu_ready, prodT_kept)
                with act.Fori(0, B // 2) as i:
                    for u in range(2):
                        n = 2 * i + u
                        act.wait_ge(hidden, done(n))
                        act.wait_ge(rounded, done(n - 2))
                        nc.scalar.activation(gated[:, u, :], gate[u][:], ACT.Silu,
                                             scale=gate_scale[:, bass.ds(n, 1)]).then_inc(silu_ready, 1)
                    for u in range(2):
                        n = 2 * i + u
                        act.wait_ge(prod_turned, done(n))
                        act.wait_ge(made, done(n - 2))
                        nc.scalar.activation(prodT[:, u, :, :], rows_of(tps[u][:, 0:HALF], 4),
                                             ACT.Copy).then_inc(prodT_kept, 1)

            @block.vector
            def _(dve):
                credit(dve, rounded, added)
                with dve.Fori(0, B // 2) as i:
                    for u in range(2):
                        n = 2 * i + u
                        dve.wait_ge(silu_ready, done(n))
                        nc.vector.scalar_tensor_tensor(prod[:, u, :], up[u][:], up_scale[:, bass.ds(n, 1)], gated[:, u, :],
                                                       ALU.mult, ALU.mult)
                        dve.drain()
                        nc.vector.tensor_reduce(peak2[:, u:u + 1], prod[:, u, :], X, ALU.max, apply_absolute_value=True)
                        dve.drain()
                        nc.vector.tensor_scalar(peak2[:, u:u + 1], peak2[:, u:u + 1], 1e-5, 1.0 / 127.0, ALU.max, ALU.mult)
                        dve.drain()
                        nc.vector.reciprocal(inv2[:, u:u + 1], peak2[:, u:u + 1])
                        nc.vector.tensor_scalar(out_scale[:, u:u + 1], peak2[:, u:u + 1], unit[:, 2:3], None, ALU.mult)
                        dve.drain()
                        nc.vector.tensor_scalar(prodf[:, u, :], prod[:, u, :], inv2[:, u:u + 1], ROUND, ALU.mult, ALU.add)
                        dve.drain()
                        dve.wait_ge(prod_turned, done(n - 2))
                        nc.vector.tensor_scalar(prodq[:, u, :], prodf[:, u, :], ROUND, None,
                                                ALU.subtract).then_inc(rounded, 1)
                    for u in range(2):
                        n = 2 * i + u
                        dve.wait_ge(made, done(n))
                        nc.vector.scalar_tensor_tensor(g.x[:, n, :], out[u][:, 0:D], out_scale[:, u:u + 1], g.x[:, n, :],
                                                       ALU.mult, ALU.add).then_inc(added, 1)



def time_mix(nc, g, w, name):
    bank = g.bank
    Q, UN = 4, H // 4
    with Stage(nc, name) as st:
        xx = st.sb("xx", [D, B, T])
        mixed = {c: st.sb("x" + c, [D, TOK]) for c in "rkvg"}
        rT, kT = st.sb("rT", [D, TOK]), st.sb("kT", [D, TOK])
        v, gate = st.sb("v", [T, B, D]), st.sb("gate", [T, B, D])
        rate, weight = st.sb("rate", [T, H]), st.sb("weight", [T, H, T])
        bonus = st.sb("bonus", [T, H, T])
        exped, projT, proj, blended, rates, powers, powers_ready = (
            st.sem(s) for s in ("exped", "projT", "proj", "blended", "rates", "powers", "powers_ready"))
        hT3 = rows_of(g.hT[:], B)
        with nc.Block() as block:
            @block.vector
            def _(dve):
                dve.wait_ge(w.loaded, 16)
                nc.vector.tensor_tensor(xx[:, :, 1:T], hT3[:, :, 0:T - 1], hT3[:, :, 1:T], ALU.subtract)
                nc.vector.tensor_scalar(xx[:, :, 0:1], hT3[:, :, 0:1], -1.0, None, ALU.mult)
                dve.drain()
                for c in "rkvg":
                    nc.vector.scalar_tensor_tensor(mixed[c][:], xx[:].rearrange("p b t -> p (b t)"), w["maa_" + c], g.hT[:],
                                                   ALU.mult, ALU.add).then_inc(blended, 1)
                dve.wait_ge(rates, 1)
                nc.vector.tensor_tensor(weight[:], bc(g.const["steps"], 1, H), bc(rate[:], 2, T), ALU.mult).then_inc(powers, 1)
                nc.vector.tensor_tensor(bonus[:], bc(g.ident, 1, H), bc(w["bonus"], 2, T), ALU.mult)
                dve.wait_ge(powers_ready, 1)
                nc.vector.tensor_tensor(weight[:], weight[:], bc(g.const["lt"], 1, H), ALU.mult)
                dve.drain()
                nc.vector.tensor_tensor(weight[:], weight[:], bonus[:], ALU.add)
                for half in range(2):
                    dve.wait_ge(proj, half + 1)
                    nc.vector.tensor_copy(v[:, 4 * half:4 * half + 4, :], rows_of(bank[4 + half][:], 4))

            @block.tensor
            def _(pe):
                for j, c in enumerate("rk"):
                    pe.wait_ge(blended, j + 1)
                    for half in range(2):
                        nc.tensor.matmul(bank[2 * j + half][:], w["w_" + c], mixed[c][:, half * HALF:(half + 1) * HALF],
                                         start=True, stop=True).then_inc(projT, 1)
                for j, c in enumerate("vg"):
                    pe.wait_ge(blended, j + 3)
                    for half in range(2):
                        for q in range(4):
                            b = 4 * half + q
                            last = nc.tensor.matmul(bank[4 + 2 * j + half][:, q * D:(q + 1) * D],
                                                    mixed[c][:, b * T:(b + 1) * T], w["w_" + c], start=True, stop=True)
                        last.then_inc(proj, 1)

            @block.scalar
            def _(act):
                act.wait_ge(w.loaded, 16)
                nc.scalar.activation(rate[:], w["decay"], ACT.Exp).then_inc(rates, 1)
                act.wait_ge(powers, 1)
                nc.scalar.activation(weight[:], weight[:], ACT.Exp, scale=-1.0).then_inc(powers_ready, 1)
                for m in range(4):
                    act.wait_ge(projT, m + 1)
                    nc.scalar.activation((rT, kT)[m // 2][:, (m % 2) * HALF:(m % 2 + 1) * HALF], bank[m][:], ACT.Copy)
                for half in range(2):
                    act.wait_ge(proj, 3 + half)
                    nc.scalar.activation(gate[:, 4 * half:4 * half + 4, :], rows_of(bank[6 + half][:], 4), ACT.Silu)

        ks, rs = st.sb("ks", [128, 2, T]), st.sb("rs", [128, 2, H, T])
        s, y = st.sb("s", [T, 2, Q, T]), st.sb("y", [T, 2, D])
        mean, var, rstd = st.sb("mean", [T, 2, H]), st.sb("var", [T, 2, H]), st.sb("rstd", [T, 2, H])
        sq, power = st.sb("sq", [T, 2, D]), st.sb("power", [T, H])
        yT = st.sb("yT", [D, 2, T])
        staged, scored, decayed, summed, var_ready, rstd_ready, y_ready, y_turned, yT_kept, made, added = (
            st.sem(x) for x in ("staged", "scored", "decayed", "summed", "var_ready", "rstd_ready", "y_ready", "y_turned",
                                "yT_kept", "made", "added"))
        score, ysum, yps, out = bank[0:4], bank[4:6], bank[6], bank[7]
        with nc.Block() as block:
            @block.gpsimd
            def _(pool):
                nc.gpsimd.memset(power[:], -0.5)
                credit(pool, staged, rstd_ready)
                with pool.Fori(0, B // 2) as i:
                    for u in range(2):
                        n = 2 * i + u
                        pool.wait_ge(scored, done(UN * (n - 2) + UN - 1))
                        nc.gpsimd.tensor_copy(ks[:, u, :], kT[:, bass.ds(n * T, T)])
                        nc.gpsimd.tensor_tensor(rs[:, u, :, :], bc(rT[:, bass.ds(n * T, T)], 1, H),
                                                bc(g.const["head"], 2, T), ALU.mult).then_inc(staged, 1)
                    for u in range(2):
                        n = 2 * i + u
                        pool.wait_ge(var_ready, done(n))
                        nc.gpsimd.tensor_tensor(rstd[:, u, :], var[:, u, :], power[:], ALU.pow).then_inc(rstd_ready, 1)

            @block.tensor
            def _(pe):
                credit(pe, scored, summed, y_turned, made)
                with pe.Fori(0, B // 2) as i:
                    def scores(k):
                        m, u, q = 2 * UN * i + k, k // UN, k % UN
                        if q == 0:
                            pe.wait_ge(staged, done(2 * i + u))
                        pe.wait_ge(decayed, done(m - 4))
                        nc.tensor.matmul(score[k % 4][:], ks[:, u, :], rs[:, u, Q * q:Q * (q + 1), :],
                                         start=True, stop=True).then_inc(scored, 1)

                    def sums(k):
                        m, u, q, e = 2 * UN * i + k, k // UN, k % UN, k % 2
                        pe.wait_ge(decayed, done(m))
                        if q == 0:
                            pe.wait_ge(y_ready, done(2 * i + u - 2))
                        for j in range(Q):
                            at = (Q * q + j) * HD
                            last = nc.tensor.matmul(ysum[u][:, at:at + HD], s[:, e, j, :], v[:, 2 * i + u, at:at + HD],
                                                    start=True, stop=True)
                        last.then_inc(summed, 1)

                    def project(u):
                        n = 2 * i + u
                        pe.wait_ge(y_ready, done(n))
                        pe.wait_ge(yT_kept, done(n - 1))
                        nc.tensor.transpose(yps[:, 0:T], y[:, u, :], g.ident).then_inc(y_turned, 1)
                        pe.wait_ge(yT_kept, done(n))
                        pe.wait_ge(added, done(n - 1))
                        nc.tensor.matmul(out[:, 0:D], yT[:, u, :], w["w_o"], start=True, stop=True).then_inc(made, 1)

                    for k in range(2 * UN + 1):
                        if k < 2 * UN:
                            scores(k)
                        if k >= 1:
                            sums(k - 1)
                    for u in range(2):
                        project(u)

            @block.scalar
            def _(act):
                credit(act, yT_kept)
                with act.Fori(0, B // 2) as i:
                    for u in range(2):
                        n = 2 * i + u
                        act.wait_ge(y_turned, done(n))
                        act.wait_ge(made, done(n - 2))
                        nc.scalar.activation(yT[:, u, :], yps[:, 0:T], ACT.Copy).then_inc(yT_kept, 1)

            @block.vector
            def _(dve):
                credit(dve, decayed, var_ready, y_ready, added)
                with dve.Fori(0, B // 2) as i:
                    for k in range(2 * UN):
                        m, u, q, e = 2 * UN * i + k, k // UN, k % UN, k % 2
                        dve.wait_ge(scored, done(m))
                        dve.wait_ge(summed, done(m - 2))
                        nc.vector.tensor_tensor(s[:, e, :, :], rows_of(score[k % 4][:], Q), weight[:, Q * q:Q * (q + 1), :],
                                                ALU.mult).then_inc(decayed, 1)
                    for u in range(2):
                        n = 2 * i + u
                        heads = lambda t: t[:, u, :].rearrange("p (h d) -> p h d", h=H)
                        dve.wait_ge(summed, done(UN * n + UN - 1))
                        nc.vector.tensor_reduce(mean[:, u, :], rows_of(ysum[u][:, 0:D], H), X, ALU.add)
                        dve.drain()
                        nc.vector.tensor_scalar(mean[:, u, :], mean[:, u, :], 1.0 / HD, None, ALU.mult)
                        dve.drain()
                        dve.wait_ge(y_turned, done(n - 2))
                        nc.vector.tensor_tensor(heads(y), rows_of(ysum[u][:, 0:D], H), bc(mean[:, u, :], 2, HD), ALU.subtract)
                        dve.drain()
                        nc.vector.tensor_tensor(sq[:, u, :], y[:, u, :], y[:, u, :], ALU.mult)
                        dve.drain()
                        nc.vector.tensor_reduce(var[:, u, :], heads(sq), X, ALU.add)
                        dve.drain()
                        nc.vector.tensor_scalar(var[:, u, :], var[:, u, :], 1.0 / HD, 64e-5, ALU.mult,
                                                ALU.add).then_inc(var_ready, 1)
                        dve.wait_ge(rstd_ready, done(n))
                        nc.vector.tensor_tensor(heads(y), heads(y), bc(rstd[:, u, :], 2, HD), ALU.mult)
                        dve.drain()
                        nc.vector.tensor_tensor(y[:, u, :], y[:, u, :], w["ln_g"], ALU.mult)
                        dve.drain()
                        nc.vector.tensor_tensor(y[:, u, :], y[:, u, :], w["ln_b"], ALU.add)
                        dve.drain()
                        nc.vector.tensor_tensor(y[:, u, :], y[:, u, :], gate[:, n, :], ALU.mult).then_inc(y_ready, 1)
                    for u in range(2):
                        n = 2 * i + u
                        dve.wait_ge(made, done(n))
                        nc.vector.tensor_tensor(g.x[:, n, :], g.x[:, n, :], out[:, 0:D], ALU.add).then_inc(added, 1)


def softplus_tail(nc, dve, e, u, log_u, fix):
    nc.vector.tensor_scalar(u, u, -1.0, None, ALU.add)
    dve.drain()
    nc.vector.tensor_scalar(fix, u, 0.0, None, ALU.is_equal)
    dve.drain()
    nc.vector.tensor_tensor(u, u, fix, ALU.add)
    nc.vector.tensor_tensor(log_u, log_u, fix, ALU.add)
    dve.drain()
    nc.vector.reciprocal(u, u)
    nc.vector.tensor_tensor(e, e, log_u, ALU.mult)
    dve.drain()
    nc.vector.tensor_tensor(e, e, u, ALU.mult)



def state_space(nc, g, w, name):
    NH, DH, DS, TAPS = 4, 64, 64, 4
    DI = NH * DH
    bank = g.bank
    with Stage(nc, name) as st:
        raw = st.sb("raw", [128, 4, B, T + TAPS - 1])
        c = st.sb("c", [128, 4, B, T])
        z = st.sb("z", [T, B, DI])
        dt, e, u1, log_u, fix = (st.sb(x, [T, B, NH]) for x in ("dt", "e", "u1", "log_u", "fix"))
        a, rate = st.sb("a", [T, B, NH]), st.sb("rate", [T, NH])
        rows = (128, 128, DS, DS)
        proj, raw_kept, convolved, z_made, z_kept, dt_made, pads_set, abs_ready, e_ready, u_ready, log_ready, rate_ready = (
            st.sem(x) for x in ("proj", "raw_kept", "convolved", "z_made", "z_kept", "dt_made", "pads_set", "abs_ready",
                                "e_ready", "u_ready", "log_ready", "rate_ready"))
        with nc.Block() as block:
            @block.gpsimd
            def _(pool):
                nc.gpsimd.memset(raw[:, :, :, 0:TAPS - 1], 0.0).then_inc(pads_set, 1)

            @block.tensor
            def _(pe):
                pe.wait_ge(w.loaded, 16)
                for b in range(B):
                    last = nc.tensor.matmul(bank[7][:, b * NH:(b + 1) * NH], g.hT[:, b * T:(b + 1) * T], w["w_dt"],
                                            start=True, stop=True)
                last.then_inc(dt_made, 1)
                at = 0
                for m in range(8):
                    j, half = m // 2, m % 2
                    if m >= 6:
                        pe.wait_ge(raw_kept, m - 5)
                    nc.tensor.matmul(bank[m % 6][0:rows[j], :], w["w_conv"][:, at:at + rows[j]],
                                     g.hT[:, half * HALF:(half + 1) * HALF], start=True, stop=True).then_inc(proj, 1)
                    at += rows[j] if half else 0
                pe.wait_ge(raw_kept, 8)
                for m in range(4):
                    for q in range(2):
                        b = 2 * m + q
                        last = nc.tensor.matmul(bank[m][:, q * DI:(q + 1) * DI], g.hT[:, b * T:(b + 1) * T], w["w_z"],
                                                start=True, stop=True)
                    last.then_inc(z_made, 1)

            @block.scalar
            def _(act):
                act.wait_ge(w.loaded, 16)
                nc.scalar.activation(rate[:], w["a_log"], ACT.Exp).then_inc(rate_ready, 1)
                act.wait_ge(abs_ready, 1)
                nc.scalar.activation(e[:], e[:], ACT.Exp, scale=-1.0).then_inc(e_ready, 1)
                act.wait_ge(u_ready, 1)
                nc.scalar.activation(log_u[:], u1[:], ACT.Ln).then_inc(log_ready, 1)
                act.wait_ge(pads_set, 1)
                for m in range(8):
                    j, half = m // 2, m % 2
                    act.wait_ge(proj, m + 1)
                    nc.scalar.activation(raw[0:rows[j], j, 4 * half:4 * half + 4, TAPS - 1:],
                                         rows_of(bank[m % 6][0:rows[j], :], 4), ACT.Copy).then_inc(raw_kept, 1)
                for m in range(4):
                    act.wait_ge(z_made, m + 1)
                    nc.scalar.activation(z[:, 2 * m:2 * m + 2, :], rows_of(bank[m][:], 2), ACT.Silu)
                for j in range(4):
                    act.wait_ge(convolved, j + 1)
                    tile = c[0:rows[j], j, :, :]
                    nc.scalar.activation(tile, tile, ACT.Silu, bias=w["conv_b"][0:rows[j], j:j + 1])

            @block.vector
            def _(dve):
                dve.wait_ge(w.loaded, 16)
                dve.wait_ge(dt_made, 1)
                nc.vector.tensor_tensor(dt[:], rows_of(bank[7][:, 0:B * NH], B), bc(w["dt_bias"], 1, B), ALU.add)
                dve.drain()
                nc.vector.scalar_tensor_tensor(e[:], dt[:], -1.0, dt[:], ALU.mult, ALU.max).then_inc(abs_ready, 1)
                dve.drain()
                nc.vector.tensor_scalar(dt[:], dt[:], 0.0, None, ALU.max)
                dve.wait_ge(e_ready, 1)
                nc.vector.tensor_scalar(u1[:], e[:], 1.0, None, ALU.add).then_inc(u_ready, 1)
                dve.wait_ge(log_ready, 1)
                softplus_tail(nc, dve, e[:], u1[:], log_u[:], fix[:])
                dve.drain()
                nc.vector.tensor_tensor(dt[:], dt[:], e[:], ALU.add)
                dve.drain()
                dve.wait_ge(rate_ready, 1)
                nc.vector.scalar_tensor_tensor(a[:], dt[:], -1.0, bc(rate[:], 1, B), ALU.mult, ALU.mult)
                for j in range(4):
                    dve.wait_ge(raw_kept, 2 * j + 2)
                    out = c[0:rows[j], j, :, :]
                    for k in range(TAPS):
                        src = raw[0:rows[j], j, :, k:k + T]
                        tap = w["conv_w"][0:rows[j], j * TAPS + k:j * TAPS + k + 1]
                        if k == 0:
                            last = nc.vector.tensor_scalar(out, src, tap, None, ALU.mult)
                        else:
                            last = nc.vector.scalar_tensor_tensor(out, src, tap, out, ALU.mult, ALU.add)
                        if k < TAPS - 1:
                            dve.drain()
                    last.then_inc(convolved, 1)

        xs, bcs = st.sb("xs", [128, 2, 2, T]), st.sb("bcs", [DS, 2, 2, T])
        later = st.sb("later", [T, 2, NH, T])
        decay, decay0 = st.sb("decay", [T, 2, NH, T]), st.sb("decay0", [T, 2, NH])
        cb = st.sb("cb", [T, 2, T])
        xt, xdt, base, y = (st.sb(x, [T, 2, DI]) for x in ("xt", "xdt", "base", "y"))
        sq, meansq, rstd, power = st.sb("sq", [T, DI]), st.sb("meansq", [T, 2]), st.sb("rstd", [T, 2]), st.sb("power", [T, 1])
        yT = st.sb("yT", [128, 2, 2, T])
        staged, prods, decay_ready, pairs, summed, y_made, rms_ready, y_ready, y_turned, yT_kept, made, added = (
            st.sem(x) for x in ("staged", "prods", "decay_ready", "pairs", "summed", "y_made", "rms_ready", "y_ready",
                                "y_turned", "yT_kept", "made", "added"))
        heads = lambda t: t.rearrange("p (h d) -> p h d", h=NH)
        mixed, seg = bank[0:2], bank[2:4]
        xps, ysum, yps, out = bank[4], bank[5], bank[6], bank[7]
        with nc.Block() as block:
            @block.gpsimd
            def _(pool):
                nc.gpsimd.memset(power[:], -0.5)
                credit(pool, staged, rms_ready)
                with pool.Fori(0, B // 2) as i:
                    for u in range(2):
                        n = 2 * i + u
                        pool.wait_ge(prods, done(n - 2))
                        nc.gpsimd.tensor_copy(xs[:, u, :, :], c[:, 0:2, n, :])
                        nc.gpsimd.tensor_copy(bcs[:, u, :, :], c[0:DS, 2:4, n, :])
                        nc.gpsimd.tensor_tensor(later[:, u, :, :], bc(g.const["gt"], 1, NH), bc(a[:, n, :], 2, T),
                                                ALU.mult).then_inc(staged, 1)
                    for u in range(2):
                        n = 2 * i + u
                        pool.wait_ge(y_made, done(n))
                        nc.gpsimd.tensor_tensor(rstd[:, u:u + 1], meansq[:, u:u + 1], power[:], ALU.pow).then_inc(rms_ready, 1)

            @block.tensor
            def _(pe):
                credit(pe, prods, summed, y_turned, made)
                with pe.Fori(0, B // 2) as i:
                    for u in range(2):
                        n = 2 * i + u
                        pe.wait_ge(staged, done(n))
                        pe.wait_ge(pairs, done(n - 1))
                        nc.tensor.matmul(mixed[u][:, 0:T], bcs[:, u, 0, :], bcs[:, u, 1, :], start=True, stop=True)
                        nc.tensor.matmul(mixed[u][:, T:T + DI], bcs[:, u, 1, :], w["init"], start=True, stop=True)
                        nc.tensor.matmul(mixed[u][:, T + DI:T + DI + NH], g.const["le"], a[:, n, :], start=True, stop=True)
                        for h in range(NH):
                            nc.tensor.matmul(seg[u][:, h * T:(h + 1) * T], later[:, u, h, :], g.const["le"],
                                             start=True, stop=True)
                        for j in range(2):
                            last = nc.tensor.transpose(xps[:, j * 128:(j + 1) * 128], xs[:, u, j, :], g.ident)
                        last.then_inc(prods, 1)
                    for u in range(2):
                        n = 2 * i + u
                        pe.wait_ge(pairs, done(n))
                        pe.wait_ge(y_made, done(n - 1))
                        for h in range(NH):
                            last = nc.tensor.matmul(ysum[:, h * DH:(h + 1) * DH], decay[:, u, h, :],
                                                    xdt[:, u, h * DH:(h + 1) * DH], start=True, stop=True)
                        last.then_inc(summed, 1)
                    for u in range(2):
                        n = 2 * i + u
                        pe.wait_ge(y_ready, done(n))
                        pe.wait_ge(yT_kept, done(n - 1))
                        for j in range(2):
                            last = nc.tensor.transpose(yps[:, j * T:(j + 1) * T], y[:, u, j * 128:(j + 1) * 128], g.ident)
                        last.then_inc(y_turned, 1)
                        pe.wait_ge(yT_kept, done(n))
                        pe.wait_ge(added, done(n - 1))
                        for j in range(2):
                            last = nc.tensor.matmul(out[:, 0:D], yT[:, u, j, :], w["w_out"][:, j * D:(j + 1) * D],
                                                    start=(j == 0), stop=(j == 1))
                        last.then_inc(made, 1)

            @block.scalar
            def _(act):
                credit(act, decay_ready, yT_kept)
                with act.Fori(0, B // 2) as i:
                    for u in range(2):
                        n = 2 * i + u
                        act.wait_ge(prods, done(n))
                        act.wait_ge(summed, done(n - 2))
                        nc.scalar.activation(decay[:, u, :, :], rows_of(seg[u][:], NH), ACT.Exp)
                        nc.scalar.activation(decay0[:, u, :], mixed[u][:, T + DI:T + DI + NH], ACT.Exp).then_inc(decay_ready, 1)
                    for u in range(2):
                        n = 2 * i + u
                        act.wait_ge(y_turned, done(n))
                        nc.scalar.activation(yT[:, u, :, :], rows_of(yps[:, 0:DI], 2), ACT.Copy).then_inc(yT_kept, 1)

            @block.vector
            def _(dve):
                credit(dve, pairs, y_made, y_ready, added)
                with dve.Fori(0, B // 2) as i:
                    for u in range(2):
                        n = 2 * i + u
                        dve.wait_ge(decay_ready, done(n))
                        nc.vector.tensor_copy(xt[:, u, :], xps[:, 0:DI])
                        nc.vector.tensor_tensor(cb[:, u, :], mixed[u][:, 0:T], g.const["le"], ALU.mult)
                        nc.vector.tensor_tensor(heads(base[:, u, :]), heads(mixed[u][:, T:T + DI]), bc(decay0[:, u, :], 2, DH),
                                                ALU.mult)
                        dve.drain()
                        nc.vector.tensor_tensor(heads(xdt[:, u, :]), heads(xt[:, u, :]), bc(dt[:, n, :], 2, DH), ALU.mult)
                        nc.vector.tensor_tensor(heads(xt[:, u, :]), heads(xt[:, u, :]), bc(w["skip"], 2, DH), ALU.mult)
                        nc.vector.tensor_tensor(decay[:, u, :, :], decay[:, u, :, :], bc(cb[:, u, :], 1, NH),
                                                ALU.mult).then_inc(pairs, 1)
                        dve.drain()
                        nc.vector.tensor_tensor(base[:, u, :], base[:, u, :], xt[:, u, :], ALU.add)
                    for u in range(2):
                        n = 2 * i + u
                        dve.wait_ge(summed, done(n))
                        nc.vector.tensor_tensor(base[:, u, :], base[:, u, :], ysum[:, 0:DI], ALU.add)
                        dve.drain()
                        dve.wait_ge(y_turned, done(n - 2))
                        nc.vector.tensor_tensor(y[:, u, :], base[:, u, :], z[:, n, :], ALU.mult)
                        dve.drain()
                        nc.vector.tensor_tensor(sq[:], y[:, u, :], y[:, u, :], ALU.mult)
                        dve.drain()
                        nc.vector.tensor_reduce(meansq[:, u:u + 1], sq[:], X, ALU.add)
                        dve.drain()
                        nc.vector.tensor_scalar(meansq[:, u:u + 1], meansq[:, u:u + 1], 1.0 / DI, 1e-5, ALU.mult,
                                                ALU.add).then_inc(y_made, 1)
                    for u in range(2):
                        n = 2 * i + u
                        dve.wait_ge(rms_ready, done(n))
                        nc.vector.scalar_tensor_tensor(y[:, u, :], y[:, u, :], rstd[:, u:u + 1], w["norm_w"],
                                                       ALU.mult, ALU.mult).then_inc(y_ready, 1)
                    for u in range(2):
                        n = 2 * i + u
                        dve.wait_ge(made, done(n))
                        nc.vector.tensor_tensor(g.x[:, n, :], g.x[:, n, :], out[:, 0:D], ALU.add).then_inc(added, 1)



def delta_gates(nc, g, w, st, rate_of, beta):
    NH = 12
    bank = g.bank
    e, u1, log_u, fix = (st.sb(x, [T, B, NH]) for x in ("e", "u1", "log_u", "fix"))
    a_rate = st.sb("a_rate", [T, NH])
    made, beta_in, beta_kept, abs_ready, e_ready, u_ready, log_ready = (
        st.sem(x) for x in ("made", "beta_in", "beta_kept", "abs_ready", "e_ready", "u_ready", "log_ready"))
    with nc.Block() as block:
        @block.tensor
        def _(pe):
            pe.wait_ge(w.loaded, 16)
            for j, name in enumerate(("w_rate", "w_beta")):
                for b in range(B):
                    last = nc.tensor.matmul(bank[j][:, b * NH:(b + 1) * NH], g.hT[:, b * T:(b + 1) * T], w[name],
                                            start=True, stop=True)
                last.then_inc(made, 1)

        @block.scalar
        def _(act):
            act.wait_ge(w.loaded, 16)
            nc.scalar.activation(a_rate[:], w["a_log"], ACT.Exp)
            act.wait_ge(abs_ready, 1)
            nc.scalar.activation(e[:], e[:], ACT.Exp, scale=-1.0).then_inc(e_ready, 1)
            act.wait_ge(u_ready, 1)
            nc.scalar.activation(log_u[:], u1[:], ACT.Ln).then_inc(log_ready, 1)
            act.wait_ge(beta_in, 1)
            nc.scalar.activation(beta[:], beta[:], ACT.Sigmoid).then_inc(beta_kept, 1)

        @block.vector
        def _(dve):
            dve.wait_ge(made, 1)
            dt = rate_of
            nc.vector.tensor_tensor(dt[:], rows_of(bank[0][:, 0:B * NH], B), bc(w["dt_bias"], 1, B), ALU.add)
            dve.wait_ge(made, 2)
            nc.vector.tensor_tensor(beta[:], rows_of(bank[1][:, 0:B * NH], B), bc(w["b_b"], 1, B), ALU.add).then_inc(beta_in, 1)
            dve.drain()
            nc.vector.scalar_tensor_tensor(e[:], dt[:], -1.0, dt[:], ALU.mult, ALU.max).then_inc(abs_ready, 1)
            dve.drain()
            nc.vector.tensor_scalar(dt[:], dt[:], 0.0, None, ALU.max)
            dve.wait_ge(e_ready, 1)
            nc.vector.tensor_scalar(u1[:], e[:], 1.0, None, ALU.add).then_inc(u_ready, 1)
            dve.wait_ge(log_ready, 1)
            softplus_tail(nc, dve, e[:], u1[:], log_u[:], fix[:])
            dve.drain()
            nc.vector.tensor_tensor(dt[:], dt[:], e[:], ALU.add)
            dve.drain()
            nc.vector.scalar_tensor_tensor(dt[:], dt[:], -1.0, bc(a_rate[:], 1, B), ALU.mult, ALU.mult)


def delta_rule(nc, g, w, name):
    NH, DK, DV, TAPS, G = 12, 64, 128, 4, 4
    LEVELS = 6
    QK = 4
    bank = g.bank
    with Stage(nc, name) as st:
        rate, beta = st.sb("rate", [T, B, NH]), st.sb("beta", [T, B, NH])
        delta_gates(nc, g, w, st, rate, beta)

        c = g.region_a[:, 0:8 * TOK].rearrange("p (m b t) -> p m b t", m=8, b=B)
        raw = st.sb("raw", [128, 2, B, T + TAPS - 1])
        spare = g.region_b[:, w.tile.shape[1]:]
        gate = spare[:, 0:B * G * DV].rearrange("p (b d) -> p b d", b=B)
        sq = spare[:, B * G * DV:B * G * DV + TOK]
        norms, power = st.sb("norms", [T, B, 2 * G]), st.sb("power", [T, B, 2 * G])
        coef, vscale, qeps = (st.sb(x, [T, B, G]) for x in ("coef", "vscale", "qeps"))
        qks, kb, vs = st.sb("qks", [128, 2, QK, T]), st.sb("kb", [128, 2, G, T]), st.sb("vs", [DV, 2, G, T])
        later, mcoef = st.sb("later", [T, 2, G, T]), st.sb("mcoef", [T, 2, G, T])
        dec, A, P = st.sb("dec", [T, 2, G, T]), st.sb("A", [T, 2, G, T]), st.sb("P", [T, 2, G, T])
        W, V, join = st.sb("W", [T, 2, G, T]), st.sb("V", [T, 2, G, T]), st.sb("join", [T, 2, G, T])
        R, PT = st.sb("R", [T, 2, G, DV]), st.sb("PT", [T, 2, G, T])
        delta, o, osq, y, yT = P, dec, A, W, join
        ssum, rstd = st.sb("ssum", [T, 2, G]), st.sb("rstd", [T, 2, G])

        for hg in range(NH // G):
            names = ("pads_set", "proj", "raw_kept", "convolved", "silu_ready", "squared", "norms_made", "norms_in",
                     "norms_ready", "gate_made", "gate_kept")
            (pads_set, proj, raw_kept, convolved, silu_ready, squared, norms_made, norms_in, norms_ready, gate_made,
             gate_kept) = (st.sem(f"{x}{hg}") for x in names)
            heads_of = slice(hg * G, hg * G + G)

            def weights_of(m):
                name, j = ("q", 2 * hg + m) if m < 2 else ("k", 2 * hg + m - 2) if m < 4 else ("v", G * hg + m - 4)
                return w["w" + name][:, j * 128:(j + 1) * 128], w["conv_" + name][:, j * TAPS:(j + 1) * TAPS]

            with nc.Block() as block:
                @block.gpsimd
                def _(pool):
                    nc.gpsimd.memset(raw[:, :, :, 0:TAPS - 1], 0.0).then_inc(pads_set, 1)
                    nc.gpsimd.memset(power[:], -0.5).then_inc(pads_set, 1)
                    pool.wait_ge(pads_set, 2)
                    pool.wait_ge(norms_in, 1)
                    nc.gpsimd.tensor_tensor(norms[:], norms[:], power[:], ALU.pow).then_inc(norms_ready, 1)

                @block.tensor
                def _(pe):
                    for m in range(8 + 1):
                        if m < 8:
                            if m >= 3:
                                pe.wait_ge(raw_kept, m - 2)
                            for half in range(2):
                                last = nc.tensor.matmul(bank[2 * (m % 3) + half][:], weights_of(m)[0],
                                                        g.hT[:, half * HALF:(half + 1) * HALF], start=True, stop=True)
                            last.then_inc(proj, 1)
                        if 1 <= m <= QK:
                            pe.wait_ge(squared, m)
                            for b in range(B):
                                at = b * 2 * G + 2 * (m - 1)
                                last = nc.tensor.matmul(bank[6][:, at:at + 2], sq[:, b * T:(b + 1) * T], g.const["half"],
                                                        start=True, stop=True)
                            last.then_inc(norms_made, 1)
                    for b in range(B):
                        j = b % 2
                        if b < 2:
                            pe.wait_ge(raw_kept, 8)
                        else:
                            pe.wait_ge(gate_kept, b - 1)
                        nc.tensor.matmul(bank[j][:], g.hT[:, b * T:(b + 1) * T], w["wg"][:, hg * HALF:(hg + 1) * HALF],
                                         start=True, stop=True).then_inc(gate_made, 1)

                @block.scalar
                def _(act):
                    for m in range(8 + 1):
                        if m < 8:
                            if m == 0:
                                act.wait_ge(pads_set, 1)
                            if m >= 2:
                                act.wait_ge(convolved, m - 1)
                            act.wait_ge(proj, m + 1)
                            for half in range(2):
                                last = nc.scalar.activation(raw[:, m % 2, 4 * half:4 * half + 4, TAPS - 1:],
                                                            rows_of(bank[2 * (m % 3) + half][:], 4), ACT.Copy)
                            last.then_inc(raw_kept, 1)
                        if m >= 1:
                            act.wait_ge(convolved, m)
                            tile = c[:, m - 1, :, :]
                            nc.scalar.activation(tile, tile, ACT.Silu).then_inc(silu_ready, 1)
                            if m <= QK:
                                act.wait_ge(silu_ready, m)
                                if m >= 2:
                                    act.wait_ge(norms_made, m - 1)
                                nc.scalar.activation(sq, tile.rearrange("p b t -> p (b t)"),
                                                     ACT.Square).then_inc(squared, 1)
                    for b in range(B):
                        act.wait_ge(gate_made, b + 1)
                        nc.scalar.activation(gate[:, b, :], bank[b % 2][:], ACT.Silu).then_inc(gate_kept, 1)

                @block.vector
                def _(dve):
                    for m in range(8):
                        dve.wait_ge(raw_kept, m + 1)
                        taps = weights_of(m)[1]
                        for k in range(TAPS):
                            src = raw[:, m % 2, :, k:k + T]
                            if k == 0:
                                last = nc.vector.tensor_scalar(c[:, m, :, :], src, taps[:, 0:1], None, ALU.mult)
                            else:
                                last = nc.vector.scalar_tensor_tensor(c[:, m, :, :], src, taps[:, k:k + 1], c[:, m, :, :],
                                                                      ALU.mult, ALU.add)
                            if k < TAPS - 1:
                                dve.drain()
                        last.then_inc(convolved, 1)
                        if m == QK + 1:
                            dve.wait_ge(norms_made, QK)
                            nc.vector.tensor_scalar(norms[:], rows_of(bank[6][:, 0:B * 2 * G], B), 1e-6, None, ALU.add)
                            dve.drain()
                            nc.vector.tensor_scalar(qeps[:], norms[:, :, 0:G], 1e-5 * DK, None, ALU.mult).then_inc(norms_in, 1)
                    dve.wait_ge(norms_ready, 1)
                    rk, bt = norms[:, :, G:2 * G], beta[:, :, heads_of]
                    nc.vector.tensor_tensor(vscale[:], rk, bt, ALU.mult)
                    dve.drain()
                    nc.vector.scalar_tensor_tensor(coef[:], vscale[:], -1.0, rk, ALU.mult, ALU.mult)
                    for b in range(B):
                        dve.wait_ge(gate_kept, b + 1)
                        nc.vector.tensor_tensor(rows_of(gate[:, b, :], G), rows_of(gate[:, b, :], G), bc(w["o_norm"], 1, G),
                                                ALU.mult)

            names = ("keys_staged", "later_staged", "staged", "kk_made", "qk_made", "decay_made", "values_made", "dec_ready",
                     "a_ready", "p_made", "p_ready", "a_turned", "p_turned", "v_ready", "pT_kept", "joined", "v_turned",
                     "w_kept", "join_kept", "grown", "grown_kept", "delta_made", "delta_kept", "o_made", "o_kept",
                     "squares_ready", "var_ready", "rstd_ready", "y_ready", "y_turned", "yT_kept", "out_made", "added",
                     "r_ready")
            (keys_staged, later_staged, staged, kk_made, qk_made, decay_made, values_made, dec_ready, a_ready, p_made,
             p_ready, a_turned, p_turned, v_ready, pT_kept, joined, v_turned, w_kept, join_kept, grown, grown_kept,
             delta_made, delta_kept, o_made, o_kept, squares_ready, var_ready, rstd_ready, y_ready, y_turned, yT_kept,
             out_made, added, r_ready) = (st.sem(f"{x}{hg}") for x in names)

            def level(n, l):
                return done(LEVELS * n + l)

            def four(t, u):
                return t[:, u, :, :]

            def flat(bk):
                return rows_of(bk[:], G)

            def all_steps(engine, step):
                step(0, 0, False, True)
                with engine.Fori(0, B // 2 - 1) as i:
                    step(2 * i + 1, 1, True, True)
                    step(2 * i + 2, 0, True, True)
                step(B - 1, 1, True, False)

            kk, qk, seg, vps = (lambda u, j=j: bank[4 * u + j] for j in range(4))
            with nc.Block() as block:
                @block.gpsimd
                def _(pool):
                    def stage_keys(n, u):
                        pool.wait_ge(qk_made, done(n - 2))
                        nc.gpsimd.tensor_copy(four(qks, u), c[:, 0:QK, n, :])
                        for j in range(2):
                            last = nc.gpsimd.tensor_tensor(kb[:, u, 2 * j:2 * j + 2, :], bc(c[:, 2 + j, n, :], 1, 2),
                                                           bc(g.const["half"], 2, T), ALU.mult)
                        last.then_inc(keys_staged, 1)
                        pool.wait_ge(decay_made, done(n - 2))
                        nc.gpsimd.tensor_tensor(four(later, u), bc(g.const["gt"], 1, G), bc(rate[:, n, heads_of], 2, T),
                                                ALU.mult).then_inc(later_staged, 1)

                    def stage_rest(n, u):
                        pool.wait_ge(a_ready, done(n - 2))
                        nc.gpsimd.tensor_tensor(four(mcoef, u), bc(g.const["gt"], 1, G), bc(coef[:, n, :], 2, T),
                                                ALU.mult)
                        pool.wait_ge(values_made, done(n - 2))
                        nc.gpsimd.tensor_copy(four(vs, u), c[:, QK:8, n, :]).then_inc(staged, 1)

                    def mask_p(n, u):
                        pool.wait_ge(p_made, done(n))
                        nc.gpsimd.tensor_tensor(four(P, u), four(P, u), bc(g.const["ge"], 1, G),
                                                ALU.mult).then_inc(p_ready, 1)

                    def step(n, u, finish, begin):
                        if begin:
                            stage_keys(n + 1, 1 - u)
                        if finish:
                            pool.wait_ge(var_ready, done(n - 1))
                            nc.gpsimd.tensor_tensor(rstd[:, 1 - u, :], ssum[:, 1 - u, :], power[:, 0, 0:G],
                                                    ALU.pow).then_inc(rstd_ready, 1)
                        if begin:
                            stage_rest(n + 1, 1 - u)
                            mask_p(n + 1, 1 - u)

                    credit(pool, keys_staged, later_staged, staged, p_ready, rstd_ready)
                    stage_keys(0, 0)
                    stage_rest(0, 0)
                    mask_p(0, 0)
                    all_steps(pool, step)
                    pool.wait_ge(var_ready, done(B - 1))
                    nc.gpsimd.tensor_tensor(rstd[:, 1, :], ssum[:, 1, :], power[:, 0, 0:G], ALU.pow).then_inc(rstd_ready, 1)

                @block.tensor
                def _(pe):
                    def keys_by_keys(n, u):
                        pe.wait_ge(keys_staged, done(n))
                        pe.wait_ge(w_kept, level(n - 2, LEVELS - 1))
                        for j in range(2):
                            last = nc.tensor.matmul(kk(u)[:, 2 * j * T:2 * (j + 1) * T], qks[:, u, 2 + j, :],
                                                    kb[:, u, 2 * j:2 * j + 2, :], start=True, stop=True)
                        last.then_inc(kk_made, 1)

                    def queries_by_keys(n, u):
                        pe.wait_ge(delta_kept, done(n - 2))
                        for j in range(2):
                            last = nc.tensor.matmul(qk(u)[:, 2 * j * T:2 * (j + 1) * T], qks[:, u, j, :],
                                                    kb[:, u, 2 * j:2 * j + 2, :], start=True, stop=True)
                        last.then_inc(qk_made, 1)

                    def decays(n, u):
                        pe.wait_ge(later_staged, done(n))
                        pe.wait_ge(squares_ready, done(n - 2))
                        nc.tensor.matmul(seg(u)[:], g.const["le"], four(later, u), start=True,
                                         stop=True).then_inc(decay_made, 1)

                    def values(n, u):
                        pe.wait_ge(staged, done(n))
                        pe.wait_ge(added, done(n - 2))
                        for h in range(G):
                            last = nc.tensor.transpose(vps(u)[:, h * DV:(h + 1) * DV], vs[:, u, h, :], g.ident)
                        last.then_inc(values_made, 1)

                    def turn_a(n, u):
                        pe.wait_ge(a_ready, done(n))
                        for h in range(G):
                            last = nc.tensor.transpose(kk(u)[:, h * T:(h + 1) * T], A[:, u, h, :], g.ident)
                        last.then_inc(a_turned, 1)

                    def turn_p(n, u):
                        pe.wait_ge(p_ready, done(n))
                        for h in range(G):
                            last = nc.tensor.transpose(qk(u)[:, h * T:(h + 1) * T], P[:, u, h, :], g.ident)
                        last.then_inc(p_turned, 1)

                    def deltas(n, u):
                        pe.wait_ge(grown_kept, level(n, LEVELS - 1))
                        pe.wait_ge(pT_kept, done(n))
                        pe.wait_ge(r_ready, done(n))
                        for h in range(G):
                            last = nc.tensor.matmul(qk(u)[:, h * DV:(h + 1) * DV], V[:, u, h, :], R[:, u, h, :],
                                                    start=True, stop=True)
                        last.then_inc(delta_made, 1)

                    def outputs(n, u):
                        pe.wait_ge(delta_kept, done(n))
                        for h in range(G):
                            last = nc.tensor.matmul(seg(u)[:, h * DV:(h + 1) * DV], PT[:, u, h, :], delta[:, u, h, :],
                                                    start=True, stop=True)
                        last.then_inc(o_made, 1)

                    def turn_y(n, u):
                        pe.wait_ge(y_ready, done(n))
                        for h in range(G):
                            last = nc.tensor.transpose(vps(u)[:, h * T:(h + 1) * T], y[:, u, h, :], g.ident)
                        last.then_inc(y_turned, 1)

                    def project(n, u):
                        pe.wait_ge(yT_kept, done(n))
                        for h in range(G):
                            at = (hg * G + h) * D
                            last = nc.tensor.matmul(vps(u)[:, 0:D], yT[:, u, h, :], w["wo"][:, at:at + D],
                                                    start=(h == 0), stop=(h == G - 1))
                        last.then_inc(out_made, 1)

                    def step(n, u, finish, begin):
                        gaps = [(deltas, outputs), (keys_by_keys, queries_by_keys), (decays, turn_y), (project, None),
                                (values, turn_a), (turn_p, None)]

                        def fill(part):
                            if finish and part in (deltas, outputs, turn_y, project):
                                part(n - 1, 1 - u)
                            if begin and part in (keys_by_keys, queries_by_keys, decays, values, turn_a, turn_p):
                                part(n + 1, 1 - u)

                        for l in range(LEVELS):
                            if l == 0:
                                pe.wait_ge(v_ready, done(n))
                            else:
                                pe.wait_ge(grown_kept, level(n, l - 1))
                            for h in range(G):
                                last = nc.tensor.matmul(seg(u)[:, h * T:(h + 1) * T], A[:, u, h, :], V[:, u, h, :],
                                                        start=True, stop=True)
                            last.then_inc(joined, 1)
                            for h in range(G):
                                last = nc.tensor.transpose(kk(u)[:, h * T:(h + 1) * T], V[:, u, h, :], g.ident)
                            last.then_inc(v_turned, 1)
                            fill(gaps[l][0])
                            pe.wait_ge(w_kept, level(n, l))
                            pe.wait_ge(join_kept, level(n, l))
                            for h in range(G):
                                last = nc.tensor.matmul(vps(u)[:, h * T:(h + 1) * T], W[:, u, h, :], join[:, u, h, :],
                                                        start=True, stop=True)
                            last.then_inc(grown, 1)
                            fill(gaps[l][1])

                    credit(pe, kk_made, qk_made, decay_made, values_made, a_turned, p_turned, joined, v_turned, grown,
                           delta_made, o_made, y_turned, out_made)
                    for part in (keys_by_keys, queries_by_keys, decays, values, turn_a, turn_p):
                        part(0, 0)
                    all_steps(pe, step)
                    for part in (deltas, outputs, turn_y, project):
                        part(B - 1, 1)

                @block.scalar
                def _(act):
                    def keep(ready, dst, src, kept, n, u):
                        act.wait_ge(ready, done(n))
                        nc.scalar.activation(four(dst, u), flat(src(u)), ACT.Copy).then_inc(kept, 1)

                    def exp_decays(n, u):
                        act.wait_ge(decay_made, done(n))
                        act.wait_ge(y_ready, done(n - 2))
                        nc.scalar.activation(four(dec, u), flat(seg(u)), ACT.Exp).then_inc(dec_ready, 1)

                    def square(n, u):
                        nc.scalar.activation(four(osq, u), flat(seg(u)), ACT.Square).then_inc(squares_ready, 1)

                    def step(n, u, finish, begin):
                        def keep_w(l):
                            act.wait_ge(v_turned, level(n, l))
                            nc.scalar.activation(four(W, u), flat(kk(u)), ACT.Copy).then_inc(w_kept, 1)

                        keep_w(0)
                        if finish:
                            keep(delta_made, delta, qk, delta_kept, n - 1, 1 - u)
                            keep(o_made, o, seg, o_kept, n - 1, 1 - u)
                            square(n - 1, 1 - u)
                        keep_w(1)
                        keep_w(2)
                        if begin:
                            exp_decays(n + 1, 1 - u)
                        if finish:
                            keep(y_turned, yT, vps, yT_kept, n - 1, 1 - u)
                        keep_w(3)
                        keep_w(4)
                        keep_w(5)
                        if begin:
                            keep(p_turned, PT, qk, pT_kept, n + 1, 1 - u)

                    credit(act, dec_ready, pT_kept, w_kept, delta_kept, o_kept, squares_ready, yT_kept)
                    exp_decays(0, 0)
                    keep(p_turned, PT, qk, pT_kept, 0, 0)
                    all_steps(act, step)
                    keep(delta_made, delta, qk, delta_kept, B - 1, 1)
                    keep(o_made, o, seg, o_kept, B - 1, 1)
                    square(B - 1, 1)
                    keep(y_turned, yT, vps, yT_kept, B - 1, 1)

                @block.vector
                def _(dve):
                    def square_sums(n, u):
                        dve.wait_ge(squares_ready, done(n))
                        nc.vector.tensor_reduce(ssum[:, u, :], four(osq, u), X, ALU.add)
                        dve.drain()
                        nc.vector.scalar_tensor_tensor(ssum[:, u, :], ssum[:, u, :], 1.0 / DV, qeps[:, n, :], ALU.mult,
                                                       ALU.add).then_inc(var_ready, 1)

                    def gate_outputs(n, u):
                        dve.wait_ge(o_kept, done(n))
                        nc.vector.tensor_tensor(four(y, u), four(o, u), rows_of(gate[:, n, :], G), ALU.mult)

                    def norm_outputs(n, u):
                        dve.drain()
                        dve.wait_ge(rstd_ready, done(n))
                        nc.vector.tensor_tensor(four(y, u), four(y, u), bc(rstd[:, u, :], 2, DV), ALU.mult).then_inc(y_ready, 1)

                    def add_outputs(n, u):
                        dve.wait_ge(out_made, done(n))
                        nc.vector.tensor_tensor(g.x[:, n, :], g.x[:, n, :], vps(u)[:, 0:D], ALU.add).then_inc(added, 1)

                    def decayed_keys(n, u):
                        dve.wait_ge(kk_made, done(n))
                        dve.wait_ge(dec_ready, done(n))
                        nc.vector.tensor_tensor(four(A, u), flat(kk(u)), four(dec, u), ALU.mult)

                    def scale_a(n, u):
                        dve.drain()
                        dve.wait_ge(staged, done(n))
                        nc.vector.tensor_tensor(four(A, u), four(A, u), four(mcoef, u), ALU.mult).then_inc(a_ready, 1)

                    def decayed_scores(n, u):
                        dve.wait_ge(qk_made, done(n))
                        nc.vector.tensor_tensor(four(P, u), flat(qk(u)), four(dec, u), ALU.mult).then_inc(p_made, 1)

                    def scale_values(n, u):
                        dve.wait_ge(values_made, done(n))
                        nc.vector.tensor_tensor(four(R, u), flat(vps(u)), bc(vscale[:, n, :], 2, DV),
                                                ALU.mult).then_inc(r_ready, 1)

                    def first_blocks(n, u):
                        dve.wait_ge(a_turned, done(n))
                        nc.vector.tensor_tensor(four(V, u), flat(kk(u)), bc(g.const["join0"], 1, G), ALU.mult)
                        dve.drain()
                        nc.vector.tensor_tensor(four(V, u), four(V, u), bc(g.ident, 1, G), ALU.add).then_inc(v_ready, 1)

                    def step(n, u, finish, begin):
                        def keep_join(l):
                            dve.wait_ge(joined, level(n, l))
                            nc.vector.tensor_tensor(four(join, u), flat(seg(u)), bc(g.const[f"join{l + 1}"], 1, G),
                                                    ALU.mult).then_inc(join_kept, 1)

                        def grow(l):
                            dve.wait_ge(grown, level(n, l))
                            nc.vector.tensor_tensor(four(V, u), four(V, u), flat(vps(u)), ALU.add).then_inc(grown_kept, 1)

                        keep_join(0)
                        grow(0)
                        keep_join(1)
                        if finish:
                            square_sums(n - 1, 1 - u)
                        grow(1)
                        if finish:
                            gate_outputs(n - 1, 1 - u)
                        keep_join(2)
                        if finish:
                            norm_outputs(n - 1, 1 - u)
                        grow(2)
                        keep_join(3)
                        if begin:
                            decayed_keys(n + 1, 1 - u)
                        grow(3)
                        if finish:
                            add_outputs(n - 1, 1 - u)
                        if begin:
                            scale_a(n + 1, 1 - u)
                        keep_join(4)
                        if begin:
                            decayed_scores(n + 1, 1 - u)
                        grow(4)
                        if begin:
                            scale_values(n + 1, 1 - u)
                        keep_join(5)
                        if begin:
                            first_blocks(n + 1, 1 - u)
                        grow(5)

                    credit(dve, a_ready, p_made, v_ready, r_ready, join_kept, grown_kept, var_ready, y_ready, added)
                    decayed_keys(0, 0)
                    scale_a(0, 0)
                    decayed_scores(0, 0)
                    first_blocks(0, 0)
                    scale_values(0, 0)
                    all_steps(dve, step)
                    square_sums(B - 1, 1)
                    gate_outputs(B - 1, 1)
                    norm_outputs(B - 1, 1)
                    add_outputs(B - 1, 1)


STAGES = [
    ("L0_attn", multi_query_attention), ("L0_xattn", attention_with_mlp), ("L0_ffn", ternary_ffn),
    ("L1_attn", state_space), ("L1_xattn", cross_attention), ("L1_ffn", gated_experts),
    ("L2_attn", delta_rule), ("L2_xattn", cross_attention), ("L2_ffn", many_experts),
    ("L3_attn", time_mix), ("L3_xattn", masked_cross_attention), ("L3_ffn", wide_experts),
]



def build(nc, dram, out, layouts, first=0, last=12):
    g = Net()
    g.dram = dram
    g.bank = [nc.alloc_psum_tensor(f"bank{n}", [128, HALF], F32) for n in range(8)]
    g.bank_bf = [t[:].bitcast(BF16) for t in g.bank]
    sb = nc.alloc_sbuf_tensor
    g.x, g.h = sb("x", [T, B, D], F32), sb("h", [T, B, D], F32)
    g.hT, g.ctxT = sb("hT", [D, TOK], F32), sb("ctxT", [D, TOK], F32)
    g.ident_bf = sb("ident_bf", [T, T], BF16)
    g.causal_bf, g.shifted_bf = sb("causal_bf", [T, 1, T], BF16), sb("shifted_bf", [T, 1, T], BF16)
    x_loaded, stored = nc.alloc_semaphore("x_loaded"), nc.alloc_semaphore("stored")
    g.x_loaded = x_loaded

    g.region_a = sb("region_a", [128, max(layouts[n][1] for n in ("L1_ffn", "L2_ffn"))], F32)
    first_b = ("L0_attn", "L0_xattn", "L0_ffn")
    g.region_b = sb("region_b", [128, max(sum(layouts[n][1] for n in first_b), layouts["L2_attn"][1],
                                          layouts["L3_ffn"][1])], F32)

    def place(name):
        places, cols = layouts[name]
        if name in ("L1_ffn", "L2_ffn"):
            tile = g.region_a[:, 0:cols]
        elif name in ("L2_attn", "L3_ffn"):
            tile = g.region_b[:, 0:cols]
        elif name in first_b:
            at = sum(layouts[n][1] for n in first_b[:first_b.index(name)])
            tile = g.region_b[:, at:at + cols]
        else:
            tile = sb(f"w_{name}", [128, cols], F32)[:]
        return Pack(tile, places, nc.alloc_semaphore(f"{name}_loaded"))

    g.const = place("const")
    run = STAGES[first:last]
    packs = {name: place(name) for name, _ in run}
    late = {"L1_attn": ["L2_attn"], "L2_xattn": ["L2_ffn", "L3_ffn"]}
    late = {at: [n for n in names if n in packs] if at in packs else [] for at, names in late.items()}
    g.ident = g.const["ident"]
    with nc.Block() as block:
        @block.sync
        def _(sp):
            sp.dma_start(g.const.tile, dram["const"]).then_inc(g.const.loaded, 16)
            sp.dma_start(g.x[:], dram["x"].rearrange("b t d -> t b d")).then_inc(x_loaded, 16)
            for name, _ in run:
                if not any(name in names for names in late.values()):
                    sp.dma_start(packs[name].tile, dram[name]).then_inc(packs[name].loaded, 16)
    turn_context(nc, g)
    for name, stage in run:
        layer_norm(nc, g, name + "_norm", [(packs[n], dram[n]) for n in late.get(name, [])])
        stage(nc, g, packs[name], name)
    with nc.Block() as block:
        @block.sync
        def _(sp):
            sp.dma_start(out.rearrange("b t d -> t b d"), g.x[:]).then_inc(stored, 16)
            sp.wait_ge(stored, 16)



def constants():
    r, c = np.arange(128)[:, None], np.arange(128)[None, :]
    f = np.float32
    return [
        ("ident", np.eye(128, dtype=f)),
        ("head", (r // HD == np.arange(H)[None, :]).astype(f)),
        ("half", (r // 64 == np.arange(2)[None, :]).astype(f)),
        ("neg_causal", np.where(c <= r, 0.0, NEG).astype(f)),
        ("neg_shifted", np.where((c < r) | ((c == 0) & (r == 0)), 0.0, NEG).astype(f)),
        ("le", (r <= c).astype(f)),
        ("gt", (r > c).astype(f)),
        ("lt", (r < c).astype(f)),
        ("ge", (r >= c).astype(f)),
        *[(f"join{l}", (r >> l + 1 == c >> l + 1).astype(f) * (r >> l < c >> l)) for l in range(7)],
        ("low0", ((r >> 1 == c >> 1) & (r > c)).astype(f)),
        ("steps", np.maximum(c - r - 1, 0).astype(f)),
        ("ones", np.ones((128, 128), f)),
    ]


def packed(pieces):
    places, at = {}, 0
    for name, a in pieces:
        places[name] = (at, a.shape[0], a.shape[1])
        at += a.shape[1]
    whole = np.zeros((128, at), np.float32)
    for name, a in pieces:
        whole[:a.shape[0], places[name][0]:places[name][0] + a.shape[1]] = a
    return whole, (places, at)


def every_row(v, rows=128):
    return np.repeat(np.asarray(v).reshape(1, -1), rows, 0)


def side_by_side(a):
    return np.ascontiguousarray(np.asarray(a).transpose(1, 0, 2)).reshape(a.shape[1], -1)


def column_tiles(a, p=128):
    a = np.asarray(a)
    return side_by_side(a.reshape(-1, p, a.shape[1]))


def column(v):
    return np.asarray(v).reshape(-1, 1)


def attention_pieces(weights, biases=None):
    pieces = [(n, np.ascontiguousarray(a.T)) for n, a in zip(("wq", "wk", "wv", "wo"), weights)]
    if biases is None:
        zeros = np.zeros(D, np.float32)
        return pieces + [("bq", column(zeros)), ("bk", column(zeros)), ("bv", every_row(zeros))]
    bq, bk, bv, bo = biases
    return pieces + [("bq", column(bq)), ("bk", column(bk)), ("bv", every_row(bv)), ("bo", every_row(bo))]


def state_space_pieces(i):
    w_in, conv_w, conv_b = i["L1_attn_in_proj_w"], i["L1_attn_conv_w"], i["L1_attn_conv_b"]
    parts = ((0, 128), (128, 256), (256, 320), (320, 384))
    taps, shift = np.zeros((128, 4, 4), np.float32), np.zeros((128, 4), np.float32)
    for j, (lo, hi) in enumerate(parts):
        taps[:hi - lo, j] = conv_w[lo:hi]
        shift[:hi - lo, j] = conv_b[lo:hi]
    return [("w_z", w_in[0:256].T), ("w_conv", w_in[256:640].T), ("w_dt", w_in[640:644].T),
            ("conv_w", taps.reshape(128, 16)), ("conv_b", shift),
            ("init", i["L1_attn_init_states"].transpose(2, 0, 1).reshape(64, 256)),
            ("dt_bias", every_row(i["L1_attn_dt_bias"])), ("a_log", every_row(i["L1_attn_A_log"])),
            ("skip", every_row(i["L1_attn_D"])), ("norm_w", every_row(i["L1_attn_norm_w"])),
            ("w_out", column_tiles(i["L1_attn_out_proj_w"].T))]


def pieces_of(i):
    null = i["L0_attn_null_kv"]
    null2 = np.zeros((128, 2), np.float32)
    null2[:64, 0] = null
    null2[64:, 1] = null
    return {
        "const": constants(),
        "L0_attn": [("wq", i["L0_attn_Wq"]), ("wkv2", np.concatenate([i["L0_attn_Wkv"]] * 2, 1)),
                    ("wout", column_tiles(i["L0_attn_Wout"])), ("null2", null2),
                    ("wqT", column_tiles(i["L0_attn_Wq"].T)), ("null_row", every_row(np.append(null, np.float32(1))))],
        "L0_xattn": [("wq", i["L0_xattn_Wq"]), ("wk", i["L0_xattn_Wk"]), ("wv", i["L0_xattn_Wv"]),
                     ("bq", column(i["L0_xattn_bq"])), ("bk", column(i["L0_xattn_bk"])),
                     ("bv", every_row(i["L0_xattn_bv"])), ("w1", i["L0_xattn_W1"]),
                     ("b1", i["L0_xattn_b1"].reshape(4, 128).T), ("w2", column_tiles(i["L0_xattn_W2"])),
                     ("b2", every_row(i["L0_xattn_b2"]))],
        "L1_attn": state_space_pieces(i),
        "L2_attn": [("w" + c.lower(), i["L2_attn_W" + c]) for c in "qkvg"]
                   + [("conv_" + c, column_tiles(i["L2_attn_conv_" + c])) for c in "qkv"]
                   + [("wo", column_tiles(i["L2_attn_Wo"])), ("w_rate", i["L2_attn_Wgk"]), ("w_beta", i["L2_attn_Wb"]),
                      ("b_b", every_row(i["L2_attn_b_b"])), ("a_log", every_row(i["L2_attn_A_log"])),
                      ("dt_bias", every_row(i["L2_attn_dt_bias"])), ("o_norm", every_row(i["L2_attn_g_norm_weight"]))],
        "L0_ffn": [("gate", i["L0_ffn_w_gate"].T), ("up", i["L0_ffn_w_up"].T),
                   ("down", column_tiles(i["L0_ffn_w_down"].T))],
        "L3_attn": [("w_" + c, i[f"L3_attn_w_{c}"].T) for c in "rkvgo"]
                   + [("maa_" + c, column(i[f"L3_attn_time_maa_{c}"])) for c in "rkvg"]
                   + [("decay", every_row(i["L3_attn_time_decay"])), ("bonus", every_row(i["L3_attn_time_faaaa"])),
                      ("ln_g", every_row(i["L3_attn_ln_g"])), ("ln_b", every_row(i["L3_attn_ln_b"]))],
        "L1_ffn": [("router", i["L1_ffn_router_w"]), ("router_scale", column(i["L1_ffn_router_scale"])),
                   ("expert_scale", every_row(i["L1_ffn_per_expert_scale"])),
                   ("up", i["L1_ffn_gating_w"].transpose(3, 0, 1, 2).reshape(D, -1)),
                   ("down", column_tiles(i["L1_ffn_linear_w"].reshape(-1, D)))],
        "L2_ffn": [("router", i["L2_ffn_router_w"].T), ("correction", every_row(i["L2_ffn_correction_bias"])),
                   ("up", np.concatenate([side_by_side(i["L2_ffn_up_w"]), i["L2_ffn_shared_up_w"]], 1)),
                   ("down", np.concatenate([column_tiles(i["L2_ffn_down_w"].reshape(-1, D)),
                                            column_tiles(i["L2_ffn_shared_down_w"])], 1))],
        "L3_ffn": [("router", i["L3_ffn_Wr"]), ("br", every_row(i["L3_ffn_br"])), ("b2", i["L3_ffn_b2"]),
                   ("up", side_by_side(i["L3_ffn_W1"])), ("b1", every_row(i["L3_ffn_b1"])),
                   ("down", column_tiles(i["L3_ffn_W2"].reshape(-1, D)))],
        "L1_xattn": attention_pieces([i[f"L1_xattn_w{c}_w"] for c in "qkvo"], [i[f"L1_xattn_w{c}_b"] for c in "qkvo"]),
        "L2_xattn": attention_pieces([i[f"L2_xattn_w_{c}"] for c in "qkvo"], [i[f"L2_xattn_b_{c}"] for c in "qkvo"]),
        "L3_xattn": attention_pieces([i[f"L3_xattn_W{c}"] for c in "qkvo"]),
    }


def laid_out(inputs):
    inputs = {k: np.asarray(v) for k, v in inputs.items()}
    arrays, layouts = {}, {}
    for name, pieces in pieces_of(inputs).items():
        arrays[name], layouts[name] = packed(pieces)
    arrays["x"] = np.ascontiguousarray(inputs["x"])
    arrays["ctx_1024"] = np.ascontiguousarray(inputs["ctx_1024"])
    arrays["mask"] = np.ascontiguousarray(inputs["mask_BxSxS2_bf0"])
    return arrays, layouts


def program(nc, arrays, layouts, first=0, last=12):
    dram = {k: nc.dram_tensor(f"in_{k}", a.shape, mybir.dt.from_np(a.dtype), kind="ExternalInput").ap()
            for k, a in arrays.items()}
    out = nc.dram_tensor("out", (B, T, D), F32, kind="ExternalOutput").ap()
    build(nc, dram, out, layouts, first, last)


def kernel(**inputs):
    import concourse.bacc as bacc
    from concourse.bass_utils import run_bass_kernel_spmd

    nc = bacc.Bacc("TRN2", target_bir_lowering=False, num_devices=1)
    arrays, layouts = laid_out(inputs)
    program(nc, arrays, layouts)
    r = run_bass_kernel_spmd(nc, [{f"in_{k}": a for k, a in arrays.items()}], core_ids=[0])
    return r.results[0]["out"]
```

```python
import numpy as np

import concourse.bass as bass
from concourse import mybir

F32 = mybir.dt.float32
BF16 = mybir.dt.bfloat16
U8 = mybir.dt.uint8
ALU = mybir.AluOpType
ACT = mybir.ActivationFunctionType
X = mybir.AxisListType.X

B, T, D = 8, 128, 128
H, HD = 16, 8
TOK = B * T
HALF = 512
NEG = -1.0e30
ROUND = 1.5 * 2.0 ** 23
CREDIT = 24


def done(m):
    return m + 1 + CREDIT


def credit(engine, *sems):
    for s in sems:
        engine.sem_inc(s, CREDIT)


def pipeline(engine, step, per, lag, units=None):
    units = B // 2 * per if units is None else units
    rounds = (units - lag) // per
    for r in range(lag):
        step(0, r)
    with engine.Fori(0, rounds) as i:
        for r in range(lag, lag + per):
            step(i, r)
    for r in range(lag, lag + units - per * rounds):
        step(rounds, r)


def has_unit(i, r, back, per, units=None):
    units = B // 2 * per if units is None else units
    return not isinstance(i, int) or 0 <= per * i + r - back < units


class Stage:

    def __init__(self, nc, name):
        self.nc, self.name = nc, name
        self.scope = nc.cleanup_on_exit()

    def __enter__(self):
        self.scope.__enter__()
        return self

    def __exit__(self, *exc):
        self.scope.__exit__(*exc)
        self.nc.all_engine_barrier()

    def sb(self, name, shape, dtype=F32):
        return self.nc.alloc_sbuf_tensor(f"{self.name}_{name}", shape, dtype)

    def sem(self, name):
        return self.nc.alloc_semaphore(f"{self.name}_{name}")


class Pack:

    def __init__(self, tile, places, loaded):
        self.tile, self.places, self.loaded = tile, places, loaded

    def __getitem__(self, name):
        at, rows, cols = self.places[name]
        return self.tile[0:rows, at:at + cols]


class Net:
    pass


def bc(ap, axis, n):
    a = ap.unsqueeze(axis)
    shape = list(a.shape)
    shape[axis] = n
    return a.to_broadcast(shape)


def rows_of(ap, n):
    return ap.rearrange("p (a b) -> p a b", a=n)


def layer_norm(nc, g, st, loads, awaited, beside, eps=1e-5):
    total, mean, sq, sumsq, var, rstd, power = g.norm_scratch
    centered, squared, var_ready, rstd_ready, h_ready, turned, power_set = (
        st.sem("norm_" + s) for s in ("centered", "squared", "var_ready", "rstd_ready", "h_ready", "turned", "power_set"))
    x, h, hT = g.x, g.h, g.hT
    halves = [slice(4 * half, 4 * half + 4) for half in range(2)]

    with nc.Block() as block:
        @block.sync
        def _(sp):
            for pack, source in loads:
                sp.dma_start(pack.tile, source).then_inc(pack.loaded, 16)
            for pack in awaited:
                sp.wait_ge(pack.loaded, 16)

        @block.vector
        def _(dve):
            for b in halves:
                nc.vector.tensor_reduce(total[:, b], x[:, b, :], X, ALU.add)
                dve.drain()
                nc.vector.tensor_scalar(mean[:, b], total[:, b], 1.0 / D, None, ALU.mult)
                dve.drain()
                nc.vector.tensor_tensor(h[:, b, :], x[:, b, :], bc(mean[:, b], 2, D), ALU.subtract).then_inc(centered, 1)
            for half, b in enumerate(halves):
                dve.wait_ge(squared, half + 1)
                nc.vector.tensor_reduce(sumsq[:, b], sq[:, b, :], X, ALU.add)
                dve.drain()
                nc.vector.tensor_scalar(var[:, b], sumsq[:, b], 1.0 / D, eps, ALU.mult, ALU.add).then_inc(var_ready, 1)
            for half, b in enumerate(halves):
                dve.wait_ge(rstd_ready, half + 1)
                nc.vector.tensor_tensor(h[:, b, :], h[:, b, :], bc(rstd[:, b], 2, D), ALU.mult).then_inc(h_ready, 1)
            beside.vector(dve)

        @block.gpsimd
        def _(pool):
            beside.gpsimd(pool)
            nc.gpsimd.memset(power[:], -0.5).then_inc(power_set, 1)
            pool.wait_ge(power_set, 1)
            for half, b in enumerate(halves):
                pool.wait_ge(var_ready, half + 1)
                nc.gpsimd.tensor_tensor(rstd[:, b], var[:, b], power[:, b], ALU.pow).then_inc(rstd_ready, 1)

        @block.tensor
        def _(pe):
            beside.tensor(pe)
            for half in range(2):
                pe.wait_ge(h_ready, half + 1)
                for j in range(4):
                    last = nc.tensor.transpose(g.bank[half][:, j * T:(j + 1) * T], h[:, 4 * half + j, :], g.ident)
                last.then_inc(turned, 1)

        @block.scalar
        def _(act):
            for half, b in enumerate(halves):
                act.wait_ge(centered, half + 1)
                nc.scalar.activation(sq[:, b, :], h[:, b, :], ACT.Square).then_inc(squared, 1)
            beside.scalar(act)
            for half in range(2):
                act.wait_ge(turned, half + 1)
                nc.scalar.activation(hT[:, half * HALF:(half + 1) * HALF], g.bank[half][:], ACT.Copy)


def turn_context(nc, g, loads):
    with Stage(nc, "context") as st:
        ctx = st.sb("ctx", [T, B, D])
        loaded, turned = st.sem("loaded"), st.sem("turned")
        with nc.Block() as block:
            @block.sync
            def _(sp):
                sp.dma_start(g.const.tile, g.dram["const"]).then_inc(g.const.loaded, 16)
                sp.dma_start(g.x[:], g.dram["x"].rearrange("b t d -> t b d")).then_inc(g.x_loaded, 16)
                sp.dma_start(ctx[:], g.dram["ctx_1024"].rearrange("b t d -> t b d")).then_inc(loaded, 16)
                for pack, source in loads:
                    sp.dma_start(pack.tile, source).then_inc(pack.loaded, 16)

            @block.tensor
            def _(pe):
                pe.wait_ge(g.const.loaded, 16)
                pe.wait_ge(loaded, 16)
                for half in range(2):
                    for j in range(4):
                        last = nc.tensor.transpose(g.bank[half][:, j * T:(j + 1) * T], ctx[:, 4 * half + j, :], g.ident)
                    last.then_inc(turned, 1)

            @block.scalar
            def _(act):
                for half in range(2):
                    act.wait_ge(turned, half + 1)
                    nc.scalar.activation(g.ctxT[:, half * HALF:(half + 1) * HALF], g.bank[half][:], ACT.Copy)

            @block.vector
            def _(dve):
                dve.wait_ge(g.const.loaded, 16)
                dve.wait_ge(g.x_loaded, 16)
                nc.vector.tensor_copy(g.ident_bf[:], g.ident)
                nc.vector.tensor_copy(g.causal_bf[:, 0, :], g.const["neg_causal"])
                nc.vector.tensor_copy(g.shifted_bf[:, 0, :], g.const["neg_shifted"])



def multi_query_attention(nc, g, w, st):
    NH, DH, Q = 16, 64, 4
    UN = NH // Q
    SCALE = DH ** -0.5
    qT = st.sb("qT", [128, NH // 2, TOK])
    kvT = st.sb("kvT", [128, TOK])
    kv = st.sb("kv", [T, B, DH + 1])
    qs, kvs = st.sb("qs", [128, 2, NH // 2, T]), st.sb("kvs", [128, 2, 2, T])
    top, top0 = st.sb("top", [T, 2, Q]), st.sb("top0", [T, 2, Q])
    p = st.sb("p", [T, 2, Q * T + Q])
    pT = st.sb("pT", [T, 2, Q * T])
    null_q, null_score = st.sb("null_q", [D, NH]), st.sb("null_score", [T, B, NH])
    null_part, sums = st.sb("null_part", [T, 2, Q, DH + 1]), st.sb("sums", [T, 2, Q, DH + 1])
    inv, o = st.sb("inv", [T, 2, Q]), st.sb("o", [T, 2, Q * DH])
    oT = st.sb("oT", [128, 2, 2, T])
    proj, kept_even, kept_odd, kv_made, null_made, null_kept = (
        st.sem(s) for s in ("proj", "kept_even", "kept_odd", "kv_made", "null_made", "null_kept"))
    names = ("staged", "staged_too", "whole", "scored", "centered", "exped", "turned", "pT_kept", "mixed", "normed", "o_turned",
             "oT_kept", "projected", "added", "null_weighed")
    staged, staged_too, whole, scored, centered, exped, turned, pT_kept, mixed, normed, o_turned, oT_kept, projected, added, null_weighed = (
        st.sem(s) for s in names)
    bank = g.bank

    with nc.Block() as block:
        @block.gpsimd
        def _(pool):
            nc.gpsimd.memset(kv[:, :, DH:DH + 1], 1.0)

        @block.tensor
        def _(pe):
            pe.wait_ge(w.loaded, 16)
            for m in range(2 * (NH // 2 + 1)):
                j, half = m // 2, m % 2
                if m >= 6:
                    pe.wait_ge(kept_odd if m % 2 else kept_even, (m - 6) // 2 + 1)
                lhsT = w["wq"][:, j * 128:(j + 1) * 128] if j < NH // 2 else w["wkv2"]
                nc.tensor.matmul(bank[m % 6][:], lhsT, g.hT[:, half * HALF:(half + 1) * HALF],
                                 start=True, stop=True).then_inc(proj, 1)
            for b in range(B):
                last = nc.tensor.matmul(bank[6][:, b * DH:(b + 1) * DH], g.hT[:, b * T:(b + 1) * T],
                                        w["wkv2"][:, 0:DH], start=True, stop=True)
            last.then_inc(kv_made, 1)
            for j in range(NH // 2):
                last = nc.tensor.matmul(bank[7][:, 2 * j:2 * j + 2], w["wqT"][:, j * D:(j + 1) * D], w["null2"],
                                        start=True, stop=True)
            last.then_inc(null_made, 1)
            pe.wait_ge(null_kept, 1)
            for b in range(B):
                last = nc.tensor.matmul(bank[7][:, b * NH:(b + 1) * NH], g.hT[:, b * T:(b + 1) * T], null_q[:],
                                        start=True, stop=True)
            last.then_inc(null_made, 1)

        @block.scalar
        def _(act):
            for m in range(0, 2 * (NH // 2 + 1), 2):
                act.wait_ge(proj, m + 1)
                dst = qT[:, m // 2, :] if m // 2 < NH // 2 else kvT[:]
                nc.scalar.activation(dst[:, 0:HALF], bank[m % 6][:], ACT.Copy).then_inc(kept_even, 1)

        @block.vector
        def _(dve):
            for m in range(1, 2 * (NH // 2 + 1), 2):
                dve.wait_ge(proj, m + 1)
                dst = qT[:, m // 2, :] if m // 2 < NH // 2 else kvT[:]
                nc.vector.tensor_copy(dst[:, HALF:TOK], bank[m % 6][:]).then_inc(kept_odd, 1)
            dve.wait_ge(kv_made, 1)
            nc.vector.tensor_copy(kv[:, :, 0:DH], rows_of(bank[6][:], B))
            dve.wait_ge(null_made, 1)
            nc.vector.tensor_copy(null_q[:], bank[7][:, 0:NH]).then_inc(null_kept, 1)
            dve.wait_ge(null_made, 2)
            nc.vector.tensor_copy(null_score[:], rows_of(bank[7][:, 0:B * NH], B))

    score, tps, mix, o_tps, outp = bank[0:2], bank[2:4], bank[4:6], bank[6][:, 0:2 * T], bank[7]
    PER, LAG = 2 * UN, 6

    def unit_of(i, k):
        return PER * i + k, 2 * i + k // UN, k // UN % 2, k % UN, k % 2

    with nc.Block() as block:
        @block.gpsimd
        def _(pool):
            def stage(n, u):
                pool.wait_ge(scored, done(UN * (n - 2) + UN - 1))
                nc.gpsimd.tensor_tensor(kvs[:, u, :, :], bc(kvT[:, bass.ds(n * T, T)], 1, 2),
                                        bc(g.const["half"], 2, T), ALU.mult)
                nc.gpsimd.tensor_copy(qs[:, u, 0:NH // 4, :], qT[:, 0:NH // 4, bass.ds(n * T, T)]).then_inc(staged, 1)

            def step(i, r):
                if has_unit(i, r, -2, PER) and (r + 2) % UN == 0:
                    m, n, u, q, e = unit_of(i, r + 2)
                    stage(n, u)
                if has_unit(i, r, 2, PER):
                    m, n, u, q, e = unit_of(i, r - 2)
                    pool.wait_ge(exped, done(m))
                    pool.wait_ge(whole, done(m - 2))
                    nc.gpsimd.tensor_tensor(null_part[:, e, :, :], bc(p[:, e, Q * T:], 2, DH + 1),
                                            bc(w["null_row"], 1, Q), ALU.mult).then_inc(null_weighed, 1)

            credit(pool, staged, null_weighed)
            stage(0, 0)
            pipeline(pool, step, PER, LAG)

        @block.tensor
        def _(pe):
            def step(i, r):
                if has_unit(i, r, 0, PER):
                    m, n, u, q, e = unit_of(i, r)
                    if q == 0:
                        pe.wait_ge(staged, done(n))
                        pe.wait_ge(staged_too, done(n))
                    pe.wait_ge(centered, done(m - 2))
                    for j in range(Q // 2):
                        cols = score[e][:, 2 * j * T:2 * (j + 1) * T]
                        nc.tensor.matmul(cols, g.ident_bf[:], bc(g.causal_bf[:, 0, :], 1, 2),
                                         start=True, stop=False)
                        last = nc.tensor.matmul(cols, qs[:, u, q * 2 + j, :], kvs[:, u, :, :],
                                                start=False, stop=True)
                    last.then_inc(scored, 1)
                if has_unit(i, r, 2, PER):
                    m, n, u, q, e = unit_of(i, r - 2)
                    pe.wait_ge(exped, done(m))
                    pe.wait_ge(pT_kept, done(m - 2))
                    for j in range(Q):
                        last = nc.tensor.transpose(tps[e][:, j * T:(j + 1) * T], p[:, e, j * T:(j + 1) * T], g.ident)
                    last.then_inc(turned, 1)
                if has_unit(i, r, 3, PER):
                    m, n, u, q, e = unit_of(i, r - 3)
                    pe.wait_ge(pT_kept, done(m))
                    pe.wait_ge(whole, done(m - 2))
                    for j in range(Q):
                        last = nc.tensor.matmul(mix[e][:, j * (DH + 1):(j + 1) * (DH + 1)], pT[:, e, j * T:(j + 1) * T],
                                                kv[:, n, :], start=True, stop=True)
                    last.then_inc(mixed, 1)
                if has_unit(i, r, 5, PER):
                    m, n, u, q, e = unit_of(i, r - 5)
                    if q == 0:
                        pe.wait_ge(added, done(n - 1))
                    pe.wait_ge(oT_kept, done(m))
                    for j in range(2):
                        last = nc.tensor.matmul(outp[:, 0:D], oT[:, e, j, :],
                                                w["wout"][:, (2 * q + j) * D:(2 * q + j + 1) * D],
                                                start=(q == 0 and j == 0), stop=(q == UN - 1 and j == 1))
                    last.then_inc(projected, 1)
                if has_unit(i, r, 4, PER):
                    m, n, u, q, e = unit_of(i, r - 4)
                    pe.wait_ge(normed, done(m))
                    pe.wait_ge(oT_kept, done(m - 1))
                    for j in range(2):
                        last = nc.tensor.transpose(o_tps[:, j * T:(j + 1) * T], o[:, e, j * T:(j + 1) * T], g.ident)
                    last.then_inc(o_turned, 1)

            credit(pe, scored, turned, mixed, o_turned, projected)
            pipeline(pe, step, PER, LAG)

        @block.scalar
        def _(act):
            def stage(n, u):
                act.wait_ge(scored, done(UN * (n - 2) + UN - 1))
                nc.scalar.activation(qs[:, u, NH // 4:, :], qT[:, NH // 4:, bass.ds(n * T, T)],
                                     ACT.Copy).then_inc(staged_too, 1)

            def step(i, r):
                if has_unit(i, r, -2, PER) and (r + 2) % UN == 0:
                    m, n, u, q, e = unit_of(i, r + 2)
                    stage(n, u)
                if has_unit(i, r, 2, PER):
                    m, n, u, q, e = unit_of(i, r - 2)
                    act.wait_ge(turned, done(m))
                    act.wait_ge(mixed, done(m - 2))
                    nc.scalar.activation(pT[:, e, :], tps[e][:], ACT.Copy).then_inc(pT_kept, 1)
                if has_unit(i, r, 0, PER):
                    m, n, u, q, e = unit_of(i, r)
                    act.wait_ge(centered, done(m))
                    nc.scalar.activation(p[:, e, :], p[:, e, :], ACT.Exp, scale=SCALE).then_inc(exped, 1)
                if has_unit(i, r, 4, PER):
                    m, n, u, q, e = unit_of(i, r - 4)
                    act.wait_ge(o_turned, done(m))
                    act.wait_ge(projected, done(m - 2))
                    nc.scalar.activation(oT[:, e, :, :], rows_of(o_tps, 2), ACT.Copy).then_inc(oT_kept, 1)

            credit(act, staged_too, exped, pT_kept, oT_kept)
            stage(0, 0)
            pipeline(act, step, PER, LAG)

        @block.vector
        def _(dve):
            def step(i, r):
                if has_unit(i, r, LAG, PER) and (r - LAG) % UN == UN - 1:
                    m, n, u, q, e = unit_of(i, r - LAG)
                    dve.wait_ge(projected, done(m))
                    nc.vector.tensor_tensor(g.x[:, n, :], g.x[:, n, :], outp[:, 0:D], ALU.add).then_inc(added, 1)
                if has_unit(i, r, 0, PER):
                    m, n, u, q, e = unit_of(i, r)
                    dve.wait_ge(scored, done(m))
                    nc.vector.tensor_reduce(top[:, e, :], rows_of(score[e][:], Q), X, ALU.max)
                    dve.drain()
                    null = null_score[:, n, q * Q:(q + 1) * Q]
                    nc.vector.tensor_tensor(top0[:, e, :], top[:, e, :], null, ALU.max)
                    dve.drain()
                    dve.wait_ge(turned, done(m - 2))
                    dve.wait_ge(null_weighed, done(m - 2))
                    nc.vector.tensor_tensor(p[:, e, Q * T:], null, top0[:, e, :], ALU.subtract)
                    nc.vector.tensor_tensor(rows_of(p[:, e, 0:Q * T], Q), rows_of(score[e][:], Q),
                                            bc(top0[:, e, :], 2, T), ALU.subtract).then_inc(centered, 1)
                if has_unit(i, r, 3, PER):
                    m, n, u, q, e = unit_of(i, r - 3)
                    dve.wait_ge(mixed, done(m))
                    dve.wait_ge(null_weighed, done(m))
                    out = sums[:, e, :, :]
                    nc.vector.tensor_tensor(out, mix[e][:, 0:Q * (DH + 1)].rearrange("p (a b) -> p a b", a=Q),
                                            null_part[:, e, :, :], ALU.add).then_inc(whole, 1)
                    dve.drain()
                    nc.vector.reciprocal(inv[:, e, :], out[:, :, DH])
                    dve.drain()
                    dve.wait_ge(o_turned, done(m - 2))
                    nc.vector.tensor_tensor(rows_of(o[:, e, :], Q), out[:, :, 0:DH],
                                            bc(inv[:, e, :], 2, DH), ALU.mult).then_inc(normed, 1)

            credit(dve, whole, centered, normed, added)
            pipeline(dve, step, PER, LAG)



class Nothing:

    def tensor(self, pe):
        pass

    scalar = vector = gpsimd = tensor


class ContextProducts:

    def __init__(self, nc, g, w, st, keys):
        self.nc, self.g, self.w, self.keys = nc, g, w, keys
        self.kT = st.sb("kT", [128, TOK])
        self.v = st.sb("v", [T, B, H, HD + 1])
        self.k_made, self.v_made = st.sem("k_made"), st.sem("v_made")

    def tensor(self, pe):
        nc, g, w, bank = self.nc, self.g, self.w, self.g.bank
        pe.wait_ge(w.loaded, 16)
        if self.keys:
            for half in range(2):
                nc.tensor.matmul(bank[2 + half][:], w["wk"], g.ctxT[:, half * HALF:(half + 1) * HALF],
                                 start=True, stop=True).then_inc(self.k_made, 1)
        for half in range(2):
            for j in range(4):
                b = 4 * half + j
                last = nc.tensor.matmul(bank[4 + half][:, j * D:(j + 1) * D], g.ctxT[:, b * T:(b + 1) * T],
                                        w["wv"], start=True, stop=True)
            last.then_inc(self.v_made, 1)

    def scalar(self, act):
        if self.keys:
            for half in range(2):
                act.wait_ge(self.k_made, half + 1)
                self.nc.scalar.activation(self.kT[:, half * HALF:(half + 1) * HALF], self.g.bank[2 + half][:],
                                          ACT.Identity, bias=self.w["bk"])

    def vector(self, dve):
        for half in range(2):
            dve.wait_ge(self.v_made, half + 1)
            for j in range(4):
                self.nc.vector.tensor_tensor(self.v[:, 4 * half + j, :, 0:HD],
                                             rows_of(self.g.bank[4 + half][:, j * D:(j + 1) * D], H),
                                             rows_of(self.w["bv"], H), ALU.add)

    def gpsimd(self, pool):
        self.nc.gpsimd.memset(self.v[:, :, :, HD:HD + 1], 1.0)


def small_head_attention(nc, g, w, st, scale, mask=None):
    Q, UN = 4, H // 4
    qT, kT, v = st.sb("qT", [128, TOK]), st.beside.kT, st.beside.v
    qs, ks = st.sb("qs", [128, 2, T]), st.sb("ks", [128, 2, H, T])
    top, inv = st.sb("top", [T, 2, Q]), st.sb("inv", [T, 2, Q])
    p, pT = st.sb("p", [T, 2, Q * T]), st.sb("pT", [T, 2, Q * T])
    o, oT = st.sb("o", [T, 2, H * HD]), st.sb("oT", [128, TOK])
    proj = st.sem("proj")
    staged, staged_too, scored, centered, exped, turned, pT_kept, mixed, normed, o_turned, oT_kept = (
        st.sem(s) for s in ("staged", "staged_too", "scored", "centered", "exped", "turned", "pT_kept", "mixed", "normed",
                            "o_turned", "oT_kept"))
    bank = g.bank

    made_here = (("wq", qT, "bq"),) if st.beside.keys else (("wq", qT, "bq"), ("wk", kT, "bk"))
    with nc.Block() as block:
        @block.tensor
        def _(pe):
            for j, (weight, _, _) in enumerate(made_here):
                for half in range(2):
                    nc.tensor.matmul(bank[2 * j + half][:], w[weight], g.hT[:, half * HALF:(half + 1) * HALF],
                                     start=True, stop=True).then_inc(proj, 1)

        @block.scalar
        def _(act):
            for j, (_, dst, bias) in enumerate(made_here):
                for half in range(2):
                    act.wait_ge(proj, 2 * j + half + 1)
                    nc.scalar.activation(dst[:, half * HALF:(half + 1) * HALF], bank[2 * j + half][:], ACT.Identity,
                                         bias=w[bias])

    PER, LAG = 2 * UN, 4

    def unit_of(i, k):
        return PER * i + k, k // UN % 2, k % UN, k % 2

    score, tps, mix, o_tps = bank[0:2], bank[2:4], bank[4:6], bank[6][:, 0:T]
    with nc.Block() as block:
        @block.gpsimd
        def _(pool):
            def stage(n, u):
                pool.wait_ge(scored, done(UN * (n - 2) + UN - 1))
                nc.gpsimd.tensor_copy(qs[:, u, :], qT[:, bass.ds(n * T, T)])
                nc.gpsimd.tensor_tensor(ks[:, u, 0:H // 2, :], bc(kT[:, bass.ds(n * T, T)], 1, H // 2),
                                        bc(g.const["head"][:, 0:H // 2], 2, T), ALU.mult).then_inc(staged, 1)

            def step(i, r):
                if has_unit(i, r, 0, PER) and (r % UN) == 0:
                    stage(2 * i + r // UN, r // UN % 2)

            credit(pool, staged)
            pipeline(pool, step, PER, LAG)

        @block.tensor
        def _(pe):
            def step(i, r):
                if has_unit(i, r, 0, PER):
                    m, u, q, e = unit_of(i, r)
                    if q == 0:
                        pe.wait_ge(staged, done(2 * i + r // UN))
                    if q == UN // 2:
                        pe.wait_ge(staged_too, done(2 * i + r // UN))
                    pe.wait_ge(centered, done(m - 2))
                    if mask is not None:
                        nc.tensor.matmul(score[e][:], g.ident_bf[:], bc(mask(2 * i + r // UN), 1, Q),
                                         start=True, stop=False)
                    nc.tensor.matmul(score[e][:], qs[:, u, :], ks[:, u, Q * q:Q * (q + 1), :],
                                     start=mask is None, stop=True).then_inc(scored, 1)
                if has_unit(i, r, 2, PER):
                    m, u, q, e = unit_of(i, r - 2)
                    pe.wait_ge(exped, done(m))
                    pe.wait_ge(pT_kept, done(m - 2))
                    for j in range(Q):
                        last = nc.tensor.transpose(tps[e][:, j * T:(j + 1) * T], p[:, e, j * T:(j + 1) * T], g.ident)
                    last.then_inc(turned, 1)
                if has_unit(i, r, 3, PER):
                    m, u, q, e = unit_of(i, r - 3)
                    pe.wait_ge(pT_kept, done(m))
                    pe.wait_ge(normed, done(m - 2))
                    for j in range(Q):
                        last = nc.tensor.matmul(mix[e][:, j * (HD + 1):(j + 1) * (HD + 1)], pT[:, e, j * T:(j + 1) * T],
                                                v[:, 2 * i + (r - 3) // UN, Q * q + j, :], start=True, stop=True)
                    last.then_inc(mixed, 1)
                if has_unit(i, r, LAG, PER) and (r - LAG) % UN == UN - 1:
                    m, u, q, e = unit_of(i, r - LAG)
                    n = 2 * i + (r - LAG) // UN
                    pe.wait_ge(normed, done(m))
                    pe.wait_ge(oT_kept, done(n - 1))
                    nc.tensor.transpose(o_tps, o[:, u, :], g.ident).then_inc(o_turned, 1)

            credit(pe, scored, turned, mixed, o_turned)
            pipeline(pe, step, PER, LAG)

        @block.scalar
        def _(act):
            def stage(n, u, h):
                for j in (h, h + 1):
                    last = nc.scalar.activation(ks[:, u, j, :], kT[:, bass.ds(n * T, T)], ACT.Copy,
                                                scale=g.const["head"][:, j:j + 1])
                if h == H - 2:
                    last.then_inc(staged_too, 1)

            def step(i, r):
                if has_unit(i, r, -2, PER):
                    stage(2 * i + (r + 2) // UN, (r + 2) // UN % 2, H // 2 + 2 * ((r + 2) % UN))
                if has_unit(i, r, 2, PER):
                    m, u, q, e = unit_of(i, r - 2)
                    act.wait_ge(turned, done(m))
                    act.wait_ge(mixed, done(m - 2))
                    nc.scalar.activation(pT[:, e, :], tps[e][:], ACT.Copy).then_inc(pT_kept, 1)
                if has_unit(i, r, LAG, PER) and (r - LAG) % UN == UN - 1:
                    n = 2 * i + (r - LAG) // UN
                    act.wait_ge(o_turned, done(n))
                    nc.scalar.activation(oT[:, bass.ds(n * T, T)], o_tps, ACT.Copy).then_inc(oT_kept, 1)
                if has_unit(i, r, 0, PER):
                    m, u, q, e = unit_of(i, r)
                    act.wait_ge(centered, done(m))
                    nc.scalar.activation(p[:, e, :], p[:, e, :], ACT.Exp, scale=scale).then_inc(exped, 1)

            credit(act, staged_too, exped, pT_kept, oT_kept)
            for h in (H // 2, H // 2 + 2):
                stage(0, 0, h)
            pipeline(act, step, PER, LAG)

        @block.vector
        def _(dve):
            def step(i, r):
                if has_unit(i, r, 0, PER):
                    m, u, q, e = unit_of(i, r)
                    dve.wait_ge(scored, done(m))
                    nc.vector.tensor_reduce(top[:, e, :], rows_of(score[e][:], Q), X, ALU.max)
                    dve.drain()
                    dve.wait_ge(turned, done(m - 2))
                    nc.vector.tensor_tensor(rows_of(p[:, e, :], Q), rows_of(score[e][:], Q),
                                            bc(top[:, e, :], 2, T), ALU.subtract).then_inc(centered, 1)
                if has_unit(i, r, 3, PER):
                    m, u, q, e = unit_of(i, r - 3)
                    out = mix[e][:, 0:Q * (HD + 1)].rearrange("p (a b) -> p a b", a=Q)
                    dve.wait_ge(mixed, done(m))
                    nc.vector.reciprocal(inv[:, e, :], out[:, :, HD])
                    dve.drain()
                    if q == 0:
                        dve.wait_ge(o_turned, done(2 * i + (r - 3) // UN - 2))
                    nc.vector.tensor_tensor(rows_of(o[:, u, Q * HD * q:Q * HD * (q + 1)], Q), out[:, :, 0:HD],
                                            bc(inv[:, e, :], 2, HD), ALU.mult).then_inc(normed, 1)

            credit(dve, centered, normed)
            pipeline(dve, step, PER, LAG)
    return oT


def add_projection(nc, g, w, st, oT):
    bank = g.bank
    biased, projected = st.sem("biased"), st.sem("projected")
    with nc.Block() as block:
        @block.tensor
        def _(pe):
            for half in range(2):
                for j in range(4):
                    b = 4 * half + j
                    last = nc.tensor.matmul(bank[half][:, j * D:(j + 1) * D], oT[:, b * T:(b + 1) * T], w["wo"],
                                            start=True, stop=True)
                last.then_inc(projected, 1)

        @block.vector
        def _(dve):
            if "bo" in w.places:
                nc.vector.tensor_tensor(g.x[:], g.x[:], bc(w["bo"], 1, B), ALU.add)
                dve.drain()
            for half in range(2):
                b = slice(4 * half, 4 * half + 4)
                dve.wait_ge(projected, half + 1)
                nc.vector.tensor_tensor(g.x[:, b, :], g.x[:, b, :], rows_of(bank[half][:], 4), ALU.add)


def cross_attention(nc, g, w, st):
    oT = small_head_attention(nc, g, w, st, HD ** -0.5)
    add_projection(nc, g, w, st, oT)


def masked_cross_attention(nc, g, w, st):
    mask8, mask = st.sb("mask8", [T, B, T], U8), st.sb("mask", [T, B, T], BF16)
    mask_loaded = st.sem("mask_loaded")
    with nc.Block() as block:
        @block.sync
        def _(sp):
            sp.dma_start(mask8[:], g.dram["mask"].rearrange("b q k -> q b k")).then_inc(mask_loaded, 16)

        @block.vector
        def _(dve):
            dve.wait_ge(mask_loaded, 16)
            nc.vector.tensor_scalar(mask[:], mask8[:], NEG, None, ALU.mult)
    oT = small_head_attention(nc, g, w, st, HD ** -0.5, lambda n: mask[:, n, :])
    add_projection(nc, g, w, st, oT)


def attention_with_mlp(nc, g, w, st):
    NJ = 4
    bank = g.bank
    oT = small_head_attention(nc, g, w, st, 1.0, lambda n: g.shifted_bf[:, 0, :])
    hid = st.sb("hid", [128, NJ, TOK])
    up, kept, down = st.sem("up"), st.sem("kept"), st.sem("down")
    with nc.Block() as block:
        @block.tensor
        def _(pe):
            for m in range(2 * NJ):
                j, half = m % NJ, m // NJ
                if m >= 6:
                    pe.wait_ge(kept, m - 5)
                nc.tensor.matmul(bank[m % 6][:], w["w1"][:, j * 128:(j + 1) * 128],
                                 oT[:, half * HALF:(half + 1) * HALF], start=True, stop=True).then_inc(up, 1)
            for b in range(B):
                if b % 4 == 0:
                    pe.wait_ge(kept, NJ * (b // 4 + 1))
                for j in range(NJ):
                    last = nc.tensor.matmul(bank[6 + b // 4][:, (b % 4) * D:(b % 4 + 1) * D],
                                            hid[:, j, b * T:(b + 1) * T], w["w2"][:, j * D:(j + 1) * D],
                                            start=(j == 0), stop=(j == NJ - 1))
                if b % 4 == 3:
                    last.then_inc(down, 1)

        @block.scalar
        def _(act):
            for m in range(2 * NJ):
                j, half = m % NJ, m // NJ
                act.wait_ge(up, m + 1)
                nc.scalar.activation(hid[:, j, half * HALF:(half + 1) * HALF], bank[m % 6][:], ACT.Gelu,
                                     bias=w["b1"][:, j:j + 1]).then_inc(kept, 1)

        @block.vector
        def _(dve):
            nc.vector.tensor_tensor(g.x[:], g.x[:], bc(w["b2"], 1, B), ALU.add)
            dve.drain()
            for half in range(2):
                b = slice(4 * half, 4 * half + 4)
                dve.wait_ge(down, half + 1)
                nc.vector.tensor_tensor(g.x[:, b, :], g.x[:, b, :], rows_of(bank[6 + half][:], 4), ALU.add)



def route_top2_softmax(nc, g, w, st, combine):
    E = 8
    bank = g.bank
    logit, best, keep = st.sb("logit", [T, B, E]), st.sb("best", [T, B, 8]), st.sb("keep", [T, B, E])
    total, combT = st.sb("total", [T, B]), st.sb("combT", [E, TOK])
    made, centered, exped, routed, combine_turned, combT_kept, biases = (
        st.sem(s) for s in ("made", "centered", "exped", "routed", "combine_turned", "combT_kept", "biases"))
    with nc.Block() as block:
        @block.tensor
        def _(pe):
            pe.wait_ge(w.loaded, 16)
            for b in range(B):
                last = nc.tensor.matmul(bank[0][:, b * E:(b + 1) * E], g.hT[:, b * T:(b + 1) * T], w["router"],
                                        start=True, stop=True)
            last.then_inc(made, 1)
            pe.wait_ge(routed, 1)
            for b in range(B):
                last = nc.tensor.transpose(bank[1 + b // 4][0:E, (b % 4) * T:(b % 4 + 1) * T], combine[:, b, :], g.ident)
            last.then_inc(combine_turned, 1)
            pe.wait_ge(combT_kept, 1)
            for b in range(B):
                last = nc.tensor.matmul(bank[3 + b // 4][:, (b % 4) * D:(b % 4 + 1) * D], combT[:, b * T:(b + 1) * T],
                                        w["b2"], start=True, stop=True)
            last.then_inc(biases, 1)

        @block.scalar
        def _(act):
            act.wait_ge(centered, 1)
            nc.scalar.activation(logit[:], logit[:], ACT.Exp).then_inc(exped, 1)
            act.wait_ge(combine_turned, 1)
            for half in range(2):
                last = nc.scalar.activation(combT[:, half * HALF:(half + 1) * HALF], bank[1 + half][0:E, :], ACT.Copy)
            last.then_inc(combT_kept, 1)

        @block.vector
        def _(dve):
            dve.wait_ge(made, 1)
            nc.vector.tensor_tensor(logit[:], rows_of(bank[0][:, 0:B * E], B), bc(w["br"], 1, B), ALU.add)
            dve.drain()
            for b in range(B):
                nc.vector.max(best[:, b, :], logit[:, b, :])
            dve.drain()
            nc.vector.tensor_tensor(keep[:], logit[:], best[:, :, 1:2].to_broadcast([T, B, E]), ALU.is_ge)
            dve.drain()
            nc.vector.tensor_tensor(logit[:], logit[:], best[:, :, 0:1].to_broadcast([T, B, E]),
                                    ALU.subtract).then_inc(centered, 1)
            dve.wait_ge(exped, 1)
            nc.vector.tensor_tensor(keep[:], keep[:], logit[:], ALU.mult)
            dve.drain()
            nc.vector.tensor_reduce(total[:], keep[:], X, ALU.add)
            dve.drain()
            nc.vector.reciprocal(total[:], total[:])
            dve.drain()
            nc.vector.tensor_tensor(combine[:], keep[:], bc(total[:], 2, E), ALU.mult).then_inc(routed, 1)
            dve.wait_ge(biases, 1)
            for half in range(2):
                b = slice(4 * half, 4 * half + 4)
                nc.vector.tensor_tensor(g.x[:, b, :], g.x[:, b, :], rows_of(bank[3 + half][:], 4), ALU.add)


def route_top2_renormed(nc, g, w, st, combine):
    E = 8
    bank = g.bank
    sq, meansq, rms = st.sb("sq", [T, B, D]), st.sb("meansq", [T, B]), st.sb("rms", [T, B])
    power, router = st.sb("power", [T, B]), st.sb("router", [D, E])
    logit, best, keep = st.sb("logit", [T, B, E]), st.sb("best", [T, B, 8]), st.sb("keep", [T, B, E])
    total, fix = st.sb("total", [T, B]), st.sb("fix", [T, B])
    power_set, squared, rms_ready, router_ready, made, centered, exped = (
        st.sem(s) for s in ("power_set", "squared", "rms_ready", "router_ready", "made", "centered", "exped"))
    with nc.Block() as block:
        @block.gpsimd
        def _(pool):
            nc.gpsimd.memset(power[:], -0.5).then_inc(power_set, 1)
            pool.wait_ge(power_set, 1)
            pool.wait_ge(squared, 1)
            nc.gpsimd.tensor_tensor(rms[:], meansq[:], power[:], ALU.pow).then_inc(rms_ready, 1)

        @block.tensor
        def _(pe):
            pe.wait_ge(router_ready, 1)
            for b in range(B):
                last = nc.tensor.matmul(bank[0][:, b * E:(b + 1) * E], g.hT[:, b * T:(b + 1) * T], router[:],
                                        start=True, stop=True)
            last.then_inc(made, 1)

        @block.scalar
        def _(act):
            act.wait_ge(centered, 1)
            nc.scalar.activation(logit[:], logit[:], ACT.Exp).then_inc(exped, 1)

        @block.vector
        def _(dve):
            dve.wait_ge(w.loaded, 16)
            nc.vector.tensor_scalar(router[:], w["router"], w["router_scale"], float(D) ** -0.5,
                                    ALU.mult, ALU.mult).then_inc(router_ready, 1)
            nc.vector.tensor_tensor(sq[:], g.h[:], g.h[:], ALU.mult)
            dve.drain()
            nc.vector.tensor_reduce(meansq[:], sq[:], X, ALU.add)
            dve.drain()
            nc.vector.tensor_scalar(meansq[:], meansq[:], 1.0 / D, 1e-6, ALU.mult, ALU.add).then_inc(squared, 1)
            dve.wait_ge(rms_ready, 1)
            dve.wait_ge(made, 1)
            nc.vector.tensor_tensor(logit[:], rows_of(bank[0][:, 0:B * E], B), bc(rms[:], 2, E), ALU.mult)
            dve.drain()
            for b in range(B):
                nc.vector.max(best[:, b, :], logit[:, b, :])
            dve.drain()
            nc.vector.tensor_tensor(keep[:], logit[:], best[:, :, 1:2].to_broadcast([T, B, E]), ALU.is_ge)
            dve.drain()
            nc.vector.tensor_tensor(logit[:], logit[:], best[:, :, 0:1].to_broadcast([T, B, E]),
                                    ALU.subtract).then_inc(centered, 1)
            dve.wait_ge(exped, 1)
            nc.vector.tensor_tensor(keep[:], keep[:], logit[:], ALU.mult)
            dve.drain()
            nc.vector.tensor_reduce(total[:], keep[:], X, ALU.add)
            dve.drain()
            nc.vector.tensor_scalar(fix[:], total[:], 0.0, None, ALU.is_le)
            dve.drain()
            nc.vector.tensor_tensor(total[:], total[:], fix[:], ALU.add)
            dve.drain()
            nc.vector.reciprocal(total[:], total[:])
            dve.drain()
            nc.vector.tensor_tensor(keep[:], keep[:], bc(total[:], 2, E), ALU.mult)
            dve.drain()
            nc.vector.tensor_tensor(combine[:], keep[:], bc(w["expert_scale"], 1, B), ALU.mult)


def route_grouped_top8(nc, g, w, st, combine):
    E, G = 64, 8
    bank = g.bank
    score, biased, chosen = st.sb("score", [T, B, E]), st.sb("biased", [T, B, E]), st.sb("chosen", [T, B, E])
    rest = st.sb("rest", [T, B, E])
    top1, top2, count = st.sb("top1", [T, B * G]), st.sb("top2", [T, B * G]), st.sb("count", [T, B * G])
    gsum, gbest, gkeep = st.sb("gsum", [T, B, G]), st.sb("gbest", [T, B, 8]), st.sb("gkeep", [T, B * G])
    best, total = st.sb("best", [T, B, 8]), st.sb("total", [T, B])
    made, sigmoid_ready = st.sem("made"), st.sem("sigmoid_ready")
    groups = lambda t: t[:].rearrange("p b (g e) -> p (b g) e", e=G)
    with nc.Block() as block:
        @block.tensor
        def _(pe):
            pe.wait_ge(w.loaded, 16)
            for b in range(B):
                last = nc.tensor.matmul(bank[0][:, b * E:(b + 1) * E], g.hT[:, b * T:(b + 1) * T], w["router"],
                                        start=True, stop=True)
            last.then_inc(made, 1)

        @block.scalar
        def _(act):
            act.wait_ge(made, 1)
            nc.scalar.activation(score[:], rows_of(bank[0][:], B), ACT.Sigmoid).then_inc(sigmoid_ready, 1)

        @block.vector
        def _(dve):
            dve.wait_ge(sigmoid_ready, 1)
            nc.vector.tensor_tensor(biased[:], score[:], bc(w["correction"], 1, B), ALU.add)
            dve.drain()
            nc.vector.tensor_reduce(top1[:], groups(biased), X, ALU.max)
            dve.drain()
            nc.vector.tensor_tensor(groups(chosen), groups(biased), bc(top1[:], 2, G), ALU.is_ge)
            dve.drain()
            nc.vector.tensor_reduce(count[:], groups(chosen), X, ALU.add)
            nc.vector.scalar_tensor_tensor(groups(rest), groups(chosen), NEG, groups(biased), ALU.mult, ALU.add)
            dve.drain()
            nc.vector.tensor_reduce(top2[:], groups(rest), X, ALU.max)
            nc.vector.tensor_scalar(count[:], count[:], 1.5, NEG, ALU.is_lt, ALU.mult)
            dve.drain()
            nc.vector.tensor_tensor(count[:], count[:], top1[:], ALU.add)
            dve.drain()
            nc.vector.tensor_tensor(top2[:], top2[:], count[:], ALU.max)
            dve.drain()
            nc.vector.tensor_tensor(gsum[:].rearrange("p b g -> p (b g)"), top1[:], top2[:], ALU.add)
            dve.drain()
            for b in range(B):
                nc.vector.max(gbest[:, b, :], gsum[:, b, :])
            dve.drain()
            nc.vector.tensor_tensor(rows_of(gkeep[:], B), gsum[:], gbest[:, :, 3:4].to_broadcast([T, B, G]), ALU.is_ge)
            dve.drain()
            nc.vector.tensor_tensor(groups(biased), groups(biased), bc(gkeep[:], 2, G), ALU.mult)
            dve.drain()
            for b in range(B):
                nc.vector.max(best[:, b, :], biased[:, b, :])
            dve.drain()
            for b in range(B):
                nc.vector.match_replace(rest[:, b, :], best[:, b, :], biased[:, b, :], NEG)
            dve.drain()
            nc.vector.tensor_scalar(chosen[:], rest[:], NEG, None, ALU.is_equal)
            dve.drain()
            nc.vector.tensor_tensor(chosen[:], chosen[:], score[:], ALU.mult)
            dve.drain()
            nc.vector.tensor_reduce(total[:], chosen[:], X, ALU.add)
            dve.drain()
            nc.vector.tensor_scalar(total[:], total[:], 1e-20, None, ALU.add)
            dve.drain()
            nc.vector.reciprocal(total[:], total[:])
            dve.drain()
            nc.vector.tensor_scalar(total[:], total[:], 2.5, None, ALU.mult)
            dve.drain()
            nc.vector.tensor_tensor(combine[:, :, 0:E], chosen[:], bc(total[:], 2, E), ALU.mult)


GATED, SQUARED, BIASED = range(3)


def experts(nc, g, w, st, combine, kind, widths):
    UN = len(widths)
    bank = g.bank
    hs = st.sb("hs", [D, 2, T])
    a, aT = st.sb("a", [T, 2, HALF]), st.sb("aT", [128, 2, 4, T])
    act_out = st.sb("act_out", [T, 2, HALF])
    staged, hidden, part, weighed, scaled, turned, aT_kept, summed, added = (
        st.sem(s) for s in ("staged", "hidden", "part", "weighed", "scaled", "turned", "aT_kept", "summed", "added"))
    up, tps, acc = bank[0:2], bank[2:4], bank[4:6]
    tile_at = [sum(widths[:q]) // 128 for q in range(UN)]
    up_width = [2 * x if kind == GATED else x for x in widths]
    up_at = [sum(up_width[:q]) for q in range(UN)]
    EXPERTS = 8

    PER, LAG = 2 * UN, 4

    def unit_of(i, k):
        return PER * i + k, 2 * i + k // UN, k // UN % 2, k % UN, k % 2

    with nc.Block() as block:
        @block.gpsimd
        def _(pool):
            def step(i, r):
                if has_unit(i, r, 0, PER) and r % UN == 0:
                    m, n, u, q, e = unit_of(i, r)
                    pool.wait_ge(hidden, done(UN * (n - 2) + UN - 1))
                    nc.gpsimd.tensor_copy(hs[:, u, :], g.hT[:, bass.ds(n * T, T)]).then_inc(staged, 1)
                if kind == SQUARED and has_unit(i, r, 2, PER):
                    m, n, u, q, e = unit_of(i, r - 2)
                    wide = widths[q]
                    pool.wait_ge(part, done(m))
                    ex = wide // (HALF // EXPERTS)
                    rows = act_out[:, e, 0:wide].rearrange("p (a b) -> p a b", a=ex)
                    nc.gpsimd.tensor_tensor(rows, rows, bc(combine[:, n, EXPERTS * q:EXPERTS * q + ex], 2,
                                                           HALF // EXPERTS), ALU.mult).then_inc(weighed, 1)

            credit(pool, staged)
            if kind == SQUARED:
                credit(pool, weighed)
            pipeline(pool, step, PER, LAG)

        @block.tensor
        def _(pe):
            def step(i, r):
                if has_unit(i, r, 0, PER):
                    m, n, u, q, e = unit_of(i, r)
                    if q == 0:
                        pe.wait_ge(staged, done(n))
                    pe.wait_ge(weighed if kind == BIASED else scaled, done(m - 2))
                    nc.tensor.matmul(up[e][:, 0:up_width[q]], hs[:, u, :], w["up"][:, up_at[q]:up_at[q] + up_width[q]],
                                     start=True, stop=True).then_inc(hidden, 1)
                if has_unit(i, r, 2, PER):
                    m, n, u, q, e = unit_of(i, r - 2)
                    pe.wait_ge(scaled, done(m))
                    pe.wait_ge(aT_kept, done(m - 2))
                    for j in range(widths[q] // 128):
                        last = nc.tensor.transpose(tps[e][:, j * T:(j + 1) * T], a[:, e, j * 128:(j + 1) * 128], g.ident)
                    last.then_inc(turned, 1)
                if has_unit(i, r, 3, PER):
                    m, n, u, q, e = unit_of(i, r - 3)
                    pe.wait_ge(aT_kept, done(m))
                    if q == 0:
                        pe.wait_ge(added, done(n - 2))
                    tiles = widths[q] // 128
                    for j in range(tiles):
                        at = (tile_at[q] + j) * D
                        last = nc.tensor.matmul(acc[u][:, 0:D], aT[:, e, j, :], w["down"][:, at:at + D],
                                                start=(q == 0 and j == 0), stop=(q == UN - 1 and j == tiles - 1))
                    last.then_inc(summed, 1)

            credit(pe, hidden, turned, summed)
            pipeline(pe, step, PER, LAG)

        @block.scalar
        def _(act):
            def activate(i, r):
                if has_unit(i, r, 0, PER):
                    m, n, u, q, e = unit_of(i, r)
                    wide = widths[q]
                    if kind == BIASED:
                        act.wait_ge(weighed, done(m))
                        nc.scalar.activation(act_out[:, e, :], act_out[:, e, :], ACT.Gelu).then_inc(part, 1)
                    else:
                        act.wait_ge(scaled, done(m - 2))
                        act.wait_ge(hidden, done(m))
                        nc.scalar.activation(act_out[:, e, 0:wide], up[e][:, 0:wide],
                                             ACT.Gelu_apprx_tanh if kind == GATED else ACT.Relu).then_inc(part, 1)

            def step(i, r):
                if kind != BIASED:
                    activate(i, r)
                if has_unit(i, r, 2, PER):
                    m, n, u, q, e = unit_of(i, r - 2)
                    act.wait_ge(turned, done(m))
                    act.wait_ge(summed, done(m - 2))
                    tiles = widths[q] // 128
                    nc.scalar.activation(aT[:, e, 0:tiles, :], rows_of(tps[e][:, 0:widths[q]], tiles),
                                         ACT.Copy).then_inc(aT_kept, 1)
                if kind == BIASED:
                    activate(i, r)

            credit(act, part, aT_kept)
            pipeline(act, step, PER, LAG)

        @block.vector
        def _(dve):
            def step(i, r):
                if kind == BIASED and has_unit(i, r, 0, PER):
                    m, n, u, q, e = unit_of(i, r)
                    dve.wait_ge(hidden, done(m))
                    dve.wait_ge(scaled, done(m - 2))
                    nc.vector.tensor_tensor(act_out[:, e, :], up[e][:], w["b1"][:, q * HALF:(q + 1) * HALF],
                                            ALU.add).then_inc(weighed, 1)
                back = 1 if kind != GATED else 0
                if has_unit(i, r, back, PER):
                    m, n, u, q, e = unit_of(i, r - back)
                    wide = widths[q]
                    dve.wait_ge(part, done(m))
                    dve.wait_ge(turned, done(m - 2))
                    if kind == GATED:
                        nc.vector.scalar_tensor_tensor(a[:, e, 0:wide], up[e][:, wide:2 * wide],
                                                       combine[:, n, q:q + 1], act_out[:, e, 0:wide],
                                                       ALU.mult, ALU.mult).then_inc(scaled, 1)
                    elif kind == SQUARED:
                        dve.wait_ge(weighed, done(m))
                        nc.vector.scalar_tensor_tensor(a[:, e, 0:wide], up[e][:, 0:wide], 0.0, act_out[:, e, 0:wide],
                                                       ALU.max, ALU.mult).then_inc(scaled, 1)
                    else:
                        nc.vector.tensor_scalar(a[:, e, :], act_out[:, e, :], combine[:, n, q:q + 1], None,
                                                ALU.mult).then_inc(scaled, 1)
                if has_unit(i, r, LAG, PER) and (r - LAG) % UN == UN - 1:
                    m, n, u, q, e = unit_of(i, r - LAG)
                    dve.wait_ge(summed, done(m))
                    nc.vector.tensor_tensor(g.x[:, n, :], g.x[:, n, :], acc[u][:, 0:D], ALU.add).then_inc(added, 1)

            credit(dve, scaled, added)
            if kind == BIASED:
                credit(dve, weighed)
            pipeline(dve, step, PER, LAG)


def gated_experts(nc, g, w, st):
    combine = st.sb("combine", [T, B, 8])
    route_top2_renormed(nc, g, w, st, combine)
    experts(nc, g, w, st, combine, GATED, [256] * 8)


def many_experts(nc, g, w, st):
    combine = st.sb("combine", [T, B, 68])
    with nc.Block() as block:
        @block.gpsimd
        def _(pool):
            nc.gpsimd.memset(combine[:, :, 64:68], 1.0)
    route_grouped_top8(nc, g, w, st, combine)
    experts(nc, g, w, st, combine, SQUARED, [HALF] * 8 + [256])


def wide_experts(nc, g, w, st):
    combine = st.sb("combine", [T, B, 8])
    route_top2_softmax(nc, g, w, st, combine)
    experts(nc, g, w, st, combine, BIASED, [HALF] * 8)



def ternary_ffn(nc, g, w, st):
    INNER = 512
    bank = g.bank
    mats = ("gate", "up", "down")
    rowsum = st.sb("rowsum", [128, 3])
    unit, unit_inv = st.sb("unit", [128, 3]), st.sb("unit_inv", [128, 3])
    wf, wq = st.sb("wf", [128, INNER]), st.sb("wq", [128, 3, INNER], BF16)
    peak, inv = st.sb("peak", [T, B]), st.sb("inv", [T, B])
    gate_scale, up_scale = st.sb("gate_scale", [T, B]), st.sb("up_scale", [T, B])
    hf, hq, hqT = st.sb("hf", [T, B, D]), st.sb("hq", [T, B, D], BF16), st.sb("hqT", [D, TOK], BF16)
    summed, means, quantised, turned, hqT_kept = (
        st.sem(s) for s in ("summed", "means", "quantised", "turned", "hqT_kept"))
    with nc.Block() as block:
        @block.tensor
        def _(pe):
            pe.wait_ge(summed, 1)
            nc.tensor.matmul(bank[2][:, 0:3], g.const["ones"], rowsum[:], start=True, stop=True).then_inc(means, 1)
            for half in range(2):
                pe.wait_ge(quantised, 1)
                for j in range(4):
                    last = nc.tensor.transpose(g.bank_bf[half][:, j * T:(j + 1) * T], hq[:, 4 * half + j, :],
                                               g.ident_bf[:])
                last.then_inc(turned, 1)

        @block.scalar
        def _(act):
            for half in range(2):
                act.wait_ge(turned, half + 1)
                nc.scalar.activation(hqT[:, half * HALF:(half + 1) * HALF], g.bank_bf[half][:, 0:HALF], ACT.Copy)

        @block.vector
        def _(dve):
            dve.wait_ge(w.loaded, 16)
            for j, name in enumerate(mats):
                nc.vector.tensor_reduce(rowsum[:, j:j + 1], w[name], X, ALU.add, apply_absolute_value=True)
            dve.drain()
            nc.vector.tensor_scalar(rowsum[:], rowsum[:], 1.0 / (INNER * D), None, ALU.mult).then_inc(summed, 1)
            nc.vector.tensor_reduce(peak[:], g.h[:], X, ALU.max, apply_absolute_value=True)
            dve.drain()
            nc.vector.tensor_scalar(peak[:], peak[:], 1e-5, 1.0 / 127.0, ALU.max, ALU.mult)
            dve.drain()
            nc.vector.reciprocal(inv[:], peak[:])
            dve.drain()
            nc.vector.tensor_tensor(hf[:], g.h[:], bc(inv[:], 2, D), ALU.mult)
            dve.drain()
            nc.vector.tensor_scalar(hf[:], hf[:], ROUND, ROUND, ALU.add, ALU.subtract)
            dve.drain()
            nc.vector.tensor_scalar(hq[:], hf[:], 127.0, -128.0, ALU.min, ALU.max).then_inc(quantised, 1)
            dve.wait_ge(means, 1)
            nc.vector.tensor_scalar(unit[:], bank[2][:, 0:3], 1e-5, None, ALU.max)
            dve.drain()
            nc.vector.reciprocal(unit_inv[:], unit[:])
            dve.drain()
            for j, name in enumerate(mats):
                nc.vector.tensor_scalar(wf[:], w[name], unit_inv[:, j:j + 1], None, ALU.mult)
                dve.drain()
                nc.vector.tensor_scalar(wf[:], wf[:], ROUND, ROUND, ALU.add, ALU.subtract)
                dve.drain()
                nc.vector.tensor_scalar(wq[:, j, :], wf[:], 1.0, -1.0, ALU.min, ALU.max)
                dve.drain()
            nc.vector.tensor_scalar(gate_scale[:], peak[:], unit[:, 0:1], None, ALU.mult)
            nc.vector.tensor_scalar(up_scale[:], peak[:], unit[:, 1:2], None, ALU.mult)

    gated, prod = st.sb("gated", [T, 2, INNER]), st.sb("prod", [T, 2, INNER])
    prodf, prodq = st.sb("prodf", [T, 2, INNER]), st.sb("prodq", [T, 2, INNER], BF16)
    peak2, inv2, out_scale = st.sb("peak2", [T, 2]), st.sb("inv2", [T, 2]), st.sb("out_scale", [T, B])
    prodT = st.sb("prodT", [128, 2, 4, T], BF16)
    hidden, silu_ready, rounded, prod_turned, prodT_kept, made, added = (
        st.sem(s) for s in ("hidden", "silu_ready", "rounded", "prod_turned", "prodT_kept", "made", "added"))
    gate, up, tps, out = bank[0:2], bank[2:4], g.bank_bf[4:6], bank[6:8]
    PER, LAG = 2, 3

    def sequence(i, k):
        return PER * i + k, k % 2

    with nc.Block() as block:
        @block.tensor
        def _(pe):
            def step(i, r):
                if has_unit(i, r, 0, PER):
                    n, u = sequence(i, r)
                    pe.wait_ge(rounded, done(n - 2))
                    for at, j in ((gate[u], 0), (up[u], 1)):
                        last = nc.tensor.matmul(at[:], hqT[:, bass.ds(n * T, T)], wq[:, j, :], start=True, stop=True)
                    last.then_inc(hidden, 1)
                if has_unit(i, r, 1, PER):
                    n, u = sequence(i, r - 1)
                    pe.wait_ge(rounded, done(n))
                    pe.wait_ge(prodT_kept, done(n - 2))
                    for j in range(4):
                        last = nc.tensor.transpose(tps[u][:, j * T:(j + 1) * T], prodq[:, u, j * 128:(j + 1) * 128],
                                                   g.ident_bf[:])
                    last.then_inc(prod_turned, 1)
                if has_unit(i, r, 2, PER):
                    n, u = sequence(i, r - 2)
                    pe.wait_ge(prodT_kept, done(n))
                    pe.wait_ge(added, done(n - 2))
                    for j in range(4):
                        last = nc.tensor.matmul(out[u][:, 0:D], prodT[:, u, j, :], wq[:, 2, j * D:(j + 1) * D],
                                                start=(j == 0), stop=(j == 3))
                    last.then_inc(made, 1)

            credit(pe, hidden, prod_turned, made)
            pipeline(pe, step, PER, LAG)

        @block.scalar
        def _(act):
            def step(i, r):
                if has_unit(i, r, 0, PER):
                    n, u = sequence(i, r)
                    act.wait_ge(hidden, done(n))
                    act.wait_ge(rounded, done(n - 2))
                    nc.scalar.activation(gated[:, u, :], gate[u][:], ACT.Silu,
                                         scale=gate_scale[:, bass.ds(n, 1)]).then_inc(silu_ready, 1)
                if has_unit(i, r, 1, PER):
                    n, u = sequence(i, r - 1)
                    act.wait_ge(prod_turned, done(n))
                    act.wait_ge(made, done(n - 2))
                    nc.scalar.activation(prodT[:, u, :, :], rows_of(tps[u][:, 0:HALF], 4),
                                         ACT.Copy).then_inc(prodT_kept, 1)

            credit(act, silu_ready, prodT_kept)
            pipeline(act, step, PER, LAG)

        @block.vector
        def _(dve):
            def step(i, r):
                if has_unit(i, r, LAG, PER):
                    n, u = sequence(i, r - LAG)
                    dve.wait_ge(made, done(n))
                    nc.vector.scalar_tensor_tensor(g.x[:, n, :], out[u][:, 0:D], out_scale[:, bass.ds(n, 1)], g.x[:, n, :],
                                                   ALU.mult, ALU.add).then_inc(added, 1)
                if has_unit(i, r, 0, PER):
                    n, u = sequence(i, r)
                    dve.wait_ge(silu_ready, done(n))
                    nc.vector.scalar_tensor_tensor(prod[:, u, :], up[u][:], up_scale[:, bass.ds(n, 1)], gated[:, u, :],
                                                   ALU.mult, ALU.mult)
                    dve.drain()
                    nc.vector.tensor_reduce(peak2[:, u:u + 1], prod[:, u, :], X, ALU.max, apply_absolute_value=True)
                    dve.drain()
                    nc.vector.tensor_scalar(peak2[:, u:u + 1], peak2[:, u:u + 1], 1e-5, 1.0 / 127.0, ALU.max, ALU.mult)
                    dve.drain()
                    nc.vector.reciprocal(inv2[:, u:u + 1], peak2[:, u:u + 1])
                    nc.vector.tensor_scalar(out_scale[:, bass.ds(n, 1)], peak2[:, u:u + 1], unit[:, 2:3], None, ALU.mult)
                    dve.drain()
                    nc.vector.tensor_scalar(prodf[:, u, :], prod[:, u, :], inv2[:, u:u + 1], ROUND, ALU.mult, ALU.add)
                    dve.drain()
                    dve.wait_ge(prod_turned, done(n - 2))
                    nc.vector.tensor_scalar(prodq[:, u, :], prodf[:, u, :], ROUND, None,
                                            ALU.subtract).then_inc(rounded, 1)

            credit(dve, rounded, added)
            pipeline(dve, step, PER, LAG)



def time_mix(nc, g, w, st):
    bank = g.bank
    Q, UN = 4, H // 4
    xx = st.sb("xx", [D, B, T])
    mixed = {c: st.sb("x" + c, [D, TOK]) for c in "rkvg"}
    rT, kT = st.sb("rT", [D, TOK]), st.sb("kT", [D, TOK])
    v, gate = st.sb("v", [T, B, D]), st.sb("gate", [T, B, D])
    rate, weight = st.sb("rate", [T, H]), st.sb("weight", [T, H, T])
    bonus = st.sb("bonus", [T, H, T])
    bonus_ready, projT, proj, blended, rates, powers, powers_ready = (
        st.sem(s) for s in ("bonus_ready", "projT", "proj", "blended", "rates", "powers", "powers_ready"))
    hT3 = rows_of(g.hT[:], B)
    vh = rows_of(g.region_a[:, 0:2 * H * (D + HD)], 2)
    with nc.Block() as block:
        @block.gpsimd
        def _(pool):
            pool.wait_ge(w.loaded, 16)
            nc.gpsimd.tensor_tensor(bonus[:], bc(g.ident, 1, H), bc(w["bonus"], 2, T), ALU.mult).then_inc(bonus_ready, 1)
            nc.gpsimd.memset(vh[:], 0.0)

        @block.vector
        def _(dve):
            dve.wait_ge(w.loaded, 16)
            nc.vector.tensor_tensor(xx[:, :, 1:T], hT3[:, :, 0:T - 1], hT3[:, :, 1:T], ALU.subtract)
            nc.vector.tensor_scalar(xx[:, :, 0:1], hT3[:, :, 0:1], -1.0, None, ALU.mult)
            dve.drain()
            for c in "rkvg":
                nc.vector.scalar_tensor_tensor(mixed[c][:], xx[:].rearrange("p b t -> p (b t)"), w["maa_" + c], g.hT[:],
                                               ALU.mult, ALU.add).then_inc(blended, 1)
                if c == "k":
                    dve.wait_ge(rates, 1)
                    nc.vector.tensor_tensor(weight[:], bc(g.tables["steps"], 1, H), bc(rate[:], 2, T),
                                            ALU.mult).then_inc(powers, 1)
            dve.wait_ge(powers_ready, 1)
            nc.vector.tensor_tensor(weight[:], weight[:], bc(g.tables["lt"], 1, H), ALU.mult)
            dve.drain()
            dve.wait_ge(bonus_ready, 1)
            nc.vector.tensor_tensor(weight[:], weight[:], bonus[:], ALU.add)
            for half in range(2):
                dve.wait_ge(proj, half + 1)
                nc.vector.tensor_copy(v[:, 4 * half:4 * half + 4, :], rows_of(bank[4 + half][:], 4))

        @block.tensor
        def _(pe):
            for j, c in enumerate("rk"):
                pe.wait_ge(blended, j + 1)
                for half in range(2):
                    nc.tensor.matmul(bank[2 * j + half][:], w["w_" + c], mixed[c][:, half * HALF:(half + 1) * HALF],
                                     start=True, stop=True).then_inc(projT, 1)
            for j, c in enumerate("vg"):
                pe.wait_ge(blended, j + 3)
                for half in range(2):
                    for q in range(4):
                        b = 4 * half + q
                        last = nc.tensor.matmul(bank[4 + 2 * j + half][:, q * D:(q + 1) * D],
                                                mixed[c][:, b * T:(b + 1) * T], w["w_" + c], start=True, stop=True)
                    last.then_inc(proj, 1)

        @block.scalar
        def _(act):
            act.wait_ge(w.loaded, 16)
            nc.scalar.activation(rate[:], w["decay"], ACT.Exp).then_inc(rates, 1)
            act.wait_ge(powers, 1)
            nc.scalar.activation(weight[:], weight[:], ACT.Exp, scale=-1.0).then_inc(powers_ready, 1)
            for m in range(4):
                act.wait_ge(projT, m + 1)
                nc.scalar.activation((rT, kT)[m // 2][:, (m % 2) * HALF:(m % 2 + 1) * HALF], bank[m][:], ACT.Copy)
            for half in range(2):
                act.wait_ge(proj, 3 + half)
                nc.scalar.activation(gate[:, 4 * half:4 * half + 4, :], rows_of(bank[6 + half][:], 4), ACT.Silu)

    ks, rs = st.sb("ks", [128, 2, T]), st.sb("rs", [128, 2, H, T])
    s, y = st.sb("s", [T, 2, Q, T]), st.sb("y", [T, 2, D])
    oT, yT, sq = rows_of(mixed["r"][:, 0:2 * T], 2), rows_of(mixed["r"][:, 2 * T:4 * T], 2), rows_of(mixed["r"][:, 4 * T:6 * T], 2)
    mean, var, rstd = st.sb("mean", [T, 2, H]), st.sb("var", [T, 2, H]), st.sb("rstd", [T, 2, H])
    power = st.sb("power", [T, H])
    oT_kept, o_made, staged, staged_too, scored, decayed, summed, var_ready, rstd_ready, y_ready, y_turned, yT_kept, made, added = (
        st.sem(x) for x in ("oT_kept", "o_made", "staged", "staged_too", "scored", "decayed", "summed", "var_ready", "rstd_ready", "y_ready", "y_turned",
                            "yT_kept", "made", "added"))
    score, ysum, yps, out = bank[0:4], bank[4:6], bank[6], bank[7]
    PER, LAG = 2 * UN, 9

    def unit_of(i, k):
        return PER * i + k, 2 * i + k // UN, k // UN % 2, k % UN, k % 2

    def ends(i, r, back):
        return has_unit(i, r, back, PER) and (r - back) % UN == UN - 1

    with nc.Block() as block:
        @block.gpsimd
        def _(pool):
            def stage(n, u):
                nc.gpsimd.tensor_tensor(rs[:, u, 0:H // 2, :], bc(rT[:, bass.ds(n * T, T)], 1, H // 2),
                                        bc(g.const["head"][:, 0:H // 2], 2, T), ALU.mult).then_inc(staged, 1)

            def step(i, r):
                if has_unit(i, r, -3, PER) and (r + 3) % UN == 0:
                    m, n, u, q, e = unit_of(i, r + 3)
                    pool.wait_ge(scored, done(UN * (n - 2) + UN - 1))
                    stage(n, u)
                if ends(i, r, 4):
                    m, n, u, q, e = unit_of(i, r - 4)
                    pool.wait_ge(var_ready, done(n))
                    nc.gpsimd.tensor_tensor(rstd[:, u, :], var[:, u, :], power[:], ALU.pow).then_inc(rstd_ready, 1)

            nc.gpsimd.memset(power[:], -0.5)
            credit(pool, staged, rstd_ready)
            stage(0, 0)
            pipeline(pool, step, PER, LAG)

        @block.tensor
        def _(pe):
            def step(i, r):
                if has_unit(i, r, 0, PER):
                    m, n, u, q, e = unit_of(i, r)
                    if q == 0:
                        pe.wait_ge(staged, done(n))
                        pe.wait_ge(staged_too, done(n))
                    pe.wait_ge(decayed, done(m - 4))
                    nc.tensor.matmul(score[r % 4][:], ks[:, u, :], rs[:, u, Q * q:Q * (q + 1), :],
                                     start=True, stop=True).then_inc(scored, 1)
                if has_unit(i, r, 2, PER):
                    m, n, u, q, e = unit_of(i, r - 2)
                    pe.wait_ge(decayed, done(m))
                    if q == 0:
                        pe.wait_ge(var_ready, done(n - 2))
                    for j in range(Q):
                        hd = Q * q + j
                        last = nc.tensor.matmul(ysum[u][:, 0:T], vh[:, u, hd * D:(hd + 1) * D], s[:, e, j, :],
                                                start=(hd == 0), stop=(hd == H - 1))
                    last.then_inc(summed, 1)
                if ends(i, r, 3):
                    m, n, u, q, e = unit_of(i, r - 3)
                    pe.wait_ge(oT_kept, done(n))
                    nc.tensor.transpose(ysum[u][:, T:2 * T], oT[:, u, :], g.ident).then_inc(o_made, 1)
                if ends(i, r, 7):
                    m, n, u, q, e = unit_of(i, r - 7)
                    pe.wait_ge(y_ready, done(n))
                    pe.wait_ge(yT_kept, done(n - 1))
                    nc.tensor.transpose(yps[:, 0:T], y[:, u, :], g.ident).then_inc(y_turned, 1)
                if ends(i, r, 8):
                    m, n, u, q, e = unit_of(i, r - 8)
                    pe.wait_ge(yT_kept, done(n))
                    pe.wait_ge(added, done(n - 1))
                    nc.tensor.matmul(out[:, 0:D], yT[:, u, :], w["w_o"], start=True, stop=True).then_inc(made, 1)

            credit(pe, o_made, scored, summed, y_turned, made)
            pipeline(pe, step, PER, LAG)

        @block.scalar
        def _(act):
            def stage(n, u):
                nc.scalar.activation(vh[:, u, :].rearrange("p (h x) -> p h x", h=H)[:, :, 0:HD], rows_of(v[:, n, :], H),
                                     ACT.Copy)
                nc.scalar.activation(ks[:, u, :], kT[:, bass.ds(n * T, T)], ACT.Copy)
                for h in range(H // 2, H):
                    last = nc.scalar.activation(rs[:, u, h, :], rT[:, bass.ds(n * T, T)], ACT.Copy,
                                                scale=g.const["head"][:, h:h + 1])
                last.then_inc(staged_too, 1)

            def step(i, r):
                if ends(i, r, 2):
                    m, n, u, q, e = unit_of(i, r - 2)
                    act.wait_ge(summed, done(m))
                    nc.scalar.activation(oT[:, u, :], ysum[u][:, 0:T], ACT.Copy).then_inc(oT_kept, 1)
                if has_unit(i, r, -2, PER) and (r + 2) % UN == 0:
                    m, n, u, q, e = unit_of(i, r + 2)
                    act.wait_ge(summed, done(UN * (n - 2) + UN - 1))
                    stage(n, u)
                if ends(i, r, 7):
                    m, n, u, q, e = unit_of(i, r - 7)
                    act.wait_ge(y_turned, done(n))
                    act.wait_ge(made, done(n - 2))
                    nc.scalar.activation(yT[:, u, :], yps[:, 0:T], ACT.Copy).then_inc(yT_kept, 1)

            credit(act, oT_kept, staged_too, yT_kept)
            stage(0, 0)
            pipeline(act, step, PER, LAG)

        @block.vector
        def _(dve):
            def center_outputs(n, u):
                heads = lambda t: t[:, u, :].rearrange("p (h d) -> p h d", h=H)
                dve.wait_ge(o_made, done(n))
                nc.vector.tensor_reduce(mean[:, u, :], rows_of(ysum[u][:, T:T + D], H), X, ALU.add)
                dve.drain()
                nc.vector.tensor_scalar(mean[:, u, :], mean[:, u, :], 1.0 / HD, None, ALU.mult)
                dve.drain()
                dve.wait_ge(y_turned, done(n - 2))
                nc.vector.tensor_tensor(heads(y), rows_of(ysum[u][:, T:T + D], H), bc(mean[:, u, :], 2, HD), ALU.subtract)
                dve.drain()
                nc.vector.tensor_tensor(sq[:, u, :], y[:, u, :], y[:, u, :], ALU.mult)
                dve.drain()
                nc.vector.tensor_reduce(var[:, u, :], heads(sq), X, ALU.add)
                dve.drain()
                nc.vector.tensor_scalar(var[:, u, :], var[:, u, :], 1.0 / HD, 64e-5, ALU.mult,
                                        ALU.add).then_inc(var_ready, 1)

            def norm_outputs(n, u):
                heads = lambda t: t[:, u, :].rearrange("p (h d) -> p h d", h=H)
                dve.wait_ge(rstd_ready, done(n))
                nc.vector.tensor_tensor(heads(y), heads(y), bc(rstd[:, u, :], 2, HD), ALU.mult)
                dve.drain()
                nc.vector.tensor_tensor(y[:, u, :], y[:, u, :], w["ln_g"], ALU.mult)
                dve.drain()
                nc.vector.tensor_tensor(y[:, u, :], y[:, u, :], w["ln_b"], ALU.add)
                dve.drain()
                nc.vector.tensor_tensor(y[:, u, :], y[:, u, :], gate[:, n, :], ALU.mult).then_inc(y_ready, 1)

            def step(i, r):
                if has_unit(i, r, 0, PER):
                    m, n, u, q, e = unit_of(i, r)
                    dve.wait_ge(scored, done(m))
                    dve.wait_ge(summed, done(m - 2))
                    nc.vector.tensor_tensor(s[:, e, :, :], rows_of(score[r % 4][:], Q), weight[:, Q * q:Q * (q + 1), :],
                                            ALU.mult).then_inc(decayed, 1)
                if ends(i, r, 3):
                    m, n, u, q, e = unit_of(i, r - 3)
                    center_outputs(n, u)
                if ends(i, r, 6):
                    m, n, u, q, e = unit_of(i, r - 6)
                    norm_outputs(n, u)
                if ends(i, r, LAG):
                    m, n, u, q, e = unit_of(i, r - LAG)
                    dve.wait_ge(made, done(n))
                    nc.vector.tensor_tensor(g.x[:, n, :], g.x[:, n, :], out[:, 0:D], ALU.add).then_inc(added, 1)

            credit(dve, decayed, var_ready, y_ready, added)
            pipeline(dve, step, PER, LAG)


def softplus_tail(nc, dve, e, u, log_u, fix):
    nc.vector.tensor_scalar(u, u, -1.0, None, ALU.add)
    dve.drain()
    nc.vector.tensor_scalar(fix, u, 0.0, None, ALU.is_equal)
    dve.drain()
    nc.vector.tensor_tensor(u, u, fix, ALU.add)
    nc.vector.tensor_tensor(log_u, log_u, fix, ALU.add)
    dve.drain()
    nc.vector.reciprocal(u, u)
    nc.vector.tensor_tensor(e, e, log_u, ALU.mult)
    dve.drain()
    nc.vector.tensor_tensor(e, e, u, ALU.mult)



def state_space(nc, g, w, st):
    NH, DH, DS, TAPS = 4, 64, 64, 4
    DI = NH * DH
    bank = g.bank
    raw = st.sb("raw", [128, 4, B, T + TAPS - 1])
    c = st.sb("c", [128, 4, B, T])
    z = st.sb("z", [T, B, DI])
    dt, e, u1, log_u, fix = (st.sb(x, [T, B, NH]) for x in ("dt", "e", "u1", "log_u", "fix"))
    a, rate = st.sb("a", [T, B, NH]), st.sb("rate", [T, NH])
    rows = (128, 128, DS, DS)
    proj, raw_kept, convolved, z_made, z_kept, dt_made, pads_set, abs_ready, e_ready, u_ready, log_ready, rate_ready = (
        st.sem(x) for x in ("proj", "raw_kept", "convolved", "z_made", "z_kept", "dt_made", "pads_set", "abs_ready",
                            "e_ready", "u_ready", "log_ready", "rate_ready"))
    with nc.Block() as block:
        @block.gpsimd
        def _(pool):
            nc.gpsimd.memset(raw[:, :, :, 0:TAPS - 1], 0.0).then_inc(pads_set, 1)

        @block.tensor
        def _(pe):
            pe.wait_ge(w.loaded, 16)
            for b in range(B):
                last = nc.tensor.matmul(bank[7][:, b * NH:(b + 1) * NH], g.hT[:, b * T:(b + 1) * T], w["w_dt"],
                                        start=True, stop=True)
            last.then_inc(dt_made, 1)
            at = 0
            for m in range(8):
                j, half = m // 2, m % 2
                if m >= 6:
                    pe.wait_ge(raw_kept, m - 5)
                nc.tensor.matmul(bank[m % 6][0:rows[j], :], w["w_conv"][:, at:at + rows[j]],
                                 g.hT[:, half * HALF:(half + 1) * HALF], start=True, stop=True).then_inc(proj, 1)
                at += rows[j] if half else 0
            pe.wait_ge(raw_kept, 8)
            for m in range(4):
                for q in range(2):
                    b = 2 * m + q
                    last = nc.tensor.matmul(bank[m][:, q * DI:(q + 1) * DI], g.hT[:, b * T:(b + 1) * T], w["w_z"],
                                            start=True, stop=True)
                last.then_inc(z_made, 1)

        @block.scalar
        def _(act):
            act.wait_ge(w.loaded, 16)
            nc.scalar.activation(rate[:], w["a_log"], ACT.Exp).then_inc(rate_ready, 1)
            act.wait_ge(abs_ready, 1)
            nc.scalar.activation(e[:], e[:], ACT.Exp, scale=-1.0).then_inc(e_ready, 1)
            act.wait_ge(u_ready, 1)
            nc.scalar.activation(log_u[:], u1[:], ACT.Ln).then_inc(log_ready, 1)
            act.wait_ge(pads_set, 1)
            for m in range(8):
                j, half = m // 2, m % 2
                act.wait_ge(proj, m + 1)
                nc.scalar.activation(raw[0:rows[j], j, 4 * half:4 * half + 4, TAPS - 1:],
                                     rows_of(bank[m % 6][0:rows[j], :], 4), ACT.Copy).then_inc(raw_kept, 1)
            for m in range(4):
                act.wait_ge(z_made, m + 1)
                nc.scalar.activation(z[:, 2 * m:2 * m + 2, :], rows_of(bank[m][:], 2), ACT.Silu)
            for j in range(4):
                act.wait_ge(convolved, j + 1)
                tile = c[0:rows[j], j, :, :]
                nc.scalar.activation(tile, tile, ACT.Silu, bias=w["conv_b"][0:rows[j], j:j + 1])

        @block.vector
        def _(dve):
            dve.wait_ge(w.loaded, 16)
            dve.wait_ge(dt_made, 1)
            nc.vector.tensor_tensor(dt[:], rows_of(bank[7][:, 0:B * NH], B), bc(w["dt_bias"], 1, B), ALU.add)
            dve.drain()
            nc.vector.scalar_tensor_tensor(e[:], dt[:], -1.0, dt[:], ALU.mult, ALU.max).then_inc(abs_ready, 1)
            dve.drain()
            nc.vector.tensor_scalar(dt[:], dt[:], 0.0, None, ALU.max)
            dve.wait_ge(e_ready, 1)
            nc.vector.tensor_scalar(u1[:], e[:], 1.0, None, ALU.add).then_inc(u_ready, 1)
            dve.wait_ge(log_ready, 1)
            softplus_tail(nc, dve, e[:], u1[:], log_u[:], fix[:])
            dve.drain()
            nc.vector.tensor_tensor(dt[:], dt[:], e[:], ALU.add)
            dve.drain()
            dve.wait_ge(rate_ready, 1)
            nc.vector.scalar_tensor_tensor(a[:], dt[:], -1.0, bc(rate[:], 1, B), ALU.mult, ALU.mult)
            for j in range(4):
                dve.wait_ge(raw_kept, 2 * j + 2)
                out = c[0:rows[j], j, :, :]
                for k in range(TAPS):
                    src = raw[0:rows[j], j, :, k:k + T]
                    tap = w["conv_w"][0:rows[j], j * TAPS + k:j * TAPS + k + 1]
                    if k == 0:
                        last = nc.vector.tensor_scalar(out, src, tap, None, ALU.mult)
                    else:
                        last = nc.vector.scalar_tensor_tensor(out, src, tap, out, ALU.mult, ALU.add)
                    if k < TAPS - 1:
                        dve.drain()
                last.then_inc(convolved, 1)

    xs, bcs = st.sb("xs", [128, 2, 2, T]), st.sb("bcs", [DS, 2, 2, T])
    later = st.sb("later", [T, 2, NH, T])
    decay, decay0 = st.sb("decay", [T, 2, NH, T]), st.sb("decay0", [T, 2, NH])
    cb = st.sb("cb", [T, 2, T])
    xt, xdt, base, y = (st.sb(x, [T, 2, DI]) for x in ("xt", "xdt", "base", "y"))
    sq, meansq, rstd, power = st.sb("sq", [T, DI]), st.sb("meansq", [T, 2]), st.sb("rstd", [T, 2]), st.sb("power", [T, 1])
    yT = st.sb("yT", [128, 2, 2, T])
    staged, exponents, prods, decay_ready, pairs, summed, y_made, rms_ready, y_ready, y_turned, yT_kept, made, added = (
        st.sem(x) for x in ("staged", "exponents", "prods", "decay_ready", "pairs", "summed", "y_made", "rms_ready", "y_ready",
                            "y_turned", "yT_kept", "made", "added"))
    heads = lambda t: t.rearrange("p (h d) -> p h d", h=NH)
    mixed, seg, xps, yps, out = bank[0:2], bank[2:4], bank[4:6], bank[6], bank[7]
    ysum = xps
    PER, LAG = 2, 4

    def sequence(i, k):
        return PER * i + k, k % 2

    with nc.Block() as block:
        @block.gpsimd
        def _(pool):
            def step(i, r):
                if has_unit(i, r, 0, PER):
                    n, u = sequence(i, r)
                    pool.wait_ge(prods, done(n - 2))
                    nc.gpsimd.tensor_copy(xs[:, u, :, :], c[:, 0:2, n, :])
                    nc.gpsimd.tensor_copy(bcs[:, u, :, :], c[0:DS, 2:4, n, :])
                    nc.gpsimd.tensor_tensor(later[:, u, :, :], bc(g.tables["gt"], 1, NH), bc(a[:, n, :], 2, T),
                                            ALU.mult).then_inc(staged, 1)
                if has_unit(i, r, 2, PER):
                    n, u = sequence(i, r - 2)
                    pool.wait_ge(y_made, done(n))
                    nc.gpsimd.tensor_tensor(rstd[:, u:u + 1], meansq[:, u:u + 1], power[:], ALU.pow).then_inc(rms_ready, 1)

            nc.gpsimd.memset(power[:], -0.5)
            credit(pool, staged, rms_ready)
            pipeline(pool, step, PER, LAG)

        @block.tensor
        def _(pe):
            def step(i, r):
                if has_unit(i, r, 0, PER):
                    n, u = sequence(i, r)
                    pe.wait_ge(staged, done(n))
                    pe.wait_ge(pairs, done(n - 2))
                    nc.tensor.matmul(mixed[u][:, 0:T], bcs[:, u, 0, :], bcs[:, u, 1, :], start=True, stop=True)
                    nc.tensor.matmul(mixed[u][:, T:T + DI], bcs[:, u, 1, :], w["init"], start=True, stop=True)
                    nc.tensor.matmul(mixed[u][:, T + DI:T + DI + NH], g.tables["le"], a[:, n, :], start=True, stop=True)
                    for h in range(NH):
                        last = nc.tensor.matmul(seg[u][:, h * T:(h + 1) * T], later[:, u, h, :], g.tables["le"],
                                                start=True, stop=True)
                    last.then_inc(exponents, 1)
                    pe.wait_ge(y_made, done(n - 2))
                    for j in range(2):
                        last = nc.tensor.transpose(xps[u][:, j * 128:(j + 1) * 128], xs[:, u, j, :], g.ident)
                    last.then_inc(prods, 1)
                if has_unit(i, r, 3, PER):
                    n, u = sequence(i, r - 3)
                    pe.wait_ge(yT_kept, done(n))
                    pe.wait_ge(added, done(n - 1))
                    for j in range(2):
                        last = nc.tensor.matmul(out[:, 0:D], yT[:, u, j, :], w["w_out"][:, j * D:(j + 1) * D],
                                                start=(j == 0), stop=(j == 1))
                    last.then_inc(made, 1)
                if has_unit(i, r, 1, PER):
                    n, u = sequence(i, r - 1)
                    pe.wait_ge(pairs, done(n))
                    for h in range(NH):
                        last = nc.tensor.matmul(ysum[u][:, h * DH:(h + 1) * DH], decay[:, u, h, :],
                                                xdt[:, u, h * DH:(h + 1) * DH], start=True, stop=True)
                    last.then_inc(summed, 1)
                if has_unit(i, r, 2, PER):
                    n, u = sequence(i, r - 2)
                    pe.wait_ge(y_ready, done(n))
                    pe.wait_ge(yT_kept, done(n - 1))
                    for j in range(2):
                        last = nc.tensor.transpose(yps[:, j * T:(j + 1) * T], y[:, u, j * 128:(j + 1) * 128], g.ident)
                    last.then_inc(y_turned, 1)

            credit(pe, exponents, prods, summed, y_turned, made)
            pipeline(pe, step, PER, LAG)

        @block.scalar
        def _(act):
            def step(i, r):
                if has_unit(i, r, 0, PER):
                    n, u = sequence(i, r)
                    act.wait_ge(exponents, done(n))
                    act.wait_ge(summed, done(n - 2))
                    nc.scalar.activation(decay[:, u, :, :], rows_of(seg[u][:], NH), ACT.Exp)
                    nc.scalar.activation(decay0[:, u, :], mixed[u][:, T + DI:T + DI + NH], ACT.Exp).then_inc(decay_ready, 1)
                if has_unit(i, r, 2, PER):
                    n, u = sequence(i, r - 2)
                    act.wait_ge(y_turned, done(n))
                    act.wait_ge(made, done(n - 2))
                    nc.scalar.activation(yT[:, u, :, :], rows_of(yps[:, 0:DI], 2), ACT.Copy).then_inc(yT_kept, 1)

            credit(act, decay_ready, yT_kept)
            pipeline(act, step, PER, LAG)

        @block.vector
        def _(dve):
            def step(i, r):
                if has_unit(i, r, LAG, PER):
                    n, u = sequence(i, r - LAG)
                    dve.wait_ge(made, done(n))
                    nc.vector.tensor_tensor(g.x[:, n, :], g.x[:, n, :], out[:, 0:D], ALU.add).then_inc(added, 1)
                if has_unit(i, r, 2, PER):
                    n, u = sequence(i, r - 2)
                    dve.wait_ge(rms_ready, done(n))
                    nc.vector.scalar_tensor_tensor(y[:, u, :], y[:, u, :], rstd[:, u:u + 1], w["norm_w"],
                                                   ALU.mult, ALU.mult).then_inc(y_ready, 1)
                if has_unit(i, r, 0, PER):
                    n, u = sequence(i, r)
                    dve.wait_ge(decay_ready, done(n))
                    dve.wait_ge(prods, done(n))
                    nc.vector.tensor_tensor(cb[:, u, :], mixed[u][:, 0:T], g.tables["le"], ALU.mult)
                    nc.vector.tensor_tensor(heads(base[:, u, :]), heads(mixed[u][:, T:T + DI]), bc(decay0[:, u, :], 2, DH),
                                            ALU.mult)
                    nc.vector.tensor_tensor(heads(xdt[:, u, :]), heads(xps[u][:, 0:DI]), bc(dt[:, n, :], 2, DH), ALU.mult)
                    nc.vector.tensor_tensor(heads(xt[:, u, :]), heads(xps[u][:, 0:DI]), bc(w["skip"], 2, DH), ALU.mult)
                    dve.drain()
                    nc.vector.tensor_tensor(decay[:, u, :, :], decay[:, u, :, :], bc(cb[:, u, :], 1, NH),
                                            ALU.mult).then_inc(pairs, 1)
                    nc.vector.tensor_tensor(base[:, u, :], base[:, u, :], xt[:, u, :], ALU.add)
                if has_unit(i, r, 1, PER):
                    n, u = sequence(i, r - 1)
                    dve.drain()
                    dve.wait_ge(summed, done(n))
                    nc.vector.tensor_tensor(base[:, u, :], base[:, u, :], ysum[u][:, 0:DI], ALU.add)
                    dve.drain()
                    dve.wait_ge(y_turned, done(n - 2))
                    nc.vector.tensor_tensor(y[:, u, :], base[:, u, :], z[:, n, :], ALU.mult)
                    dve.drain()
                    nc.vector.tensor_tensor(sq[:], y[:, u, :], y[:, u, :], ALU.mult)
                    dve.drain()
                    nc.vector.tensor_reduce(meansq[:, u:u + 1], sq[:], X, ALU.add)
                    dve.drain()
                    nc.vector.tensor_scalar(meansq[:, u:u + 1], meansq[:, u:u + 1], 1.0 / DI, 1e-5, ALU.mult,
                                            ALU.add).then_inc(y_made, 1)

            credit(dve, pairs, y_made, y_ready, added)
            pipeline(dve, step, PER, LAG)



def delta_gates(nc, g, w, st, rate_of, beta):
    NH = 12
    bank = g.bank
    e, u1, log_u, fix = (st.sb(x, [T, B, NH]) for x in ("e", "u1", "log_u", "fix"))
    a_rate = st.sb("a_rate", [T, NH])
    made, beta_in, beta_kept, abs_ready, e_ready, u_ready, log_ready = (
        st.sem(x) for x in ("made", "beta_in", "beta_kept", "abs_ready", "e_ready", "u_ready", "log_ready"))
    with nc.Block() as block:
        @block.tensor
        def _(pe):
            pe.wait_ge(w.loaded, 16)
            for j, name in enumerate(("w_rate", "w_beta")):
                for b in range(B):
                    last = nc.tensor.matmul(bank[j][:, b * NH:(b + 1) * NH], g.hT[:, b * T:(b + 1) * T], w[name],
                                            start=True, stop=True)
                last.then_inc(made, 1)

        @block.scalar
        def _(act):
            act.wait_ge(w.loaded, 16)
            nc.scalar.activation(a_rate[:], w["a_log"], ACT.Exp)
            act.wait_ge(abs_ready, 1)
            nc.scalar.activation(e[:], e[:], ACT.Exp, scale=-1.0).then_inc(e_ready, 1)
            act.wait_ge(u_ready, 1)
            nc.scalar.activation(log_u[:], u1[:], ACT.Ln).then_inc(log_ready, 1)
            act.wait_ge(beta_in, 1)
            nc.scalar.activation(beta[:], beta[:], ACT.Sigmoid).then_inc(beta_kept, 1)

        @block.vector
        def _(dve):
            dve.wait_ge(w.loaded, 16)
            nc.vector.tensor_scalar(w["wo"], w["wo"], w["o_norm"], None, ALU.mult)
            dve.wait_ge(made, 1)
            dt = rate_of
            nc.vector.tensor_tensor(dt[:], rows_of(bank[0][:, 0:B * NH], B), bc(w["dt_bias"], 1, B), ALU.add)
            dve.wait_ge(made, 2)
            nc.vector.tensor_tensor(beta[:], rows_of(bank[1][:, 0:B * NH], B), bc(w["b_b"], 1, B), ALU.add).then_inc(beta_in, 1)
            dve.drain()
            nc.vector.scalar_tensor_tensor(e[:], dt[:], -1.0, dt[:], ALU.mult, ALU.max).then_inc(abs_ready, 1)
            dve.drain()
            nc.vector.tensor_scalar(dt[:], dt[:], 0.0, None, ALU.max)
            dve.wait_ge(e_ready, 1)
            nc.vector.tensor_scalar(u1[:], e[:], 1.0, None, ALU.add).then_inc(u_ready, 1)
            dve.wait_ge(log_ready, 1)
            softplus_tail(nc, dve, e[:], u1[:], log_u[:], fix[:])
            dve.drain()
            nc.vector.tensor_tensor(dt[:], dt[:], e[:], ALU.add)
            dve.drain()
            nc.vector.scalar_tensor_tensor(dt[:], dt[:], -1.0, bc(a_rate[:], 1, B), ALU.mult, ALU.mult)


def delta_rule(nc, g, w, st):
    NH, DK, DV, TAPS, G = 12, 64, 128, 4, 4
    LEVELS = 6
    QK = 4
    ORDER = (2, 3, 0, 1, 4, 5, 6, 7)
    bank = g.bank
    rate, beta = st.sb("rate", [T, B, NH]), st.sb("beta", [T, B, NH])
    delta_gates(nc, g, w, st, rate, beta)

    c = g.region_a[:, 0:8 * TOK].rearrange("p (m b t) -> p m b t", m=8, b=B)
    raw = st.sb("raw", [128, 2, B, T + TAPS - 1])
    spare = g.region_b[:, w.tile.shape[1]:]
    gate = spare[:, 0:B * G * DV].rearrange("p (b d) -> p b d", b=B)
    sq = spare[:, B * G * DV:B * G * DV + TOK]
    rk, power = st.sb("rk", [T, B, G]), st.sb("power", [T, B, G])
    coef, vscale, qeps = (st.sb(x, [T, B, G]) for x in ("coef", "vscale", "qeps"))
    qks, kb, vs = st.sb("qks", [128, 2, QK, T]), st.sb("kb", [128, 2, G, T]), st.sb("vs", [DV, 2, G, T])
    later, mcoef = st.sb("later", [T, 2, G, T]), st.sb("mcoef", [T, 2, G, T])
    dec, A, P = st.sb("dec", [T, 2, G, T]), st.sb("A", [T, 2, G, T]), st.sb("P", [T, 2, G, T])
    W, V, join = st.sb("W", [T, 2, G, T]), st.sb("V", [T, 2, G, T]), st.sb("join", [T, 2, G, T])
    R, PT = st.sb("R", [T, 2, G, DV]), st.sb("PT", [T, 2, G, T])
    delta, o, osq, y, yT = P, dec, A, W, join
    ssum, rstd = st.sb("ssum", [T, 2, G]), st.sb("rstd", [T, 2, G])

    for hg in range(NH // G):
        with Stage(nc, f"{st.name}_{hg}") as group:
            names = ("pads_set", "power_set", "proj", "raw_kept", "tapped", "convolved", "silu_ready", "squared",
                     "norms_made", "norms_in", "norms_ready", "gate_made", "gate_kept")
            (pads_set, power_set, proj, raw_kept, tapped, convolved, silu_ready, squared, norms_made, norms_in,
             norms_ready, gate_made, gate_kept) = (group.sem(x) for x in names)
            heads_of = slice(hg * G, hg * G + G)

            def weights_of(m):
                name, j = ("q", 2 * hg + m) if m < 2 else ("k", 2 * hg + m - 2) if m < 4 else ("v", G * hg + m - 4)
                return w["w" + name][:, j * 128:(j + 1) * 128], w["conv_" + name][:, j * TAPS:(j + 1) * TAPS]

            with nc.Block() as block:
                @block.gpsimd
                def _(pool):
                    nc.gpsimd.memset(raw[:, :, :, 0:TAPS - 1], 0.0).then_inc(pads_set, 1)
                    nc.gpsimd.memset(power[:], -0.5).then_inc(power_set, 1)
                    pool.wait_ge(power_set, 1)
                    for m in range(QK):
                        pool.wait_ge(silu_ready, m + 1)
                        if m >= 1:
                            pool.wait_ge(norms_made, m)
                        tile = c[:, ORDER[m], :, :].rearrange("p b t -> p (b t)")
                        nc.gpsimd.tensor_tensor(sq, tile, tile, ALU.mult).then_inc(squared, 1)
                    pool.wait_ge(norms_in, 1)
                    nc.gpsimd.tensor_tensor(rk[:], rk[:], power[:], ALU.pow).then_inc(norms_ready, 1)

                @block.tensor
                def _(pe):
                    for m in range(8):
                        if m >= 3:
                            pe.wait_ge(raw_kept, m - 2)
                        for half in range(2):
                            last = nc.tensor.matmul(bank[2 * (m % 3) + half][:], weights_of(ORDER[m])[0],
                                                    g.hT[:, half * HALF:(half + 1) * HALF], start=True, stop=True)
                        last.then_inc(proj, 1)
                        if m >= 1:
                            pe.wait_ge(gate_kept, m)
                        nc.tensor.matmul(bank[7][:], g.hT[:, m * T:(m + 1) * T], w["wg"][:, hg * HALF:(hg + 1) * HALF],
                                         start=True, stop=True).then_inc(gate_made, 1)
                        if 3 <= m < 3 + QK:
                            pe.wait_ge(squared, m - 2)
                            if m == 5:
                                pe.wait_ge(norms_in, 1)
                            for b in range(B):
                                at = b * 2 * G + 2 * ORDER[m - 3]
                                last = nc.tensor.matmul(bank[6][:, at:at + 2], sq[:, b * T:(b + 1) * T], g.const["half"],
                                                        start=True, stop=True)
                            last.then_inc(norms_made, 1)

                @block.scalar
                def _(act):
                    for m in range(8 + 1):
                        if m < 8:
                            if m == 0:
                                act.wait_ge(pads_set, 1)
                            if m >= 2:
                                act.wait_ge(convolved, m - 1)
                            act.wait_ge(proj, m + 1)
                            for half in range(2):
                                last = nc.scalar.activation(raw[:, m % 2, 4 * half:4 * half + 4, TAPS - 1:],
                                                            rows_of(bank[2 * (m % 3) + half][:], 4), ACT.Copy)
                            last.then_inc(raw_kept, 1)
                            act.wait_ge(raw_kept, m + 1)
                            nc.scalar.activation(c[:, ORDER[m], :, :], raw[:, m % 2, :, 0:T], ACT.Copy,
                                                 scale=weights_of(ORDER[m])[1][:, 0:1]).then_inc(tapped, 1)
                            act.wait_ge(gate_made, m + 1)
                            nc.scalar.activation(gate[:, m, :], bank[7][:], ACT.Silu).then_inc(gate_kept, 1)
                        if m >= 1:
                            act.wait_ge(convolved, m)
                            tile = c[:, ORDER[m - 1], :, :]
                            nc.scalar.activation(tile, tile, ACT.Silu).then_inc(silu_ready, 1)

                @block.vector
                def _(dve):
                    for m in range(8):
                        dve.wait_ge(tapped, m + 1)
                        tile, taps = c[:, ORDER[m], :, :], weights_of(ORDER[m])[1]
                        for k in range(1, TAPS):
                            last = nc.vector.scalar_tensor_tensor(tile, raw[:, m % 2, :, k:k + T], taps[:, k:k + 1], tile,
                                                                  ALU.mult, ALU.add)
                            if k < TAPS - 1:
                                dve.drain()
                        last.then_inc(convolved, 1)
                        if m == 3:
                            dve.wait_ge(norms_made, 2)
                            nc.vector.tensor_scalar(rk[:], rows_of(bank[6][:, 0:B * 2 * G], B)[:, :, G:2 * G], 1e-6, None,
                                                    ALU.add).then_inc(norms_in, 1)
                    dve.wait_ge(norms_made, QK)
                    nc.vector.tensor_scalar(qeps[:], rows_of(bank[6][:, 0:B * 2 * G], B)[:, :, 0:G], 1e-6, 1e-5 * DK,
                                            ALU.add, ALU.mult)
                    dve.wait_ge(norms_ready, 1)
                    nc.vector.tensor_tensor(vscale[:], rk[:], beta[:, :, heads_of], ALU.mult)
                    dve.drain()
                    nc.vector.scalar_tensor_tensor(coef[:], vscale[:], -1.0, rk[:], ALU.mult, ALU.mult)

            names = ("keys_staged", "later_staged", "staged", "kk_made", "qk_made", "decay_made", "values_made", "dec_ready",
                     "a_ready", "p_made", "p_ready", "a_turned", "p_turned", "v_ready", "pT_kept", "joined", "v_turned",
                     "w0_ready", "w_kept", "join_kept", "grown", "grown_kept", "delta_made", "delta_kept", "o_made", "o_kept",
                     "squares_ready", "var_ready", "rstd_ready", "y_ready", "y_turned", "yT_kept", "out_made", "added",
                     "r_ready", "first_staged")
            (keys_staged, later_staged, staged, kk_made, qk_made, decay_made, values_made, dec_ready, a_ready, p_made,
             p_ready, a_turned, p_turned, v_ready, pT_kept, joined, v_turned, w0_ready, w_kept, join_kept, grown, grown_kept,
             delta_made, delta_kept, o_made, o_kept, squares_ready, var_ready, rstd_ready, y_ready, y_turned, yT_kept,
             out_made, added, r_ready, first_staged) = (group.sem(x) for x in names)

            def turned_level(n, l):
                return done((LEVELS - 1) * n + l - 1)

            def level_pair(n, l, j):
                return done(2 * (LEVELS * n + l) + j)

            def pair(t, u, j):
                return t[:, u, 2 * j:2 * j + 2, :]

            def four(t, u):
                return t[:, u, :, :]

            def flat(bk):
                return rows_of(bk[:], G)

            def all_steps(engine, step):
                step(0, 0, False, True)
                with engine.Fori(0, B // 2 - 1) as i:
                    step(2 * i + 1, 1, True, True)
                    step(2 * i + 2, 0, True, True)
                step(B - 1, 1, True, False)

            kk, qk, seg, vps = (lambda u, j=j: bank[4 * u + j] for j in range(4))

            def pair_bank(u, j):
                return (seg, vps)[j](u)
            with nc.Block() as block:
                @block.gpsimd
                def _(pool):
                    def stage_keys(n, u):
                        pool.wait_ge(qk_made, done(n - 2))
                        nc.gpsimd.tensor_copy(four(qks, u), c[:, 0:QK, n, :])
                        for j in range(2):
                            last = nc.gpsimd.tensor_tensor(kb[:, u, 2 * j:2 * j + 2, :], bc(c[:, 2 + j, n, :], 1, 2),
                                                           bc(g.const["half"], 2, T), ALU.mult)
                        last.then_inc(keys_staged, 1)
                        stage_decays(n, u)

                    def stage_decays(n, u):
                        pool.wait_ge(decay_made, done(n - 2))
                        nc.gpsimd.tensor_tensor(four(later, u), bc(g.tables["gt"], 1, G), bc(rate[:, n, heads_of], 2, T),
                                                ALU.mult).then_inc(later_staged, 1)

                    def stage_rest(n, u):
                        pool.wait_ge(a_ready, done(n - 2))
                        nc.gpsimd.tensor_tensor(four(mcoef, u), bc(g.tables["gt"], 1, G), bc(coef[:, n, :], 2, T),
                                                ALU.mult)
                        pool.wait_ge(values_made, done(n - 2))
                        nc.gpsimd.tensor_copy(four(vs, u), c[:, QK:8, n, :]).then_inc(staged, 1)

                    def first_blocks(n, u):
                        pool.wait_ge(a_ready, done(n))
                        nc.gpsimd.tensor_tensor(four(W, u), four(A, u), bc(g.tables["low0"], 1, G), ALU.mult)
                        pool.drain()
                        nc.gpsimd.tensor_tensor(four(W, u), four(W, u), bc(g.ident, 1, G), ALU.add).then_inc(w0_ready, 1)

                    def mask_p(n, u):
                        pool.wait_ge(p_made, done(n))
                        nc.gpsimd.tensor_tensor(four(P, u), four(P, u), bc(g.tables["ge"], 1, G),
                                                ALU.mult).then_inc(p_ready, 1)

                    def step(n, u, finish, begin):
                        if begin:
                            stage_keys(n + 1, 1 - u)
                        if finish:
                            pool.wait_ge(var_ready, done(n - 1))
                            nc.gpsimd.tensor_tensor(rstd[:, 1 - u, :], ssum[:, 1 - u, :], power[:, 0, 0:G],
                                                    ALU.pow).then_inc(rstd_ready, 1)
                        if begin:
                            stage_rest(n + 1, 1 - u)
                            mask_p(n + 1, 1 - u)
                            first_blocks(n + 1, 1 - u)

                    credit(pool, w0_ready, keys_staged, later_staged, staged, p_ready, rstd_ready)
                    pool.sem_inc(keys_staged, 1)
                    stage_decays(0, 0)
                    nc.gpsimd.tensor_tensor(four(mcoef, 0), bc(g.tables["gt"], 1, G), bc(coef[:, 0, :], 2, T),
                                            ALU.mult).then_inc(staged, 1)
                    mask_p(0, 0)
                    first_blocks(0, 0)
                    all_steps(pool, step)
                    pool.wait_ge(var_ready, done(B - 1))
                    nc.gpsimd.tensor_tensor(rstd[:, 1, :], ssum[:, 1, :], power[:, 0, 0:G], ALU.pow).then_inc(rstd_ready, 1)

                @block.tensor
                def _(pe):
                    def keys_by_keys(n, u):
                        pe.wait_ge(keys_staged, done(n))
                        pe.wait_ge(w_kept, turned_level(n - 2, LEVELS - 1))
                        for j in range(2):
                            last = nc.tensor.matmul(kk(u)[:, 2 * j * T:2 * (j + 1) * T], qks[:, u, 2 + j, :],
                                                    kb[:, u, 2 * j:2 * j + 2, :], start=True, stop=True)
                        last.then_inc(kk_made, 1)

                    def queries_by_keys(n, u):
                        pe.wait_ge(delta_kept, done(n - 2))
                        for j in range(2):
                            last = nc.tensor.matmul(qk(u)[:, 2 * j * T:2 * (j + 1) * T], qks[:, u, j, :],
                                                    kb[:, u, 2 * j:2 * j + 2, :], start=True, stop=True)
                        last.then_inc(qk_made, 1)

                    def decays(n, u):
                        pe.wait_ge(later_staged, done(n))
                        pe.wait_ge(squares_ready, done(n - 2))
                        nc.tensor.matmul(seg(u)[:], g.tables["le"], four(later, u), start=True,
                                         stop=True).then_inc(decay_made, 1)

                    def values(n, u):
                        pe.wait_ge(staged, done(n))
                        pe.wait_ge(added, done(n - 2))
                        for h in range(G):
                            last = nc.tensor.transpose(vps(u)[:, h * DV:(h + 1) * DV], vs[:, u, h, :], g.ident)
                        last.then_inc(values_made, 1)

                    def turn_a(n, u):
                        pe.wait_ge(a_ready, done(n))
                        for h in range(G):
                            last = nc.tensor.transpose(kk(u)[:, h * T:(h + 1) * T], A[:, u, h, :], g.ident)
                        last.then_inc(a_turned, 1)

                    def turn_p(n, u):
                        pe.wait_ge(p_ready, done(n))
                        for h in range(G):
                            last = nc.tensor.transpose(qk(u)[:, h * T:(h + 1) * T], P[:, u, h, :], g.ident)
                        last.then_inc(p_turned, 1)

                    def deltas(n, u):
                        pe.wait_ge(grown_kept, level_pair(n, LEVELS - 1, 1))
                        pe.wait_ge(pT_kept, done(n))
                        pe.wait_ge(r_ready, done(n))
                        for h in range(G):
                            last = nc.tensor.matmul(qk(u)[:, h * DV:(h + 1) * DV], V[:, u, h, :], R[:, u, h, :],
                                                    start=True, stop=True)
                        last.then_inc(delta_made, 1)

                    def outputs(n, u):
                        pe.wait_ge(delta_kept, done(n))
                        for h in range(G):
                            last = nc.tensor.matmul(seg(u)[:, h * DV:(h + 1) * DV], PT[:, u, h, :], delta[:, u, h, :],
                                                    start=True, stop=True)
                        last.then_inc(o_made, 1)

                    def turn_y(n, u):
                        pe.wait_ge(y_ready, done(n))
                        for h in range(G):
                            last = nc.tensor.transpose(vps(u)[:, h * T:(h + 1) * T], y[:, u, h, :], g.ident)
                        last.then_inc(y_turned, 1)

                    def project(n, u):
                        pe.wait_ge(yT_kept, done(n))
                        for h in range(G):
                            at = (hg * G + h) * D
                            last = nc.tensor.matmul(vps(u)[:, 0:D], yT[:, u, h, :], w["wo"][:, at:at + D],
                                                    start=(h == 0), stop=(h == G - 1))
                        last.then_inc(out_made, 1)

                    def step(n, u, finish, begin):
                        gaps = [(deltas, outputs), (keys_by_keys, queries_by_keys), (decays, turn_y), (project, None),
                                (values, turn_a), (turn_p, None)]

                        def fill(part):
                            if finish and part in (deltas, outputs, turn_y, project):
                                part(n - 1, 1 - u)
                            if begin and part in (keys_by_keys, queries_by_keys, decays, values, turn_a, turn_p):
                                part(n + 1, 1 - u)

                        for l in range(LEVELS):
                            if l == 0:
                                pe.wait_ge(v_ready, done(n))
                                pe.wait_ge(r_ready, done(n))
                            for j in range(2):
                                if l > 0:
                                    pe.wait_ge(grown_kept, level_pair(n, l - 1, j))
                                for h in (2 * j, 2 * j + 1):
                                    last = nc.tensor.matmul(pair_bank(u, j)[:, h % 2 * T:(h % 2 + 1) * T], A[:, u, h, :],
                                                            V[:, u, h, :], start=True, stop=True)
                                last.then_inc(joined, 1)
                            if l > 0:
                                for h in range(G):
                                    last = nc.tensor.transpose(kk(u)[:, h * T:(h + 1) * T], V[:, u, h, :], g.ident)
                                last.then_inc(v_turned, 1)
                            fill(gaps[l][0])
                            if l == 0:
                                pe.wait_ge(w0_ready, done(n))
                            else:
                                pe.wait_ge(w_kept, turned_level(n, l))
                            for j in range(2):
                                pe.wait_ge(join_kept, level_pair(n, l, j))
                                for h in (2 * j, 2 * j + 1):
                                    last = nc.tensor.matmul(pair_bank(u, j)[:, h % 2 * T:(h % 2 + 1) * T], W[:, u, h, :],
                                                            join[:, u, h, :], start=True, stop=True)
                                last.then_inc(grown, 1)
                            fill(gaps[l][1])

                    credit(pe, kk_made, qk_made, decay_made, values_made, a_turned, p_turned, joined, v_turned, grown,
                           delta_made, o_made, y_turned, out_made)
                    decays(0, 0)
                    pe.wait_ge(first_staged, 1)
                    for part in (keys_by_keys, queries_by_keys):
                        part(0, 0)
                    pe.wait_ge(first_staged, 2)
                    for part in (values, turn_a, turn_p):
                        part(0, 0)
                    all_steps(pe, step)
                    for part in (deltas, outputs, turn_y, project):
                        part(B - 1, 1)

                @block.scalar
                def _(act):
                    def keep(ready, dst, src, kept, n, u):
                        act.wait_ge(ready, done(n))
                        nc.scalar.activation(four(dst, u), flat(src(u)), ACT.Copy).then_inc(kept, 1)

                    def exp_decays(n, u):
                        act.wait_ge(decay_made, done(n))
                        act.wait_ge(y_ready, done(n - 2))
                        nc.scalar.activation(four(dec, u), flat(seg(u)), ACT.Exp).then_inc(dec_ready, 1)

                    def square(n, u):
                        nc.scalar.activation(four(osq, u), flat(seg(u)), ACT.Square).then_inc(squares_ready, 1)

                    def step(n, u, finish, begin):
                        def keep_w(l):
                            act.wait_ge(v_turned, turned_level(n, l))
                            nc.scalar.activation(four(W, u), flat(kk(u)), ACT.Copy).then_inc(w_kept, 1)

                        if finish:
                            keep(delta_made, delta, qk, delta_kept, n - 1, 1 - u)
                            keep(o_made, o, seg, o_kept, n - 1, 1 - u)
                            square(n - 1, 1 - u)
                        keep_w(1)
                        keep_w(2)
                        if begin:
                            exp_decays(n + 1, 1 - u)
                        if finish:
                            keep(y_turned, yT, vps, yT_kept, n - 1, 1 - u)
                        keep_w(3)
                        keep_w(4)
                        keep_w(5)
                        if begin:
                            keep(p_turned, PT, qk, pT_kept, n + 1, 1 - u)

                    credit(act, dec_ready, pT_kept, w_kept, delta_kept, o_kept, squares_ready, yT_kept)
                    exp_decays(0, 0)
                    keep(p_turned, PT, qk, pT_kept, 0, 0)
                    all_steps(act, step)
                    keep(delta_made, delta, qk, delta_kept, B - 1, 1)
                    keep(o_made, o, seg, o_kept, B - 1, 1)
                    square(B - 1, 1)
                    keep(y_turned, yT, vps, yT_kept, B - 1, 1)

                @block.vector
                def _(dve):
                    def square_sums(n, u):
                        dve.wait_ge(squares_ready, done(n))
                        nc.vector.tensor_reduce(ssum[:, u, :], four(osq, u), X, ALU.add)
                        dve.drain()
                        nc.vector.scalar_tensor_tensor(ssum[:, u, :], ssum[:, u, :], 1.0 / DV, qeps[:, n, :], ALU.mult,
                                                       ALU.add).then_inc(var_ready, 1)

                    def gate_outputs(n, u):
                        dve.wait_ge(o_kept, done(n))
                        nc.vector.tensor_tensor(four(y, u), four(o, u), rows_of(gate[:, n, :], G), ALU.mult)

                    def norm_outputs(n, u):
                        dve.drain()
                        dve.wait_ge(rstd_ready, done(n))
                        nc.vector.tensor_tensor(four(y, u), four(y, u), bc(rstd[:, u, :], 2, DV), ALU.mult).then_inc(y_ready, 1)

                    def add_outputs(n, u):
                        dve.wait_ge(out_made, done(n))
                        nc.vector.tensor_tensor(g.x[:, n, :], g.x[:, n, :], vps(u)[:, 0:D], ALU.add).then_inc(added, 1)

                    def decayed_keys(n, u):
                        dve.wait_ge(kk_made, done(n))
                        dve.wait_ge(dec_ready, done(n))
                        nc.vector.tensor_tensor(four(A, u), flat(kk(u)), four(dec, u), ALU.mult)

                    def scale_a(n, u):
                        dve.drain()
                        dve.wait_ge(staged, done(n))
                        nc.vector.tensor_tensor(four(A, u), four(A, u), four(mcoef, u), ALU.mult).then_inc(a_ready, 1)

                    def decayed_scores(n, u):
                        dve.wait_ge(qk_made, done(n))
                        nc.vector.tensor_tensor(four(P, u), flat(qk(u)), four(dec, u), ALU.mult).then_inc(p_made, 1)

                    def scale_values(n, u):
                        dve.wait_ge(values_made, done(n))
                        nc.vector.tensor_tensor(four(R, u), flat(vps(u)), bc(vscale[:, n, :], 2, DV),
                                                ALU.mult).then_inc(r_ready, 1)

                    def first_blocks(n, u):
                        dve.wait_ge(a_turned, done(n))
                        nc.vector.tensor_tensor(four(V, u), flat(kk(u)), bc(g.tables["join0"], 1, G), ALU.mult)
                        dve.drain()
                        nc.vector.tensor_tensor(four(V, u), four(V, u), bc(g.ident, 1, G), ALU.add).then_inc(v_ready, 1)

                    def step(n, u, finish, begin):
                        def keep_join(l):
                            for j in range(2):
                                dve.wait_ge(joined, level_pair(n, l, j))
                                nc.vector.tensor_tensor(pair(join, u, j), rows_of(pair_bank(u, j)[:, 0:2 * T], 2),
                                                        bc(g.tables[f"join{l + 1}"], 1, 2), ALU.mult).then_inc(join_kept, 1)

                        def grow(l):
                            for j in range(2):
                                dve.wait_ge(grown, level_pair(n, l, j))
                                nc.vector.tensor_tensor(pair(V, u, j), pair(V, u, j), rows_of(pair_bank(u, j)[:, 0:2 * T], 2),
                                                        ALU.add).then_inc(grown_kept, 1)

                        keep_join(0)
                        grow(0)
                        keep_join(1)
                        if finish:
                            square_sums(n - 1, 1 - u)
                        grow(1)
                        if finish:
                            gate_outputs(n - 1, 1 - u)
                        keep_join(2)
                        if finish:
                            norm_outputs(n - 1, 1 - u)
                        grow(2)
                        keep_join(3)
                        if begin:
                            decayed_keys(n + 1, 1 - u)
                        grow(3)
                        if finish:
                            add_outputs(n - 1, 1 - u)
                        if begin:
                            scale_a(n + 1, 1 - u)
                        keep_join(4)
                        if begin:
                            decayed_scores(n + 1, 1 - u)
                        grow(4)
                        if begin:
                            scale_values(n + 1, 1 - u)
                        keep_join(5)
                        if begin:
                            first_blocks(n + 1, 1 - u)
                        grow(5)

                    credit(dve, a_ready, p_made, v_ready, r_ready, join_kept, grown_kept, var_ready, y_ready, added)
                    nc.vector.tensor_copy(four(qks, 0), c[:, 0:QK, 0, :])
                    for j in range(2):
                        last = nc.vector.tensor_tensor(kb[:, 0, 2 * j:2 * j + 2, :], bc(c[:, 2 + j, 0, :], 1, 2),
                                                       bc(g.const["half"], 2, T), ALU.mult)
                    last.then_inc(first_staged, 1)
                    nc.vector.tensor_copy(four(vs, 0), c[:, QK:8, 0, :]).then_inc(first_staged, 1)
                    decayed_keys(0, 0)
                    scale_a(0, 0)
                    decayed_scores(0, 0)
                    first_blocks(0, 0)
                    scale_values(0, 0)
                    all_steps(dve, step)
                    square_sums(B - 1, 1)
                    gate_outputs(B - 1, 1)
                    norm_outputs(B - 1, 1)
                    add_outputs(B - 1, 1)


STAGES = [
    ("L0_attn", multi_query_attention), ("L0_xattn", attention_with_mlp), ("L0_ffn", ternary_ffn),
    ("L1_attn", state_space), ("L1_xattn", cross_attention), ("L1_ffn", gated_experts),
    ("L2_attn", delta_rule), ("L2_xattn", cross_attention), ("L2_ffn", many_experts),
    ("L3_attn", time_mix), ("L3_xattn", masked_cross_attention), ("L3_ffn", wide_experts),
]



def build(nc, dram, out, layouts, first=0, last=12):
    g = Net()
    g.dram = dram
    g.bank = [nc.alloc_psum_tensor(f"bank{n}", [128, HALF], F32) for n in range(8)]
    g.bank_bf = [t[:].bitcast(BF16) for t in g.bank]
    sb = nc.alloc_sbuf_tensor
    g.x, g.h = sb("x", [T, B, D], F32), sb("h", [T, B, D], F32)
    g.hT, g.ctxT = sb("hT", [D, TOK], F32), sb("ctxT", [D, TOK], F32)
    g.ident_bf = sb("ident_bf", [T, T], BF16)
    g.causal_bf, g.shifted_bf = sb("causal_bf", [T, 1, T], BF16), sb("shifted_bf", [T, 1, T], BF16)
    g.norm_scratch = [sb(f"norm_{n}", [T, B] + [D] * (n == "squares"), F32)
                      for n in ("total", "mean", "squares", "sumsq", "var", "rstd", "power")]
    x_loaded, stored = nc.alloc_semaphore("x_loaded"), nc.alloc_semaphore("stored")
    g.x_loaded = x_loaded

    g.region_a = sb("region_a", [128, max(layouts[n][1] for n in ("L1_ffn", "L2_ffn"))], F32)
    first_b = ("L0_attn", "L0_xattn", "L0_ffn")
    g.region_b = sb("region_b", [128, max(sum(layouts[n][1] for n in first_b), layouts["L2_attn"][1],
                                          layouts["L3_ffn"][1])], F32)

    def place(name):
        places, cols = layouts[name]
        if name in ("L1_ffn", "L2_ffn"):
            tile = g.region_a[:, 0:cols]
        elif name in ("L2_attn", "L3_ffn"):
            tile = g.region_b[:, 0:cols]
        elif name in first_b:
            at = sum(layouts[n][1] for n in first_b[:first_b.index(name)])
            tile = g.region_b[:, at:at + cols]
        else:
            tile = sb(f"w_{name}", [128, cols], F32)[:]
        return Pack(tile, places, nc.alloc_semaphore(f"{name}_loaded"))

    g.const, g.tables = place("const"), place("tables")
    run = STAGES[first:last]
    packs = {name: place(name) for name, _ in run}
    late = {"L1_attn": ["L2_attn"], "L2_xattn": ["L2_ffn", "L3_ffn"]}
    late = {at: [n for n in names if n in packs] if at in packs else [] for at, names in late.items()}
    g.ident = g.const["ident"]
    early = [name for name, _ in run if not any(name in names for names in late.values())]
    early.insert(3, "tables")
    packs["tables"] = g.tables
    turn_context(nc, g, [(packs[n], dram[n]) for n in early])
    tables_from = next((name for name, _ in run if name in [n for n, _ in STAGES[3:]]), None)
    for name, stage in run:
        with Stage(nc, name) as st:
            values = stage in (cross_attention, masked_cross_attention, attention_with_mlp)
            keys = values and stage is not attention_with_mlp
            st.beside = ContextProducts(nc, g, packs[name], st, keys) if values else Nothing()
            layer_norm(nc, g, st, [(packs[n], dram[n]) for n in late.get(name, [])],
                       [g.tables] if name == tables_from else [], st.beside)
            stage(nc, g, packs[name], st)
    with nc.Block() as block:
        @block.sync
        def _(sp):
            sp.dma_start(out.rearrange("b t d -> t b d"), g.x[:]).then_inc(stored, 16)
            sp.wait_ge(stored, 16)



def constants():
    r, c = np.arange(128)[:, None], np.arange(128)[None, :]
    f = np.float32
    return [
        ("ident", np.eye(128, dtype=f)),
        ("head", (r // HD == np.arange(H)[None, :]).astype(f)),
        ("half", (r // 64 == np.arange(2)[None, :]).astype(f)),
        ("neg_causal", np.where(c <= r, 0.0, NEG).astype(f)),
        ("neg_shifted", np.where((c < r) | ((c == 0) & (r == 0)), 0.0, NEG).astype(f)),
        ("ones", np.ones((128, 128), f)),
    ]


def tables():
    r, c = np.arange(128)[:, None], np.arange(128)[None, :]
    f = np.float32
    return [
        ("le", (r <= c).astype(f)),
        ("gt", (r > c).astype(f)),
        ("lt", (r < c).astype(f)),
        ("ge", (r >= c).astype(f)),
        *[(f"join{l}", (r >> l + 1 == c >> l + 1).astype(f) * (r >> l < c >> l)) for l in range(7)],
        ("low0", ((r >> 1 == c >> 1) & (r > c)).astype(f)),
        ("steps", np.maximum(c - r - 1, 0).astype(f)),
    ]


def packed(pieces):
    places, at = {}, 0
    for name, a in pieces:
        places[name] = (at, a.shape[0], a.shape[1])
        at += a.shape[1]
    whole = np.zeros((128, at), np.float32)
    for name, a in pieces:
        whole[:a.shape[0], places[name][0]:places[name][0] + a.shape[1]] = a
    return whole, (places, at)


def every_row(v, rows=128):
    return np.repeat(np.asarray(v).reshape(1, -1), rows, 0)


def side_by_side(a):
    return np.ascontiguousarray(np.asarray(a).transpose(1, 0, 2)).reshape(a.shape[1], -1)


def column_tiles(a, p=128):
    a = np.asarray(a)
    return side_by_side(a.reshape(-1, p, a.shape[1]))


def column(v):
    return np.asarray(v).reshape(-1, 1)


def attention_pieces(weights, biases=None):
    pieces = [(n, np.ascontiguousarray(a.T)) for n, a in zip(("wq", "wk", "wv", "wo"), weights)]
    if biases is None:
        zeros = np.zeros(D, np.float32)
        return pieces + [("bq", column(zeros)), ("bk", column(zeros)), ("bv", every_row(zeros))]
    bq, bk, bv, bo = biases
    return pieces + [("bq", column(bq)), ("bk", column(bk)), ("bv", every_row(bv)), ("bo", every_row(bo))]


def state_space_pieces(i):
    w_in, conv_w, conv_b = i["L1_attn_in_proj_w"], i["L1_attn_conv_w"], i["L1_attn_conv_b"]
    parts = ((0, 128), (128, 256), (256, 320), (320, 384))
    taps, shift = np.zeros((128, 4, 4), np.float32), np.zeros((128, 4), np.float32)
    for j, (lo, hi) in enumerate(parts):
        taps[:hi - lo, j] = conv_w[lo:hi]
        shift[:hi - lo, j] = conv_b[lo:hi]
    return [("w_z", w_in[0:256].T), ("w_conv", w_in[256:640].T), ("w_dt", w_in[640:644].T),
            ("conv_w", taps.reshape(128, 16)), ("conv_b", shift),
            ("init", i["L1_attn_init_states"].transpose(2, 0, 1).reshape(64, 256)),
            ("dt_bias", every_row(i["L1_attn_dt_bias"])), ("a_log", every_row(i["L1_attn_A_log"])),
            ("skip", every_row(i["L1_attn_D"])), ("norm_w", every_row(i["L1_attn_norm_w"])),
            ("w_out", column_tiles(i["L1_attn_out_proj_w"].T))]


def pieces_of(i):
    null = i["L0_attn_null_kv"]
    null2 = np.zeros((128, 2), np.float32)
    null2[:64, 0] = null
    null2[64:, 1] = null
    return {
        "const": constants(),
        "tables": tables(),
        "L0_attn": [("wq", i["L0_attn_Wq"]), ("wkv2", np.concatenate([i["L0_attn_Wkv"]] * 2, 1)),
                    ("wout", column_tiles(i["L0_attn_Wout"])), ("null2", null2),
                    ("wqT", column_tiles(i["L0_attn_Wq"].T)), ("null_row", every_row(np.append(null, np.float32(1))))],
        "L0_xattn": [("wq", i["L0_xattn_Wq"]), ("wk", i["L0_xattn_Wk"]), ("wv", i["L0_xattn_Wv"]),
                     ("bq", column(i["L0_xattn_bq"])), ("bk", column(i["L0_xattn_bk"])),
                     ("bv", every_row(i["L0_xattn_bv"])), ("w1", i["L0_xattn_W1"]),
                     ("b1", i["L0_xattn_b1"].reshape(4, 128).T), ("w2", column_tiles(i["L0_xattn_W2"])),
                     ("b2", every_row(i["L0_xattn_b2"]))],
        "L1_attn": state_space_pieces(i),
        "L2_attn": [("w" + c.lower(), i["L2_attn_W" + c]) for c in "qkvg"]
                   + [("conv_" + c, column_tiles(i["L2_attn_conv_" + c])) for c in "qkv"]
                   + [("wo", column_tiles(i["L2_attn_Wo"])), ("w_rate", i["L2_attn_Wgk"]), ("w_beta", i["L2_attn_Wb"]),
                      ("b_b", every_row(i["L2_attn_b_b"])), ("a_log", every_row(i["L2_attn_A_log"])),
                      ("dt_bias", every_row(i["L2_attn_dt_bias"])), ("o_norm", column(i["L2_attn_g_norm_weight"]))],
        "L0_ffn": [("gate", i["L0_ffn_w_gate"].T), ("up", i["L0_ffn_w_up"].T),
                   ("down", column_tiles(i["L0_ffn_w_down"].T))],
        "L3_attn": [("w_" + c, i[f"L3_attn_w_{c}"].T) for c in "rkvgo"]
                   + [("maa_" + c, column(i[f"L3_attn_time_maa_{c}"])) for c in "rkvg"]
                   + [("decay", every_row(i["L3_attn_time_decay"])), ("bonus", every_row(i["L3_attn_time_faaaa"])),
                      ("ln_g", every_row(i["L3_attn_ln_g"])), ("ln_b", every_row(i["L3_attn_ln_b"]))],
        "L1_ffn": [("router", i["L1_ffn_router_w"]), ("router_scale", column(i["L1_ffn_router_scale"])),
                   ("expert_scale", every_row(i["L1_ffn_per_expert_scale"])),
                   ("up", i["L1_ffn_gating_w"].transpose(3, 0, 1, 2).reshape(D, -1)),
                   ("down", column_tiles(i["L1_ffn_linear_w"].reshape(-1, D)))],
        "L2_ffn": [("router", i["L2_ffn_router_w"].T), ("correction", every_row(i["L2_ffn_correction_bias"])),
                   ("up", np.concatenate([side_by_side(i["L2_ffn_up_w"]), i["L2_ffn_shared_up_w"]], 1)),
                   ("down", np.concatenate([column_tiles(i["L2_ffn_down_w"].reshape(-1, D)),
                                            column_tiles(i["L2_ffn_shared_down_w"])], 1))],
        "L3_ffn": [("router", i["L3_ffn_Wr"]), ("br", every_row(i["L3_ffn_br"])), ("b2", i["L3_ffn_b2"]),
                   ("up", side_by_side(i["L3_ffn_W1"])), ("b1", every_row(i["L3_ffn_b1"])),
                   ("down", column_tiles(i["L3_ffn_W2"].reshape(-1, D)))],
        "L1_xattn": attention_pieces([i[f"L1_xattn_w{c}_w"] for c in "qkvo"], [i[f"L1_xattn_w{c}_b"] for c in "qkvo"]),
        "L2_xattn": attention_pieces([i[f"L2_xattn_w_{c}"] for c in "qkvo"], [i[f"L2_xattn_b_{c}"] for c in "qkvo"]),
        "L3_xattn": attention_pieces([i[f"L3_xattn_W{c}"] for c in "qkvo"]),
    }


def laid_out(inputs):
    inputs = {k: np.asarray(v) for k, v in inputs.items()}
    arrays, layouts = {}, {}
    for name, pieces in pieces_of(inputs).items():
        arrays[name], layouts[name] = packed(pieces)
    arrays["x"] = np.ascontiguousarray(inputs["x"])
    arrays["ctx_1024"] = np.ascontiguousarray(inputs["ctx_1024"])
    arrays["mask"] = np.ascontiguousarray(inputs["mask_BxSxS2_bf0"])
    return arrays, layouts


def program(nc, arrays, layouts, first=0, last=12):
    dram = {k: nc.dram_tensor(f"in_{k}", a.shape, mybir.dt.from_np(a.dtype), kind="ExternalInput").ap()
            for k, a in arrays.items()}
    out = nc.dram_tensor("out", (B, T, D), F32, kind="ExternalOutput").ap()
    build(nc, dram, out, layouts, first, last)


def kernel(**inputs):
    import concourse.bacc as bacc
    from concourse.bass_utils import run_bass_kernel_spmd

    nc = bacc.Bacc("TRN2", target_bir_lowering=False, num_devices=1)
    arrays, layouts = laid_out(inputs)
    program(nc, arrays, layouts)
    r = run_bass_kernel_spmd(nc, [{f"in_{k}": a for k, a in arrays.items()}], core_ids=[0])
    return r.results[0]["out"]
```
